# Optimizing a Trainium2 kernel written in Bass

```python
import numpy as np
import jax
import jax.numpy as jnp

def _softmax(x, axis=-1):
    return jax.nn.softmax(x, axis=axis)

def _gelu(x):
    return jax.nn.gelu(x, approximate=True)

def _silu(x):
    return jax.nn.silu(x)

def _sigmoid(x):
    return jax.nn.sigmoid(x)

def _layernorm(x, axis=-1, eps=1e-05):
    m = jnp.mean(x, axis=axis, keepdims=True)
    v = jnp.var(x, axis=axis, keepdims=True)
    return (x - m) / jnp.sqrt(v + eps)

def _scatter_add(tgt, idx, src, axis=0):
    return tgt.at[idx].add(src)

def _segment_sum(src, seg, n):
    return jax.ops.segment_sum(src, seg, n)
kernel_name = 'mk_perceiver_d4_seqx_r8_39d433'

def setup_inputs(seed: int=0):
    np.random.seed(seed)
    _w = jnp.asarray

    def _rec_inputs():
        import jax
        import jax.numpy as jnp
        _rk = jax.random.key(seed)
        x = -0.0002928 + 1 * jax.random.normal(jax.random.fold_in(_rk, 1), (128, 32, 128), jnp.float32)
        _lenS = 32 - jax.random.randint(jax.random.fold_in(_rk, 7), (128,), 0, max(1, 32 // 4) + 1, jnp.int32)
        _lenS2 = 257 - jax.random.randint(jax.random.fold_in(_rk, 8), (128,), 0, max(1, 257 // 4) + 1, jnp.int32)
        _ctx_1024P = jax.random.normal(jax.random.fold_in(_rk, 11), (128, 16, 128), jnp.float32)
        _ctx_1024c = jax.random.dirichlet(jax.random.fold_in(_rk, 511), 0.3 * jnp.ones((16,), jnp.float32), (128, 257))
        _ctx_1024t = jnp.einsum('bsk,bkd->bsd', _ctx_1024c, _ctx_1024P)
        _ctx_1024t = _ctx_1024t * jax.lax.rsqrt(jnp.mean(jnp.square(_ctx_1024t)) + 1e-12) * 0.953939
        ctx_1024 = 4.13588e-05 + 0.999923 * (_ctx_1024t + 0.3 * jax.random.normal(jax.random.fold_in(_rk, 611), (128, 257, 128), jnp.float32))
        _validS = jnp.arange(32)[None, :] < _lenS[:, None]
        _validS2 = jnp.arange(257)[None, :] < _lenS2[:, None]
        _causal = jnp.tril(jnp.ones((32, 32), dtype=bool))
        mask_BxS2_bk0 = jnp.logical_not(jnp.broadcast_to(_validS2[:, :], (128, 257)))
        mask_BxS2_bf1 = jnp.ones((128, 257), dtype=bool)
        return (x, ctx_1024, mask_BxS2_bk0, mask_BxS2_bf1)
    x, ctx_1024, mask_BxS2_bk0, mask_BxS2_bf1 = _rec_inputs()

    def _L0_xattn_setup():
        import jax, jax.numpy as jnp
        import numpy as np
        D_MODEL = 128
        N_HEAD = 16
        D_H = D_MODEL // N_HEAD
        key = jax.random.key(seed)
        ks = jax.random.split(key, 12)
        B, LQ, LK = (4, 128, 256)
        s = 1.0 / np.sqrt(D_MODEL)
        inp = {'q_input': jax.random.normal(ks[0], (B, LQ, D_MODEL), jnp.float32), 'kv_input': jax.random.normal(ks[1], (B, LK, D_MODEL), jnp.float32), 'key_padding_mask': jax.random.randint(ks[2], (B, LK), 0, 2) > 0, 'W_Q': jax.random.normal(ks[3], (D_MODEL, D_MODEL), jnp.float32) * s, 'b_Q': jnp.zeros((D_MODEL,), jnp.float32), 'W_K': jax.random.normal(ks[4], (D_MODEL, D_MODEL), jnp.float32) * s, 'b_K': jnp.zeros((D_MODEL,), jnp.float32), 'W_V': jax.random.normal(ks[5], (D_MODEL, D_MODEL), jnp.float32) * s, 'b_V': jnp.zeros((D_MODEL,), jnp.float32), 'W_O': jax.random.normal(ks[6], (D_MODEL, D_MODEL), jnp.float32) * s, 'b_O': jnp.zeros((D_MODEL,), jnp.float32)}
        return inp
    _L0_xattn_all = _L0_xattn_setup()
    _L0_xattn_in = {k: v for k, v in _L0_xattn_all.items() if k in ('W_Q', 'b_Q', 'W_K', 'b_K', 'W_V', 'b_V', 'W_O', 'b_O')}
    del _L0_xattn_all

    def _L0_attn_setup():
        import jax, jax.numpy as jnp
        import numpy as np
        HIDDEN = 128
        EXPAND = 2
        D_REC = HIDDEN * EXPAND
        INTER = 512
        B, T = (4, 512)

        def _rmsnorm(x, w, eps=1e-06):
            var = jnp.mean(x * x, axis=-1, keepdims=True)
            return x * jax.lax.rsqrt(var + eps) * w

        def _hawk_scan(x_in, a):
            xs = jnp.moveaxis(x_in, 1, 0)
            As = jnp.moveaxis(a, 1, 0)

            def step(state, inp):
                a_t, x_t = inp
                new = a_t * state + jnp.sqrt(1.0 - a_t * a_t + 1e-08) * x_t
                return (new, new)
            init = jnp.zeros(x_in.shape[::2], dtype=x_in.dtype)
            _, ys = jax.lax.scan(step, init, (As, xs))
            return jnp.moveaxis(ys, 0, 1)
        key = jax.random.key(seed)
        ks = jax.random.split(key, 11)
        s = lambda fan: 1.0 / np.sqrt(fan)
        return {'x': jax.random.normal(ks[0], (B, T, HIDDEN), dtype=jnp.float32), 'ln1_w': jnp.ones((HIDDEN,), dtype=jnp.float32), 'ln2_w': jnp.ones((HIDDEN,), dtype=jnp.float32), 'w_in': jax.random.normal(ks[1], (D_REC, HIDDEN), dtype=jnp.float32) * s(HIDDEN), 'w_gate': jax.random.normal(ks[2], (D_REC, HIDDEN), dtype=jnp.float32) * s(HIDDEN), 'a_param': jax.random.normal(ks[3], (D_REC,), dtype=jnp.float32) * 0.1, 'w_a': jax.random.normal(ks[4], (D_REC, D_REC), dtype=jnp.float32) * s(D_REC), 'w_out': jax.random.normal(ks[5], (HIDDEN, D_REC), dtype=jnp.float32) * s(D_REC), 'w_mlp_gate': jax.random.normal(ks[6], (INTER, HIDDEN), dtype=jnp.float32) * s(HIDDEN), 'w_mlp_up': jax.random.normal(ks[7], (INTER, HIDDEN), dtype=jnp.float32) * s(HIDDEN), 'w_mlp_down': jax.random.normal(ks[8], (HIDDEN, INTER), dtype=jnp.float32) * s(INTER)}
    _L0_attn_all = _L0_attn_setup()
    _L0_attn_in = {k: v for k, v in _L0_attn_all.items() if k in ('ln1_w', 'ln2_w', 'w_in', 'w_gate', 'a_param', 'w_a', 'w_out', 'w_mlp_gate', 'w_mlp_up', 'w_mlp_down')}
    del _L0_attn_all

    def _L0_ffn_setup():
        import jax, jax.numpy as jnp
        import numpy as np
        B, S, D_MODEL, D_FF = (4, 256, 128, 512)

        def _quantum_transform(hidden, theta, w_real, w_imag):
            imag = w_imag * jnp.sin(theta + hidden * 0.1)
            quantum_phase = jnp.cos(theta) * w_real + jnp.sin(theta) * w_imag
            return hidden + quantum_phase * imag * 0.1
        key = jax.random.key(seed)
        ks = jax.random.split(key, 8)
        return {'x': jax.random.normal(ks[0], (B, S, D_MODEL), dtype=jnp.float32), 'W1': jax.random.normal(ks[1], (D_MODEL, D_FF), dtype=jnp.float32) * (1.0 / np.sqrt(D_MODEL)), 'b1': jnp.zeros((D_FF,), dtype=jnp.float32), 'quantum_phases': jax.random.normal(ks[2], (D_FF,), dtype=jnp.float32) * (2.0 * np.pi), 'quantum_weights_real': jax.random.normal(ks[3], (D_FF,), dtype=jnp.float32) * 0.1, 'quantum_weights_imag': jax.random.normal(ks[4], (D_FF,), dtype=jnp.float32) * 0.1, 'W2': jax.random.normal(ks[5], (D_FF, D_MODEL), dtype=jnp.float32) * (1.0 / np.sqrt(D_FF)), 'b2': jnp.zeros((D_MODEL,), dtype=jnp.float32)}
    _L0_ffn_all = _L0_ffn_setup()
    _L0_ffn_in = {k: v for k, v in _L0_ffn_all.items() if k in ('W1', 'b1', 'quantum_phases', 'quantum_weights_real', 'quantum_weights_imag', 'W2', 'b2')}
    del _L0_ffn_all

    def _L1_xattn_setup():
        import jax, jax.numpy as jnp
        import numpy as np
        import math
        D_MODEL = 128
        N_HEADS = 16
        key = jax.random.key(seed)
        ks = jax.random.split(key, 11)
        N, L, S = (2, 256, 256)
        d = D_MODEL
        s = 1.0 / math.sqrt(d)
        return {'queries': jax.random.normal(ks[0], (N, L, d), dtype=jnp.float32), 'keys': jax.random.normal(ks[1], (N, S, d), dtype=jnp.float32), 'values': jax.random.normal(ks[2], (N, S, d), dtype=jnp.float32), 'Wq': jax.random.normal(ks[3], (d, d), dtype=jnp.float32) * s, 'bq': jax.random.normal(ks[4], (d,), dtype=jnp.float32) * s, 'Wk': jax.random.normal(ks[5], (d, d), dtype=jnp.float32) * s, 'bk': jax.random.normal(ks[6], (d,), dtype=jnp.float32) * s, 'Wv': jax.random.normal(ks[7], (d, d), dtype=jnp.float32) * s, 'bv': jax.random.normal(ks[8], (d,), dtype=jnp.float32) * s, 'Wo': jax.random.normal(ks[9], (d, d), dtype=jnp.float32) * s, 'bo': jax.random.normal(ks[10], (d,), dtype=jnp.float32) * s}
    _L1_xattn_all = _L1_xattn_setup()
    _L1_xattn_in = {k: v for k, v in _L1_xattn_all.items() if k in ('Wq', 'bq', 'Wk', 'bk', 'Wv', 'bv', 'Wo', 'bo')}
    del _L1_xattn_all

    def _L1_attn_setup():
        import jax, jax.numpy as jnp
        import numpy as np
        D_MODEL = 128
        N_HEADS = 16
        D_K = D_MODEL // N_HEADS
        key = jax.random.key(seed)
        k_x, k_q, k_k, k_v, k_o = jax.random.split(key, 5)
        s = 0.02
        return {'x': jax.random.normal(k_x, (4, 256, D_MODEL), dtype=jnp.float32), 'W_q': jax.random.normal(k_q, (D_MODEL, D_MODEL), dtype=jnp.float32) * s, 'W_k': jax.random.normal(k_k, (D_MODEL, D_K), dtype=jnp.float32) * s, 'W_v': jax.random.normal(k_v, (D_MODEL, D_K), dtype=jnp.float32) * s, 'W_o': jax.random.normal(k_o, (D_MODEL, D_MODEL), dtype=jnp.float32) * s}
    _L1_attn_all = _L1_attn_setup()
    _L1_attn_in = {k: v for k, v in _L1_attn_all.items() if k in ('W_q', 'W_k', 'W_v', 'W_o')}
    del _L1_attn_all

    def _L1_ffn_setup():
        import jax, jax.numpy as jnp
        import numpy as np
        TOP_K = 2
        key = jax.random.key(seed)
        ks = jax.random.split(key, 6)
        B, S, D, BN, E = (32, 256, 128, 64, 8)
        return {'x': jax.random.normal(ks[0], (B, S, D), dtype=jnp.float32), 'gate_w': jax.random.normal(ks[1], (E, D), dtype=jnp.float32) * 0.02, 'down_w': jax.random.normal(ks[2], (E, BN, D), dtype=jnp.float32) * 0.02, 'down_b': jax.random.normal(ks[3], (E, BN), dtype=jnp.float32) * 0.02, 'up_w': jax.random.normal(ks[4], (E, D, BN), dtype=jnp.float32) * 0.02, 'up_b': jax.random.normal(ks[5], (E, D), dtype=jnp.float32) * 0.02}
    _L1_ffn_all = _L1_ffn_setup()
    _L1_ffn_in = {k: v for k, v in _L1_ffn_all.items() if k in ('gate_w', 'down_w', 'down_b', 'up_w', 'up_b')}
    del _L1_ffn_all

    def _L2_xattn_setup():
        import jax, jax.numpy as jnp
        import numpy as np
        B, N, M = (4, 256, 256)
        QUERY_DIM = 128
        CONTEXT_DIM = 128
        HEADS = 16
        DIM_HEAD = 64
        INNER = HEADS * DIM_HEAD
        key = jax.random.key(seed)
        ks = jax.random.split(key, 7)
        x = jax.random.normal(ks[0], (B, N, QUERY_DIM), dtype=jnp.float32)
        context = jax.random.normal(ks[1], (B, M, CONTEXT_DIM), dtype=jnp.float32)
        mask = jnp.ones((B, M), dtype=bool)
        s_q = 1.0 / np.sqrt(QUERY_DIM)
        s_c = 1.0 / np.sqrt(CONTEXT_DIM)
        s_i = 1.0 / np.sqrt(INNER)
        Wq = jax.random.normal(ks[2], (QUERY_DIM, INNER), dtype=jnp.float32) * s_q
        Wk = jax.random.normal(ks[3], (CONTEXT_DIM, INNER), dtype=jnp.float32) * s_c
        Wv = jax.random.normal(ks[4], (CONTEXT_DIM, INNER), dtype=jnp.float32) * s_c
        Wo = jax.random.normal(ks[5], (INNER, QUERY_DIM), dtype=jnp.float32) * s_i
        bo = jax.random.normal(ks[6], (QUERY_DIM,), dtype=jnp.float32) * 0.01
        return {'x': x, 'context': context, 'mask': mask, 'Wq': Wq, 'Wk': Wk, 'Wv': Wv, 'Wo': Wo, 'bo': bo}
    _L2_xattn_all = _L2_xattn_setup()
    _L2_xattn_in = {k: v for k, v in _L2_xattn_all.items() if k in ('Wq', 'Wk', 'Wv', 'Wo', 'bo')}
    del _L2_xattn_all

    def _L2_attn_setup():
        import jax, jax.numpy as jnp
        import numpy as np
        import math
        N_EMBD = 128
        DIM_ATT = 128
        N_LAYER = 24
        LAYER_ID = 12
        B, T = (4, 512)

        def _init_params():
            r01 = LAYER_ID / (N_LAYER - 1)
            r1a0 = 1.0 - LAYER_ID / N_LAYER
            ddd = np.arange(N_EMBD, dtype=np.float32) / N_EMBD
            h = np.arange(DIM_ATT, dtype=np.float32)
            decay_speed = -5.0 + 8.0 * (h / (DIM_ATT - 1)) ** (0.7 + 1.3 * r01)
            zigzag = ((np.arange(DIM_ATT) + 1) % 3 - 1).astype(np.float32) * 0.5
            time_first = np.float32(math.log(0.3)) + zigzag
            return {'time_decay': jnp.asarray(decay_speed, jnp.float32), 'time_first': jnp.asarray(time_first, jnp.float32), 'time_mix_k': jnp.asarray(ddd ** r1a0, jnp.float32), 'time_mix_v': jnp.asarray(ddd ** r1a0 + 0.3 * r01, jnp.float32), 'time_mix_r': jnp.asarray(ddd ** (0.5 * r1a0), jnp.float32)}

        def _wkv(w, u, k, v):

            def step(carry, kv):
                aa, bb, pp = carry
                kt, vt = kv
                ww = u + kt
                p = jnp.maximum(pp, ww)
                e1 = jnp.exp(pp - p)
                e2 = jnp.exp(ww - p)
                y = (e1 * aa + e2 * vt) / (e1 * bb + e2)
                ww2 = pp + w
                p2 = jnp.maximum(ww2, kt)
                e1b = jnp.exp(ww2 - p2)
                e2b = jnp.exp(kt - p2)
                return ((e1b * aa + e2b * vt, e1b * bb + e2b, p2), y)
            Bb, Tt, C = k.shape
            init = (jnp.zeros((Bb, C), k.dtype), jnp.zeros((Bb, C), k.dtype), jnp.full((Bb, C), -1e+38, k.dtype))
            _, ys = jax.lax.scan(step, init, (jnp.swapaxes(k, 0, 1), jnp.swapaxes(v, 0, 1)))
            return jnp.swapaxes(ys, 0, 1)
        key = jax.random.key(seed)
        ks = jax.random.split(key, 5)
        inp = {'x': jax.random.normal(ks[0], (B, T, N_EMBD), jnp.float32)}
        inp.update(_init_params())
        s = 1.0 / math.sqrt(N_EMBD)
        inp['Wk'] = jax.random.normal(ks[1], (DIM_ATT, N_EMBD), jnp.float32) * s
        inp['Wv'] = jax.random.normal(ks[2], (DIM_ATT, N_EMBD), jnp.float32) * s
        inp['Wr'] = jax.random.normal(ks[3], (DIM_ATT, N_EMBD), jnp.float32) * s
        inp['Wo'] = jax.random.normal(ks[4], (N_EMBD, DIM_ATT), jnp.float32) * (1.0 / math.sqrt(DIM_ATT))
        return inp
    _L2_attn_all = _L2_attn_setup()
    _L2_attn_in = {k: v for k, v in _L2_attn_all.items() if k in ('time_decay', 'time_first', 'time_mix_k', 'time_mix_v', 'time_mix_r', 'Wk', 'Wv', 'Wr', 'Wo')}
    del _L2_attn_all

    def _L2_ffn_setup():
        import jax, jax.numpy as jnp
        import numpy as np
        B, S, D, E, F = (2, 128, 128, 14, 256)
        key = jax.random.key(seed)
        k0, k1, k2, k3 = jax.random.split(key, 4)
        h = jax.random.normal(k0, (B, S, D), jnp.float32)
        gate_w = jax.random.normal(k1, (E, D), jnp.float32) * 0.02
        w1 = jax.random.normal(k2, (E, D, F), jnp.float32) * (1.0 / np.sqrt(D).astype(np.float32))
        b1 = jnp.zeros((E, F), jnp.float32)
        w2 = jax.random.normal(k3, (E, F, D), jnp.float32) * (1.0 / np.sqrt(F).astype(np.float32))
        b2 = jnp.zeros((E, D), jnp.float32)
        return {'h': h, 'gate_w': gate_w, 'w1': w1, 'b1': b1, 'w2': w2, 'b2': b2}
    _L2_ffn_all = _L2_ffn_setup()
    _L2_ffn_in = {k: v for k, v in _L2_ffn_all.items() if k in ('gate_w', 'w1', 'b1', 'w2', 'b2')}
    del _L2_ffn_all

    def _L3_xattn_setup():
        import jax, jax.numpy as jnp
        import numpy as np
        B, T_Q, T_KV, D = (4, 256, 512, 128)
        H = 16
        HD = D // H
        EPS_LN = 1e-05
        EPS_NORM = 1e-12

        def _layernorm(x, g, b):
            mu = jnp.mean(x, axis=-1, keepdims=True)
            var = jnp.mean(jnp.square(x - mu), axis=-1, keepdims=True)
            return (x - mu) * jax.lax.rsqrt(var + EPS_LN) * g + b
        key = jax.random.key(seed)
        ks = jax.random.split(key, 12)
        inp = {'query': jax.random.normal(ks[0], (B, T_Q, D), jnp.float32), 'key': jax.random.normal(ks[1], (B, T_KV, D), jnp.float32), 'value': jax.random.normal(ks[2], (B, T_KV, D), jnp.float32), 'Wq': jax.random.normal(ks[3], (D, D), jnp.float32) * 0.02, 'Wk': jax.random.normal(ks[4], (D, D), jnp.float32) * 0.02, 'Wv': jax.random.normal(ks[5], (D, D), jnp.float32) * 0.02, 'Wo': jax.random.normal(ks[6], (D, D), jnp.float32) * 0.01, 'bo': jnp.zeros((D,), jnp.float32), 'Wbeta': jax.random.normal(ks[7], (H, D), jnp.float32) * 0.02, 'bbeta': jnp.zeros((H,), jnp.float32), 'Walpha': jax.random.normal(ks[8], (H, D), jnp.float32) * 0.02, 'balpha': jnp.full((H,), -1.0, jnp.float32), 'gq': jnp.ones((HD,), jnp.float32), 'bq': jnp.zeros((HD,), jnp.float32), 'gk': jnp.ones((HD,), jnp.float32), 'bk': jnp.zeros((HD,), jnp.float32)}
        return inp
    _L3_xattn_all = _L3_xattn_setup()
    _L3_xattn_in = {k: v for k, v in _L3_xattn_all.items() if k in ('Wq', 'Wk', 'Wv', 'Wo', 'bo', 'Wbeta', 'bbeta', 'Walpha', 'balpha', 'gq', 'bq', 'gk', 'bk')}
    del _L3_xattn_all

    def _L3_attn_setup():
        import jax, jax.numpy as jnp
        import numpy as np
        H = 128
        NH = 8
        DQK = H // NH
        DV = 2 * H // NH
        VDIM = 2 * H
        B, L = (2, 256)
        EPS = 1e-05
        ROPE_BASE = 10000.0

        def rope(x):
            b, t, h, d = x.shape
            inv_freq = 1.0 / ROPE_BASE ** (jnp.arange(0, d, 2, dtype=jnp.float32) / d)
            ang = jnp.arange(t, dtype=jnp.float32)[:, None] * inv_freq[None, :]
            cos = jnp.cos(ang)[None, :, None, :]
            sin = jnp.sin(ang)[None, :, None, :]
            xp = x.reshape(b, t, h, d // 2, 2)
            x0, x1 = (xp[..., 0], xp[..., 1])
            out = jnp.stack([x0 * cos - x1 * sin, x1 * cos + x0 * sin], axis=-1)
            return out.reshape(b, t, h, d).astype(x.dtype)
        key = jax.random.key(seed)
        ks = jax.random.split(key, 6)

        def w(k, shape):
            lim = 2 ** (-2.5) * np.sqrt(6.0 / (shape[0] + shape[1]))
            return jax.random.uniform(k, shape, jnp.float32, -lim, lim)
        return {'hidden_states': jax.random.normal(ks[0], (B, L, H), jnp.float32), 'Wq': w(ks[1], (H, H)), 'Wk': w(ks[2], (H, H)), 'Wv': w(ks[3], (H, VDIM)), 'Wg': w(ks[4], (H, VDIM)), 'Wo': w(ks[5], (VDIM, H)), 'g_norm_w': jnp.ones((DV,), jnp.float32)}
    _L3_attn_all = _L3_attn_setup()
    _L3_attn_in = {k: v for k, v in _L3_attn_all.items() if k in ('Wq', 'Wk', 'Wv', 'Wg', 'Wo', 'g_norm_w')}
    del _L3_attn_all

    def _L3_ffn_setup():
        import jax, jax.numpy as jnp
        import numpy as np
        from jax import lax
        DIM = 128
        HID = 256
        E = 8
        K = 2
        B, T = (2, 64)
        key = jax.random.key(seed)
        ks = jax.random.split(key, 5)
        scale = 1.0 / np.sqrt(DIM)
        x = jax.random.normal(ks[0], (B, T, DIM), dtype=jnp.float32)
        router_w = jax.random.normal(ks[1], (E, DIM), dtype=jnp.float32) * scale
        w_gate = jax.random.normal(ks[2], (E, HID, DIM), dtype=jnp.float32) * scale
        w_up = jax.random.normal(ks[3], (E, HID, DIM), dtype=jnp.float32) * scale
        w_down = jax.random.normal(ks[4], (E, DIM, HID), dtype=jnp.float32) * (1.0 / np.sqrt(HID))
        return {'x': x, 'router_w': router_w, 'w_gate': w_gate, 'w_up': w_up, 'w_down': w_down}
    _L3_ffn_all = _L3_ffn_setup()
    _L3_ffn_in = {k: v for k, v in _L3_ffn_all.items() if k in ('router_w', 'w_gate', 'w_up', 'w_down')}
    del _L3_ffn_all
    return {'x': x, 'ctx_1024': ctx_1024, 'mask_BxS2_bk0': mask_BxS2_bk0, 'mask_BxS2_bf1': mask_BxS2_bf1, 'L0_xattn_W_Q': _L0_xattn_in['W_Q'], 'L0_xattn_b_Q': _L0_xattn_in['b_Q'], 'L0_xattn_W_K': _L0_xattn_in['W_K'], 'L0_xattn_b_K': _L0_xattn_in['b_K'], 'L0_xattn_W_V': _L0_xattn_in['W_V'], 'L0_xattn_b_V': _L0_xattn_in['b_V'], 'L0_xattn_W_O': _L0_xattn_in['W_O'], 'L0_xattn_b_O': _L0_xattn_in['b_O'], 'L0_attn_ln1_w': _L0_attn_in['ln1_w'], 'L0_attn_ln2_w': _L0_attn_in['ln2_w'], 'L0_attn_w_in': _L0_attn_in['w_in'], 'L0_attn_w_gate': _L0_attn_in['w_gate'], 'L0_attn_a_param': _L0_attn_in['a_param'], 'L0_attn_w_a': _L0_attn_in['w_a'], 'L0_attn_w_out': _L0_attn_in['w_out'], 'L0_attn_w_mlp_gate': _L0_attn_in['w_mlp_gate'], 'L0_attn_w_mlp_up': _L0_attn_in['w_mlp_up'], 'L0_attn_w_mlp_down': _L0_attn_in['w_mlp_down'], 'L0_ffn_W1': _L0_ffn_in['W1'], 'L0_ffn_b1': _L0_ffn_in['b1'], 'L0_ffn_quantum_phases': _L0_ffn_in['quantum_phases'], 'L0_ffn_quantum_weights_real': _L0_ffn_in['quantum_weights_real'], 'L0_ffn_quantum_weights_imag': _L0_ffn_in['quantum_weights_imag'], 'L0_ffn_W2': _L0_ffn_in['W2'], 'L0_ffn_b2': _L0_ffn_in['b2'], 'L1_xattn_Wq': _L1_xattn_in['Wq'], 'L1_xattn_bq': _L1_xattn_in['bq'], 'L1_xattn_Wk': _L1_xattn_in['Wk'], 'L1_xattn_bk': _L1_xattn_in['bk'], 'L1_xattn_Wv': _L1_xattn_in['Wv'], 'L1_xattn_bv': _L1_xattn_in['bv'], 'L1_xattn_Wo': _L1_xattn_in['Wo'], 'L1_xattn_bo': _L1_xattn_in['bo'], 'L1_attn_W_q': _L1_attn_in['W_q'], 'L1_attn_W_k': _L1_attn_in['W_k'], 'L1_attn_W_v': _L1_attn_in['W_v'], 'L1_attn_W_o': _L1_attn_in['W_o'], 'L1_ffn_gate_w': _L1_ffn_in['gate_w'], 'L1_ffn_down_w': _L1_ffn_in['down_w'], 'L1_ffn_down_b': _L1_ffn_in['down_b'], 'L1_ffn_up_w': _L1_ffn_in['up_w'], 'L1_ffn_up_b': _L1_ffn_in['up_b'], 'L2_xattn_Wq': _L2_xattn_in['Wq'], 'L2_xattn_Wk': _L2_xattn_in['Wk'], 'L2_xattn_Wv': _L2_xattn_in['Wv'], 'L2_xattn_Wo': _L2_xattn_in['Wo'], 'L2_xattn_bo': _L2_xattn_in['bo'], 'L2_attn_time_decay': _L2_attn_in['time_decay'], 'L2_attn_time_first': _L2_attn_in['time_first'], 'L2_attn_time_mix_k': _L2_attn_in['time_mix_k'], 'L2_attn_time_mix_v': _L2_attn_in['time_mix_v'], 'L2_attn_time_mix_r': _L2_attn_in['time_mix_r'], 'L2_attn_Wk': _L2_attn_in['Wk'], 'L2_attn_Wv': _L2_attn_in['Wv'], 'L2_attn_Wr': _L2_attn_in['Wr'], 'L2_attn_Wo': _L2_attn_in['Wo'], 'L2_ffn_gate_w': _L2_ffn_in['gate_w'], 'L2_ffn_w1': _L2_ffn_in['w1'], 'L2_ffn_b1': _L2_ffn_in['b1'], 'L2_ffn_w2': _L2_ffn_in['w2'], 'L2_ffn_b2': _L2_ffn_in['b2'], 'L3_xattn_Wq': _L3_xattn_in['Wq'], 'L3_xattn_Wk': _L3_xattn_in['Wk'], 'L3_xattn_Wv': _L3_xattn_in['Wv'], 'L3_xattn_Wo': _L3_xattn_in['Wo'], 'L3_xattn_bo': _L3_xattn_in['bo'], 'L3_xattn_Wbeta': _L3_xattn_in['Wbeta'], 'L3_xattn_bbeta': _L3_xattn_in['bbeta'], 'L3_xattn_Walpha': _L3_xattn_in['Walpha'], 'L3_xattn_balpha': _L3_xattn_in['balpha'], 'L3_xattn_gq': _L3_xattn_in['gq'], 'L3_xattn_bq': _L3_xattn_in['bq'], 'L3_xattn_gk': _L3_xattn_in['gk'], 'L3_xattn_bk': _L3_xattn_in['bk'], 'L3_attn_Wq': _L3_attn_in['Wq'], 'L3_attn_Wk': _L3_attn_in['Wk'], 'L3_attn_Wv': _L3_attn_in['Wv'], 'L3_attn_Wg': _L3_attn_in['Wg'], 'L3_attn_Wo': _L3_attn_in['Wo'], 'L3_attn_g_norm_w': _L3_attn_in['g_norm_w'], 'L3_ffn_router_w': _L3_ffn_in['router_w'], 'L3_ffn_w_gate': _L3_ffn_in['w_gate'], 'L3_ffn_w_up': _L3_ffn_in['w_up'], 'L3_ffn_w_down': _L3_ffn_in['w_down']}

def reference(x, ctx_1024, mask_BxS2_bk0, mask_BxS2_bf1, L0_xattn_W_Q, L0_xattn_b_Q, L0_xattn_W_K, L0_xattn_b_K, L0_xattn_W_V, L0_xattn_b_V, L0_xattn_W_O, L0_xattn_b_O, L0_attn_ln1_w, L0_attn_ln2_w, L0_attn_w_in, L0_attn_w_gate, L0_attn_a_param, L0_attn_w_a, L0_attn_w_out, L0_attn_w_mlp_gate, L0_attn_w_mlp_up, L0_attn_w_mlp_down, L0_ffn_W1, L0_ffn_b1, L0_ffn_quantum_phases, L0_ffn_quantum_weights_real, L0_ffn_quantum_weights_imag, L0_ffn_W2, L0_ffn_b2, L1_xattn_Wq, L1_xattn_bq, L1_xattn_Wk, L1_xattn_bk, L1_xattn_Wv, L1_xattn_bv, L1_xattn_Wo, L1_xattn_bo, L1_attn_W_q, L1_attn_W_k, L1_attn_W_v, L1_attn_W_o, L1_ffn_gate_w, L1_ffn_down_w, L1_ffn_down_b, L1_ffn_up_w, L1_ffn_up_b, L2_xattn_Wq, L2_xattn_Wk, L2_xattn_Wv, L2_xattn_Wo, L2_xattn_bo, L2_attn_time_decay, L2_attn_time_first, L2_attn_time_mix_k, L2_attn_time_mix_v, L2_attn_time_mix_r, L2_attn_Wk, L2_attn_Wv, L2_attn_Wr, L2_attn_Wo, L2_ffn_gate_w, L2_ffn_w1, L2_ffn_b1, L2_ffn_w2, L2_ffn_b2, L3_xattn_Wq, L3_xattn_Wk, L3_xattn_Wv, L3_xattn_Wo, L3_xattn_bo, L3_xattn_Wbeta, L3_xattn_bbeta, L3_xattn_Walpha, L3_xattn_balpha, L3_xattn_gq, L3_xattn_bq, L3_xattn_gk, L3_xattn_bk, L3_attn_Wq, L3_attn_Wk, L3_attn_Wv, L3_attn_Wg, L3_attn_Wo, L3_attn_g_norm_w, L3_ffn_router_w, L3_ffn_w_gate, L3_ffn_w_up, L3_ffn_w_down):
    import jax
    import jax.numpy as jnp

    def _L0_xattn_ref(q_input, kv_input, key_padding_mask, W_Q, b_Q, W_K, b_K, W_V, b_V, W_O, b_O):
        import jax, jax.numpy as jnp
        import numpy as np
        D_MODEL = 128
        N_HEAD = 16
        D_H = D_MODEL // N_HEAD
        B, LQ, _ = q_input.shape
        LK = kv_input.shape[1]
        q = q_input @ W_Q + b_Q
        k = kv_input @ W_K + b_K
        v = kv_input @ W_V + b_V
        q = q.reshape(B, LQ, N_HEAD, D_H).transpose(0, 2, 1, 3)
        k = k.reshape(B, LK, N_HEAD, D_H).transpose(0, 2, 1, 3)
        v = v.reshape(B, LK, N_HEAD, D_H).transpose(0, 2, 1, 3)
        sim = jnp.einsum('bhqd,bhkd->bhqk', q, k) / jnp.sqrt(jnp.float32(D_H))
        neg_inf = jnp.finfo(sim.dtype).min
        mask = key_padding_mask[:, None, None, :]
        sim = jnp.where(mask, neg_inf, sim)
        attn = jax.nn.softmax(sim, axis=-1)
        out = jnp.einsum('bhqk,bhkd->bhqd', attn, v)
        out = out.transpose(0, 2, 1, 3).reshape(B, LQ, D_MODEL)
        return out @ W_O + b_O

    def _L0_attn_ref(x, ln1_w, ln2_w, w_in, w_gate, a_param, w_a, w_out, w_mlp_gate, w_mlp_up, w_mlp_down):
        import jax, jax.numpy as jnp
        import numpy as np
        HIDDEN = 128
        EXPAND = 2
        D_REC = HIDDEN * EXPAND
        INTER = 512
        B, T = (4, 512)

        def _rmsnorm(x, w, eps=1e-06):
            var = jnp.mean(x * x, axis=-1, keepdims=True)
            return x * jax.lax.rsqrt(var + eps) * w

        def _hawk_scan(x_in, a):
            xs = jnp.moveaxis(x_in, 1, 0)
            As = jnp.moveaxis(a, 1, 0)

            def step(state, inp):
                a_t, x_t = inp
                new = a_t * state + jnp.sqrt(1.0 - a_t * a_t + 1e-08) * x_t
                return (new, new)
            init = jnp.zeros(x_in.shape[::2], dtype=x_in.dtype)
            _, ys = jax.lax.scan(step, init, (As, xs))
            return jnp.moveaxis(ys, 0, 1)
        h = _rmsnorm(x, ln1_w)
        x_in = h @ w_in.T
        gate = jax.nn.sigmoid(h @ w_gate.T)
        a = jax.nn.sigmoid(a_param + x_in @ w_a.T)
        y = gate * _hawk_scan(x_in, a)
        x = x + y @ w_out.T
        h2 = _rmsnorm(x, ln2_w)
        mlp = jax.nn.silu(h2 @ w_mlp_gate.T) * (h2 @ w_mlp_up.T) @ w_mlp_down.T
        return x + mlp

    def _L0_ffn_ref(x, W1, b1, quantum_phases, quantum_weights_real, quantum_weights_imag, W2, b2):
        import jax, jax.numpy as jnp
        import numpy as np
        B, S, D_MODEL, D_FF = (4, 256, 128, 512)

        def _quantum_transform(hidden, theta, w_real, w_imag):
            imag = w_imag * jnp.sin(theta + hidden * 0.1)
            quantum_phase = jnp.cos(theta) * w_real + jnp.sin(theta) * w_imag
            return hidden + quantum_phase * imag * 0.1
        hidden = jnp.einsum('bsd,df->bsf', x, W1) + b1
        q = _quantum_transform(hidden, quantum_phases, quantum_weights_real, quantum_weights_imag)
        act = jax.nn.relu(q)
        return jnp.einsum('bsf,fd->bsd', act, W2) + b2

    def _L1_xattn_ref(queries, keys, values, Wq, bq, Wk, bk, Wv, bv, Wo, bo):
        import jax, jax.numpy as jnp
        import numpy as np
        import math
        D_MODEL = 128
        N_HEADS = 16
        N, L, _ = queries.shape
        S = keys.shape[1]
        H = N_HEADS
        q = (queries @ Wq.T + bq).reshape(N, L, H, -1)
        k = (keys @ Wk.T + bk).reshape(N, S, H, -1)
        v = (values @ Wv.T + bv).reshape(N, S, H, -1)
        D = k.shape[-1]
        sm = jnp.einsum('nlhd,nshd->nlhs', q, k) / math.sqrt(D)
        causal_mask = jnp.triu(jnp.ones((L, S), dtype=bool), k=1)
        sm = jnp.where(causal_mask[None, :, None, :], -jnp.inf, sm)
        sm = jax.nn.softmax(sm, axis=-1)
        attn = jnp.einsum('nlhs,nshd->nlhd', sm, v)
        new_values = attn.reshape(N, L, H * D)
        return new_values @ Wo.T + bo

    def _L1_attn_ref(x, W_q, W_k, W_v, W_o):
        import jax, jax.numpy as jnp
        import numpy as np
        D_MODEL = 128
        N_HEADS = 16
        D_K = D_MODEL // N_HEADS
        B, S, _ = x.shape
        scale = 1.0 / jnp.sqrt(jnp.asarray(D_K, x.dtype))
        Q = (x @ W_q).reshape(B, S, N_HEADS, D_K)
        K = x @ W_k
        V = x @ W_v
        scores = jnp.einsum('bqhd,bkd->bhqk', Q, K) * scale
        attn = jax.nn.softmax(scores, axis=-1)
        out = jnp.einsum('bhqk,bkd->bqhd', attn, V).reshape(B, S, D_MODEL)
        return out @ W_o

    def _L1_ffn_ref(x, gate_w, down_w, down_b, up_w, up_b):
        import jax, jax.numpy as jnp
        import numpy as np
        TOP_K = 2
        pooled = x.mean(axis=1)
        gate = jax.nn.softmax(pooled @ gate_w.T, axis=-1)
        top_w, top_i = jax.lax.top_k(gate, TOP_K)
        top_w = top_w / (top_w.sum(axis=-1, keepdims=True) + 1e-08)
        Wd = down_w[top_i]
        bd = down_b[top_i]
        Wu = up_w[top_i]
        bu = up_b[top_i]
        h = jax.nn.gelu(jnp.einsum('bsd,bkcd->bksc', x, Wd) + bd[:, :, None, :], approximate=False)
        h = h * top_w[:, :, None, None]
        out = jnp.einsum('bksc,bkdc->bsd', h, Wu)
        out = out + (top_w[:, :, None] * bu).sum(axis=1)[:, None, :]
        return out

    def _L2_xattn_ref(x, context, mask, Wq, Wk, Wv, Wo, bo):
        import jax, jax.numpy as jnp
        import numpy as np
        B, N, M = (4, 256, 256)
        QUERY_DIM = 128
        CONTEXT_DIM = 128
        HEADS = 16
        DIM_HEAD = 64
        INNER = HEADS * DIM_HEAD
        h, d = (HEADS, DIM_HEAD)
        scale = d ** (-0.5)
        b, n, _ = x.shape
        m = context.shape[1]
        q = (x @ Wq).reshape(b, n, h, d)
        k = (context @ Wk).reshape(b, m, h, d)
        v = (context @ Wv).reshape(b, m, h, d)
        sim = jnp.einsum('bihd,bjhd->bhij', q, k) * scale
        neg = -jnp.finfo(sim.dtype).max
        sim = jnp.where(mask[:, None, None, :], sim, neg)
        attn = jax.nn.softmax(sim, axis=-1)
        out = jnp.einsum('bhij,bjhd->bihd', attn, v)
        out = out.reshape(b, n, h * d)
        return out @ Wo + bo

    def _L2_attn_ref(x, time_decay, time_first, time_mix_k, time_mix_v, time_mix_r, Wk, Wv, Wr, Wo):
        import jax, jax.numpy as jnp
        import numpy as np
        import math
        N_EMBD = 128
        DIM_ATT = 128
        N_LAYER = 24
        LAYER_ID = 12
        B, T = (4, 512)

        def _init_params():
            r01 = LAYER_ID / (N_LAYER - 1)
            r1a0 = 1.0 - LAYER_ID / N_LAYER
            ddd = np.arange(N_EMBD, dtype=np.float32) / N_EMBD
            h = np.arange(DIM_ATT, dtype=np.float32)
            decay_speed = -5.0 + 8.0 * (h / (DIM_ATT - 1)) ** (0.7 + 1.3 * r01)
            zigzag = ((np.arange(DIM_ATT) + 1) % 3 - 1).astype(np.float32) * 0.5
            time_first = np.float32(math.log(0.3)) + zigzag
            return {'time_decay': jnp.asarray(decay_speed, jnp.float32), 'time_first': jnp.asarray(time_first, jnp.float32), 'time_mix_k': jnp.asarray(ddd ** r1a0, jnp.float32), 'time_mix_v': jnp.asarray(ddd ** r1a0 + 0.3 * r01, jnp.float32), 'time_mix_r': jnp.asarray(ddd ** (0.5 * r1a0), jnp.float32)}

        def _wkv(w, u, k, v):

            def step(carry, kv):
                aa, bb, pp = carry
                kt, vt = kv
                ww = u + kt
                p = jnp.maximum(pp, ww)
                e1 = jnp.exp(pp - p)
                e2 = jnp.exp(ww - p)
                y = (e1 * aa + e2 * vt) / (e1 * bb + e2)
                ww2 = pp + w
                p2 = jnp.maximum(ww2, kt)
                e1b = jnp.exp(ww2 - p2)
                e2b = jnp.exp(kt - p2)
                return ((e1b * aa + e2b * vt, e1b * bb + e2b, p2), y)
            Bb, Tt, C = k.shape
            init = (jnp.zeros((Bb, C), k.dtype), jnp.zeros((Bb, C), k.dtype), jnp.full((Bb, C), -1e+38, k.dtype))
            _, ys = jax.lax.scan(step, init, (jnp.swapaxes(k, 0, 1), jnp.swapaxes(v, 0, 1)))
            return jnp.swapaxes(ys, 0, 1)
        xx = jnp.pad(x, ((0, 0), (1, 0), (0, 0)))[:, :-1]
        xk = x * time_mix_k + xx * (1.0 - time_mix_k)
        xv = x * time_mix_v + xx * (1.0 - time_mix_v)
        xr = x * time_mix_r + xx * (1.0 - time_mix_r)
        k = jnp.einsum('btc,dc->btd', xk, Wk)
        v = jnp.einsum('btc,dc->btd', xv, Wv)
        sr = jax.nn.sigmoid(jnp.einsum('btc,dc->btd', xr, Wr))
        w = -jnp.exp(time_decay)
        rwkv = sr * _wkv(w, time_first, k, v)
        return jnp.einsum('btd,cd->btc', rwkv, Wo)

    def _L2_ffn_ref(h, gate_w, w1, b1, w2, b2):
        import jax, jax.numpy as jnp
        import numpy as np
        B, S, D, E, F = (2, 128, 128, 14, 256)
        Bb, Ss, Dd = h.shape
        x = h.reshape(Bb * Ss, Dd)
        logits = x @ gate_w.T
        probs = jax.nn.softmax(logits, axis=-1)
        top2_p, top2_i = jax.lax.top_k(probs, 2)
        w = top2_p / jnp.maximum(top2_p.sum(-1, keepdims=True), 1e-10)
        hh = jnp.einsum('nd,edf->nef', x, w1) + b1
        hh = jax.nn.gelu(hh, approximate=False)
        all_out = jnp.einsum('nef,efd->ned', hh, w2) + b2
        n = jnp.arange(x.shape[0])
        out0 = all_out[n, top2_i[:, 0]]
        out1 = all_out[n, top2_i[:, 1]]
        moe_out = w[:, 0:1] * out0 + w[:, 1:2] * out1
        result = jnp.clip(x + moe_out, -100.0, 100.0).reshape(Bb, Ss, Dd)
        return result

    def _L3_xattn_ref(query, key, value, Wq, Wk, Wv, Wo, bo, Wbeta, bbeta, Walpha, balpha, gq, bq, gk, bk):
        import jax, jax.numpy as jnp
        import numpy as np
        B, T_Q, T_KV, D = (4, 256, 512, 128)
        H = 16
        HD = D // H
        EPS_LN = 1e-05
        EPS_NORM = 1e-12

        def _layernorm(x, g, b):
            mu = jnp.mean(x, axis=-1, keepdims=True)
            var = jnp.mean(jnp.square(x - mu), axis=-1, keepdims=True)
            return (x - mu) * jax.lax.rsqrt(var + EPS_LN) * g + b
        Bq, Tq, Dm = query.shape
        Tkv = key.shape[1]
        q = (query @ Wq.T).reshape(Bq, Tq, H, HD)
        k = (key @ Wk.T).reshape(Bq, Tkv, H, HD)
        v = (value @ Wv.T).reshape(Bq, Tkv, H, HD)
        q = _layernorm(q, gq, bq)
        k = _layernorm(k, gk, bk)
        k = k / jnp.maximum(jnp.linalg.norm(k, axis=-1, keepdims=True), EPS_NORM)
        beta = jax.nn.sigmoid(key @ Wbeta.T + bbeta)
        alpha = jax.nn.sigmoid(key @ Walpha.T + balpha)
        k_t = jnp.moveaxis(k, 1, 0)
        v_t = jnp.moveaxis(v, 1, 0)
        b_t = jnp.moveaxis(beta, 1, 0)
        a_t = jnp.moveaxis(alpha, 1, 0)
        M0 = jnp.zeros((Bq, H, HD, HD), query.dtype)

        def step(M, inputs):
            kt, vt, bt, at = inputs
            Mk = jnp.einsum('bhij,bhj->bhi', M, kt)
            erase = at[..., None, None] * jnp.einsum('bhi,bhj->bhij', Mk, kt)
            write = bt[..., None, None] * jnp.einsum('bhi,bhj->bhij', vt, kt)
            return (M - erase + write, None)
        M, _ = jax.lax.scan(step, M0, (k_t, v_t, b_t, a_t))
        out = jnp.einsum('bhij,bthj->bthi', M, q).reshape(Bq, Tq, Dm)
        out = out @ Wo.T + bo
        return out

    def _L3_attn_ref(hidden_states, Wq, Wk, Wv, Wg, Wo, g_norm_w):
        import jax, jax.numpy as jnp
        import numpy as np
        H = 128
        NH = 8
        DQK = H // NH
        DV = 2 * H // NH
        VDIM = 2 * H
        B, L = (2, 256)
        EPS = 1e-05
        ROPE_BASE = 10000.0

        def rope(x):
            b, t, h, d = x.shape
            inv_freq = 1.0 / ROPE_BASE ** (jnp.arange(0, d, 2, dtype=jnp.float32) / d)
            ang = jnp.arange(t, dtype=jnp.float32)[:, None] * inv_freq[None, :]
            cos = jnp.cos(ang)[None, :, None, :]
            sin = jnp.sin(ang)[None, :, None, :]
            xp = x.reshape(b, t, h, d // 2, 2)
            x0, x1 = (xp[..., 0], xp[..., 1])
            out = jnp.stack([x0 * cos - x1 * sin, x1 * cos + x0 * sin], axis=-1)
            return out.reshape(b, t, h, d).astype(x.dtype)
        b, l, _ = hidden_states.shape
        q = (hidden_states @ Wq).reshape(b, l, NH, DQK)
        k = (hidden_states @ Wk).reshape(b, l, NH, DQK)
        v = (hidden_states @ Wv).reshape(b, l, NH, DV)
        q = rope(q)
        k = rope(k)
        q = jnp.transpose(q, (0, 2, 1, 3)).astype(jnp.float32)
        k = jnp.transpose(k, (0, 2, 1, 3)).astype(jnp.float32)
        v = jnp.transpose(v, (0, 2, 1, 3)).astype(jnp.float32)
        s = jnp.log2(1.0 - jnp.exp2(-5.0 - jnp.arange(NH, dtype=jnp.float32)))
        pos = jnp.arange(l, dtype=jnp.float32)
        diff = pos[:, None] - pos[None, :]
        decay = jnp.where(diff >= 0, jnp.exp2(diff[None] * s[:, None, None]), 0.0)
        scores = jnp.einsum('bhqd,bhkd,hqk->bhqk', q * DQK ** (-0.5), k, decay)
        o = jnp.einsum('bhqk,bhkd->bhqd', scores, v)
        o = jnp.transpose(o, (0, 2, 1, 3))
        o = o * jax.lax.rsqrt(jnp.mean(o * o, axis=-1, keepdims=True) + EPS) * g_norm_w
        g = hidden_states @ Wg
        o = o.reshape(b, l, VDIM) * (g * jax.nn.sigmoid(g))
        return o @ Wo

    def _L3_ffn_ref(x, router_w, w_gate, w_up, w_down):
        import jax, jax.numpy as jnp
        import numpy as np
        from jax import lax
        DIM = 128
        HID = 256
        E = 8
        K = 2
        B, T = (2, 64)
        Bb, Tt, D = x.shape
        N = Bb * Tt
        xf = x.reshape(N, D)
        logits = xf @ router_w.T
        routing = jax.nn.softmax(logits, axis=-1)
        top_w, top_i = lax.top_k(routing, K)
        top_w = top_w / jnp.sum(top_w, axis=-1, keepdims=True)
        combine = jnp.zeros((N, E), dtype=x.dtype)
        combine = combine.at[jnp.arange(N)[:, None], top_i].add(top_w)
        g = jnp.einsum('nd,ehd->neh', xf, w_gate)
        u = jnp.einsum('nd,ehd->neh', xf, w_up)
        h = jax.nn.silu(g) * u
        y = jnp.einsum('neh,edh->ned', h, w_down)
        out = jnp.einsum('ned,ne->nd', y, combine)
        return out.reshape(Bb, Tt, D)
    x = x + _L0_xattn_ref(_layernorm(x, axis=-1), ctx_1024, mask_BxS2_bk0, L0_xattn_W_Q, L0_xattn_b_Q, L0_xattn_W_K, L0_xattn_b_K, L0_xattn_W_V, L0_xattn_b_V, L0_xattn_W_O, L0_xattn_b_O)
    x = x + _L0_attn_ref(_layernorm(x, axis=-1), L0_attn_ln1_w, L0_attn_ln2_w, L0_attn_w_in, L0_attn_w_gate, L0_attn_a_param, L0_attn_w_a, L0_attn_w_out, L0_attn_w_mlp_gate, L0_attn_w_mlp_up, L0_attn_w_mlp_down)
    x = x + _L0_ffn_ref(_layernorm(x, axis=-1), L0_ffn_W1, L0_ffn_b1, L0_ffn_quantum_phases, L0_ffn_quantum_weights_real, L0_ffn_quantum_weights_imag, L0_ffn_W2, L0_ffn_b2)
    x = x + _L1_xattn_ref(_layernorm(x, axis=-1), ctx_1024, ctx_1024, L1_xattn_Wq, L1_xattn_bq, L1_xattn_Wk, L1_xattn_bk, L1_xattn_Wv, L1_xattn_bv, L1_xattn_Wo, L1_xattn_bo)
    x = x + _L1_attn_ref(_layernorm(x, axis=-1), L1_attn_W_q, L1_attn_W_k, L1_attn_W_v, L1_attn_W_o)
    x = x + _L1_ffn_ref(_layernorm(x, axis=-1), L1_ffn_gate_w, L1_ffn_down_w, L1_ffn_down_b, L1_ffn_up_w, L1_ffn_up_b)
    x = x + _L2_xattn_ref(_layernorm(x, axis=-1), ctx_1024, mask_BxS2_bf1, L2_xattn_Wq, L2_xattn_Wk, L2_xattn_Wv, L2_xattn_Wo, L2_xattn_bo)
    x = x + _L2_attn_ref(_layernorm(x, axis=-1), L2_attn_time_decay, L2_attn_time_first, L2_attn_time_mix_k, L2_attn_time_mix_v, L2_attn_time_mix_r, L2_attn_Wk, L2_attn_Wv, L2_attn_Wr, L2_attn_Wo)
    x = x + _L2_ffn_ref(_layernorm(x, axis=-1), L2_ffn_gate_w, L2_ffn_w1, L2_ffn_b1, L2_ffn_w2, L2_ffn_b2)
    x = x + _L3_xattn_ref(_layernorm(x, axis=-1), ctx_1024, ctx_1024, L3_xattn_Wq, L3_xattn_Wk, L3_xattn_Wv, L3_xattn_Wo, L3_xattn_bo, L3_xattn_Wbeta, L3_xattn_bbeta, L3_xattn_Walpha, L3_xattn_balpha, L3_xattn_gq, L3_xattn_bq, L3_xattn_gk, L3_xattn_bk)
    x = x + _L3_attn_ref(_layernorm(x, axis=-1), L3_attn_Wq, L3_attn_Wk, L3_attn_Wv, L3_attn_Wg, L3_attn_Wo, L3_attn_g_norm_w)
    x = x + _L3_ffn_ref(_layernorm(x, axis=-1), L3_ffn_router_w, L3_ffn_w_gate, L3_ffn_w_up, L3_ffn_w_down)
    return x

_drawn_inputs = setup_inputs


def setup_inputs(seed=0):
    import zlib

    import numpy as np

    out = dict(_drawn_inputs(seed))
    spreads = {'L0_xattn_b_Q': (0.0, 0.1),
     'L0_xattn_b_K': (0.0, 2.0),
     'L0_xattn_b_V': (0.0, 0.1),
     'L0_xattn_b_O': (0.0, 0.1),
     'L0_attn_ln1_w': (1.0, 0.2),
     'L0_attn_ln2_w': (1.0, 0.2),
     'L0_ffn_b1': (0.0, 0.1),
     'L0_ffn_b2': (0.0, 0.1),
     'L2_ffn_b1': (0.0, 0.501),
     'L2_ffn_b2': (0.0, 0.335),
     'L3_xattn_bo': (0.0, 0.274),
     'L3_xattn_bbeta': (0.0, 0.8),
     'L3_xattn_balpha': (-1.0, 0.6),
     'L3_xattn_gq': (1.0, 0.6),
     'L3_xattn_bq': (0.0, 0.8),
     'L3_xattn_gk': (1.0, 0.6),
     'L3_xattn_bk': (0.0, 0.8),
     'L3_attn_g_norm_w': (1.0, 0.6)}
    factors = {'L0_attn_a_param': 3.212,
     'L0_ffn_quantum_phases': 8.0,
     'L0_ffn_quantum_weights_real': 8.0,
     'L0_ffn_quantum_weights_imag': 8.0,
     'L1_xattn_bq': 3.1,
     'L1_xattn_bk': 200.0,
     'L1_attn_W_q': 8.0,
     'L1_attn_W_k': 8.0,
     'L1_attn_W_v': 2.897,
     'L1_attn_W_o': 2.715,
     'L1_ffn_gate_w': 4.077,
     'L1_ffn_down_w': 4.39,
     'L1_ffn_down_b': 8.0,
     'L1_ffn_up_w': 4.738,
     'L1_ffn_up_b': 4.59,
     'L2_xattn_bo': 4.429,
     'L2_attn_time_first': 62.144,
     'L3_xattn_Wbeta': 8.0,
     'L3_xattn_Walpha': 8.0,
     'L3_attn_Wq': 8.0,
     'L3_attn_Wk': 8.0,
     'L3_attn_Wv': 8.0,
     'L3_attn_Wg': 8.0,
     'L3_attn_Wo': 8.0}
    for name, (base, spread) in spreads.items():
        noise = np.random.default_rng([zlib.crc32(name.encode()), seed]).standard_normal(out[name].shape)
        drawn = base * np.exp(spread * noise) if base else spread * noise
        out[name] = jnp.asarray(drawn.astype(out[name].dtype))
    for name, factor in factors.items():
        out[name] = (out[name] * factor).astype(out[name].dtype)
    return out
```

```python
from contextlib import ExitStack

import numpy as np

import concourse.bass as bass
from concourse import mybir

F32 = mybir.dt.float32
BF16 = mybir.dt.bfloat16
U8 = mybir.dt.uint8
U32 = mybir.dt.uint32
ALU = mybir.AluOpType
ACT = mybir.ActivationFunctionType
AX = mybir.AxisListType

B, S, D = 128, 32, 128
T = 257
P = 128
TILES = B * S // P
SEQS = P // S
G = TILES // 4
H = 16
DH = D // H
C = 4
LN_EPS = 1e-5
MASKED = -float(2 ** 100)


class Signal:

    def __init__(self, sem):
        self.sem, self.total = sem, 0

    def use(self, per, iters):
        u = Use(self.sem, self.total, per)
        self.total += per * iters
        return u


class Use:

    def __init__(self, sem, base, per):
        self.sem, self.base, self.per = sem, base, per

    def at(self, i, k=None):
        return i * self.per + (self.base + (self.per if k is None else k))


class Steps:

    def __init__(self, use):
        self.u, self.sem, self.n = use, use.sem, 0

    def start(self):
        self.n = 0

    def next(self, i=0):
        self.n += 1
        return self.u.at(i, self.n)

    def done(self):
        assert self.n == self.u.per, ("steps", self.n, self.u.per)


def constants():
    p = np.arange(P)
    c = {}
    c["ident"] = np.eye(P)
    c["head4"] = (p[:, None] % 32 // 8 == np.arange(4)[None, :])
    c["odiag"] = (np.arange(32)[None, :] // 8 == p[:, None] // 32)
    c["samequery"] = (p[:, None] % 32 == np.arange(32)[None, :])
    c["causal"] = np.where(np.arange(32)[None, :] > p[:, None] % 32, MASKED, 0.0)
    c["seqmean"] = (p[:, None] // 32 == np.arange(4)[None, :]) / 32.0
    c["ones"] = np.ones((P, P))
    freq = 1.0 / 10000.0 ** (np.arange(0, 16, 2, dtype=np.float32) / 16)
    ang = (np.arange(S, dtype=np.float32)[None, :] * freq[p % 16 // 2][:, None].astype(np.float32))
    c["ropecos"] = np.cos(ang)
    c["ropesin"] = np.where(p % 2 == 0, -1.0, 1.0)[:, None] * np.sin(ang)
    s = np.log2(1.0 - np.exp2(-5.0 - np.arange(8)))
    diff = (p[None, :] - p[:, None])
    keep = (diff >= 0) & (p[None, :] // 32 == p[:, None] // 32)
    c["decay"] = np.concatenate([np.where(keep, np.exp2(np.where(keep, diff, 0) * s[h]), 0.0) for h in range(8)], 1) * 0.25
    c["head2"] = (p[:, None] % 32 // 16 == np.arange(2)[None, :])
    c["mean32"] = (p[:, None] // 32 == p[None, :] // 32) / 32.0
    c["exp2rows"] = np.concatenate([(p[:, None] == 2 * j + p[None, :] // 64) for j in range(4)], 1)
    c["iota14"] = np.broadcast_to(np.arange(14), (P, 14))
    c["rowquarter"] = (p[:, None] == p[None, :] // 32 % 2)
    c["center8"] = np.eye(P) - (p[:, None] // 8 == p[None, :] // 8) / 8.0
    c["headcol"] = (p[:, None] // 8 == np.arange(16)[None, :])
    c["eps8"] = np.full((P, 1), 1e-8)
    c["eps5"] = np.full((P, 1), 1e-5)
    c["ones33"] = np.broadcast_to(np.where(np.arange(33) == 0, 0.0, 1.0), (P, 33))
    out, at, n = [], {}, 0
    for k, v in c.items():
        v = np.asarray(v, np.float32)
        at[k] = (n, v.shape[1])
        n += v.shape[1]
        out.append(v)
    return np.ascontiguousarray(np.concatenate(out, 1)), at


def rows(w, k):
    n = w.shape[1]
    return w.reshape(k, P, n).transpose(1, 0, 2).reshape(P, k * n)


def bc(v):
    return np.broadcast_to(np.asarray(v).reshape(1, -1), (P, v.size))


def cols(v):
    return np.asarray(v).reshape(-1, P).T


def pad(w):
    out = np.zeros((P, w.shape[1]), w.dtype)
    out[:w.shape[0]] = w
    return out


def layouts(a):
    L = {}
    L["L0_xattn"] = [("wq", a["L0_xattn_W_Q"]), ("wk", a["L0_xattn_W_K"]), ("wv", a["L0_xattn_W_V"]),
                     ("wo", a["L0_xattn_W_O"]), ("bq", cols(a["L0_xattn_b_Q"])), ("bk", cols(a["L0_xattn_b_K"])),
                     ("bv", cols(a["L0_xattn_b_V"])), ("bo", bc(a["L0_xattn_b_O"]))]
    L["L0_attn"] = [("ln1", cols(a["L0_attn_ln1_w"])), ("ln2", cols(a["L0_attn_ln2_w"])), ("ap", cols(a["L0_attn_a_param"])),
                    ("win", a["L0_attn_w_in"].T), ("wgate", a["L0_attn_w_gate"].T), ("wa", rows(a["L0_attn_w_a"].T, 2)),
                    ("wout", rows(a["L0_attn_w_out"].T, 2)), ("wmg", a["L0_attn_w_mlp_gate"].T),
                    ("wmu", a["L0_attn_w_mlp_up"].T), ("wmd", rows(a["L0_attn_w_mlp_down"].T, 4))]
    L["L0_ffn"] = [("w1", a["L0_ffn_W1"]), ("b1", cols(a["L0_ffn_b1"])), ("theta", cols(a["L0_ffn_quantum_phases"])),
                   ("wr", cols(a["L0_ffn_quantum_weights_real"])), ("wi", cols(a["L0_ffn_quantum_weights_imag"])),
                   ("w2", rows(a["L0_ffn_W2"], 4)), ("b2", bc(a["L0_ffn_b2"]))]
    L["L1_xattn"] = [("wq", a["L1_xattn_Wq"].T), ("wk", a["L1_xattn_Wk"].T), ("wv", a["L1_xattn_Wv"].T),
                     ("wo", a["L1_xattn_Wo"].T), ("bq", cols(a["L1_xattn_bq"])), ("bk", cols(a["L1_xattn_bk"])),
                     ("bv", cols(a["L1_xattn_bv"])), ("bo", bc(a["L1_xattn_bo"]))]
    L["L1_attn"] = [("wq", a["L1_attn_W_q"]), ("wk", np.tile(a["L1_attn_W_k"], (1, H))),
                    ("wv", np.tile(a["L1_attn_W_v"], (1, H))), ("wo", a["L1_attn_W_o"])]
    L["L1_ffn"] = [("gate", a["L1_ffn_gate_w"].T), ("down", a["L1_ffn_down_w"].reshape(512, D).T),
                   ("bd", cols(a["L1_ffn_down_b"].reshape(-1))),
                   ("up", rows(a["L1_ffn_up_w"].transpose(0, 2, 1).reshape(512, D), 4)), ("bu", pad(a["L1_ffn_up_b"]))]
    wq, wk = (a[f"L2_xattn_W{n}"].reshape(D, 16, 64).transpose(2, 1, 0).reshape(64, -1) for n in "qk")
    wv = a["L2_xattn_Wv"].reshape(D, 16, 64).transpose(2, 1, 0).reshape(64, -1)
    wo = a["L2_xattn_Wo"].reshape(16, 64, D).transpose(1, 0, 2).reshape(64, -1)
    L["L2_xattn"] = [("wq", pad(wq)), ("wk", pad(wk)), ("wv", pad(wv)), ("wo", pad(wo)), ("bo", bc(a["L2_xattn_bo"]))]
    L["L2_attn"] = [("td", cols(a["L2_attn_time_decay"])), ("tf", cols(a["L2_attn_time_first"])),
                    ("mk", cols(a["L2_attn_time_mix_k"])), ("mv", cols(a["L2_attn_time_mix_v"])),
                    ("mr", cols(a["L2_attn_time_mix_r"])), ("wk", a["L2_attn_Wk"].T), ("wv", a["L2_attn_Wv"].T),
                    ("wr", a["L2_attn_Wr"].T), ("wo", a["L2_attn_Wo"].T)]
    L["L2_ffn"] = [("gate", a["L2_ffn_gate_w"].T), ("w1", a["L2_ffn_w1"].transpose(1, 0, 2).reshape(D, -1)),
                   ("b1", cols(a["L2_ffn_b1"].reshape(-1))), ("w2", rows(a["L2_ffn_w2"].reshape(-1, D), 28)),
                   ("b2", pad(a["L2_ffn_b2"]))]
    L["L3_xattn"] = [("wq", a["L3_xattn_Wq"]), ("wk", a["L3_xattn_Wk"]), ("wv", a["L3_xattn_Wv"].T),
                     ("wb", a["L3_xattn_Wbeta"].T), ("wa", a["L3_xattn_Walpha"].T), ("wo", a["L3_xattn_Wo"].T),
                     ("bo", bc(a["L3_xattn_bo"])), ("bb", bc(a["L3_xattn_bbeta"])), ("ba", bc(a["L3_xattn_balpha"])),
                     ("gq", bc(np.tile(a["L3_xattn_gq"], H))), ("bq", bc(np.tile(a["L3_xattn_bq"], H))),
                     ("gk", bc(np.tile(a["L3_xattn_gk"], H))), ("bk", bc(np.tile(a["L3_xattn_bk"], H)))]
    swap = np.arange(D) ^ 1
    L["L3_attn"] = [("wq", a["L3_attn_Wq"]), ("wk", a["L3_attn_Wk"]), ("wqs", a["L3_attn_Wq"][:, swap]),
                    ("wks", a["L3_attn_Wk"][:, swap]), ("wv", a["L3_attn_Wv"]), ("wg", a["L3_attn_Wg"]),
                    ("wo", rows(a["L3_attn_Wo"], 2)), ("gn", cols(np.tile(a["L3_attn_g_norm_w"], 4)))]
    L["L3_ffn"] = [("gate", a["L3_ffn_router_w"].T), ("wg", a["L3_ffn_w_gate"].reshape(-1, D).T),
                   ("wu", a["L3_ffn_w_up"].reshape(-1, D).T),
                   ("wd", rows(a["L3_ffn_w_down"].transpose(0, 2, 1).reshape(-1, D), 16))]
    return L


def columns(parts):
    at, n = {}, 0
    for name, w in parts:
        at[name] = (n, w.shape[1])
        n += w.shape[1]
    return at, n


class Net:

    def __init__(self, nc, ctx, wdram, where, consts_at, ctx_dram, masks):
        self.nc, self.ctx, self.wdram, self.where = nc, ctx, wdram, where
        self.ctx_dram, self.masks = ctx_dram, masks
        self.signals = {}
        self.X = self.sb("x", [P, TILES, D])
        self.stats = self.sb("stats", [P, TILES, 6])
        self.mean = self.sb("mean", [P, TILES])
        self.rstd = self.sb("rstd", [P, TILES])
        self.lntmp = self.sb("lntmp", [P, 4, TILES])
        nconst = max(a + n for a, n in consts_at.values())
        self.K = self.sb("consts", [P, nconst])
        self.consts_at = consts_at
        self.W = [self.sb(f"w{i}", [P, max(n for _, n in where.values())]) for i in range(2)]
        self.PS = ctx.enter_context(nc.psum_tensor("banks", [P, 8, 512], F32))
        self.PB = [self.PS[:, i, :] for i in range(8)]
        self.index = {}

    def sb(self, name, shape, dt=F32, ctx=None):
        return (ctx or self.ctx).enter_context(self.nc.sbuf_tensor(name, shape, dt))

    def const(self, name):
        a, n = self.consts_at[name]
        return self.K[:, a:a + n]

    def sig(self, name, per=1, iters=1):
        if name not in self.signals:
            self.signals[name] = Signal(self.ctx.enter_context(self.nc.semaphore(name)))
        return self.signals[name].use(per, iters)


class Block:

    iters, group, name = G, 4, None
    vsteps = 0

    def __init__(self, net, index):
        self.net, self.index = net, index
        at, _ = net.where[self.name]
        wbuf = net.W[index % 2]
        self.w = {k: wbuf[:, a:a + n] for k, (a, n) in at.items()}
        self.scratch = ExitStack()
        self.weights = net.sig(f"weights_loaded_{("even", "odd")[index % 2]}", 16)
        self.lnchain = Steps(net.sig("layernorm_steps", 7))
        self.var = net.sig("variance_ready")
        self.std = net.sig("std_ready")
        self.setup_chain = Steps(net.sig("setup_steps", self.setup_steps))
        self.chain = Steps(net.sig("vector_steps", self.vsteps, self.iters))
        self.xn_r = net.sig("xn_ready", 1, self.iters)
        if self.whole_xnT:
            self.xnT_ps = net.sig("xnT_in_psum", 1, self.iters)
            self.xnT_r = net.sig("xnT_ready", 1, self.iters)
        self.res = net.sig("residual_added", 1, self.iters)
        self.xn = self.sb("xn", [P, self.group, D])
        self.xnT = self.sb("xnT", [P, self.group * P])
        self.plan()
        self.scratch.close()

    setup_steps = 0
    whole_xnT = True

    def sb(self, name, shape, dt=F32):
        return self.net.sb(f"{self.name}_{name}", shape, dt, self.scratch)

    def sig(self, name, per=1, iters=None):
        return self.net.sig(name, per, self.iters if iters is None else iters)

    def ln_vector(self, e):
        n = self.net
        e.wait_ge(self.weights.sem, self.weights.at(0))
        e.wait_ge(self.res.sem, self.res.at(0, 0))
        st, c = n.stats, self.lnchain
        me, ve, mo, vo = (st[:, :, j] for j in (1, 2, 4, 5))
        t = n.lntmp
        c.start()
        e.tensor_tensor(t[:, 0, :], me, mo, ALU.add).then_inc(c.sem, 1)
        e.wait_ge(c.sem, c.next())
        e.tensor_scalar(n.mean[:, :], t[:, 0, :], 0.5, None, ALU.mult).then_inc(c.sem, 1)
        e.wait_ge(c.sem, c.next())
        e.tensor_tensor(t[:, 1, :], me, mo, ALU.subtract).then_inc(c.sem, 1)
        e.wait_ge(c.sem, c.next())
        e.scalar_tensor_tensor(out=t[:, 2, :], in0=t[:, 1, :], scalar=32.0, in1=t[:, 1, :], op0=ALU.mult, op1=ALU.mult).then_inc(c.sem, 1)
        e.wait_ge(c.sem, c.next())
        e.tensor_tensor(t[:, 3, :], ve, vo, ALU.add).then_inc(c.sem, 1)
        e.wait_ge(c.sem, c.next())
        e.tensor_tensor(t[:, 0, :], t[:, 3, :], t[:, 2, :], ALU.add).then_inc(c.sem, 1)
        e.wait_ge(c.sem, c.next())
        e.tensor_scalar(t[:, 1, :], t[:, 0, :], 1.0 / D, LN_EPS, ALU.mult, ALU.add).then_inc(self.var.sem, 1)
        e.wait_ge(self.std.sem, self.std.at(0))
        e.reciprocal(n.rstd[:, :], t[:, 2, :]).then_inc(c.sem, 1)
        e.wait_ge(c.sem, c.next())
        c.done()

    def ln_scalar(self, e):
        e.wait_ge(self.weights.sem, self.weights.at(0))
        e.wait_ge(self.var.sem, self.var.at(0))
        e.activation(self.net.lntmp[:, 2, :], self.net.lntmp[:, 1, :], ACT.Sqrt).then_inc(self.std.sem, 1)

    def norm(self, e, i):
        n = self.net
        e.wait_ge(self.res.sem, self.res.at(i, 0))
        for j in range(self.group):
            t = i * self.group + j
            ins = e.tensor_scalar(self.xn[:, j, :], n.X[:, bass.ds(t, 1), :], n.mean[:, bass.ds(t, 1)], n.rstd[:, bass.ds(t, 1)],
                                  ALU.subtract, ALU.mult)
        ins.then_inc(self.xn_r.sem, 1)

    def transpose_xn(self, e, i, bank):
        e.wait_ge(self.xn_r.sem, self.xn_r.at(i))
        for j in range(self.group):
            ins = e.transpose(bank[:, j * P:(j + 1) * P], self.xn[:, j, :], self.net.const("ident"))
        ins.then_inc(self.xnT_ps.sem, 1)

    def copy_xnT(self, e, i, bank):
        e.wait_ge(self.xnT_ps.sem, self.xnT_ps.at(i))
        e.copy(self.xnT[:, :], bank[:, 0:self.group * P]).then_inc(self.xnT_r.sem, 1)

    def add_residual(self, e, i, y, ready):
        n = self.net
        g = self.group
        e.wait_ge(ready.sem, ready.at(i))
        xs = n.X[:, bass.ds(i * g, g), :]
        e.tensor_tensor(xs, y, xs, ALU.add).then_inc(self.chain.sem, 1)
        e.wait_ge(self.chain.sem, self.chain.next(i))
        for j in range(g):
            ins = e.bn_stats(n.stats[:, bass.ds(i * g + j, 1), :], n.X[:, bass.ds(i * g + j, 1), :])
        ins.then_inc(self.res.sem, 1)

    def project(self, e, bank, lhs, w, bias=None, tiles=4):
        for j in range(tiles):
            o = bank[:, j * P:(j + 1) * P]
            if bias is not None:
                e.matmul(o, self.net.const("ones")[0:1, :], bias[0:1, :], start=True, stop=False)
            for k in range(len(lhs)):
                ins = e.matmul(o, lhs[k][:, j * P:(j + 1) * P], w[k], start=(k == 0 and bias is None), stop=(k == len(lhs) - 1))
        return ins


TWO_PI = 6.283185307179586
PI_IN = 3.1415925
ROUND = 12582912.0
PI_HI = 6.28125
PI_LO = TWO_PI - PI_HI


class L0Ffn(Block):

    name = "L0_ffn"
    vsteps = 7
    setup_steps = 13

    def plan(self):
        self.hid = self.sb("hid", [P, 4, 512])
        self.arg = self.sb("arg", [P, 4, 512])
        self.tmp = self.sb("tmp", [P, 4, 512])
        self.f = self.sb("features", [P, 8, 4])
        self.angles = self.sig("angles_ready", 1, 1)
        self.sines = self.sig("sines_ready", 1, 1)
        self.hid_ps = self.sig("hidden_in_psum")
        self.hid_r = self.sig("hidden_ready")
        self.arg_r = self.sig("argument_ready")
        self.sin_r = self.sig("sine_ready")
        self.act_r = self.sig("activated_ready")
        self.y_ps = self.sig("y_in_psum")

    def vector(self, e):
        self.ln_vector(e)
        w, f, c = self.w, self.f, self.setup_chain
        k, th, co, cf = f[:, 0, :], f[:, 1, :], f[:, 2, :], f[:, 7, :]
        e.tensor_scalar(k, w["theta"], 1 / TWO_PI, ROUND, ALU.mult, ALU.add).then_inc(c.sem, 1)
        e.wait_ge(c.sem, c.next())
        e.tensor_scalar(k, k, ROUND, None, ALU.subtract).then_inc(c.sem, 1)
        e.wait_ge(c.sem, c.next())
        e.scalar_tensor_tensor(out=th, in0=k, scalar=-PI_HI, in1=w["theta"], op0=ALU.mult, op1=ALU.add).then_inc(c.sem, 1)
        e.wait_ge(c.sem, c.next())
        e.scalar_tensor_tensor(out=th, in0=k, scalar=-PI_LO, in1=th, op0=ALU.mult, op1=ALU.add).then_inc(c.sem, 1)
        e.wait_ge(c.sem, c.next())
        e.tensor_scalar(th, th, PI_IN, -PI_IN, ALU.min, ALU.max).then_inc(c.sem, 1)
        e.wait_ge(c.sem, c.next())
        e.tensor_scalar(co, th, TWO_PI / 4, None, ALU.add).then_inc(c.sem, 1)
        e.wait_ge(c.sem, c.next())
        e.tensor_scalar(k, co, TWO_PI / 2, -TWO_PI, ALU.is_gt, ALU.mult).then_inc(c.sem, 1)
        e.wait_ge(c.sem, c.next())
        e.tensor_tensor(co, co, k, ALU.add).then_inc(c.sem, 1)
        e.wait_ge(c.sem, c.next())
        e.tensor_scalar(co, co, PI_IN, -PI_IN, ALU.min, ALU.max).then_inc(c.sem, 1)
        e.wait_ge(c.sem, c.next())
        e.tensor_copy(k, th).then_inc(self.angles.sem, 1)
        e.wait_ge(self.sines.sem, self.sines.at(0))
        e.tensor_tensor(f[:, 5, :], f[:, 4, :], w["wr"], ALU.mult).then_inc(c.sem, 1)
        e.wait_ge(c.sem, c.next())
        e.tensor_tensor(f[:, 6, :], f[:, 3, :], w["wi"], ALU.mult).then_inc(c.sem, 1)
        e.wait_ge(c.sem, c.next())
        e.tensor_tensor(f[:, 5, :], f[:, 5, :], f[:, 6, :], ALU.add).then_inc(c.sem, 1)
        e.wait_ge(c.sem, c.next())
        e.scalar_tensor_tensor(out=cf, in0=f[:, 5, :], scalar=0.1, in1=w["wi"], op0=ALU.mult, op1=ALU.mult).then_inc(c.sem, 1)
        e.wait_ge(c.sem, c.next())
        c.done()
        with e.Fori(0, self.iters) as i:
            self.chain.start()
            self.norm(e, i)
            e.wait_ge(self.hid_r.sem, self.hid_r.at(i))
            for j in range(4):
                ins = e.tensor_scalar(self.arg[:, j, :], self.hid[:, j, :], 0.1, th[:, j:j + 1], ALU.mult, ALU.add)
            ins.then_inc(self.chain.sem, 1)
            e.wait_ge(self.chain.sem, self.chain.next(i))
            e.tensor_scalar(self.tmp[:], self.arg[:], 1 / TWO_PI, ROUND, ALU.mult, ALU.add).then_inc(self.chain.sem, 1)
            e.wait_ge(self.chain.sem, self.chain.next(i))
            e.tensor_scalar(self.tmp[:], self.tmp[:], ROUND, -TWO_PI, ALU.subtract, ALU.mult).then_inc(self.chain.sem, 1)
            e.wait_ge(self.chain.sem, self.chain.next(i))
            e.tensor_tensor(self.arg[:], self.arg[:], self.tmp[:], ALU.add).then_inc(self.chain.sem, 1)
            e.wait_ge(self.chain.sem, self.chain.next(i))
            e.tensor_scalar(self.arg[:], self.arg[:], PI_IN, -PI_IN, ALU.min, ALU.max).then_inc(self.arg_r.sem, 1)
            e.wait_ge(self.sin_r.sem, self.sin_r.at(i))
            for j in range(4):
                ins = e.scalar_tensor_tensor(out=self.hid[:, j, :], in0=self.tmp[:, j, :], scalar=cf[:, j:j + 1],
                                             in1=self.hid[:, j, :], op0=ALU.mult, op1=ALU.add)
                if j == 2:
                    ins.then_inc(self.chain.sem, 1)
                    e.wait_ge(self.chain.sem, self.chain.next(i))
            ins.then_inc(self.chain.sem, 1)
            e.wait_ge(self.chain.sem, self.chain.next(i))
            e.tensor_scalar(self.arg[:], self.hid[:], 0.0, None, ALU.max).then_inc(self.act_r.sem, 1)
            self.add_residual(e, i, self.net.PB[5][:, :].rearrange("p (j d) -> p j d", j=4), self.y_ps)
        self.chain.done()

    def scalar(self, e):
        self.ln_scalar(e)
        f = self.f
        e.wait_ge(self.angles.sem, self.angles.at(0))
        e.activation(f[:, 3, :], f[:, 1, :], ACT.Sin)
        e.activation(f[:, 4, :], f[:, 2, :], ACT.Sin).then_inc(self.sines.sem, 1)
        with e.Fori(0, self.iters) as i:
            self.copy_xnT(e, i, self.net.PB[0])
            e.wait_ge(self.hid_ps.sem, self.hid_ps.at(i))
            for j in range(4):
                ins = e.activation(self.hid[:, j, :], self.net.PB[1 + j][:, :], ACT.Identity, bias=self.w["b1"][:, j:j + 1])
            ins.then_inc(self.hid_r.sem, 1)
            e.wait_ge(self.arg_r.sem, self.arg_r.at(i))
            e.activation(self.tmp[:], self.arg[:], ACT.Sin).then_inc(self.sin_r.sem, 1)

    def tensor(self, e):
        w, n = self.w, self.net
        e.wait_ge(self.weights.sem, self.weights.at(0))
        with e.Fori(0, self.iters) as i:
            self.transpose_xn(e, i, n.PB[0])
            e.wait_ge(self.xnT_r.sem, self.xnT_r.at(i))
            for j in range(4):
                ins = e.matmul(n.PB[1 + j][:, :], w["w1"][:, j * P:(j + 1) * P], self.xnT[:, :], start=True, stop=True)
            ins.then_inc(self.hid_ps.sem, 1)
            e.wait_ge(self.act_r.sem, self.act_r.at(i))
            self.project(e, n.PB[5], [self.arg[:, k, :] for k in range(4)], [w["w2"][:, k * P:(k + 1) * P] for k in range(4)],
                         w["b2"]).then_inc(self.y_ps.sem, 1)

    def gpsimd(self, e):
        pass

    def sync(self, e):
        pass


class L0Attn(Block):

    name = "L0_attn"
    whole_xnT = False
    vsteps = 13

    def plan(self):
        self.ms = self.sb("meansquare", [P, 2, 3, 4])
        self.sq = self.sb("squares", [P, 4, D])
        self.hn = self.sb("hn", [P, 4, D])
        self.hT = self.sb("hT", [P, 512])
        self.xin = self.sb("xin", [P, 2, 512])
        self.gate = self.sb("gate", [P, 2, 512])
        self.a = self.sb("decay", [P, 2, 512])
        self.t = self.sb("t", [P, 2, 512])
        self.y = self.sb("y", [P, 2, 512])
        self.x2 = self.sb("x2", [P, 4, D])
        self.sg = self.sb("sg", [P, 4, 512])
        self.m = self.sb("m", [P, 4, 512])
        self.sq_r = self.sig("squares_summed", 2)
        self.ms_r = self.sig("meansquare_ready", 2)
        self.rt_r = self.sig("root_ready", 2)
        self.hn_r = self.sig("rms_normed", 2)
        self.x2_r = self.sig("x2_ready")
        self.hT_ps = self.sig("rms_in_psum", 2)
        self.hT_r = self.sig("rms_transposed", 2)
        self.in_ps = self.sig("hidden_in_psum")
        self.xin_r = self.sig("xin_ready")
        self.gate_r = self.sig("gate_ready")
        self.a_ps = self.sig("decay_in_psum")
        self.a_r = self.sig("decay_ready")
        self.t_r = self.sig("one_minus_square_ready")
        self.rest_r = self.sig("complement_ready")
        self.y_r = self.sig("activated_ready")
        self.wo_ps = self.sig("recurrence_in_psum")
        self.mlp_ps = self.sig("mlp_in_psum")
        self.sg_r = self.sig("mlp_sigmoid_ready")
        self.m_r = self.sig("mlp_hidden_ready")
        self.y_ps = self.sig("y_in_psum")

    def rms_vector(self, e, i, k, src):
        m = self.ms[:, k - 1]
        e.wait_ge(self.sq_r.sem, self.sq_r.at(i, k))
        e.tensor_scalar(m[:, 1, :], m[:, 0, :], 1.0 / D, 1e-6, ALU.mult, ALU.add).then_inc(self.ms_r.sem, 1)
        e.wait_ge(self.rt_r.sem, self.rt_r.at(i, k))
        e.reciprocal(m[:, 2, :], m[:, 2, :]).then_inc(self.chain.sem, 1)
        e.wait_ge(self.chain.sem, self.chain.next(i))
        for j in range(4):
            ins = e.tensor_scalar(self.hn[:, j, :], src[:, j, :], m[:, 2, j:j + 1], None, ALU.mult)
        ins.then_inc(self.hn_r.sem, 1)

    def rms_scalar(self, e, i, k, src, ln, bank, ready):
        m = self.ms[:, k - 1]
        e.wait_ge(ready.sem, ready.at(i))
        for j in range(4):
            ins = e.activation(self.sq[:, j, :], src[:, j, :], ACT.Square, accum_out=m[:, 0, j:j + 1])
        ins.then_inc(self.sq_r.sem, 1)
        e.wait_ge(self.ms_r.sem, self.ms_r.at(i, k))
        e.activation(m[:, 2, :], m[:, 1, :], ACT.Sqrt).then_inc(self.rt_r.sem, 1)
        e.wait_ge(self.hT_ps.sem, self.hT_ps.at(i, k))
        e.activation(self.hT[:, :], bank[:, :], ACT.Copy, scale=ln).then_inc(self.hT_r.sem, 1)

    def rms_tensor(self, e, i, k, bank):
        e.wait_ge(self.hn_r.sem, self.hn_r.at(i, k))
        for j in range(4):
            ins = e.transpose(bank[:, j * P:(j + 1) * P], self.hn[:, j, :], self.net.const("ident"))
        ins.then_inc(self.hT_ps.sem, 1)
        e.wait_ge(self.hT_r.sem, self.hT_r.at(i, k))

    def vector(self, e):
        self.ln_vector(e)
        PB = self.net.PB
        with e.Fori(0, self.iters) as i:
            c = self.chain
            c.start()
            self.norm(e, i)
            self.rms_vector(e, i, 1, self.xn)
            e.wait_ge(self.in_ps.sem, self.in_ps.at(i))
            for j in range(2):
                ins = e.tensor_copy(self.xin[:, j, :], PB[1 + j][:, :])
            ins.then_inc(self.xin_r.sem, 1)
            e.wait_ge(self.a_r.sem, self.a_r.at(i))
            e.tensor_tensor(self.t[:], self.a[:], self.a[:], ALU.mult).then_inc(c.sem, 1)
            e.wait_ge(c.sem, c.next(i))
            e.tensor_scalar(self.t[:], self.t[:], -1.0, 1.0, ALU.mult, ALU.add).then_inc(self.t_r.sem, 1)
            e.memset(self.a[:].rearrange("p j (b s) -> p (j b) s", s=S)[:, :, 0:1], 0.0).then_inc(c.sem, 1)
            e.wait_ge(c.sem, c.next(i))
            e.wait_ge(self.rest_r.sem, self.rest_r.at(i))
            e.tensor_tensor(self.t[:], self.t[:], self.xin[:], ALU.mult).then_inc(c.sem, 1)
            e.wait_ge(c.sem, c.next(i))
            for j in range(2):
                e.tensor_tensor_scan(self.y[:, j, :], self.a[:, j, :], self.t[:, j, :], 0.0, ALU.mult, ALU.add).then_inc(c.sem, 1)
                e.wait_ge(c.sem, c.next(i))
            e.wait_ge(self.gate_r.sem, self.gate_r.at(i))
            e.tensor_tensor(self.y[:], self.y[:], self.gate[:], ALU.mult).then_inc(self.y_r.sem, 1)
            e.wait_ge(self.wo_ps.sem, self.wo_ps.at(i))
            e.tensor_tensor(self.x2[:], PB[7][:, :].rearrange("p (j d) -> p j d", j=4), self.xn[:], ALU.add).then_inc(self.x2_r.sem, 1)
            self.rms_vector(e, i, 2, self.x2)
            e.wait_ge(self.sg_r.sem, self.sg_r.at(i))
            for j in range(4):
                e.tensor_tensor(self.sg[:, j, :], PB[j][:, :], self.sg[:, j, :], ALU.mult).then_inc(c.sem, 1)
                e.wait_ge(c.sem, c.next(i))
            for j in range(4):
                ins = e.tensor_tensor(self.m[:, j, :], PB[4 + j][:, :], self.sg[:, j, :], ALU.mult)
            ins.then_inc(self.m_r.sem, 1)
            xs = self.net.X[:, bass.ds(i * 4, 4), :]
            e.tensor_tensor(xs, self.x2[:], xs, ALU.add).then_inc(c.sem, 1)
            e.wait_ge(c.sem, c.next(i))
            self.add_residual(e, i, PB[0][:, :].rearrange("p (j d) -> p j d", j=4), self.y_ps)
        self.chain.done()

    def scalar(self, e):
        self.ln_scalar(e)
        PB, w = self.net.PB, self.w
        with e.Fori(0, self.iters) as i:
            self.rms_scalar(e, i, 1, self.xn, w["ln1"], PB[0], self.xn_r)
            e.wait_ge(self.in_ps.sem, self.in_ps.at(i))
            for j in range(2):
                ins = e.activation(self.gate[:, j, :], PB[3 + j][:, :], ACT.Sigmoid)
            ins.then_inc(self.gate_r.sem, 1)
            e.wait_ge(self.a_ps.sem, self.a_ps.at(i))
            for j in range(2):
                ins = e.activation(self.a[:, j, :], PB[5 + j][:, :], ACT.Sigmoid, bias=w["ap"][:, j:j + 1])
            ins.then_inc(self.a_r.sem, 1)
            e.wait_ge(self.t_r.sem, self.t_r.at(i))
            e.activation(self.t[:], self.t[:], ACT.Sqrt, bias=self.net.const("eps8")).then_inc(self.rest_r.sem, 1)
            self.rms_scalar(e, i, 2, self.x2, w["ln2"], PB[0], self.x2_r)
            e.wait_ge(self.mlp_ps.sem, self.mlp_ps.at(i))
            for j in range(4):
                ins = e.activation(self.sg[:, j, :], PB[j][:, :], ACT.Sigmoid)
            ins.then_inc(self.sg_r.sem, 1)

    def tensor(self, e):
        PB, w = self.net.PB, self.w
        with e.Fori(0, self.iters) as i:
            self.rms_tensor(e, i, 1, PB[0])
            for j in range(2):
                e.matmul(PB[1 + j][:, :], w["win"][:, j * P:(j + 1) * P], self.hT[:, :], start=True, stop=True)
            for j in range(2):
                ins = e.matmul(PB[3 + j][:, :], w["wgate"][:, j * P:(j + 1) * P], self.hT[:, :], start=True, stop=True)
            ins.then_inc(self.in_ps.sem, 1)
            e.wait_ge(self.xin_r.sem, self.xin_r.at(i))
            for j in range(2):
                for k in range(2):
                    a = k * 256 + j * P
                    ins = e.matmul(PB[5 + j][:, :], w["wa"][:, a:a + P], self.xin[:, k, :], start=(k == 0), stop=(k == 1))
            ins.then_inc(self.a_ps.sem, 1)
            e.wait_ge(self.y_r.sem, self.y_r.at(i))
            self.project(e, PB[7], [self.y[:, k, :] for k in range(2)], [w["wout"][:, k * P:(k + 1) * P] for k in range(2)])\
                .then_inc(self.wo_ps.sem, 1)
            self.rms_tensor(e, i, 2, PB[0])
            for name, b in (("wmg", 0), ("wmu", 4)):
                for j in range(4):
                    ins = e.matmul(PB[b + j][:, :], w[name][:, j * P:(j + 1) * P], self.hT[:, :], start=True, stop=True)
            ins.then_inc(self.mlp_ps.sem, 1)
            e.wait_ge(self.m_r.sem, self.m_r.at(i))
            self.project(e, PB[0], [self.m[:, k, :] for k in range(4)], [w["wmd"][:, k * P:(k + 1) * P] for k in range(4)])\
                .then_inc(self.y_ps.sem, 1)

    def gpsimd(self, e):
        pass

    def sync(self, e):
        pass


class L2Attn(Block):

    name = "L2_attn"
    vsteps = 17
    setup_steps = 4

    def plan(self):
        s3 = [P, 16, 33]
        self.xs = self.sb("xs", s3)
        self.mix = self.sb("mixed", [P, 3, 16, S])
        self.dx = self.sb("dx", [P, 16, S])
        self.k = self.sb("k", s3)
        self.v = self.sb("v", [P, 16, S])
        self.sr = self.sb("sr", [P, 16, S])
        self.wdec = self.sb("wdecay", s3)
        self.pp = self.sb("pp", s3)
        self.e1 = self.sb("e1", s3)
        self.e2 = self.sb("e2", s3)
        self.ev = self.sb("ev", s3)
        self.aa = self.sb("aa", s3)
        self.bb = self.sb("bb", s3)
        self.p = self.sb("p", [P, 2, 16, S])
        self.q = self.sb("q", [P, 2, 16, S])
        self.num = self.sb("num", [P, 2, 16, S])
        self.neg = self.sb("negw", [P, 2])
        self.expw = self.sig("decay_exp_ready", 1, 1)
        self.mix_r = self.sig("mixed_ready", 3)
        self.kvr_ps = self.sig("hidden_in_psum")
        self.kvr_r = self.sig("kvr_ready")
        self.arg1 = self.sig("exponents_ready", 2)
        self.exp1 = self.sig("exps_ready", 2)
        self.act_r = self.sig("activated_ready")
        self.y_ps = self.sig("y_in_psum")

    def vector(self, e):
        self.ln_vector(e)
        w, c = self.w, self.setup_chain
        now, before = slice(1, 33), slice(0, 32)
        e.memset(self.xs[:, :, 0:1], 0.0)
        e.memset(self.k[:, :, 0:1], -1e38)
        e.memset(self.e1[:, :, 0:1], 0.0)
        e.memset(self.e2[:, :, 0:1], 0.0)
        e.memset(self.ev[:, :, 0:1], 0.0).then_inc(c.sem, 1)
        e.wait_ge(c.sem, c.next())
        e.wait_ge(self.expw.sem, self.expw.at(0))
        e.tensor_scalar(self.neg[:, 1:2], self.neg[:, 0:1], -1.0, None, ALU.mult).then_inc(c.sem, 1)
        e.wait_ge(c.sem, c.next())
        e.memset(self.wdec[:], 0.0).then_inc(c.sem, 1)
        e.wait_ge(c.sem, c.next())
        e.tensor_scalar(self.wdec[:, :, now], self.wdec[:, :, now], self.neg[:, 1:2], None, ALU.add)
        e.memset(self.wdec[:, :, 0:1], -1e38).then_inc(c.sem, 1)
        e.wait_ge(c.sem, c.next())
        c.done()
        flat = lambda t: t[:].rearrange("p b s -> p (b s)")
        with e.Fori(0, self.iters) as i:
            c = self.chain
            c.start()
            self.norm(e, i)
            e.wait_ge(self.xnT_r.sem, self.xnT_r.at(i))
            e.tensor_tensor(self.dx[:], self.xs[:, :, now], self.xs[:, :, before], ALU.subtract).then_inc(c.sem, 1)
            e.wait_ge(c.sem, c.next(i))
            for j, m in enumerate(("mk", "mv", "mr")):
                e.scalar_tensor_tensor(out=self.mix[:, j], in0=self.dx[:], scalar=w[m], in1=self.xs[:, :, before],
                                       op0=ALU.mult, op1=ALU.add).then_inc(self.mix_r.sem, 1)
            e.wait_ge(self.kvr_r.sem, self.kvr_r.at(i))
            e.tensor_tensor_scan(flat(self.pp), flat(self.wdec), flat(self.k), -1e38, ALU.add, ALU.max).then_inc(c.sem, 1)
            e.wait_ge(c.sem, c.next(i))
            pb, pn, kn = self.pp[:, :, before], self.pp[:, :, now], self.k[:, :, now]
            e.scalar_tensor_tensor(out=self.p[:, 0], in0=pb, scalar=self.neg[:, 1:2], in1=pn, op0=ALU.add, op1=ALU.subtract).then_inc(c.sem, 1)
            e.wait_ge(c.sem, c.next(i))
            e.tensor_tensor(self.p[:, 1], kn, pn, ALU.subtract).then_inc(self.arg1.sem, 1)
            e.tensor_scalar(self.num[:, 0], kn, w["tf"], None, ALU.add).then_inc(c.sem, 1)
            e.wait_ge(c.sem, c.next(i))
            e.tensor_tensor(self.num[:, 1], self.num[:, 0], pb, ALU.max).then_inc(c.sem, 1)
            e.wait_ge(c.sem, c.next(i))
            e.tensor_tensor(self.q[:, 0], pb, self.num[:, 1], ALU.subtract).then_inc(c.sem, 1)
            e.wait_ge(c.sem, c.next(i))
            e.tensor_tensor(self.q[:, 1], self.num[:, 0], self.num[:, 1], ALU.subtract).then_inc(self.arg1.sem, 1)
            e.wait_ge(self.exp1.sem, self.exp1.at(i, 1))
            e.tensor_tensor(self.ev[:, :, now], self.e2[:, :, now], self.v[:], ALU.mult).then_inc(c.sem, 1)
            e.wait_ge(c.sem, c.next(i))
            e.tensor_tensor_scan(flat(self.aa), flat(self.e1), flat(self.ev), 0.0, ALU.mult, ALU.add).then_inc(c.sem, 1)
            e.wait_ge(c.sem, c.next(i))
            e.tensor_tensor_scan(flat(self.bb), flat(self.e1), flat(self.e2), 0.0, ALU.mult, ALU.add).then_inc(c.sem, 1)
            e.wait_ge(c.sem, c.next(i))
            e.wait_ge(self.exp1.sem, self.exp1.at(i, 2))
            e.tensor_tensor(self.num[:, 0], self.q[:, 0], self.aa[:, :, before], ALU.mult).then_inc(c.sem, 1)
            e.wait_ge(c.sem, c.next(i))
            e.tensor_tensor(self.num[:, 1], self.q[:, 0], self.bb[:, :, before], ALU.mult).then_inc(c.sem, 1)
            e.wait_ge(c.sem, c.next(i))
            e.tensor_tensor(self.p[:, 0], self.q[:, 1], self.v[:], ALU.mult).then_inc(c.sem, 1)
            e.wait_ge(c.sem, c.next(i))
            e.tensor_tensor(self.p[:, 0], self.p[:, 0], self.num[:, 0], ALU.add).then_inc(c.sem, 1)
            e.wait_ge(c.sem, c.next(i))
            e.tensor_tensor(self.p[:, 1], self.q[:, 1], self.num[:, 1], ALU.add).then_inc(c.sem, 1)
            e.wait_ge(c.sem, c.next(i))
            e.reciprocal(self.p[:, 1], self.p[:, 1]).then_inc(c.sem, 1)
            e.wait_ge(c.sem, c.next(i))
            e.tensor_tensor(self.p[:, 0], self.p[:, 0], self.p[:, 1], ALU.mult).then_inc(c.sem, 1)
            e.wait_ge(c.sem, c.next(i))
            e.tensor_tensor(self.q[:, 0], self.p[:, 0], self.sr[:], ALU.mult).then_inc(self.act_r.sem, 1)
            self.add_residual(e, i, self.net.PB[4][:, :].rearrange("p (j d) -> p j d", j=4), self.y_ps)
        self.chain.done()

    def scalar(self, e):
        self.ln_scalar(e)
        PB = self.net.PB
        e.activation(self.neg[:, 0:1], self.w["td"], ACT.Exp).then_inc(self.expw.sem, 1)
        seqs = lambda b: b[:, :].rearrange("p (b s) -> p b s", s=S)
        with e.Fori(0, self.iters) as i:
            e.wait_ge(self.xnT_ps.sem, self.xnT_ps.at(i))
            e.activation(self.xs[:, :, 1:33], seqs(PB[0]), ACT.Copy).then_inc(self.xnT_r.sem, 1)
            e.wait_ge(self.kvr_ps.sem, self.kvr_ps.at(i))
            e.activation(self.k[:, :, 1:33], seqs(PB[1]), ACT.Copy)
            e.activation(self.v[:], seqs(PB[2]), ACT.Copy)
            e.activation(self.sr[:], seqs(PB[3]), ACT.Sigmoid).then_inc(self.kvr_r.sem, 1)
            e.wait_ge(self.arg1.sem, self.arg1.at(i, 1))
            e.activation(self.e1[:, :, 1:33], self.p[:, 0], ACT.Exp)
            e.activation(self.e2[:, :, 1:33], self.p[:, 1], ACT.Exp).then_inc(self.exp1.sem, 1)
            e.wait_ge(self.arg1.sem, self.arg1.at(i, 2))
            e.activation(self.q[:], self.q[:], ACT.Exp).then_inc(self.exp1.sem, 1)

    def tensor(self, e):
        PB, w = self.net.PB, self.w
        with e.Fori(0, self.iters) as i:
            self.transpose_xn(e, i, PB[0])
            for j, m in enumerate(("wk", "wv", "wr")):
                e.wait_ge(self.mix_r.sem, self.mix_r.at(i, j + 1))
                ins = e.matmul(PB[1 + j][:, :], w[m], self.mix[:, j].rearrange("p b s -> p (b s)"), start=True, stop=True)
            ins.then_inc(self.kvr_ps.sem, 1)
            e.wait_ge(self.act_r.sem, self.act_r.at(i))
            self.project(e, PB[4], [self.q[:, 0].rearrange("p b s -> p (b s)")], [w["wo"]]).then_inc(self.y_ps.sem, 1)

    def gpsimd(self, e):
        pass

    def sync(self, e):
        pass


def router(c, i, e, block, lg, n, E, probs, floor, plus):
    r = block
    big = lambda t: t[:, :].rearrange("p (n o) -> p n o", o=1).to_broadcast([P, n, E])
    e.tensor_reduce(r.mx[:, :], lg, AX.X, ALU.max).then_inc(c.sem, 1)
    e.wait_ge(c.sem, c.next(i))
    e.tensor_tensor(r.ex[:], lg, big(r.mx), ALU.subtract).then_inc(r.lg_r.sem, 1)
    e.wait_ge(probs.sem, probs.at(i))
    e.tensor_reduce(r.mx[:, :], r.ex[:], AX.X, ALU.add).then_inc(c.sem, 1)
    e.wait_ge(c.sem, c.next(i))
    e.reciprocal(r.mx[:, :], r.mx[:, :]).then_inc(c.sem, 1)
    e.wait_ge(c.sem, c.next(i))
    e.tensor_tensor(r.ex[:], r.ex[:], big(r.mx), ALU.mult).then_inc(c.sem, 1)
    e.wait_ge(c.sem, c.next(i))
    e.memset(r.held[:, 0:1], 0.0)
    for j in range(n):
        ins = e.max(r.top[:, j, :], r.ex[:, j, :])
    ins.then_inc(c.sem, 1)
    e.wait_ge(c.sem, c.next(i))
    e.memset(r.held[:, 1:2], 0.0)
    for j in range(n):
        ins = e.max_index(r.idx[:, j, :], r.top[:, j, :], r.ex[:, j, :])
    ins.then_inc(c.sem, 1)
    e.wait_ge(c.sem, c.next(i))
    e.tensor_copy(r.idf[:], r.idx[:]).then_inc(c.sem, 1)
    e.wait_ge(c.sem, c.next(i))
    e.tensor_tensor(r.mx[:, :], r.top[:, :, 0], r.top[:, :, 1], ALU.add).then_inc(c.sem, 1)
    e.wait_ge(c.sem, c.next(i))
    e.tensor_scalar(r.mx[:, :], r.mx[:, :], plus, floor, ALU.add, ALU.max).then_inc(c.sem, 1)
    e.wait_ge(c.sem, c.next(i))
    e.reciprocal(r.mx[:, :], r.mx[:, :]).then_inc(c.sem, 1)
    e.wait_ge(c.sem, c.next(i))
    e.tensor_tensor(r.top[:, :, 0:2], r.top[:, :, 0:2],
                           r.mx[:, :].rearrange("p (n o) -> p n o", o=1).to_broadcast([P, n, 2]), ALU.mult).then_inc(c.sem, 1)
    e.wait_ge(c.sem, c.next(i))
    iota = r.net.const("iota14")[:, 0:E]
    for j in range(n):
        e.tensor_scalar(r.cw[:, j, :], iota, r.idf[:, j, 0:1], r.top[:, j, 0:1], ALU.is_equal, ALU.mult)
        ins = e.tensor_scalar(r.one[:, j, :], iota, r.idf[:, j, 1:2], r.top[:, j, 1:2], ALU.is_equal, ALU.mult)
    ins.then_inc(c.sem, 1)
    e.wait_ge(c.sem, c.next(i))
    return e.tensor_tensor(r.cw[:], r.cw[:], r.one[:], ALU.add)


def router_buffers(b, n, E):
    b.held = b.sb("held", [P, 2])
    b.mx = b.sb("rowmax", [P, n])
    b.ex = b.sb("probs", [P, n, E])
    b.top = b.sb("top", [P, n, 8])
    b.idx = b.sb("topindex", [P, n, 8], U32)
    b.idf = b.sb("topindexf", [P, n, 8])
    b.cw = b.sb("expertweights", [P, n, E])
    b.one = b.sb("second", [P, n, E])


class TokenMoE(Block):

    E, halves = 14, 2

    def plan(self):
        E = self.E
        router_buffers(self, 4, E)
        self.h = self.sb("hidden", [P, 4, 512])
        self.sg = self.sb("silu", [P, 2, 512])
        self.acc = self.sb("acc", [P, 4, D])
        self.cwT = self.sb("cwT", [P, 512])
        self.lg_ps = self.sig("logits_in_psum")
        self.lg_r = self.sig("logits_ready")
        self.ex_r = self.sig("probs_ready")
        self.cw_r = self.sig("expertweights_ready")
        if self.has_start:
            self.cwT_ps = self.sig("expertweights_in_psum")
            self.cwT_r = self.sig("expertweights_transposed")
            self.bias_ps = self.sig("expertbias_in_psum")
        self.hid_ps = self.sig("hidden_in_psum", 2 * E)
        if self.gated:
            self.silu_r = self.sig("silu_ready", 2 * E)
        self.hid_r = self.sig("hidden_ready", 2 * E)
        self.e_ps = self.sig("expert_in_psum", E)
        self.acc_r = self.sig("expert_added", E)

    def router_tensor(self, e, i):
        PB = self.net.PB
        for j in range(4):
            ins = e.matmul(PB[7][:, j * self.E:(j + 1) * self.E], self.xnT[:, j * P:(j + 1) * P], self.w["gate"], start=True, stop=True)
        ins.then_inc(self.lg_ps.sem, 1)

    def combine(self, e, i, x):
        for x in range(self.E):
            e.wait_ge(self.e_ps.sem, self.e_ps.at(i, x + 1))
            if x:
                e.wait_ge(self.acc_r.sem, self.acc_r.at(i, x))
            for j in range(4):
                y = self.net.PB[4 + x % 2][:, j * P:(j + 1) * P]
                if x == 0 and not self.has_start:
                    ins = e.tensor_scalar(self.acc[:, j, :], y, self.cw[:, j, x:x + 1], None, ALU.mult)
                else:
                    ins = e.scalar_tensor_tensor(out=self.acc[:, j, :], in0=y, scalar=self.cw[:, j, x:x + 1], in1=self.acc[:, j, :],
                                                 op0=ALU.mult, op1=ALU.add)
            ins.then_inc(self.acc_r.sem, 1)
            if self.gated and x + 1 < self.E:
                self.gate_vector(e, i, x + 1)
        e.wait_ge(self.acc_r.sem, self.acc_r.at(i))

    def down(self, e, i, x, w):
        e.wait_ge(self.hid_r.sem, self.hid_r.at(i, 2 * x + 2))
        if x >= 2:
            e.wait_ge(self.acc_r.sem, self.acc_r.at(i, x - 1))
        for j in range(4):
            for k in range(2):
                a = (2 * x + k) * P
                ins = e.matmul(self.net.PB[4 + x % 2][:, j * P:(j + 1) * P], self.h[:, (2 * x + k) % 4, j * P:(j + 1) * P],
                               w[:, a:a + P], start=(k == 0), stop=(k == 1))
        ins.then_inc(self.e_ps.sem, 1)

    def gpsimd(self, e):
        pass

    def sync(self, e):
        pass


class L2Ffn(TokenMoE):

    name, E, gated, has_start = "L2_ffn", 14, False, True
    vsteps = 15

    def vector(self, e):
        self.ln_vector(e)
        PB, c = self.net.PB, self.chain
        with e.Fori(0, self.iters) as i:
            c.start()
            self.norm(e, i)
            e.wait_ge(self.lg_ps.sem, self.lg_ps.at(i))
            router(c, i, e, self, PB[7][:, 0:4 * self.E].rearrange("p (n e) -> p n e", n=4), 4, self.E,
                   self.ex_r, 1e-10, 0.0).then_inc(self.cw_r.sem, 1)
            e.wait_ge(self.bias_ps.sem, self.bias_ps.at(i))
            e.tensor_tensor(self.acc[:], PB[6][:, :].rearrange("p (j d) -> p j d", j=4), self.xn[:], ALU.add).then_inc(c.sem, 1)
            e.wait_ge(c.sem, c.next(i))
            self.combine(e, i, 0)
            e.tensor_scalar(self.acc[:], self.acc[:], -100.0, 100.0, ALU.max, ALU.min).then_inc(c.sem, 1)
            e.wait_ge(c.sem, c.next(i))
            self.add_residual(e, i, self.acc[:], self.acc_r)
        c.done()

    def scalar(self, e):
        self.ln_scalar(e)
        PB = self.net.PB
        with e.Fori(0, self.iters) as i:
            self.copy_xnT(e, i, PB[6])
            e.wait_ge(self.lg_r.sem, self.lg_r.at(i))
            e.activation(self.ex[:], self.ex[:], ACT.Exp).then_inc(self.ex_r.sem, 1)
            e.wait_ge(self.cwT_ps.sem, self.cwT_ps.at(i))
            e.copy(self.cwT[0:self.E, :], PB[7][0:self.E, :]).then_inc(self.cwT_r.sem, 1)
            for n in range(2 * self.E):
                e.wait_ge(self.hid_ps.sem, self.hid_ps.at(i, n + 1))
                if n >= 4:
                    e.wait_ge(self.e_ps.sem, self.e_ps.at(i, n // 2 - 1))
                e.activation(self.h[:, n % 4, :], PB[n % 4][:, :], ACT.Gelu, bias=self.w["b1"][:, n:n + 1]).then_inc(self.hid_r.sem, 1)

    def tensor(self, e):
        PB, w, E = self.net.PB, self.w, self.E

        def up(x):
            for n in (2 * x, 2 * x + 1):
                if n >= 4:
                    e.wait_ge(self.hid_r.sem, self.hid_r.at(i, n - 3))
                e.matmul(PB[n % 4][:, :], w["w1"][:, n * P:(n + 1) * P], self.xnT[:, :], start=True, stop=True)\
                    .then_inc(self.hid_ps.sem, 1)

        with e.Fori(0, self.iters) as i:
            self.transpose_xn(e, i, PB[6])
            e.wait_ge(self.xnT_r.sem, self.xnT_r.at(i))
            self.router_tensor(e, i)
            up(0)
            e.wait_ge(self.cw_r.sem, self.cw_r.at(i))
            for j in range(4):
                ins = e.matmul(PB[7][0:E, j * P:(j + 1) * P], self.cw[:, j, :], self.net.const("ident"), start=True, stop=True)
            ins.then_inc(self.cwT_ps.sem, 1)
            up(1)
            e.wait_ge(self.cwT_r.sem, self.cwT_r.at(i))
            for j in range(4):
                ins = e.matmul(PB[6][:, j * P:(j + 1) * P], self.cwT[0:E, j * P:(j + 1) * P], w["b2"][0:E, :], start=True, stop=True)
            ins.then_inc(self.bias_ps.sem, 1)
            for x in range(E):
                if 1 < x + 1 < E:
                    up(x + 1)
                self.down(e, i, x, w["w2"])


class L3Ffn(TokenMoE):

    name, E, gated, has_start = "L3_ffn", 8, True, False
    vsteps = 13

    def gate_vector(self, e, i, x):
        for n in (2 * x, 2 * x + 1):
            e.wait_ge(self.silu_r.sem, self.silu_r.at(i, n + 1))
            if n >= 4:
                e.wait_ge(self.e_ps.sem, self.e_ps.at(i, n // 2 - 1))
            e.tensor_tensor(self.h[:, n % 4, :], self.net.PB[2 * (n % 2) + 1][:, :], self.sg[:, n % 2, :], ALU.mult)\
                .then_inc(self.hid_r.sem, 1)

    def vector(self, e):
        self.ln_vector(e)
        PB, c = self.net.PB, self.chain
        with e.Fori(0, self.iters) as i:
            c.start()
            self.norm(e, i)
            e.wait_ge(self.lg_ps.sem, self.lg_ps.at(i))
            router(c, i, e, self, PB[7][:, 0:4 * self.E].rearrange("p (n e) -> p n e", n=4), 4, self.E,
                   self.ex_r, 1e-30, 0.0).then_inc(self.cw_r.sem, 1)
            e.wait_ge(self.cw_r.sem, self.cw_r.at(i))
            self.gate_vector(e, i, 0)
            self.combine(e, i, 0)
            self.add_residual(e, i, self.acc[:], self.acc_r)
        c.done()

    def scalar(self, e):
        self.ln_scalar(e)
        PB = self.net.PB
        with e.Fori(0, self.iters) as i:
            self.copy_xnT(e, i, PB[6])
            e.wait_ge(self.lg_r.sem, self.lg_r.at(i))
            e.activation(self.ex[:], self.ex[:], ACT.Exp).then_inc(self.ex_r.sem, 1)
            for n in range(2 * self.E):
                e.wait_ge(self.hid_ps.sem, self.hid_ps.at(i, n + 1))
                if n >= 2:
                    e.wait_ge(self.hid_r.sem, self.hid_r.at(i, n - 1))
                e.activation(self.sg[:, n % 2, :], PB[2 * (n % 2)][:, :], ACT.Silu).then_inc(self.silu_r.sem, 1)

    def tensor(self, e):
        PB, w, E = self.net.PB, self.w, self.E

        def up(x):
            for n in (2 * x, 2 * x + 1):
                if n >= 2:
                    e.wait_ge(self.hid_r.sem, self.hid_r.at(i, n - 1))
                e.matmul(PB[2 * (n % 2)][:, :], w["wg"][:, n * P:(n + 1) * P], self.xnT[:, :], start=True, stop=True)
                e.matmul(PB[2 * (n % 2) + 1][:, :], w["wu"][:, n * P:(n + 1) * P], self.xnT[:, :], start=True, stop=True)\
                    .then_inc(self.hid_ps.sem, 1)

        with e.Fori(0, self.iters) as i:
            self.transpose_xn(e, i, PB[6])
            e.wait_ge(self.xnT_r.sem, self.xnT_r.at(i))
            self.router_tensor(e, i)
            up(0)
            for x in range(E):
                if x + 1 < E:
                    up(x + 1)
                self.down(e, i, x, w["wd"])


class L1Ffn(Block):

    name = "L1_ffn"
    E, C = 8, 64
    vsteps = 1
    setup_steps = 12

    def plan(self):
        router_buffers(self, 1, self.E)
        self.pooledT = self.sb("pooledT", [P, P])
        self.cwT = self.sb("cwT", [P, P])
        self.cwx = self.sb("cwx", [P, 4, P])
        self.cwe = self.sb("cwe", [P, 16, S])
        self.h = self.sb("h", [P, 4, 512])
        self.h2 = self.sb("h2", [P, 4, 512])
        self.pxn_r = self.sig("pool_xn_ready")
        self.pool_ps = self.sig("pooled_in_psum")
        self.pool_r = self.sig("pooled_ready")
        self.lg_ps = self.sig("logits_in_psum", 1, 1)
        self.lg_r = self.sig("logits_ready", 1, 1)
        self.ex_r = self.sig("probs_ready", 1, 1)
        self.cw_r = self.sig("expertweights_ready", 1, 1)
        self.cwT_ps = self.sig("expertweights_in_psum", 1, 1)
        self.cwT_r = self.sig("expertweights_transposed", 1, 1)
        self.cwx_ps = self.sig("expertbias_in_psum", 1, 1)
        self.cwx_r = self.sig("expert_added", 1, 1)
        self.cwe_r = self.sig("activated_ready")
        self.hid_ps = self.sig("hidden_in_psum")
        self.hid_r = self.sig("hidden_ready")
        self.h2_r = self.sig("mlp_hidden_ready")
        self.y_ps = self.sig("y_in_psum")

    def vector(self, e):
        self.ln_vector(e)
        n, PB = self.net, self.net.PB
        with e.Fori(0, self.iters) as i:
            for j in range(4):
                t = i * 4 + j
                ins = e.tensor_scalar(self.xn[:, j, :], n.X[:, bass.ds(t, 1), :], n.mean[:, bass.ds(t, 1)], n.rstd[:, bass.ds(t, 1)],
                                      ALU.subtract, ALU.mult)
            ins.then_inc(self.pxn_r.sem, 1)
            e.wait_ge(self.pool_ps.sem, self.pool_ps.at(i))
            e.tensor_copy(self.pooledT[:, bass.ds(i * 16, 16)], PB[6][:, 0:16]).then_inc(self.pool_r.sem, 1)
        e.wait_ge(self.lg_ps.sem, self.lg_ps.at(0))
        router(self.setup_chain, 0, e, self, PB[7][:, 0:8].rearrange("p (n e) -> p n e", n=1), 1, self.E,
               self.ex_r, 0.0, 1e-8).then_inc(self.cw_r.sem, 1)
        e.wait_ge(self.cwx_ps.sem, self.cwx_ps.at(0))
        e.tensor_copy(self.cwx[:], PB[6][:, :].rearrange("p (j b) -> p j b", j=4)).then_inc(self.cwx_r.sem, 1)
        e.wait_ge(self.cwx_r.sem, self.cwx_r.at(0))
        self.setup_chain.done()
        with e.Fori(0, self.iters) as i:
            self.chain.start()
            self.norm(e, i)
            e.tensor_copy(self.cwe[0:8], self.cwT[0:8, bass.ds(i * 16, 16)].rearrange("p (b o) -> p b o", o=1).to_broadcast([8, 16, S]))\
                .then_inc(self.cwe_r.sem, 1)
            e.wait_ge(self.hid_r.sem, self.hid_r.at(i))
            for j in range(4):
                ins = e.tensor_tensor(self.h2[:, j, :].rearrange("p (b s) -> p b s", s=S), self.h[:, j, :].rearrange("p (b s) -> p b s", s=S),
                                      self.cwx[:, j, bass.ds(i * 16, 16)].rearrange("p (b o) -> p b o", o=1).to_broadcast([P, 16, S]), ALU.mult)
            ins.then_inc(self.h2_r.sem, 1)
            self.add_residual(e, i, PB[5][:, :].rearrange("p (j d) -> p j d", j=4), self.y_ps)
        self.chain.done()

    def scalar(self, e):
        self.ln_scalar(e)
        PB = self.net.PB
        e.wait_ge(self.lg_r.sem, self.lg_r.at(0))
        e.activation(self.ex[:], self.ex[:], ACT.Exp).then_inc(self.ex_r.sem, 1)
        e.wait_ge(self.cwT_ps.sem, self.cwT_ps.at(0))
        e.copy(self.cwT[0:8, :], PB[7][0:8, 0:P]).then_inc(self.cwT_r.sem, 1)
        with e.Fori(0, self.iters) as i:
            self.copy_xnT(e, i, PB[0])
            e.wait_ge(self.hid_ps.sem, self.hid_ps.at(i))
            for j in range(4):
                ins = e.activation(self.h[:, j, :], PB[1 + j][:, :], ACT.Gelu, bias=self.w["bd"][:, j:j + 1])
            ins.then_inc(self.hid_r.sem, 1)

    def tensor(self, e):
        PB, w, n = self.net.PB, self.w, self.net
        with e.Fori(0, self.iters) as i:
            e.wait_ge(self.pxn_r.sem, self.pxn_r.at(i))
            for j in range(4):
                ins = e.matmul(PB[6][:, 4 * j:4 * j + 4], self.xn[:, j, :], n.const("seqmean"), start=True, stop=True)
            ins.then_inc(self.pool_ps.sem, 1)
        e.wait_ge(self.pool_r.sem, self.pool_r.at(self.iters - 1))
        e.matmul(PB[7][:, 0:8], self.pooledT[:, :], w["gate"], start=True, stop=True).then_inc(self.lg_ps.sem, 1)
        e.wait_ge(self.cw_r.sem, self.cw_r.at(0))
        e.matmul(PB[7][0:8, 0:P], self.cw[:, 0, :], n.const("ident"), start=True, stop=True).then_inc(self.cwT_ps.sem, 1)
        e.wait_ge(self.cwT_r.sem, self.cwT_r.at(0))
        for j in range(4):
            ins = e.matmul(PB[6][:, j * P:(j + 1) * P], n.const("exp2rows")[0:8, j * P:(j + 1) * P], self.cwT[0:8, :], start=True, stop=True)
        ins.then_inc(self.cwx_ps.sem, 1)
        with e.Fori(0, self.iters) as i:
            self.transpose_xn(e, i, PB[0])
            e.wait_ge(self.xnT_r.sem, self.xnT_r.at(i))
            for j in range(4):
                ins = e.matmul(PB[1 + j][:, :], w["down"][:, j * P:(j + 1) * P], self.xnT[:, :], start=True, stop=True)
            ins.then_inc(self.hid_ps.sem, 1)
            e.wait_ge(self.h2_r.sem, self.h2_r.at(i))
            e.wait_ge(self.cwe_r.sem, self.cwe_r.at(i))
            for j in range(4):
                o = PB[5][:, j * P:(j + 1) * P]
                e.matmul(o, self.cwe[0:8, 4 * j:4 * j + 4, :].rearrange("p b s -> p (b s)"), w["bu"][0:8, :], start=True, stop=False)
                for k in range(4):
                    ins = e.matmul(o, self.h2[:, k, j * P:(j + 1) * P], w["up"][:, k * P:(k + 1) * P], start=False, stop=(k == 3))
            ins.then_inc(self.y_ps.sem, 1)

    def gpsimd(self, e):
        pass

    def sync(self, e):
        pass

QSCALE = 1.0 / float(np.sqrt(8.0))


class SmallAttn(Block):

    vsteps = 6
    cross = False

    def plan(self):
        if self.cross:
            self.ct = self.sb("ctx", [P, 4, D])
            self.ctT = self.sb("ctxT", [P, 512])
            self.ctx_l = self.sig("context_loaded", 64)
            self.ctT_ps = self.sig("ctxT_in_psum")
            self.ctT_r = self.sig("ctxT_ready")
            self.bqs = self.sb("bqs", [P, 1])
            self.bqs_r = self.sig("scaled_bias_ready", 1, 1)
        self.qT = self.sb("qT", [P, 16, S])
        self.kT = self.sb("kT", [P, 512])
        self.v = self.sb("v", [P, 4, D])
        self.qx = self.sb("qx", [P, 16, 4, S])
        self.e = self.sb("e", [P, 64, S])
        self.pt = self.sb("pt", [P, C, 4, P])
        self.rm = self.sb("rm", [P, 4, 4, C, 32])
        self.o = self.sb("o", [P, 4, 4, C * 32])
        self.oT = self.sb("oT", [P, 512])
        self.mx = self.sb("mx", [P, 64])
        self.rs = self.sb("rs", [P, 64])
        self.qkv_ps = self.sig("hidden_in_psum")
        self.q_r = self.sig("hidden_ready")
        self.qx_r = self.sig("spread_ready")
        self.s_ps = self.sig("scores_in_psum")
        self.d_r = self.sig("exponents_ready")
        self.e_r = self.sig("exps_ready")
        self.pt_ps = self.sig("probsT_in_psum")
        self.pta_r = self.sig("probsT_low_ready")
        self.ptv_r = self.sig("probsT_high_ready")
        self.o_ps = self.sig("heads_in_psum")
        self.o_r = self.sig("heads_ready")
        self.oT_ps = self.sig("headsT_in_psum")
        self.oT_r = self.sig("headsT_ready")
        self.y_ps = self.sig("y_in_psum")

    def vector(self, e):
        self.ln_vector(e)
        n, c = self.net, self.chain
        PS = n.PS
        with e.Fori(0, self.iters) as i:
            c.start()
            self.norm(e, i)
            e.wait_ge(self.qkv_ps.sem, self.qkv_ps.at(i))
            e.tensor_copy(self.v[:], PS[:, 6, :].rearrange("p (t d) -> p t d", t=4)).then_inc(c.sem, 1)
            e.wait_ge(c.sem, c.next(i))
            e.wait_ge(self.q_r.sem, self.q_r.at(i))
            e.tensor_tensor(self.qx[:], self.qT[:].rearrange("p b (o s) -> p b o s", o=1).to_broadcast([P, 16, 4, S]),
                            n.const("head4").rearrange("p (a h b) -> p a h b", a=1, b=1).to_broadcast([P, 16, 4, S]), ALU.mult)\
                .then_inc(self.qx_r.sem, 1)
            e.wait_ge(self.s_ps.sem, self.s_ps.at(i))
            sc = PS[:, 0:4, :].rearrange("p c (b k) -> p (c b) k", k=S)
            if self.cross:
                e.tensor_tensor(self.e[:], sc, n.const("causal").rearrange("p (o k) -> p o k", o=1).to_broadcast([P, 64, S]), ALU.add).then_inc(c.sem, 1)
                e.wait_ge(c.sem, c.next(i))
                sc = self.e[:]
            e.tensor_reduce(self.mx[:, :], sc, AX.X, ALU.max).then_inc(c.sem, 1)
            e.wait_ge(c.sem, c.next(i))
            e.tensor_tensor(self.e[:], sc, self.mx[:, :].rearrange("p (n o) -> p n o", o=1).to_broadcast([P, 64, S]), ALU.subtract)\
                .then_inc(self.d_r.sem, 1)
            e.wait_ge(self.e_r.sem, self.e_r.at(i))
            e.tensor_reduce(self.rs[:, :], self.e[:], AX.X, ALU.add).then_inc(c.sem, 1)
            e.wait_ge(c.sem, c.next(i))
            e.reciprocal(self.rs[:, :], self.rs[:, :]).then_inc(c.sem, 1)
            e.wait_ge(c.sem, c.next(i))
            r4 = self.rs[:, :].rearrange("p (c t r) -> p r t c", c=C, r=4)
            for r in range(4):
                ins = e.tensor_tensor(self.rm[:, r], r4[:, r].rearrange("p t (c o) -> p t c o", o=1).to_broadcast([P, 4, C, 32]),
                                      n.const("odiag").rearrange("p (a b j) -> p a b j", a=1, b=1).to_broadcast([P, 4, C, 32]), ALU.mult)
            ins.then_inc(c.sem, 1)
            e.wait_ge(c.sem, c.next(i))
            e.wait_ge(self.pt_ps.sem, self.pt_ps.at(i))
            for q in (2, 3):
                ins = e.tensor_copy(self.pt[:, q].rearrange("p t h -> p (t h)"), PS[:, 4 + q, :])
            ins.then_inc(self.ptv_r.sem, 1)
            e.wait_ge(self.o_ps.sem, self.o_ps.at(i))
            e.tensor_tensor(self.o[:].rearrange("p r t c -> p r (t c)"), PS[:, 0:4, :], self.rm[:].rearrange("p r t c j -> p r (t c j)"), ALU.mult)\
                .then_inc(self.o_r.sem, 1)
            self.add_residual(e, i, PS[:, 5, :].rearrange("p (j d) -> p j d", j=4), self.y_ps)
        c.done()

    def scalar(self, e):
        self.ln_scalar(e)
        PB, w = self.net.PB, self.w
        if self.cross:
            e.mul(self.bqs[:, :], w["bq"], QSCALE).then_inc(self.bqs_r.sem, 1)
            e.wait_ge(self.bqs_r.sem, self.bqs_r.at(0))
        with e.Fori(0, self.iters) as i:
            self.copy_xnT(e, i, PB[0])
            if self.cross:
                e.wait_ge(self.ctT_ps.sem, self.ctT_ps.at(i))
                e.copy(self.ctT[:, :], PB[1]).then_inc(self.ctT_r.sem, 1)
            e.wait_ge(self.qkv_ps.sem, self.qkv_ps.at(i))
            if self.cross:
                e.activation(self.qT[:].rearrange("p b s -> p (b s)"), PB[4], ACT.Identity, bias=self.bqs[:, :], scale=QSCALE)
                e.activation(self.kT[:, :], PB[5], ACT.Identity, bias=w["bk"]).then_inc(self.q_r.sem, 1)
            else:
                e.activation(self.qT[:].rearrange("p b s -> p (b s)"), PB[4], ACT.Copy, scale=QSCALE)
                e.copy(self.kT[:, :], PB[5]).then_inc(self.q_r.sem, 1)
            e.wait_ge(self.d_r.sem, self.d_r.at(i))
            e.activation(self.e[:], self.e[:], ACT.Exp).then_inc(self.e_r.sem, 1)
            e.wait_ge(self.pt_ps.sem, self.pt_ps.at(i))
            for q in (0, 1):
                ins = e.copy(self.pt[:, q].rearrange("p t h -> p (t h)"), PB[4 + q])
            ins.then_inc(self.pta_r.sem, 1)
            e.wait_ge(self.oT_ps.sem, self.oT_ps.at(i))
            if self.cross:
                e.activation(self.oT[:, :], PB[4], ACT.Identity, bias=w["bv"]).then_inc(self.oT_r.sem, 1)
            else:
                e.copy(self.oT[:, :], PB[4]).then_inc(self.oT_r.sem, 1)

    def tensor(self, e):
        PB, w, n = self.net.PB, self.w, self.net
        with e.Fori(0, self.iters) as i:
            self.transpose_xn(e, i, PB[0])
            if self.cross:
                e.wait_ge(self.ctx_l.sem, self.ctx_l.at(i))
                for j in range(4):
                    ins = e.transpose(PB[1][:, j * P:(j + 1) * P], self.ct[:, j, :], n.const("ident"))
                ins.then_inc(self.ctT_ps.sem, 1)
            e.wait_ge(self.xnT_r.sem, self.xnT_r.at(i))
            e.matmul(PB[4], w["wq"], self.xnT[:, :], start=True, stop=True)
            kv = self.xnT
            if self.cross:
                e.wait_ge(self.ctT_r.sem, self.ctT_r.at(i))
                kv = self.ctT
            e.matmul(PB[5], w["wk"], kv[:, :], start=True, stop=True)
            for j in range(4):
                ins = e.matmul(PB[6][:, j * P:(j + 1) * P], kv[:, j * P:(j + 1) * P], w["wv"], start=True, stop=True)
            ins.then_inc(self.qkv_ps.sem, 1)
            e.wait_ge(self.qx_r.sem, self.qx_r.at(i))
            for b in range(16):
                for c in range(C):
                    r = slice(32 * c, 32 * c + 32)
                    ins = e.matmul(PB[c][:, b * S:(b + 1) * S], self.qx[r, b].rearrange("p h s -> p (h s)"),
                                   self.kT[r, b * S:(b + 1) * S], start=True, stop=True)
            ins.then_inc(self.s_ps.sem, 1)
            e.wait_ge(self.e_r.sem, self.e_r.at(i))
            for c in range(C):
                for t in range(4):
                    k = c * 16 + t * 4
                    ins = e.transpose(PB[4 + c][:, t * P:(t + 1) * P], self.e[:, k:k + 4, :].rearrange("p b k -> p (b k)"), n.const("ident"))
            ins.then_inc(self.pt_ps.sem, 1)
            e.wait_ge(self.pta_r.sem, self.pta_r.at(i))
            e.wait_ge(self.ptv_r.sem, self.ptv_r.at(i))
            for t in range(4):
                for c in range(C):
                    for r in range(4):
                        q = slice(32 * r, 32 * r + 32)
                        ins = e.matmul(PB[r][:, (t * C + c) * 32:(t * C + c + 1) * 32], self.pt[q, c, t, :], self.v[q, t, 32 * c:32 * c + 32],
                                       start=True, stop=True)
            ins.then_inc(self.o_ps.sem, 1)
            e.wait_ge(self.o_r.sem, self.o_r.at(i))
            for t in range(4):
                for r in range(4):
                    b = 4 * t + r
                    ins = e.matmul(PB[4][:, b * S:(b + 1) * S], self.o[:, r, t, :], n.const("samequery"), start=True, stop=True)
            ins.then_inc(self.oT_ps.sem, 1)
            e.wait_ge(self.oT_r.sem, self.oT_r.at(i))
            self.project(e, PB[5], [self.oT[:, :]], [w["wo"]], w["bo"] if self.cross else None).then_inc(self.y_ps.sem, 1)

    def gpsimd(self, e):
        pass

    def sync(self, e):
        if self.cross:
            with e.Fori(0, self.iters) as i:
                e.wait_ge(self.res.sem, self.res.at(i, 0))
                for r in range(4):
                    src = self.net.ctx_dram[bass.ds(i * 16, 16), 0:S, :].rearrange("(t r) k d -> r k t d", r=4)[r]
                    e.dma_start(self.ct[32 * r:32 * r + 32], src).then_inc(self.ctx_l.sem, 16)


class L1Attn(SmallAttn):

    name = "L1_attn"


class L1Xattn(SmallAttn):

    name, cross, vsteps = "L1_xattn", True, 7


class L3Attn(Block):

    name = "L3_attn"
    vsteps = 7

    def plan(self):
        self.t = self.sb("t", [P, 4, 512])
        self.kr = self.sb("kr", [P, 512])
        self.qr = self.sb("qr", [P, 512])
        self.qm = self.sb("qm", [P, 2, 512])
        self.v = self.sb("v", [P, 4, 256])
        self.sg = self.sb("sg", [P, 2, 512])
        self.st = self.sb("st", [P, 4, 8, P])
        self.sq = self.sb("sq", [P, 2, 512])
        self.rt = self.sb("rt", [P, 2, 512])
        self.o = self.sb("o", [P, 2, 512])
        self.qk_ps = self.sig("hidden_in_psum")
        self.vg_ps = self.sig("value_gate_in_psum")
        self.v_r = self.sig("hidden_ready")
        self.sg_r = self.sig("silu_ready")
        self.q_r = self.sig("spread_ready")
        self.s_ps = self.sig("scores_in_psum", 4)
        self.st_r = self.sig("decayed_ready", 4)
        self.o_ps = self.sig("heads_in_psum")
        self.sq_r = self.sig("squares_summed")
        self.ms_ps = self.sig("meansquare_in_psum")
        self.rt_r = self.sig("root_ready")
        self.o_r = self.sig("heads_ready")
        self.y_ps = self.sig("y_in_psum")

    def vector(self, e):
        self.ln_vector(e)
        n, c, PS = self.net, self.chain, self.net.PS
        seqs = lambda b: b.rearrange("p (b s) -> p b s", s=S)
        table = lambda k: n.const(k).rearrange("p (o s) -> p o s", o=1).to_broadcast([P, 16, S])
        with e.Fori(0, self.iters) as i:
            c.start()
            self.norm(e, i)
            e.wait_ge(self.qk_ps.sem, self.qk_ps.at(i))
            for j, k in enumerate(("ropecos", "ropesin", "ropecos", "ropesin")):
                ins = e.tensor_tensor(seqs(self.t[:, j, :]), seqs(PS[:, 1 + j, :]), table(k), ALU.mult)
            ins.then_inc(c.sem, 1)
            e.wait_ge(c.sem, c.next(i))
            e.tensor_tensor(self.qr[:, :], self.t[:, 0, :], self.t[:, 1, :], ALU.add).then_inc(c.sem, 1)
            e.wait_ge(c.sem, c.next(i))
            e.tensor_tensor(self.kr[:, :], self.t[:, 2, :], self.t[:, 3, :], ALU.add).then_inc(c.sem, 1)
            e.wait_ge(c.sem, c.next(i))
            for h in range(2):
                ins = e.tensor_scalar(self.qm[:, h, :], self.qr[:, :], n.const("head2")[:, h:h + 1], None, ALU.mult)
            ins.then_inc(self.q_r.sem, 1)
            for j in range(4):
                e.wait_ge(self.s_ps.sem, self.s_ps.at(i, j + 1))
                b = 4 * (j % 2)
                e.tensor_tensor(self.st[:, j].rearrange("p (c h) q -> p c (h q)", h=2), PS[:, b:b + 4, 0:256],
                                n.const("decay").rearrange("p (c x) -> p c x", c=4), ALU.mult).then_inc(self.st_r.sem, 1)
            e.wait_ge(self.rt_r.sem, self.rt_r.at(i))
            e.reciprocal(self.rt[:], self.rt[:]).then_inc(c.sem, 1)
            e.wait_ge(c.sem, c.next(i))
            for j in range(2):
                ins = e.scalar_tensor_tensor(out=self.o[:, j, :], in0=PS[:, 4 + j, :], scalar=self.w["gn"], in1=self.rt[:, j, :],
                                             op0=ALU.mult, op1=ALU.mult)
                ins.then_inc(c.sem, 1)
                e.wait_ge(c.sem, c.next(i))
            e.wait_ge(self.sg_r.sem, self.sg_r.at(i))
            e.tensor_tensor(self.o[:], self.o[:], self.sg[:], ALU.mult).then_inc(self.o_r.sem, 1)
            self.add_residual(e, i, PS[:, 0, :].rearrange("p (j d) -> p j d", j=4), self.y_ps)
        c.done()

    def scalar(self, e):
        self.ln_scalar(e)
        PB, PS = self.net.PB, self.net.PS
        with e.Fori(0, self.iters) as i:
            self.copy_xnT(e, i, PB[0])
            e.wait_ge(self.vg_ps.sem, self.vg_ps.at(i))
            for j in range(2):
                ins = e.copy(self.v[:, 2 * j:2 * j + 2].rearrange("p a b -> p (a b)"), PB[5 + j])
            ins.then_inc(self.v_r.sem, 1)
            e.activation(self.sg[:, 0, :], PB[7], ACT.Silu)
            e.activation(self.sg[:, 1, :], PB[0], ACT.Silu).then_inc(self.sg_r.sem, 1)
            e.wait_ge(self.o_ps.sem, self.o_ps.at(i))
            e.activation(self.sq[:], PS[:, 4:6, :], ACT.Square).then_inc(self.sq_r.sem, 1)
            e.wait_ge(self.ms_ps.sem, self.ms_ps.at(i))
            e.activation(self.rt[:], PS[:, 6:8, :], ACT.Sqrt, bias=self.net.const("eps5")).then_inc(self.rt_r.sem, 1)

    def tensor(self, e):
        PB, w, n = self.net.PB, self.w, self.net
        with e.Fori(0, self.iters) as i:
            self.transpose_xn(e, i, PB[0])
            e.wait_ge(self.xnT_r.sem, self.xnT_r.at(i))
            for j, k in enumerate(("wq", "wqs", "wk", "wks")):
                ins = e.matmul(PB[1 + j], w[k], self.xnT[:, :], start=True, stop=True)
            ins.then_inc(self.qk_ps.sem, 1)
            for j in range(4):
                e.matmul(PB[5 + j // 2][:, (j % 2) * 256:(j % 2) * 256 + 256], self.xnT[:, j * P:(j + 1) * P], w["wv"], start=True, stop=True)
            e.matmul(PB[7], w["wg"][:, 0:P], self.xnT[:, :], start=True, stop=True)
            e.matmul(PB[0], w["wg"][:, P:2 * P], self.xnT[:, :], start=True, stop=True).then_inc(self.vg_ps.sem, 1)
            e.wait_ge(self.q_r.sem, self.q_r.at(i))
            e.wait_ge(self.sg_r.sem, self.sg_r.at(i))
            for j in range(4):
                if j >= 2:
                    e.wait_ge(self.st_r.sem, self.st_r.at(i, j - 1))
                t = slice(j * P, (j + 1) * P)
                for c in range(4):
                    r = slice(32 * c, 32 * c + 32)
                    for h in range(2):
                        ins = e.matmul(PB[4 * (j % 2) + c][:, h * P:(h + 1) * P], self.kr[r, t], self.qm[r, h, t], start=True, stop=True)
                ins.then_inc(self.s_ps.sem, 1)
            e.wait_ge(self.st_r.sem, self.st_r.at(i))
            for j in range(4):
                for h in range(8):
                    q = 32 * (h % 4)
                    ins = e.matmul(PB[4 + h // 4][q:q + 32, j * P:(j + 1) * P], self.v[:, j, 32 * h:32 * h + 32], self.st[:, j, h, :],
                                   start=True, stop=True)
            ins.then_inc(self.o_ps.sem, 1)
            e.wait_ge(self.sq_r.sem, self.sq_r.at(i))
            for j in range(2):
                ins = e.matmul(PB[6 + j], n.const("mean32"), self.sq[:, j, :], start=True, stop=True)
            ins.then_inc(self.ms_ps.sem, 1)
            e.wait_ge(self.o_r.sem, self.o_r.at(i))
            self.project(e, PB[0], [self.o[:, k, :] for k in range(2)], [w["wo"][:, k * P:(k + 1) * P] for k in range(2)])\
                .then_inc(self.y_ps.sem, 1)

    def gpsimd(self, e):
        pass

    def sync(self, e):
        pass


class CrossAttn(Block):

    iters, group = TILES, 1
    KT = T // P

    def plan_common(self):
        self.qx = self.sb("qx", [P, SEQS, 16, S])
        self.cx = [self.sb(f"cx{b}", [P, self.KT, D]) for b in range(SEQS)]
        self.cT = [self.sb(f"cT{b}", [P, T + 1]) for b in range(2)]
        self.mw = self.sb("maskwords", [P, T], U32)
        self.mb = self.sb("maskbias", [P, SEQS * T], BF16)
        self.onesb = self.sb("onesb", [P, P], BF16)
        self.e = [self.sb(f"e{k}", [P, 2, T]) for k in range(2)]
        self.pt = [self.sb(f"pt{k}", [P, self.KT, 2, P]) for k in range(2)]
        self.pl = [self.sb(f"pl{k}", [2, P]) for k in range(2)]
        self.nm = self.sb("negmax", [P, 8, 2])
        self.rs = self.sb("rowsum", [P, 8, 2])
        self.mask_l = self.sig("mask_loaded", 16)
        self.ones_r = self.sig("scaled_bias_ready", 1, 1)
        self.cx_l = [self.sig(f"context{b}_loaded", 16 * self.cx_dmas) for b in range(SEQS)]
        self.mb_r = self.sig("maskbias_ready")
        self.cT_ps = self.sig("ctxT_in_psum", 4)
        self.cT_r = self.sig("ctxT_ready", 4)
        self.s_ps = self.sig("scores_in_psum", 8)
        self.nm_r = self.sig("exponents_ready", 8)
        self.e_r = self.sig("exps_ready", 8)
        self.pt_ps = self.sig("probsT_in_psum", 8)
        self.pt_r = self.sig("probsT_low_ready", 8)
        self.o_ps = self.sig("heads_in_psum", 8)
        self.o_r = self.sig("heads_ready", 8)
        self.qx_r = self.sig("spread_ready")
        self.y_ps = self.sig("y_in_psum")

    def maskbias(self, e, i):
        e.wait_ge(self.mask_l.sem, self.mask_l.at(i))
        m = self.mw[:, :].bitcast(U8)
        (s1, s2) = self.mask_ops
        e.tensor_scalar(self.mb[:, :], m, s1, s2, ALU.add, ALU.mult).then_inc(self.mb_r.sem, 1)

    def context_T(self, e, i, b):
        if b:
            self.bank6_free(e, i, b)
        e.wait_ge(self.cx_l[b].sem, self.cx_l[b].at(i))
        for k in range(self.KT):
            e.transpose(self.net.PB[6][:, k * P:(k + 1) * P], self.cx[b][:, k, :], self.net.const("ident"))
        e.matmul(self.net.PB[6][:, T - 1:T + 1], self.last_row(b), self.net.const("ones")[0:1, 0:2], start=True, stop=True)\
            .then_inc(self.cT_ps.sem, 1)

    def copy_context_T(self, e, i, b):
        e.wait_ge(self.cT_ps.sem, self.cT_ps.at(i, b + 1))
        if b >= 2:
            self.cT_free(e, i, b)
        e.copy(self.cT[b % 2][:, :], self.net.PB[6][:, 0:T + 1]).then_inc(self.cT_r.sem, 1)

    def scores(self, e, i, u):
        b, half = u // 2, u % 2
        if u >= 2:
            e.wait_ge(self.pt_r.sem, self.pt_r.at(i, u - 1))
        for cc in range(2):
            c = 2 * half + cc
            bank = self.net.PB[2 * (u % 2) + cc][:, 0:T]
            r = self.mask_row(c)
            e.matmul(bank, self.onesb[r:r + 1, :], self.mb[r:r + 1, b * T:(b + 1) * T], start=True, stop=False)
            ins = self.score_product(e, bank, b, c)
        ins.then_inc(self.s_ps.sem, 1)

    def negmax(self, e, i, u):
        e.wait_ge(self.s_ps.sem, self.s_ps.at(i, u + 1))
        e.tensor_reduce(self.nm[:, u, :], self.net.PS[:, 2 * (u % 2):2 * (u % 2) + 2, 0:T], AX.X, ALU.max, negate=True)\
            .then_inc(self.nm_r.sem, 1)

    def exps(self, e, i, u):
        e.wait_ge(self.nm_r.sem, self.nm_r.at(i, u + 1))
        if u >= 2:
            e.wait_ge(self.pt_ps.sem, self.pt_ps.at(i, u - 1))
        for cc in range(2):
            ins = e.activation(self.e[u % 2][:, cc, :], self.net.PB[2 * (u % 2) + cc][:, 0:T], ACT.Exp, bias=self.nm[:, u, cc:cc + 1],
                               accum_out=self.rs[:, u, cc:cc + 1])
        ins.then_inc(self.e_r.sem, 1)

    def transposes(self, e, i, u):
        if u >= 2:
            e.wait_ge(self.pt_r.sem, self.pt_r.at(i, u - 1))
        for k in range(self.KT):
            for cc in range(2):
                a = (2 * k + cc) * P
                e.transpose(self.net.PB[4 + u % 2][:, a:a + P], self.e[u % 2][:, cc, k * P:(k + 1) * P], self.net.const("ident"))
        e.matmul(self.net.PB[2 * (u % 2)][0:2, 384:512], self.e[u % 2][:, :, T - 1:T].rearrange("p c o -> p (c o)"),
                 self.net.const("ident"), start=True, stop=True).then_inc(self.pt_ps.sem, 1)

    def copy_probs(self, e, i, u):
        e.wait_ge(self.pt_ps.sem, self.pt_ps.at(i, u + 1))
        if u >= 2:
            e.wait_ge(self.o_ps.sem, self.o_ps.at(i, u - 1))
        e.copy(self.pl[u % 2][:, :], self.net.PB[2 * (u % 2)][0:2, 384:512])
        e.copy(self.pt[u % 2][:].rearrange("p k c h -> p (k c h)"), self.net.PB[4 + u % 2]).then_inc(self.pt_r.sem, 1)

    def load_masks(self, e, i):
        e.dma_start(self.mw[:, :], self.mask[bass.ds(i, 1), :].to_broadcast([P, T])).then_inc(self.mask_l.sem, 16)

    def sync(self, e):
        e.wait_ge(self.res.sem, self.res.at(0, 0))
        e.wait_ge(self.ones_r.sem, self.ones_r.at(0))
        self.load_masks(e, 0)
        for b in range(SEQS):
            self.load(e, 0, b)
        with e.Fori(1, self.iters) as i:
            e.wait_ge(self.mb_r.sem, self.mb_r.at(i - 1))
            self.load_masks(e, i)
            for b in range(SEQS):
                self.slot_free(e, i - 1, b)
                self.load(e, i, b)

    def gpsimd(self, e):
        pass


class L0Xattn(CrossAttn):

    name = "L0_xattn"
    vsteps = 9
    cx_dmas = 2
    mask_ops = (0.0, MASKED)

    def plan(self):
        self.mask = self.net.masks[0]
        self.plan_common()
        self.cl = self.sb("cl", [1, SEQS, D])
        self.bqs = self.sb("bqs", [P, 1])
        self.qT = self.sb("qT", [P, SEQS, S])
        self.kT = [self.sb(f"kT{b}", [P, T]) for b in range(2)]
        self.v = [self.sb(f"v{b}", [P, self.KT, D]) for b in range(2)]
        self.vl = [self.sb(f"vl{b}", [2, D]) for b in range(2)]
        self.rm = self.sb("rm", [P, 2, 2, 32])
        self.o = self.sb("o", [P, SEQS, C, 32])
        self.oT = self.sb("oT", [P, P])
        self.q_ps = self.sig("hidden_in_psum")
        self.q_r = self.sig("hidden_ready")
        self.kT_ps = self.sig("keysT_in_psum", 4)
        self.kT_r = self.sig("keysT_ready", 4)
        self.v_ps = self.sig("values_in_psum", 4)
        self.v_r = self.sig("values_ready", 4)
        self.rm_r = self.sig("reciprocals_ready", 8)
        self.oT_ps = self.sig("headsT_in_psum")
        self.oT_r = self.sig("headsT_ready")

    def mask_row(self, c):
        return 32 * c

    def bank6_free(self, e, i, b):
        e.wait_ge(self.v_r.sem, self.v_r.at(i, b))

    def cT_free(self, e, i, b):
        e.wait_ge(self.v_ps.sem, self.v_ps.at(i, b - 1))

    def last_row(self, b):
        return self.cl[0:1, b, :]

    def slot_free(self, e, i, b):
        e.wait_ge(self.cT_ps.sem, self.cT_ps.at(i, b + 1))

    def load(self, e, i, b):
        src = self.net.ctx_dram[bass.ds(i * SEQS + b, 1)]
        e.dma_start(self.cx[b][:], src[:, 0:self.KT * P, :].rearrange("o (k p) d -> p (o k) d", p=P)).then_inc(self.cx_l[b].sem, 16)
        e.dma_start(self.cl[0:1, b, :], src[:, T - 1, :]).then_inc(self.cx_l[b].sem, 16)

    def score_product(self, e, bank, b, c):
        r = slice(32 * c, 32 * c + 32)
        return e.matmul(bank, self.qx[r, b, 0:4, :].rearrange("p h s -> p (h s)"), self.kT[b % 2][r, :], start=False, stop=True)

    def keysT(self, e, i, b):
        e.wait_ge(self.cT_r.sem, self.cT_r.at(i, b + 1))
        e.matmul(self.net.PB[6][:, 0:T], self.w["wk"], self.cT[b % 2][:, 0:T], start=True, stop=True).then_inc(self.kT_ps.sem, 1)

    def values(self, e, i, b):
        e.wait_ge(self.kT_r.sem, self.kT_r.at(i, b + 1))
        for k in range(self.KT):
            e.matmul(self.net.PB[6][:, k * P:(k + 1) * P], self.cT[b % 2][:, k * P:(k + 1) * P], self.w["wv"], start=True, stop=True)
        e.matmul(self.net.PB[6][0:2, 2 * P:3 * P], self.cT[b % 2][:, T - 1:T + 1], self.w["wv"], start=True, stop=True)\
            .then_inc(self.v_ps.sem, 1)

    def heads(self, e, i, u):
        b, half = u // 2, u % 2
        e.wait_ge(self.pt_r.sem, self.pt_r.at(i, u + 1))
        if half == 0:
            e.wait_ge(self.v_r.sem, self.v_r.at(i, b + 1))
        if u:
            e.wait_ge(self.o_r.sem, self.o_r.at(i, u))
        for cc in range(2):
            f = slice(32 * (2 * half + cc), 32 * (2 * half + cc) + 32)
            o = self.net.PB[7][:, 32 * cc:32 * cc + 32]
            for k in range(self.KT):
                e.matmul(o, self.pt[u % 2][:, k, cc, :], self.v[b % 2][:, k, f], start=(k == 0), stop=False)
            ins = e.matmul(o, self.pl[u % 2][0:2, :], self.vl[b % 2][0:2, f], start=False, stop=True)
        ins.then_inc(self.o_ps.sem, 1)

    def tensor(self, e):
        PB, w, n = self.net.PB, self.w, self.net
        with e.Fori(0, self.iters) as i:
            self.transpose_xn(e, i, PB[7])
            self.context_T(e, i, 0)
            self.keysT(e, i, 0)
            e.wait_ge(self.xnT_r.sem, self.xnT_r.at(i))
            e.matmul(PB[7][:, 0:P], w["wq"], self.xnT[:, :], start=True, stop=True).then_inc(self.q_ps.sem, 1)
            self.values(e, i, 0)
            e.wait_ge(self.qx_r.sem, self.qx_r.at(i))
            e.wait_ge(self.mb_r.sem, self.mb_r.at(i))
            self.scores(e, i, 0)
            for u in range(8):
                b, half = u // 2, u % 2
                if half == 0 and b < 3:
                    self.context_T(e, i, b + 1)
                if half == 1 and b < 3:
                    self.values(e, i, b + 1)
                if u + 1 < 8:
                    self.scores(e, i, u + 1)
                e.wait_ge(self.e_r.sem, self.e_r.at(i, u + 1))
                self.transposes(e, i, u)
                if half == 0 and b < 3:
                    self.keysT(e, i, b + 1)
                if u:
                    self.heads(e, i, u - 1)
            self.heads(e, i, 7)
            e.wait_ge(self.o_r.sem, self.o_r.at(i))
            for b in range(SEQS):
                ins = e.matmul(PB[7][:, b * S:(b + 1) * S], self.o[:, b].rearrange("p c j -> p (c j)"), n.const("samequery"), start=True, stop=True)
            ins.then_inc(self.oT_ps.sem, 1)
            e.wait_ge(self.oT_r.sem, self.oT_r.at(i))
            self.project(e, PB[7], [self.oT[:, :]], [w["wo"]], w["bo"], tiles=1).then_inc(self.y_ps.sem, 1)

    def scalar(self, e):
        self.ln_scalar(e)
        PB, w = self.net.PB, self.w
        e.mul(self.bqs[:, :], w["bq"], QSCALE)
        e.copy(self.onesb[:, :], self.net.const("ones")).then_inc(self.ones_r.sem, 1)
        e.wait_ge(self.ones_r.sem, self.ones_r.at(0))

        def keys(i, b):
            e.wait_ge(self.kT_ps.sem, self.kT_ps.at(i, b + 1))
            if b >= 2:
                e.wait_ge(self.s_ps.sem, self.s_ps.at(i, 2 * b - 2))
            e.activation(self.kT[b % 2][:, :], PB[6][:, 0:T], ACT.Identity, bias=w["bk"]).then_inc(self.kT_r.sem, 1)

        with e.Fori(0, self.iters) as i:
            self.copy_xnT(e, i, PB[7])
            self.copy_context_T(e, i, 0)
            keys(i, 0)
            e.wait_ge(self.q_ps.sem, self.q_ps.at(i))
            e.activation(self.qT[:].rearrange("p b s -> p (b s)"), PB[7][:, 0:P], ACT.Identity, bias=self.bqs[:, :], scale=QSCALE)\
                .then_inc(self.q_r.sem, 1)
            for u in range(8):
                b, half = u // 2, u % 2
                self.exps(e, i, u)
                if half == 0 and b < 3:
                    self.copy_context_T(e, i, b + 1)
                self.copy_probs(e, i, u)
                if half == 0 and b < 3:
                    keys(i, b + 1)
            e.wait_ge(self.oT_ps.sem, self.oT_ps.at(i))
            e.activation(self.oT[:, :], PB[7][:, 0:P], ACT.Identity, bias=w["bv"]).then_inc(self.oT_r.sem, 1)

    def vector(self, e):
        self.ln_vector(e)
        n, c, PB = self.net, self.chain, self.net.PB

        def values(i, b):
            e.wait_ge(self.v_ps.sem, self.v_ps.at(i, b + 1))
            if b >= 2:
                e.wait_ge(self.o_ps.sem, self.o_ps.at(i, 2 * b - 2))
            e.tensor_copy(self.v[b % 2][:].rearrange("p k d -> p (k d)"), PB[6][:, 0:2 * P])
            e.tensor_tensor(self.vl[b % 2][:, :], PB[6][0:2, 2 * P:3 * P], n.const("rowquarter")[0:2, :], ALU.mult).then_inc(self.v_r.sem, 1)

        def normalise(i, u):
            b, half = u // 2, u % 2
            e.wait_ge(self.rm_r.sem, self.rm_r.at(i, u + 1))
            e.wait_ge(self.o_ps.sem, self.o_ps.at(i, u + 1))
            e.tensor_tensor(self.o[:, b, 2 * half:2 * half + 2], PB[7][:, 0:64].rearrange("p (c j) -> p c j", c=2), self.rm[:, u % 2], ALU.mult)\
                .then_inc(self.o_r.sem, 1)

        with e.Fori(0, self.iters) as i:
            c.start()
            self.norm(e, i)
            self.maskbias(e, i)
            values(i, 0)
            e.wait_ge(self.q_r.sem, self.q_r.at(i))
            e.tensor_tensor(self.qx[:, :, 0:4, :], self.qT[:].rearrange("p b (o s) -> p b o s", o=1).to_broadcast([P, SEQS, 4, S]),
                            n.const("head4").rearrange("p (a h b) -> p a h b", a=1, b=1).to_broadcast([P, SEQS, 4, S]), ALU.mult)\
                .then_inc(self.qx_r.sem, 1)
            self.negmax(e, i, 0)
            for u in range(8):
                if u % 2 == 1 and u < 7:
                    values(i, u // 2 + 1)
                if u + 1 < 8:
                    self.negmax(e, i, u + 1)
                if u:
                    normalise(i, u - 1)
                e.wait_ge(self.e_r.sem, self.e_r.at(i, u + 1))
                e.reciprocal(self.rs[:, u, :], self.rs[:, u, :]).then_inc(c.sem, 1)
                e.wait_ge(c.sem, c.next(i))
                e.tensor_tensor(self.rm[:, u % 2], self.rs[:, u, :].rearrange("p (c o) -> p c o", o=1).to_broadcast([P, 2, 32]),
                                n.const("odiag").rearrange("p (a j) -> p a j", a=1).to_broadcast([P, 2, 32]), ALU.mult).then_inc(self.rm_r.sem, 1)
            normalise(i, 7)
            self.add_residual(e, i, PB[7][:, 0:P].rearrange("p (j d) -> p j d", j=1), self.y_ps)
        c.done()


class L2Xattn(CrossAttn):

    name = "L2_xattn"
    vsteps = 9
    cx_dmas = 3
    mask_ops = (-1.0, -MASKED)

    def plan(self):
        self.mask = self.net.masks[1]
        self.plan_common()
        self.A = self.sb("wqk", [P, 16 * P])
        self.WVO = self.sb("wvo", [P, 16 * P])
        self.cl = [self.sb(f"cl{b}", [2, 2, D]) for b in range(SEQS)]
        self.oT = self.sb("oT", [P, 16, P])
        self.w_ps = self.sig("weights_product_in_psum", 1, 1)
        self.w_r = self.sig("weights_product_ready", 1, 1)
        self.cl_r = self.sig("last_rows_cleared", 1, 1)
        self.q_ps = self.sig("hidden_in_psum")
        self.qa_r = self.sig("hidden_ready")
        self.p_r = self.sig("activated_ready", 8)

    def mask_row(self, c):
        return 0

    def bank6_free(self, e, i, b):
        e.wait_ge(self.cT_r.sem, self.cT_r.at(i, b))

    def cT_free(self, e, i, b):
        e.wait_ge(self.s_ps.sem, self.s_ps.at(i, 2 * b - 2))

    def last_row(self, b):
        return self.cl[b][0:1, 0, :]

    def slot_free(self, e, i, b):
        e.wait_ge(self.o_ps.sem, self.o_ps.at(i, 2 * b + 2))

    def load(self, e, i, b):
        src = self.net.ctx_dram[bass.ds(i * SEQS + b, 1)]
        e.dma_start(self.cx[b][:], src[:, 0:self.KT * P, :].rearrange("o (k p) d -> p (o k) d", p=P)).then_inc(self.cx_l[b].sem, 16)
        for c in range(2):
            e.dma_start(self.cl[b][c:c + 1, c, :], src[:, T - 1, :]).then_inc(self.cx_l[b].sem, 16)

    def score_product(self, e, bank, b, c):
        return e.matmul(bank, self.qx[:, b, 4 * c:4 * c + 4, :].rearrange("p h s -> p (h s)"), self.cT[b % 2][:, 0:T], start=False, stop=True)

    def heads(self, e, i, u):
        b = u // 2
        e.wait_ge(self.pt_r.sem, self.pt_r.at(i, u + 1))
        if u:
            e.wait_ge(self.o_r.sem, self.o_r.at(i, u))
        o = self.net.PB[7]
        block = lambda k, **f: e.matmul(o[:, 0:2 * P], self.cx[b][:, k, :], self.pt[u % 2][:, k].rearrange("p c h -> p (c h)"), **f)
        block(0, start=True, stop=False)
        for cc in range(2):
            e.matmul(o[:, cc * P:(cc + 1) * P], self.cl[b][0:2, cc, :], self.pl[u % 2][0:2, :], start=False, stop=False, skip_group_check=True)
        ins = block(1, start=False, stop=True)
        ins.then_inc(self.o_ps.sem, 1)

    def tensor(self, e):
        PB, w, n = self.net.PB, self.w, self.net
        for h in range(16):
            a = slice(h * P, (h + 1) * P)
            o = slice(h % 4 * P, (h % 4 + 1) * P)
            e.matmul(PB[h // 4][:, o], w["wq"][0:64, a], w["wk"][0:64, a], start=True, stop=True)
            ins = e.matmul(PB[4 + h // 4][:, o], w["wv"][0:64, a], w["wo"][0:64, a], start=True, stop=True)
        ins.then_inc(self.w_ps.sem, 1)
        e.wait_ge(self.w_r.sem, self.w_r.at(0))
        with e.Fori(0, self.iters) as i:
            self.transpose_xn(e, i, PB[7])
            self.context_T(e, i, 0)
            e.wait_ge(self.xnT_r.sem, self.xnT_r.at(i))
            for h in range(16):
                ins = e.matmul(PB[h // 4][:, h % 4 * P:(h % 4 + 1) * P], self.A[:, h * P:(h + 1) * P], self.xnT[:, :], start=True, stop=True)
            ins.then_inc(self.q_ps.sem, 1)
            e.wait_ge(self.qx_r.sem, self.qx_r.at(i))
            e.wait_ge(self.qa_r.sem, self.qa_r.at(i))
            e.wait_ge(self.mb_r.sem, self.mb_r.at(i))
            e.wait_ge(self.cT_r.sem, self.cT_r.at(i, 1))
            self.scores(e, i, 0)
            for u in range(8):
                b, half = u // 2, u % 2
                if half == 0 and b < 3:
                    self.context_T(e, i, b + 1)
                if half == 1 and b < 3:
                    e.wait_ge(self.cT_r.sem, self.cT_r.at(i, b + 2))
                if u + 1 < 8:
                    self.scores(e, i, u + 1)
                e.wait_ge(self.p_r.sem, self.p_r.at(i, u + 1))
                self.transposes(e, i, u)
                if u:
                    self.heads(e, i, u - 1)
            self.heads(e, i, 7)
            e.wait_ge(self.o_r.sem, self.o_r.at(i))
            o = PB[7][:, 0:P]
            e.matmul(o, n.const("ones")[0:1, :], w["bo"][0:1, :], start=True, stop=False)
            for h in range(16):
                ins = e.matmul(o, self.oT[:, h, :], self.WVO[:, h * P:(h + 1) * P], start=False, stop=(h == 15))
            ins.then_inc(self.y_ps.sem, 1)

    def spread_q(self, e, i, k):
        src = self.net.PB[k].rearrange("p (h b s) -> p b h s", h=4, b=SEQS)
        f = e.copy if k < 2 else e.tensor_copy
        return f(self.qx[:, :, 4 * k:4 * k + 4, :], src)

    def scalar(self, e):
        self.ln_scalar(e)
        PB = self.net.PB
        e.wait_ge(self.w_ps.sem, self.w_ps.at(0))
        for k in range(4):
            a = slice(k * 512, (k + 1) * 512)
            e.mul(self.A[:, a], PB[k], 0.125)
            ins = e.copy(self.WVO[:, a], PB[4 + k])
        ins.then_inc(self.w_r.sem, 1)
        e.copy(self.onesb[:, :], self.net.const("ones")).then_inc(self.ones_r.sem, 1)
        with e.Fori(0, self.iters) as i:
            self.copy_xnT(e, i, PB[7])
            self.copy_context_T(e, i, 0)
            e.wait_ge(self.q_ps.sem, self.q_ps.at(i))
            self.spread_q(e, i, 0)
            self.spread_q(e, i, 1).then_inc(self.qa_r.sem, 1)
            for u in range(8):
                b, half = u // 2, u % 2
                self.exps(e, i, u)
                if half == 0 and b < 3:
                    self.copy_context_T(e, i, b + 1)
                self.copy_probs(e, i, u)

    def vector(self, e):
        self.ln_vector(e)
        n, c, PB = self.net, self.chain, self.net.PB
        for b in range(SEQS):
            ins = e.memset(self.cl[b][:], 0.0)
        ins.then_inc(self.cl_r.sem, 1)

        def copy_heads(i, u):
            b, half = u // 2, u % 2
            e.wait_ge(self.o_ps.sem, self.o_ps.at(i, u + 1))
            e.tensor_copy(self.oT[:, 8 * half:8 * half + 8, b * S:(b + 1) * S], PB[7][:, 0:2 * P].rearrange("p (h s) -> p h s", s=S))\
                .then_inc(self.o_r.sem, 1)

        with e.Fori(0, self.iters) as i:
            c.start()
            self.norm(e, i)
            self.maskbias(e, i)
            e.wait_ge(self.q_ps.sem, self.q_ps.at(i))
            self.spread_q(e, i, 2)
            self.spread_q(e, i, 3).then_inc(self.qx_r.sem, 1)
            self.negmax(e, i, 0)
            for u in range(8):
                if u + 1 < 8:
                    self.negmax(e, i, u + 1)
                e.wait_ge(self.e_r.sem, self.e_r.at(i, u + 1))
                e.reciprocal(self.rs[:, u, :], self.rs[:, u, :]).then_inc(c.sem, 1)
                e.wait_ge(c.sem, c.next(i))
                for cc in range(2):
                    ins = e.tensor_scalar(self.e[u % 2][:, cc, :], self.e[u % 2][:, cc, :], self.rs[:, u, cc:cc + 1], None, ALU.mult)
                ins.then_inc(self.p_r.sem, 1)
                if u:
                    copy_heads(i, u - 1)
            copy_heads(i, 7)
            self.add_residual(e, i, PB[7][:, 0:P].rearrange("p (j d) -> p j d", j=1), self.y_ps)
        c.done()

    def sync(self, e):
        e.wait_ge(self.cl_r.sem, self.cl_r.at(0))
        super().sync(e)


class L3Xattn(Block):

    name = "L3_xattn"
    vsteps = 5
    STEPS = 4
    GROUPS = (T - 1) // STEPS
    W = 288

    def plan(self):
        n = self.STEPS
        self.wqc = self.sb("wqc", [P, P])
        self.wkv = self.sb("wkv", [P, self.W])
        self.bba = self.sb("bba", [P, 2, H])
        self.cx = self.sb("cx", [P, n, D])
        self.cxT = self.sb("cxT", [P, n, P])
        self.kc = self.sb("kc", [P, n, D])
        self.sq = self.sb("sq", [P, n, D])
        self.ba = self.sb("ba", [P, n, 2, H])
        self.ss = self.sb("ss", [P, 3, n * H])
        self.kb = self.sb("kb", [P, n, D])
        self.vb = self.sb("vb", [P, n, D])
        self.ab = self.sb("ab", [P, n, H])
        self.M = self.sb("M", [P, DH, H, DH])
        self.t1 = self.sb("t1", [P, DH, H, DH])
        self.t2 = self.sb("t2", [P, DH, H, 4])
        self.mk = self.sb("mk", [P, DH, H])
        self.MT = self.sb("MT", [P, DH, P])
        self.Mbd = self.sb("Mbd", [P, 16, H, DH])
        self.qc = self.sb("qc", [P, 4, D])
        self.qn = self.sb("qn", [P, 4, D])
        self.qT = self.sb("qT", [P, 512])
        self.oT = self.sb("oT", [P, 512])
        g = self.GROUPS
        one = lambda name, per=1: (self.net.sig(name, per, 1), self.net.sig(name, per, g))
        self.w_ps = self.sig("weights_product_in_psum", 1, 1)
        self.w_r = self.sig("weights_product_ready", 1, 1)
        self.cx_l = one("context0_loaded", 16)
        self.cxT_ps = one("ctxT_in_psum")
        self.cxT_r = one("ctxT_ready")
        self.kv_ps = one("keysT_in_psum")
        self.sq_r = one("squares_summed", 2)
        self.ms_r = one("meansquare_ready", 2)
        self.rt_r = one("root_ready", 2)
        self.kn_r = one("rms_normed")
        self.ba_r = one("keysT_ready")
        self.in_r = one("scan_input_ready")
        self.scan_r = one("scan_group_done")
        self.pchain = [Steps(u) for u in one("prepare_steps", 9)]
        self.gchain = [Steps(self.net.sig("scan_steps", 7, 1)), Steps(self.net.sig("scan_steps", 8 * n - 1, g))]
        self.m0_r = self.sig("memory_cleared", 1, 1)
        self.MT_ps = self.sig("heads_in_psum", 1, 1)
        self.MT_r = self.sig("heads_ready", 1, 1)
        self.q_ps = self.sig("hidden_in_psum")
        self.qsq_r = self.sig("silu_ready")
        self.qms_r = self.sig("logits_ready")
        self.qrt_r = self.sig("probs_ready")
        self.qn_r = self.sig("spread_ready")
        self.qT_ps = self.sig("probsT_in_psum")
        self.qT_r = self.sig("probsT_low_ready")
        self.mbd_r = self.sig("expert_added")
        self.o_ps = self.sig("headsT_in_psum")
        self.oT_r = self.sig("headsT_ready")
        self.y_ps = self.sig("y_in_psum")

    def prepare_tensor(self, e, z, i, n):
        PB = self.net.PB
        e.wait_ge(self.cx_l[z].sem, self.cx_l[z].at(i))
        for t in range(n):
            ins = e.transpose(PB[0][:, t * P:(t + 1) * P], self.cx[:, t, :], self.net.const("ident"))
        ins.then_inc(self.cxT_ps[z].sem, 1)
        e.wait_ge(self.cxT_r[z].sem, self.cxT_r[z].at(i))
        if z == 0:
            e.wait_ge(self.w_r.sem, self.w_r.at(0))
        else:
            e.wait_ge(self.ba_r[0].sem, self.ba_r[1].at(i, 0))
            e.wait_ge(self.in_r[0].sem, self.in_r[1].at(i, 0))
        for t in range(n):
            ins = e.matmul(PB[1 + t][:, 0:self.W], self.cxT[:, t, :], self.wkv[:, :], start=True, stop=True)
        ins.then_inc(self.kv_ps[z].sem, 1)

    def prepare_scalar(self, e, z, i, n):
        PS = self.net.PS
        e.wait_ge(self.cxT_ps[z].sem, self.cxT_ps[z].at(i))
        e.copy(self.cxT[:, 0:n, :].rearrange("p t b -> p (t b)"), PS[:, 0, 0:n * P]).then_inc(self.cxT_r[z].sem, 1)
        e.wait_ge(self.kv_ps[z].sem, self.kv_ps[z].at(i))
        e.activation(self.sq[:, 0:n, :], PS[:, 1:1 + n, 0:P], ACT.Square).then_inc(self.sq_r[z].sem, 1)
        e.wait_ge(self.ms_r[z].sem, self.ms_r[z].at(i, 1))
        e.activation(self.ss[:, 1, 0:n * H], self.ss[:, 0, 0:n * H], ACT.Sqrt).then_inc(self.rt_r[z].sem, 1)
        e.wait_ge(self.kn_r[z].sem, self.kn_r[z].at(i))
        e.activation(self.sq[:, 0:n, :], self.kc[:, 0:n, :], ACT.Square).then_inc(self.sq_r[z].sem, 1)
        e.wait_ge(self.ms_r[z].sem, self.ms_r[z].at(i, 2))
        e.activation(self.ss[:, 1, 0:n * H], self.ss[:, 0, 0:n * H], ACT.Sqrt).then_inc(self.rt_r[z].sem, 1)
        ba = self.ba[:, 0:n].rearrange("p t two h -> p t (two h)")
        e.activation(ba, ba, ACT.Sigmoid).then_inc(self.ba_r[z].sem, 1)

    def prepare_vector(self, e, z, i, n):
        PS, w, c = self.net.PS, self.w, self.pchain[z]
        c.start()
        heads = lambda a: a.rearrange("p t (h j) -> p (t h) j", j=DH)
        wide = lambda a: a.rearrange("p (n o) -> p n o", o=1).to_broadcast([P, n * H, DH])
        rows = lambda a: a.rearrange("p (o d) -> p o d", o=1).to_broadcast([P, n, D])
        ss, kc = self.ss[:, :, 0:n * H], self.kc[:, 0:n, :]
        e.wait_ge(self.sq_r[z].sem, self.sq_r[z].at(i, 1))
        e.tensor_reduce(ss[:, 0, :], heads(self.sq[:, 0:n, :]), AX.X, ALU.add).then_inc(c.sem, 1)
        e.wait_ge(c.sem, c.next(i))
        e.tensor_scalar(ss[:, 0, :], ss[:, 0, :], 1.0 / DH, LN_EPS, ALU.mult, ALU.add).then_inc(self.ms_r[z].sem, 1)
        e.tensor_tensor(kc, PS[:, 1:1 + n, 0:P], rows(w["gk"]), ALU.mult).then_inc(c.sem, 1)
        e.wait_ge(c.sem, c.next(i))
        e.tensor_tensor(self.ba[:, 0:n].rearrange("p t two h -> p t (two h)"), PS[:, 1:1 + n, 2 * P:2 * P + 32],
                               self.bba[:].rearrange("p (o two) h -> p o (two h)", o=1).to_broadcast([P, n, 32]), ALU.add).then_inc(c.sem, 1)
        e.wait_ge(c.sem, c.next(i))
        e.wait_ge(self.rt_r[z].sem, self.rt_r[z].at(i, 1))
        e.reciprocal(ss[:, 2, :], ss[:, 1, :]).then_inc(c.sem, 1)
        e.wait_ge(c.sem, c.next(i))
        e.tensor_tensor(heads(kc), heads(kc), wide(ss[:, 2, :]), ALU.mult).then_inc(c.sem, 1)
        e.wait_ge(c.sem, c.next(i))
        e.tensor_tensor(kc, kc, rows(w["bk"]), ALU.add).then_inc(self.kn_r[z].sem, 1)
        e.wait_ge(self.sq_r[z].sem, self.sq_r[z].at(i, 2))
        e.tensor_reduce(ss[:, 0, :], heads(self.sq[:, 0:n, :]), AX.X, ALU.add).then_inc(c.sem, 1)
        e.wait_ge(c.sem, c.next(i))
        e.tensor_scalar(ss[:, 0, :], ss[:, 0, :], 1.0, 0.0, ALU.mult, ALU.max).then_inc(self.ms_r[z].sem, 1)
        e.wait_ge(self.rt_r[z].sem, self.rt_r[z].at(i, 2))
        e.tensor_scalar(ss[:, 1, :], ss[:, 1, :], 1e-12, None, ALU.max).then_inc(c.sem, 1)
        e.wait_ge(c.sem, c.next(i))
        e.reciprocal(ss[:, 2, :], ss[:, 1, :]).then_inc(c.sem, 1)
        e.wait_ge(c.sem, c.next(i))
        if z:
            e.wait_ge(self.scan_r[0].sem, self.scan_r[1].at(i, 0))
        e.tensor_tensor(heads(self.kb[:, 0:n, :]), heads(kc), wide(ss[:, 2, :]), ALU.mult).then_inc(c.sem, 1)
        e.wait_ge(c.sem, c.next(i))
        e.wait_ge(self.ba_r[z].sem, self.ba_r[z].at(i))
        e.tensor_copy(self.ab[:, 0:n, :], self.ba[:, 0:n, 1, :])
        for t in range(n):
            ins = e.tensor_tensor(self.vb[:, t, :].rearrange("p (h j) -> p h j", j=DH), PS[:, 1 + t, P:2 * P].rearrange("p (h j) -> p h j", j=DH),
                                  self.ba[:, t, 0, :].rearrange("p (h o) -> p h o", o=1).to_broadcast([P, H, DH]), ALU.mult)
        ins.then_inc(self.in_r[z].sem, 1)
        c.done()

    def scan_pool(self, e, z, i, n):
        c = self.gchain[z]
        c.start()
        e.wait_ge(self.in_r[z].sem, self.in_r[z].at(i))
        if z:
            e.wait_ge(self.scan_r[0].sem, self.scan_r[1].at(i, 0))
        for t in range(n):
            full = [P, DH, H, DH]
            k = self.kb[:, t, :].rearrange("p (o h j) -> p o h j", h=H, o=1).to_broadcast(full)
            a = self.ab[:, t, :].rearrange("p (o h) -> p o h", o=1).to_broadcast([P, DH, H])
            v = self.vb[:, t, :].rearrange("p (h i) -> p i h", h=H)
            e.tensor_tensor(self.t1[:], self.M[:], k, ALU.mult).then_inc(c.sem, 1)
            e.wait_ge(c.sem, c.next(i))
            e.tensor_tensor(self.t2[:], self.t1[:, :, :, 0:4], self.t1[:, :, :, 4:8], ALU.add).then_inc(c.sem, 1)
            e.wait_ge(c.sem, c.next(i))
            e.tensor_tensor(self.t1[:, :, :, 0:2], self.t2[:, :, :, 0:2], self.t2[:, :, :, 2:4], ALU.add).then_inc(c.sem, 1)
            e.wait_ge(c.sem, c.next(i))
            e.tensor_tensor(self.mk[:], self.t1[:, :, :, 0], self.t1[:, :, :, 1], ALU.add).then_inc(c.sem, 1)
            e.wait_ge(c.sem, c.next(i))
            e.tensor_tensor(self.mk[:], self.mk[:], a, ALU.mult).then_inc(c.sem, 1)
            e.wait_ge(c.sem, c.next(i))
            e.tensor_tensor(self.mk[:], v, self.mk[:], ALU.subtract).then_inc(c.sem, 1)
            e.wait_ge(c.sem, c.next(i))
            e.tensor_tensor(self.t1[:], self.mk[:].rearrange("p i (h o) -> p i h o", o=1).to_broadcast(full), k, ALU.mult).then_inc(c.sem, 1)
            e.wait_ge(c.sem, c.next(i))
            ins = e.tensor_tensor(self.M[:], self.M[:], self.t1[:], ALU.add)
            if t == n - 1:
                ins.then_inc(self.scan_r[z].sem, 1)
            else:
                ins.then_inc(c.sem, 1)
                e.wait_ge(c.sem, c.next(i))
        c.done()

    def gpsimd(self, e):
        e.wait_ge(self.res.sem, self.res.at(0, 0))
        e.memset(self.M[:], 0.0).then_inc(self.m0_r.sem, 1)
        e.wait_ge(self.m0_r.sem, self.m0_r.at(0))
        self.scan_pool(e, 0, 0, 1)
        with e.Fori(0, self.GROUPS) as i:
            self.scan_pool(e, 1, i, self.STEPS)

    def sync(self, e):
        e.wait_ge(self.res.sem, self.res.at(0, 0))
        e.dma_start(self.cx[:, 0:1, :], self.net.ctx_dram[:, 0:1, :]).then_inc(self.cx_l[0].sem, 16)
        with e.Fori(0, self.GROUPS) as i:
            e.wait_ge(self.cxT_ps[0].sem, self.cxT_ps[1].at(i, 0))
            e.dma_start(self.cx[:, :, :], self.net.ctx_dram[:, bass.ds(i * self.STEPS + 1, self.STEPS), :]).then_inc(self.cx_l[1].sem, 16)

    def tensor(self, e):
        PB, w, n = self.net.PB, self.w, self.net
        e.matmul(PB[7][:, 0:P], w["wk"], n.const("center8"), start=True, stop=True)
        e.matmul(PB[7][:, P:2 * P], w["wq"], n.const("center8"), start=True, stop=True).then_inc(self.w_ps.sem, 1)
        self.prepare_tensor(e, 0, 0, 1)
        with e.Fori(0, self.GROUPS) as i:
            self.prepare_tensor(e, 1, i, self.STEPS)
        e.wait_ge(self.scan_r[1].sem, self.scan_r[1].at(self.GROUPS - 1))
        e.wait_ge(self.in_r[1].sem, self.in_r[1].at(self.GROUPS - 1))
        for k in range(DH):
            ins = e.transpose(PB[1 + k // 4][:, k % 4 * P:(k % 4 + 1) * P], self.M[:, k].rearrange("p h j -> p (h j)"), n.const("ident"))
        ins.then_inc(self.MT_ps.sem, 1)
        with e.Fori(0, self.iters) as i:
            self.transpose_xn(e, i, PB[0])
            e.wait_ge(self.xnT_r.sem, self.xnT_r.at(i))
            for j in range(4):
                ins = e.matmul(PB[3][:, j * P:(j + 1) * P], self.xnT[:, j * P:(j + 1) * P], self.wqc[:, :], start=True, stop=True)
            ins.then_inc(self.q_ps.sem, 1)
            e.wait_ge(self.qn_r.sem, self.qn_r.at(i))
            for j in range(4):
                ins = e.transpose(PB[4][:, j * P:(j + 1) * P], self.qn[:, j, :], n.const("ident"))
            ins.then_inc(self.qT_ps.sem, 1)
            e.wait_ge(self.qT_r.sem, self.qT_r.at(i))
            e.wait_ge(self.mbd_r.sem, self.mbd_r.at(i))
            for b in range(16):
                ins = e.matmul(PB[5][:, b * S:(b + 1) * S], self.Mbd[:, b].rearrange("p h i -> p (h i)"), self.qT[:, b * S:(b + 1) * S],
                               start=True, stop=True)
            ins.then_inc(self.o_ps.sem, 1)
            e.wait_ge(self.oT_r.sem, self.oT_r.at(i))
            self.project(e, PB[6], [self.oT[:, :]], [w["wo"]], w["bo"]).then_inc(self.y_ps.sem, 1)

    def scalar(self, e):
        self.ln_scalar(e)
        n, w, PS = self.net, self.w, self.net.PS
        e.wait_ge(self.w_ps.sem, self.w_ps.at(0))
        e.copy(self.wkv[:, 0:P], PS[:, 7, 0:P])
        e.copy(self.wqc[:, :], PS[:, 7, P:2 * P])
        e.copy(self.wkv[:, P:2 * P], w["wv"])
        e.copy(self.wkv[:, 2 * P:2 * P + H], w["wb"])
        e.copy(self.bba[:, 0, :], w["bb"])
        e.copy(self.bba[:, 1, :], w["ba"])
        e.copy(self.wkv[:, 2 * P + H:self.W], w["wa"]).then_inc(self.w_r.sem, 1)
        self.prepare_scalar(e, 0, 0, 1)
        with e.Fori(0, self.GROUPS) as i:
            self.prepare_scalar(e, 1, i, self.STEPS)
        e.wait_ge(self.MT_ps.sem, self.MT_ps.at(0))
        for k in range(2):
            ins = e.copy(self.MT[:, 4 * k:4 * k + 4, :].rearrange("p i b -> p (i b)"), n.PB[1 + k])
        ins.then_inc(self.MT_r.sem, 1)
        with e.Fori(0, self.iters) as i:
            self.copy_xnT(e, i, n.PB[0])
            e.wait_ge(self.q_ps.sem, self.q_ps.at(i))
            e.activation(self.qn[:].rearrange("p j d -> p (j d)"), n.PB[3], ACT.Square).then_inc(self.qsq_r.sem, 1)
            e.wait_ge(self.qms_r.sem, self.qms_r.at(i))
            e.activation(self.ss[:, 1, :], self.ss[:, 0, :], ACT.Sqrt).then_inc(self.qrt_r.sem, 1)
            e.wait_ge(self.qT_ps.sem, self.qT_ps.at(i))
            e.copy(self.qT[:, :], n.PB[4]).then_inc(self.qT_r.sem, 1)
            e.wait_ge(self.o_ps.sem, self.o_ps.at(i))
            e.copy(self.oT[:, :], n.PB[5]).then_inc(self.oT_r.sem, 1)

    def vector(self, e):
        self.ln_vector(e)
        n, w, PS, c = self.net, self.w, self.net.PS, self.chain
        e.wait_ge(self.w_r.sem, self.w_r.at(0))
        self.prepare_vector(e, 0, 0, 1)
        with e.Fori(0, self.GROUPS) as i:
            self.prepare_vector(e, 1, i, self.STEPS)
        e.wait_ge(self.MT_r.sem, self.MT_r.at(0))
        heads = lambda a: a.rearrange("p t (h j) -> p (t h) j", j=DH)
        wide = lambda a: a.rearrange("p (n o) -> p n o", o=1).to_broadcast([P, 4 * H, DH])
        rows = lambda a: a.rearrange("p (o d) -> p o d", o=1).to_broadcast([P, 4, D])
        with e.Fori(0, self.iters) as i:
            c.start()
            self.norm(e, i)
            for h in range(2):
                ins = e.tensor_tensor(self.Mbd[:, 8 * h:8 * h + 8], self.MT[:, :, bass.ds(i * 16 + 8 * h, 8)].rearrange("p i (b o) -> p b o i", o=1).to_broadcast([P, 8, H, DH]),
                                      n.const("headcol").rearrange("p (a h b) -> p a h b", a=1, b=1).to_broadcast([P, 8, H, DH]), ALU.mult)
            ins.then_inc(self.mbd_r.sem, 1)
            e.wait_ge(self.qsq_r.sem, self.qsq_r.at(i))
            e.tensor_reduce(self.ss[:, 0, :], heads(self.qn[:]), AX.X, ALU.add).then_inc(c.sem, 1)
            e.wait_ge(c.sem, c.next(i))
            e.tensor_scalar(self.ss[:, 0, :], self.ss[:, 0, :], 1.0 / DH, LN_EPS, ALU.mult, ALU.add).then_inc(self.qms_r.sem, 1)
            e.tensor_tensor(self.qc[:], PS[:, 3, :].rearrange("p (j d) -> p j d", j=4), rows(w["gq"]), ALU.mult).then_inc(c.sem, 1)
            e.wait_ge(c.sem, c.next(i))
            e.wait_ge(self.qrt_r.sem, self.qrt_r.at(i))
            e.reciprocal(self.ss[:, 2, :], self.ss[:, 1, :]).then_inc(c.sem, 1)
            e.wait_ge(c.sem, c.next(i))
            e.tensor_tensor(heads(self.qc[:]), heads(self.qc[:]), wide(self.ss[:, 2, :]), ALU.mult).then_inc(c.sem, 1)
            e.wait_ge(c.sem, c.next(i))
            e.tensor_tensor(self.qn[:], self.qc[:], rows(w["bq"]), ALU.add).then_inc(self.qn_r.sem, 1)
            self.add_residual(e, i, PS[:, 6, :].rearrange("p (j d) -> p j d", j=4), self.y_ps)
        c.done()


BLOCKS = [L0Ffn, L0Attn, L2Attn, L1Ffn, L2Ffn, L3Ffn, L1Attn, L1Xattn, L3Attn, L0Xattn, L2Xattn, L3Xattn]


def build(nc, x, context, mask0, mask1, consts, consts_at, wdram, where, out, names):
    blocks = {c.name: c for c in BLOCKS}
    with ExitStack() as ctx:
        net = Net(nc, ctx, wdram, where, consts_at, context, (mask0, mask1))
        loaded = net.sig("x_loaded", 16, 2)
        first = net.sig("residual_added", 1)
        stored = net.sig("output_stored", 16)
        layers = [blocks[n](net, i) for i, n in enumerate(names)]
        xd = x.rearrange("(t p) d -> p t d", p=P)
        od = out.rearrange("(t p) d -> p t d", p=P)
        block = ctx.enter_context(nc.Block())

        @block.sync
        def _(e):
            e.dma_start(net.X[:], xd).then_inc(loaded.sem, 16)
            e.dma_start(net.K[:], consts).then_inc(loaded.sem, 16)
            for i, l in enumerate(layers):
                if i >= 1:
                    e.wait_ge(layers[i - 1].res.sem, layers[i - 1].res.at(0, 0))
                n = where[l.name][1]
                e.dma_start(net.W[i % 2][:, 0:n], wdram[l.name]).then_inc(l.weights.sem, 16)
                l.sync(e)
            last = layers[-1].res
            e.wait_ge(last.sem, last.at(layers[-1].iters - 1))
            e.dma_start(od, net.X[:]).then_inc(stored.sem, 16)
            e.wait_ge(stored.sem, stored.at(0))

        @block.vector
        def _(e):
            e.wait_ge(loaded.sem, loaded.at(1))
            for t in range(TILES):
                ins = e.bn_stats(net.stats[:, t, :], net.X[:, t, :])
            ins.then_inc(first.sem, 1)
            for l in layers:
                l.vector(e)

        @block.scalar
        def _(e):
            e.wait_ge(loaded.sem, loaded.at(1))
            for l in layers:
                l.scalar(e)

        @block.tensor
        def _(e):
            e.wait_ge(loaded.sem, loaded.at(1))
            for l in layers:
                e.wait_ge(l.res.sem, l.res.at(0, 0))
                e.wait_ge(l.weights.sem, l.weights.at(0))
                l.tensor(e)

        @block.gpsimd
        def _(e):
            e.wait_ge(loaded.sem, loaded.at(1))
            for l in layers:
                l.gpsimd(e)


NAMES = ["L0_xattn", "L0_attn", "L0_ffn", "L1_xattn", "L1_attn", "L1_ffn",
         "L2_xattn", "L2_attn", "L2_ffn", "L3_xattn", "L3_attn", "L3_ffn"]


def kernel(**inputs):
    import concourse.bacc as bacc
    from concourse.bass_utils import run_bass_kernel_spmd

    names = NAMES
    nc = bacc.Bacc("TRN2", target_bir_lowering=False, num_devices=1)
    a = {k: np.asarray(v) for k, v in inputs.items()}
    consts, consts_at = constants()
    arrays = {"x": a["x"].reshape(B * S, D), "context": a["ctx_1024"], "consts": consts,
              "mask0": a["mask_BxS2_bk0"].reshape(TILES, -1).view(np.uint32), "mask1": a["mask_BxS2_bf1"].reshape(TILES, -1).view(np.uint32)}
    parts = layouts(a)
    where = {k: columns(v) for k, v in parts.items()}
    for k in names:
        arrays["w_" + k] = np.concatenate([np.asarray(w) for _, w in parts[k]], 1)
    arrays = {k: np.ascontiguousarray(v) for k, v in arrays.items()}
    d = {k: nc.dram_tensor("in_" + k, v.shape, mybir.dt.from_np(v.dtype), kind="ExternalInput").ap() for k, v in arrays.items()}
    out = nc.dram_tensor("out", (B * S, D), F32, kind="ExternalOutput").ap()
    build(nc, d["x"], d["context"], d["mask0"], d["mask1"], d["consts"], consts_at,
          {k: d["w_" + k] for k in names}, {k: where[k] for k in names}, out, names)
    r = run_bass_kernel_spmd(nc, [{"in_" + k: v for k, v in arrays.items()}], core_ids=[0])
    return r.results[0]["out"].reshape(B, S, D)
```

```python
from contextlib import ExitStack

import numpy as np

import concourse.bass as bass
from concourse import mybir

F32 = mybir.dt.float32
BF16 = mybir.dt.bfloat16
U8 = mybir.dt.uint8
U32 = mybir.dt.uint32
ALU = mybir.AluOpType
ACT = mybir.ActivationFunctionType
AX = mybir.AxisListType

B, S, D = 128, 32, 128
T = 257
P = 128
TILES = B * S // P
SEQS = P // S
G = TILES // 4
H = 16
DH = D // H
C = 4
LN_EPS = 1e-5
MASKED = -float(2 ** 100)


class Signal:

    def __init__(self, sem):
        self.sem, self.total = sem, 0

    def use(self, per, iters):
        u = Use(self.sem, self.total, per)
        self.total += per * iters
        return u


class Use:

    def __init__(self, sem, base, per):
        self.sem, self.base, self.per = sem, base, per

    def at(self, i, k=None):
        return i * self.per + (self.base + (self.per if k is None else k))


class Steps:

    def __init__(self, use):
        self.u, self.sem, self.n = use, use.sem, 0

    def start(self):
        self.n = 0

    def next(self, i=0):
        self.n += 1
        return self.u.at(i, self.n)

    def done(self):
        assert self.n == self.u.per, ("steps", self.n, self.u.per)


def constants():
    p = np.arange(P)
    c = {}
    c["ident"] = np.eye(P)
    c["head4"] = (p[:, None] % 32 // 8 == np.arange(4)[None, :])
    c["odiag"] = (np.arange(32)[None, :] // 8 == p[:, None] // 32)
    c["samequery"] = (p[:, None] % 32 == np.arange(32)[None, :])
    c["causal"] = np.where(np.arange(32)[None, :] > p[:, None] % 32, MASKED, 0.0)
    c["seqmean"] = (p[:, None] // 32 == np.arange(4)[None, :]) / 32.0
    c["ones"] = np.ones((P, P))
    freq = 1.0 / 10000.0 ** (np.arange(0, 16, 2, dtype=np.float32) / 16)
    ang = (np.arange(S, dtype=np.float32)[None, :] * freq[p % 16 // 2][:, None].astype(np.float32))
    c["ropecos"] = np.cos(ang)
    c["ropesin"] = np.where(p % 2 == 0, -1.0, 1.0)[:, None] * np.sin(ang)
    s = np.log2(1.0 - np.exp2(-5.0 - np.arange(8)))
    diff = (p[None, :] - p[:, None])
    keep = (diff >= 0) & (p[None, :] // 32 == p[:, None] // 32)
    c["decay"] = np.concatenate([np.where(keep, np.exp2(np.where(keep, diff, 0) * s[h]), 0.0) for h in range(8)], 1) * 0.25
    c["head2"] = (p[:, None] % 32 // 16 == np.arange(2)[None, :])
    c["mean32"] = (p[:, None] // 32 == p[None, :] // 32) / 32.0
    c["exp2rows"] = np.concatenate([(p[:, None] == 2 * j + p[None, :] // 64) for j in range(4)], 1)
    c["iota14"] = np.broadcast_to(np.arange(14), (P, 14))
    c["quarter"] = (p[:, None] // 32 == np.arange(4)[None, :])
    c["rowquarter"] = (p[:, None] == p[None, :] // 32 % 2)
    c["center8"] = np.eye(P) - (p[:, None] // 8 == p[None, :] // 8) / 8.0
    c["headcol"] = (p[:, None] // 8 == np.arange(16)[None, :])
    c["eps8"] = np.full((P, 1), 1e-8)
    c["eps5"] = np.full((P, 1), 1e-5)
    c["ones33"] = np.broadcast_to(np.where(np.arange(33) == 0, 0.0, 1.0), (P, 33))
    out, at, n = [], {}, 0
    for k, v in c.items():
        v = np.asarray(v, np.float32)
        at[k] = (n, v.shape[1])
        n += v.shape[1]
        out.append(v)
    return np.ascontiguousarray(np.concatenate(out, 1)), at


def rows(w, k):
    n = w.shape[1]
    return w.reshape(k, P, n).transpose(1, 0, 2).reshape(P, k * n)


def bc(v):
    return np.broadcast_to(np.asarray(v).reshape(1, -1), (P, v.size))


def cols(v):
    return np.asarray(v).reshape(-1, P).T


def pad(w):
    out = np.zeros((P, w.shape[1]), w.dtype)
    out[:w.shape[0]] = w
    return out


def layouts(a):
    L = {}
    L["L0_xattn"] = [("wq", a["L0_xattn_W_Q"]), ("wk", a["L0_xattn_W_K"]), ("wv", a["L0_xattn_W_V"]),
                     ("wo", a["L0_xattn_W_O"]), ("bq", cols(a["L0_xattn_b_Q"])), ("bk", cols(a["L0_xattn_b_K"])),
                     ("bv", cols(a["L0_xattn_b_V"])), ("bo", bc(a["L0_xattn_b_O"]))]
    L["L0_attn"] = [("ln1", cols(a["L0_attn_ln1_w"])), ("ln2", cols(a["L0_attn_ln2_w"])), ("ap", cols(a["L0_attn_a_param"])),
                    ("win", a["L0_attn_w_in"].T), ("wgate", a["L0_attn_w_gate"].T), ("wa", rows(a["L0_attn_w_a"].T, 2)),
                    ("wout", rows(a["L0_attn_w_out"].T, 2)), ("wmg", a["L0_attn_w_mlp_gate"].T),
                    ("wmu", a["L0_attn_w_mlp_up"].T), ("wmd", rows(a["L0_attn_w_mlp_down"].T, 4))]
    L["L0_ffn"] = [("w1", a["L0_ffn_W1"]), ("b1", cols(a["L0_ffn_b1"])), ("theta", cols(a["L0_ffn_quantum_phases"])),
                   ("wr", cols(a["L0_ffn_quantum_weights_real"])), ("wi", cols(a["L0_ffn_quantum_weights_imag"])),
                   ("w2", rows(a["L0_ffn_W2"], 4)), ("b2", bc(a["L0_ffn_b2"]))]
    L["L1_xattn"] = [("wq", a["L1_xattn_Wq"].T), ("wk", a["L1_xattn_Wk"].T), ("wv", a["L1_xattn_Wv"].T),
                     ("wo", a["L1_xattn_Wo"].T), ("bq", cols(a["L1_xattn_bq"])), ("bk", cols(a["L1_xattn_bk"])),
                     ("bv", cols(a["L1_xattn_bv"])), ("bo", bc(a["L1_xattn_bo"]))]
    L["L1_attn"] = [("wq", a["L1_attn_W_q"]), ("wk", np.tile(a["L1_attn_W_k"], (1, H))),
                    ("wv", np.tile(a["L1_attn_W_v"], (1, H))), ("wo", a["L1_attn_W_o"])]
    L["L1_ffn"] = [("gate", a["L1_ffn_gate_w"].T), ("down", a["L1_ffn_down_w"].reshape(512, D).T),
                   ("bd", cols(a["L1_ffn_down_b"].reshape(-1))),
                   ("up", rows(a["L1_ffn_up_w"].transpose(0, 2, 1).reshape(512, D), 4)), ("bu", pad(a["L1_ffn_up_b"]))]
    wq, wk = (a[f"L2_xattn_W{n}"].reshape(D, 16, 64).transpose(2, 1, 0).reshape(64, -1) for n in "qk")
    wv = a["L2_xattn_Wv"].reshape(D, 16, 64).transpose(2, 1, 0).reshape(64, -1)
    wo = a["L2_xattn_Wo"].reshape(16, 64, D).transpose(1, 0, 2).reshape(64, -1)
    L["L2_xattn"] = [("wq", pad(wq)), ("wk", pad(wk)), ("wv", pad(wv)), ("wo", pad(wo)), ("bo", bc(a["L2_xattn_bo"]))]
    L["L2_attn"] = [("td", cols(a["L2_attn_time_decay"])), ("tf", cols(a["L2_attn_time_first"])),
                    ("mk", cols(a["L2_attn_time_mix_k"])), ("mv", cols(a["L2_attn_time_mix_v"])),
                    ("mr", cols(a["L2_attn_time_mix_r"])), ("wk", a["L2_attn_Wk"].T), ("wv", a["L2_attn_Wv"].T),
                    ("wr", a["L2_attn_Wr"].T), ("wo", a["L2_attn_Wo"].T)]
    L["L2_ffn"] = [("gate", a["L2_ffn_gate_w"].T), ("w1", a["L2_ffn_w1"].transpose(1, 0, 2).reshape(D, -1)),
                   ("b1", cols(a["L2_ffn_b1"].reshape(-1))), ("w2", rows(a["L2_ffn_w2"].reshape(-1, D), 28)),
                   ("b2", pad(a["L2_ffn_b2"]))]
    L["L3_memory"] = [("wk", a["L3_xattn_Wk"]), ("wv", a["L3_xattn_Wv"].T), ("wb", a["L3_xattn_Wbeta"].T),
                      ("wa", a["L3_xattn_Walpha"].T), ("bb", bc(a["L3_xattn_bbeta"])), ("ba", bc(a["L3_xattn_balpha"])),
                      ("gk", bc(np.tile(a["L3_xattn_gk"], H))), ("bk", bc(np.tile(a["L3_xattn_bk"], H)))]
    L["L3_xattn"] = [("wq", a["L3_xattn_Wq"]), ("wo", a["L3_xattn_Wo"].T), ("bo", bc(a["L3_xattn_bo"])),
                     ("gq", bc(np.tile(a["L3_xattn_gq"], H))), ("bq", bc(np.tile(a["L3_xattn_bq"], H)))]
    swap = np.arange(D) ^ 1
    L["L3_attn"] = [("wq", a["L3_attn_Wq"]), ("wk", a["L3_attn_Wk"]), ("wqs", a["L3_attn_Wq"][:, swap]),
                    ("wks", a["L3_attn_Wk"][:, swap]), ("wv", a["L3_attn_Wv"]), ("wg", a["L3_attn_Wg"]),
                    ("wo", rows(a["L3_attn_Wo"], 2)), ("gn", cols(np.tile(a["L3_attn_g_norm_w"], 4)))]
    L["L3_ffn"] = [("gate", a["L3_ffn_router_w"].T), ("wg", a["L3_ffn_w_gate"].reshape(-1, D).T),
                   ("wu", a["L3_ffn_w_up"].reshape(-1, D).T),
                   ("wd", rows(a["L3_ffn_w_down"].transpose(0, 2, 1).reshape(-1, D), 16))]
    return L


def columns(parts):
    at, n = {}, 0
    for name, w in parts:
        at[name] = (n, w.shape[1])
        n += w.shape[1]
    return at, n


class Net:

    def __init__(self, nc, ctx, wdram, where, consts_at, ctx_dram, masks):
        self.nc, self.ctx, self.wdram, self.where = nc, ctx, wdram, where
        self.ctx_dram, self.masks = ctx_dram, masks
        self.signals = {}
        self.X = self.sb("x", [P, TILES, D])
        self.stats = self.sb("stats", [P, TILES, 6])
        self.mean = self.sb("mean", [P, TILES])
        self.rstd = self.sb("rstd", [P, TILES])
        self.lntmp = self.sb("lntmp", [P, 4, TILES])
        nconst = max(a + n for a, n in consts_at.values())
        self.K = self.sb("consts", [P, nconst])
        self.consts_at = consts_at
        self.W = [self.sb(f"w{i}", [P, max(n for _, n in where.values())]) for i in range(2)]
        self.PS = ctx.enter_context(nc.psum_tensor("banks", [P, 8, 512], F32))
        self.PB = [self.PS[:, i, :] for i in range(8)]
        self.index = {}

    def sb(self, name, shape, dt=F32, ctx=None):
        return (ctx or self.ctx).enter_context(self.nc.sbuf_tensor(name, shape, dt))

    def const(self, name):
        a, n = self.consts_at[name]
        return self.K[:, a:a + n]

    def sig(self, name, per=1, iters=1):
        if name not in self.signals:
            self.signals[name] = Signal(self.ctx.enter_context(self.nc.semaphore(name)))
        return self.signals[name].use(per, iters)


class Block:

    iters, group, name = G, 4, None
    vsteps = 0

    def __init__(self, net, index):
        self.net, self.index = net, index
        at, _ = net.where[self.name]
        wbuf = net.W[index % 2]
        self.w = {k: wbuf[:, a:a + n] for k, (a, n) in at.items()}
        self.scratch = ExitStack()
        self.weights = net.sig(f"weights_loaded_{("even", "odd")[index % 2]}", 16)
        self.lnchain = Steps(net.sig("layernorm_steps", 7))
        self.var = net.sig("variance_ready")
        self.std = net.sig("std_ready")
        self.setup_chain = Steps(net.sig("setup_steps", self.setup_steps))
        self.chain = Steps(net.sig("vector_steps", self.vsteps, self.iters))
        self.xn_r = net.sig("xn_ready", 1, self.iters)
        if self.whole_xnT:
            self.xnT_ps = net.sig("xnT_in_psum", 1, self.iters)
            self.xnT_r = net.sig("xnT_ready", 1, self.iters)
        self.res = net.sig("residual_added", 1, self.iters)
        self.xn = self.sb("xn", [P, self.group, D])
        self.xnT = self.sb("xnT", [P, self.group * P])
        self.plan()
        self.scratch.close()

    setup_steps = 0
    whole_xnT = True

    def sb(self, name, shape, dt=F32):
        return self.net.sb(f"{self.name}_{name}", shape, dt, self.scratch)

    def sig(self, name, per=1, iters=None):
        return self.net.sig(name, per, self.iters if iters is None else iters)

    def ln_vector(self, e):
        n = self.net
        e.wait_ge(self.weights.sem, self.weights.at(0))
        e.wait_ge(self.res.sem, self.res.at(0, 0))
        st, c = n.stats, self.lnchain
        me, ve, mo, vo = (st[:, :, j] for j in (1, 2, 4, 5))
        t = n.lntmp
        c.start()
        e.tensor_tensor(t[:, 0, :], me, mo, ALU.add).then_inc(c.sem, 1)
        e.wait_ge(c.sem, c.next())
        e.tensor_scalar(n.mean[:, :], t[:, 0, :], 0.5, None, ALU.mult).then_inc(c.sem, 1)
        e.wait_ge(c.sem, c.next())
        e.tensor_tensor(t[:, 1, :], me, mo, ALU.subtract).then_inc(c.sem, 1)
        e.wait_ge(c.sem, c.next())
        e.scalar_tensor_tensor(out=t[:, 2, :], in0=t[:, 1, :], scalar=32.0, in1=t[:, 1, :], op0=ALU.mult, op1=ALU.mult).then_inc(c.sem, 1)
        e.wait_ge(c.sem, c.next())
        e.tensor_tensor(t[:, 3, :], ve, vo, ALU.add).then_inc(c.sem, 1)
        e.wait_ge(c.sem, c.next())
        e.tensor_tensor(t[:, 0, :], t[:, 3, :], t[:, 2, :], ALU.add).then_inc(c.sem, 1)
        e.wait_ge(c.sem, c.next())
        e.tensor_scalar(t[:, 1, :], t[:, 0, :], 1.0 / D, LN_EPS, ALU.mult, ALU.add).then_inc(self.var.sem, 1)
        e.wait_ge(self.std.sem, self.std.at(0))
        e.reciprocal(n.rstd[:, :], t[:, 2, :]).then_inc(c.sem, 1)
        e.wait_ge(c.sem, c.next())
        c.done()

    def ln_scalar(self, e):
        e.wait_ge(self.weights.sem, self.weights.at(0))
        e.wait_ge(self.var.sem, self.var.at(0))
        e.activation(self.net.lntmp[:, 2, :], self.net.lntmp[:, 1, :], ACT.Sqrt).then_inc(self.std.sem, 1)

    def norm(self, e, i):
        n = self.net
        e.wait_ge(self.res.sem, self.res.at(i, 0))
        for j in range(self.group):
            t = i * self.group + j
            ins = e.tensor_scalar(self.xn[:, j, :], n.X[:, bass.ds(t, 1), :], n.mean[:, bass.ds(t, 1)], n.rstd[:, bass.ds(t, 1)],
                                  ALU.subtract, ALU.mult)
        ins.then_inc(self.xn_r.sem, 1)

    def transpose_xn(self, e, i, bank):
        e.wait_ge(self.xn_r.sem, self.xn_r.at(i))
        for j in range(self.group):
            ins = e.transpose(bank[:, j * P:(j + 1) * P], self.xn[:, j, :], self.net.const("ident"))
        ins.then_inc(self.xnT_ps.sem, 1)

    def copy_xnT(self, e, i, bank):
        e.wait_ge(self.xnT_ps.sem, self.xnT_ps.at(i))
        e.copy(self.xnT[:, :], bank[:, 0:self.group * P]).then_inc(self.xnT_r.sem, 1)

    def add_residual(self, e, i, y, ready):
        n = self.net
        g = self.group
        e.wait_ge(ready.sem, ready.at(i))
        xs = n.X[:, bass.ds(i * g, g), :]
        e.tensor_tensor(xs, y, xs, ALU.add).then_inc(self.chain.sem, 1)
        e.wait_ge(self.chain.sem, self.chain.next(i))
        for j in range(g):
            ins = e.bn_stats(n.stats[:, bass.ds(i * g + j, 1), :], n.X[:, bass.ds(i * g + j, 1), :])
        ins.then_inc(self.res.sem, 1)

    def project(self, e, bank, lhs, w, bias=None, tiles=4):
        for j in range(tiles):
            o = bank[:, j * P:(j + 1) * P]
            if bias is not None:
                e.matmul(o, self.net.const("ones")[0:1, :], bias[0:1, :], start=True, stop=False)
            for k in range(len(lhs)):
                ins = e.matmul(o, lhs[k][:, j * P:(j + 1) * P], w[k], start=(k == 0 and bias is None), stop=(k == len(lhs) - 1))
        return ins


TWO_PI = 6.283185307179586
PI_IN = 3.1415925
ROUND = 12582912.0
PI_HI = 6.28125
PI_LO = TWO_PI - PI_HI


class L0Ffn(Block):

    name = "L0_ffn"
    vsteps = 7
    setup_steps = 13

    def plan(self):
        self.hid = self.sb("hid", [P, 4, 512])
        self.arg = self.sb("arg", [P, 4, 512])
        self.tmp = self.sb("tmp", [P, 4, 512])
        self.f = self.sb("features", [P, 8, 4])
        self.angles = self.sig("angles_ready", 1, 1)
        self.sines = self.sig("sines_ready", 1, 1)
        self.hid_ps = self.sig("hidden_in_psum")
        self.hid_r = self.sig("hidden_ready")
        self.arg_r = self.sig("argument_ready")
        self.sin_r = self.sig("sine_ready")
        self.act_r = self.sig("activated_ready")
        self.y_ps = self.sig("y_in_psum")

    def vector(self, e):
        self.ln_vector(e)
        w, f, c = self.w, self.f, self.setup_chain
        k, th, co, cf = f[:, 0, :], f[:, 1, :], f[:, 2, :], f[:, 7, :]
        e.tensor_scalar(k, w["theta"], 1 / TWO_PI, ROUND, ALU.mult, ALU.add).then_inc(c.sem, 1)
        e.wait_ge(c.sem, c.next())
        e.tensor_scalar(k, k, ROUND, None, ALU.subtract).then_inc(c.sem, 1)
        e.wait_ge(c.sem, c.next())
        e.scalar_tensor_tensor(out=th, in0=k, scalar=-PI_HI, in1=w["theta"], op0=ALU.mult, op1=ALU.add).then_inc(c.sem, 1)
        e.wait_ge(c.sem, c.next())
        e.scalar_tensor_tensor(out=th, in0=k, scalar=-PI_LO, in1=th, op0=ALU.mult, op1=ALU.add).then_inc(c.sem, 1)
        e.wait_ge(c.sem, c.next())
        e.tensor_scalar(th, th, PI_IN, -PI_IN, ALU.min, ALU.max).then_inc(c.sem, 1)
        e.wait_ge(c.sem, c.next())
        e.tensor_scalar(co, th, TWO_PI / 4, None, ALU.add).then_inc(c.sem, 1)
        e.wait_ge(c.sem, c.next())
        e.tensor_scalar(k, co, TWO_PI / 2, -TWO_PI, ALU.is_gt, ALU.mult).then_inc(c.sem, 1)
        e.wait_ge(c.sem, c.next())
        e.tensor_tensor(co, co, k, ALU.add).then_inc(c.sem, 1)
        e.wait_ge(c.sem, c.next())
        e.tensor_scalar(co, co, PI_IN, -PI_IN, ALU.min, ALU.max).then_inc(c.sem, 1)
        e.wait_ge(c.sem, c.next())
        e.tensor_copy(k, th).then_inc(self.angles.sem, 1)
        e.wait_ge(self.sines.sem, self.sines.at(0))
        e.tensor_tensor(f[:, 5, :], f[:, 4, :], w["wr"], ALU.mult).then_inc(c.sem, 1)
        e.wait_ge(c.sem, c.next())
        e.tensor_tensor(f[:, 6, :], f[:, 3, :], w["wi"], ALU.mult).then_inc(c.sem, 1)
        e.wait_ge(c.sem, c.next())
        e.tensor_tensor(f[:, 5, :], f[:, 5, :], f[:, 6, :], ALU.add).then_inc(c.sem, 1)
        e.wait_ge(c.sem, c.next())
        e.scalar_tensor_tensor(out=cf, in0=f[:, 5, :], scalar=0.1, in1=w["wi"], op0=ALU.mult, op1=ALU.mult).then_inc(c.sem, 1)
        e.wait_ge(c.sem, c.next())
        c.done()
        with e.Fori(0, self.iters) as i:
            self.chain.start()
            self.norm(e, i)
            e.wait_ge(self.hid_r.sem, self.hid_r.at(i))
            for j in range(4):
                ins = e.tensor_scalar(self.arg[:, j, :], self.hid[:, j, :], 0.1, th[:, j:j + 1], ALU.mult, ALU.add)
            ins.then_inc(self.chain.sem, 1)
            e.wait_ge(self.chain.sem, self.chain.next(i))
            e.tensor_scalar(self.tmp[:], self.arg[:], 1 / TWO_PI, ROUND, ALU.mult, ALU.add).then_inc(self.chain.sem, 1)
            e.wait_ge(self.chain.sem, self.chain.next(i))
            e.tensor_scalar(self.tmp[:], self.tmp[:], ROUND, -TWO_PI, ALU.subtract, ALU.mult).then_inc(self.chain.sem, 1)
            e.wait_ge(self.chain.sem, self.chain.next(i))
            e.tensor_tensor(self.arg[:], self.arg[:], self.tmp[:], ALU.add).then_inc(self.chain.sem, 1)
            e.wait_ge(self.chain.sem, self.chain.next(i))
            e.tensor_scalar(self.arg[:], self.arg[:], PI_IN, -PI_IN, ALU.min, ALU.max).then_inc(self.arg_r.sem, 1)
            e.wait_ge(self.sin_r.sem, self.sin_r.at(i))
            for j in range(4):
                ins = e.scalar_tensor_tensor(out=self.hid[:, j, :], in0=self.tmp[:, j, :], scalar=cf[:, j:j + 1],
                                             in1=self.hid[:, j, :], op0=ALU.mult, op1=ALU.add)
                if j == 2:
                    ins.then_inc(self.chain.sem, 1)
                    e.wait_ge(self.chain.sem, self.chain.next(i))
            ins.then_inc(self.chain.sem, 1)
            e.wait_ge(self.chain.sem, self.chain.next(i))
            e.tensor_scalar(self.arg[:], self.hid[:], 0.0, None, ALU.max).then_inc(self.act_r.sem, 1)
            self.add_residual(e, i, self.net.PB[5][:, :].rearrange("p (j d) -> p j d", j=4), self.y_ps)
        self.chain.done()

    def scalar(self, e):
        self.ln_scalar(e)
        f = self.f
        e.wait_ge(self.angles.sem, self.angles.at(0))
        e.activation(f[:, 3, :], f[:, 1, :], ACT.Sin)
        e.activation(f[:, 4, :], f[:, 2, :], ACT.Sin).then_inc(self.sines.sem, 1)
        with e.Fori(0, self.iters) as i:
            self.copy_xnT(e, i, self.net.PB[0])
            e.wait_ge(self.hid_ps.sem, self.hid_ps.at(i))
            for j in range(4):
                ins = e.activation(self.hid[:, j, :], self.net.PB[1 + j][:, :], ACT.Identity, bias=self.w["b1"][:, j:j + 1])
            ins.then_inc(self.hid_r.sem, 1)
            e.wait_ge(self.arg_r.sem, self.arg_r.at(i))
            e.activation(self.tmp[:], self.arg[:], ACT.Sin).then_inc(self.sin_r.sem, 1)

    def tensor(self, e):
        w, n = self.w, self.net
        e.wait_ge(self.weights.sem, self.weights.at(0))
        with e.Fori(0, self.iters) as i:
            self.transpose_xn(e, i, n.PB[0])
            e.wait_ge(self.xnT_r.sem, self.xnT_r.at(i))
            for j in range(4):
                ins = e.matmul(n.PB[1 + j][:, :], w["w1"][:, j * P:(j + 1) * P], self.xnT[:, :], start=True, stop=True)
            ins.then_inc(self.hid_ps.sem, 1)
            e.wait_ge(self.act_r.sem, self.act_r.at(i))
            self.project(e, n.PB[5], [self.arg[:, k, :] for k in range(4)], [w["w2"][:, k * P:(k + 1) * P] for k in range(4)],
                         w["b2"]).then_inc(self.y_ps.sem, 1)

    def gpsimd(self, e):
        pass

    def sync(self, e):
        pass


class L0Attn(Block):

    name = "L0_attn"
    whole_xnT = False
    vsteps = 13

    def plan(self):
        self.ms = self.sb("meansquare", [P, 2, 3, 4])
        self.sq = self.sb("squares", [P, 4, D])
        self.hn = self.sb("hn", [P, 4, D])
        self.hT = self.sb("hT", [P, 512])
        self.xin = self.sb("xin", [P, 2, 512])
        self.gate = self.sb("gate", [P, 2, 512])
        self.a = self.sb("decay", [P, 2, 512])
        self.t = self.sb("t", [P, 2, 512])
        self.y = self.sb("y", [P, 2, 512])
        self.x2 = self.sb("x2", [P, 4, D])
        self.sg = self.sb("sg", [P, 4, 512])
        self.m = self.sb("m", [P, 4, 512])
        self.sq_r = self.sig("squares_summed", 2)
        self.ms_r = self.sig("meansquare_ready", 2)
        self.rt_r = self.sig("root_ready", 2)
        self.hn_r = self.sig("rms_normed", 2)
        self.x2_r = self.sig("x2_ready")
        self.hT_ps = self.sig("rms_in_psum", 2)
        self.hT_r = self.sig("rms_transposed", 2)
        self.in_ps = self.sig("hidden_in_psum")
        self.xin_r = self.sig("xin_ready")
        self.gate_r = self.sig("gate_ready")
        self.a_ps = self.sig("decay_in_psum")
        self.a_r = self.sig("decay_ready")
        self.t_r = self.sig("one_minus_square_ready")
        self.rest_r = self.sig("complement_ready")
        self.y_r = self.sig("activated_ready")
        self.wo_ps = self.sig("recurrence_in_psum")
        self.mlp_ps = self.sig("mlp_in_psum")
        self.sg_r = self.sig("mlp_sigmoid_ready")
        self.m_r = self.sig("mlp_hidden_ready")
        self.y_ps = self.sig("y_in_psum")

    def rms_vector(self, e, i, k, src):
        m = self.ms[:, k - 1]
        e.wait_ge(self.sq_r.sem, self.sq_r.at(i, k))
        e.tensor_scalar(m[:, 1, :], m[:, 0, :], 1.0 / D, 1e-6, ALU.mult, ALU.add).then_inc(self.ms_r.sem, 1)
        e.wait_ge(self.rt_r.sem, self.rt_r.at(i, k))
        e.reciprocal(m[:, 2, :], m[:, 2, :]).then_inc(self.chain.sem, 1)
        e.wait_ge(self.chain.sem, self.chain.next(i))
        for j in range(4):
            ins = e.tensor_scalar(self.hn[:, j, :], src[:, j, :], m[:, 2, j:j + 1], None, ALU.mult)
        ins.then_inc(self.hn_r.sem, 1)

    def rms_scalar(self, e, i, k, src, ln, bank, ready):
        m = self.ms[:, k - 1]
        e.wait_ge(ready.sem, ready.at(i))
        for j in range(4):
            ins = e.activation(self.sq[:, j, :], src[:, j, :], ACT.Square, accum_out=m[:, 0, j:j + 1])
        ins.then_inc(self.sq_r.sem, 1)
        e.wait_ge(self.ms_r.sem, self.ms_r.at(i, k))
        e.activation(m[:, 2, :], m[:, 1, :], ACT.Sqrt).then_inc(self.rt_r.sem, 1)
        e.wait_ge(self.hT_ps.sem, self.hT_ps.at(i, k))
        e.activation(self.hT[:, :], bank[:, :], ACT.Copy, scale=ln).then_inc(self.hT_r.sem, 1)

    def rms_tensor(self, e, i, k, bank):
        e.wait_ge(self.hn_r.sem, self.hn_r.at(i, k))
        for j in range(4):
            ins = e.transpose(bank[:, j * P:(j + 1) * P], self.hn[:, j, :], self.net.const("ident"))
        ins.then_inc(self.hT_ps.sem, 1)
        e.wait_ge(self.hT_r.sem, self.hT_r.at(i, k))

    def vector(self, e):
        self.ln_vector(e)
        PB = self.net.PB
        with e.Fori(0, self.iters) as i:
            c = self.chain
            c.start()
            self.norm(e, i)
            self.rms_vector(e, i, 1, self.xn)
            e.wait_ge(self.in_ps.sem, self.in_ps.at(i))
            for j in range(2):
                ins = e.tensor_copy(self.xin[:, j, :], PB[1 + j][:, :])
            ins.then_inc(self.xin_r.sem, 1)
            e.wait_ge(self.a_r.sem, self.a_r.at(i))
            e.tensor_tensor(self.t[:], self.a[:], self.a[:], ALU.mult).then_inc(c.sem, 1)
            e.wait_ge(c.sem, c.next(i))
            e.tensor_scalar(self.t[:], self.t[:], -1.0, 1.0, ALU.mult, ALU.add).then_inc(self.t_r.sem, 1)
            e.memset(self.a[:].rearrange("p j (b s) -> p (j b) s", s=S)[:, :, 0:1], 0.0).then_inc(c.sem, 1)
            e.wait_ge(c.sem, c.next(i))
            e.wait_ge(self.rest_r.sem, self.rest_r.at(i))
            e.tensor_tensor(self.t[:], self.t[:], self.xin[:], ALU.mult).then_inc(c.sem, 1)
            e.wait_ge(c.sem, c.next(i))
            for j in range(2):
                e.tensor_tensor_scan(self.y[:, j, :], self.a[:, j, :], self.t[:, j, :], 0.0, ALU.mult, ALU.add).then_inc(c.sem, 1)
                e.wait_ge(c.sem, c.next(i))
            e.wait_ge(self.gate_r.sem, self.gate_r.at(i))
            e.tensor_tensor(self.y[:], self.y[:], self.gate[:], ALU.mult).then_inc(self.y_r.sem, 1)
            e.wait_ge(self.wo_ps.sem, self.wo_ps.at(i))
            e.tensor_tensor(self.x2[:], PB[7][:, :].rearrange("p (j d) -> p j d", j=4), self.xn[:], ALU.add).then_inc(self.x2_r.sem, 1)
            self.rms_vector(e, i, 2, self.x2)
            e.wait_ge(self.sg_r.sem, self.sg_r.at(i))
            for j in range(4):
                e.tensor_tensor(self.sg[:, j, :], PB[j][:, :], self.sg[:, j, :], ALU.mult).then_inc(c.sem, 1)
                e.wait_ge(c.sem, c.next(i))
            for j in range(4):
                ins = e.tensor_tensor(self.m[:, j, :], PB[4 + j][:, :], self.sg[:, j, :], ALU.mult)
            ins.then_inc(self.m_r.sem, 1)
            xs = self.net.X[:, bass.ds(i * 4, 4), :]
            e.tensor_tensor(xs, self.x2[:], xs, ALU.add).then_inc(c.sem, 1)
            e.wait_ge(c.sem, c.next(i))
            self.add_residual(e, i, PB[0][:, :].rearrange("p (j d) -> p j d", j=4), self.y_ps)
        self.chain.done()

    def scalar(self, e):
        self.ln_scalar(e)
        PB, w = self.net.PB, self.w
        with e.Fori(0, self.iters) as i:
            self.rms_scalar(e, i, 1, self.xn, w["ln1"], PB[0], self.xn_r)
            e.wait_ge(self.in_ps.sem, self.in_ps.at(i))
            for j in range(2):
                ins = e.activation(self.gate[:, j, :], PB[3 + j][:, :], ACT.Sigmoid)
            ins.then_inc(self.gate_r.sem, 1)
            e.wait_ge(self.a_ps.sem, self.a_ps.at(i))
            for j in range(2):
                ins = e.activation(self.a[:, j, :], PB[5 + j][:, :], ACT.Sigmoid, bias=w["ap"][:, j:j + 1])
            ins.then_inc(self.a_r.sem, 1)
            e.wait_ge(self.t_r.sem, self.t_r.at(i))
            e.activation(self.t[:], self.t[:], ACT.Sqrt, bias=self.net.const("eps8")).then_inc(self.rest_r.sem, 1)
            self.rms_scalar(e, i, 2, self.x2, w["ln2"], PB[0], self.x2_r)
            e.wait_ge(self.mlp_ps.sem, self.mlp_ps.at(i))
            for j in range(4):
                ins = e.activation(self.sg[:, j, :], PB[j][:, :], ACT.Sigmoid)
            ins.then_inc(self.sg_r.sem, 1)

    def tensor(self, e):
        PB, w = self.net.PB, self.w
        with e.Fori(0, self.iters) as i:
            self.rms_tensor(e, i, 1, PB[0])
            for j in range(2):
                e.matmul(PB[1 + j][:, :], w["win"][:, j * P:(j + 1) * P], self.hT[:, :], start=True, stop=True)
            for j in range(2):
                ins = e.matmul(PB[3 + j][:, :], w["wgate"][:, j * P:(j + 1) * P], self.hT[:, :], start=True, stop=True)
            ins.then_inc(self.in_ps.sem, 1)
            e.wait_ge(self.xin_r.sem, self.xin_r.at(i))
            for j in range(2):
                for k in range(2):
                    a = k * 256 + j * P
                    ins = e.matmul(PB[5 + j][:, :], w["wa"][:, a:a + P], self.xin[:, k, :], start=(k == 0), stop=(k == 1))
            ins.then_inc(self.a_ps.sem, 1)
            e.wait_ge(self.y_r.sem, self.y_r.at(i))
            self.project(e, PB[7], [self.y[:, k, :] for k in range(2)], [w["wout"][:, k * P:(k + 1) * P] for k in range(2)])\
                .then_inc(self.wo_ps.sem, 1)
            self.rms_tensor(e, i, 2, PB[0])
            for name, b in (("wmg", 0), ("wmu", 4)):
                for j in range(4):
                    ins = e.matmul(PB[b + j][:, :], w[name][:, j * P:(j + 1) * P], self.hT[:, :], start=True, stop=True)
            ins.then_inc(self.mlp_ps.sem, 1)
            e.wait_ge(self.m_r.sem, self.m_r.at(i))
            self.project(e, PB[0], [self.m[:, k, :] for k in range(4)], [w["wmd"][:, k * P:(k + 1) * P] for k in range(4)])\
                .then_inc(self.y_ps.sem, 1)

    def gpsimd(self, e):
        pass

    def sync(self, e):
        pass


class L2Attn(Block):

    name = "L2_attn"
    vsteps = 17
    setup_steps = 4

    def plan(self):
        s3 = [P, 16, 33]
        self.xs = self.sb("xs", s3)
        self.mix = self.sb("mixed", [P, 3, 16, S])
        self.dx = self.sb("dx", [P, 16, S])
        self.k = self.sb("k", s3)
        self.v = self.sb("v", [P, 16, S])
        self.sr = self.sb("sr", [P, 16, S])
        self.wdec = self.sb("wdecay", s3)
        self.pp = self.sb("pp", s3)
        self.e1 = self.sb("e1", s3)
        self.e2 = self.sb("e2", s3)
        self.ev = self.sb("ev", s3)
        self.aa = self.sb("aa", s3)
        self.bb = self.sb("bb", s3)
        self.p = self.sb("p", [P, 2, 16, S])
        self.q = self.sb("q", [P, 2, 16, S])
        self.num = self.sb("num", [P, 2, 16, S])
        self.neg = self.sb("negw", [P, 2])
        self.expw = self.sig("decay_exp_ready", 1, 1)
        self.mix_r = self.sig("mixed_ready", 3)
        self.kvr_ps = self.sig("hidden_in_psum")
        self.kvr_r = self.sig("kvr_ready")
        self.arg1 = self.sig("exponents_ready", 2)
        self.exp1 = self.sig("exps_ready", 2)
        self.act_r = self.sig("activated_ready")
        self.y_ps = self.sig("y_in_psum")

    def vector(self, e):
        self.ln_vector(e)
        w, c = self.w, self.setup_chain
        now, before = slice(1, 33), slice(0, 32)
        e.memset(self.xs[:, :, 0:1], 0.0)
        e.memset(self.k[:, :, 0:1], -1e38)
        e.memset(self.e1[:, :, 0:1], 0.0)
        e.memset(self.e2[:, :, 0:1], 0.0)
        e.memset(self.ev[:, :, 0:1], 0.0).then_inc(c.sem, 1)
        e.wait_ge(c.sem, c.next())
        e.wait_ge(self.expw.sem, self.expw.at(0))
        e.tensor_scalar(self.neg[:, 1:2], self.neg[:, 0:1], -1.0, None, ALU.mult).then_inc(c.sem, 1)
        e.wait_ge(c.sem, c.next())
        e.memset(self.wdec[:], 0.0).then_inc(c.sem, 1)
        e.wait_ge(c.sem, c.next())
        e.tensor_scalar(self.wdec[:, :, now], self.wdec[:, :, now], self.neg[:, 1:2], None, ALU.add)
        e.memset(self.wdec[:, :, 0:1], -1e38).then_inc(c.sem, 1)
        e.wait_ge(c.sem, c.next())
        c.done()
        flat = lambda t: t[:].rearrange("p b s -> p (b s)")
        with e.Fori(0, self.iters) as i:
            c = self.chain
            c.start()
            self.norm(e, i)
            e.wait_ge(self.xnT_r.sem, self.xnT_r.at(i))
            e.tensor_tensor(self.dx[:], self.xs[:, :, now], self.xs[:, :, before], ALU.subtract).then_inc(c.sem, 1)
            e.wait_ge(c.sem, c.next(i))
            for j, m in enumerate(("mk", "mv", "mr")):
                e.scalar_tensor_tensor(out=self.mix[:, j], in0=self.dx[:], scalar=w[m], in1=self.xs[:, :, before],
                                       op0=ALU.mult, op1=ALU.add).then_inc(self.mix_r.sem, 1)
            e.wait_ge(self.kvr_r.sem, self.kvr_r.at(i))
            e.tensor_tensor_scan(flat(self.pp), flat(self.wdec), flat(self.k), -1e38, ALU.add, ALU.max).then_inc(c.sem, 1)
            e.wait_ge(c.sem, c.next(i))
            pb, pn, kn = self.pp[:, :, before], self.pp[:, :, now], self.k[:, :, now]
            e.scalar_tensor_tensor(out=self.p[:, 0], in0=pb, scalar=self.neg[:, 1:2], in1=pn, op0=ALU.add, op1=ALU.subtract).then_inc(c.sem, 1)
            e.wait_ge(c.sem, c.next(i))
            e.tensor_tensor(self.p[:, 1], kn, pn, ALU.subtract).then_inc(self.arg1.sem, 1)
            e.tensor_scalar(self.num[:, 0], kn, w["tf"], None, ALU.add).then_inc(c.sem, 1)
            e.wait_ge(c.sem, c.next(i))
            e.tensor_tensor(self.num[:, 1], self.num[:, 0], pb, ALU.max).then_inc(c.sem, 1)
            e.wait_ge(c.sem, c.next(i))
            e.tensor_tensor(self.q[:, 0], pb, self.num[:, 1], ALU.subtract).then_inc(c.sem, 1)
            e.wait_ge(c.sem, c.next(i))
            e.tensor_tensor(self.q[:, 1], self.num[:, 0], self.num[:, 1], ALU.subtract).then_inc(self.arg1.sem, 1)
            e.wait_ge(self.exp1.sem, self.exp1.at(i, 1))
            e.tensor_tensor(self.ev[:, :, now], self.e2[:, :, now], self.v[:], ALU.mult).then_inc(c.sem, 1)
            e.wait_ge(c.sem, c.next(i))
            e.tensor_tensor_scan(flat(self.aa), flat(self.e1), flat(self.ev), 0.0, ALU.mult, ALU.add).then_inc(c.sem, 1)
            e.wait_ge(c.sem, c.next(i))
            e.tensor_tensor_scan(flat(self.bb), flat(self.e1), flat(self.e2), 0.0, ALU.mult, ALU.add).then_inc(c.sem, 1)
            e.wait_ge(c.sem, c.next(i))
            e.wait_ge(self.exp1.sem, self.exp1.at(i, 2))
            e.tensor_tensor(self.num[:, 0], self.q[:, 0], self.aa[:, :, before], ALU.mult).then_inc(c.sem, 1)
            e.wait_ge(c.sem, c.next(i))
            e.tensor_tensor(self.num[:, 1], self.q[:, 0], self.bb[:, :, before], ALU.mult).then_inc(c.sem, 1)
            e.wait_ge(c.sem, c.next(i))
            e.tensor_tensor(self.p[:, 0], self.q[:, 1], self.v[:], ALU.mult).then_inc(c.sem, 1)
            e.wait_ge(c.sem, c.next(i))
            e.tensor_tensor(self.p[:, 0], self.p[:, 0], self.num[:, 0], ALU.add).then_inc(c.sem, 1)
            e.wait_ge(c.sem, c.next(i))
            e.tensor_tensor(self.p[:, 1], self.q[:, 1], self.num[:, 1], ALU.add).then_inc(c.sem, 1)
            e.wait_ge(c.sem, c.next(i))
            e.reciprocal(self.p[:, 1], self.p[:, 1]).then_inc(c.sem, 1)
            e.wait_ge(c.sem, c.next(i))
            e.tensor_tensor(self.p[:, 0], self.p[:, 0], self.p[:, 1], ALU.mult).then_inc(c.sem, 1)
            e.wait_ge(c.sem, c.next(i))
            e.tensor_tensor(self.q[:, 0], self.p[:, 0], self.sr[:], ALU.mult).then_inc(self.act_r.sem, 1)
            self.add_residual(e, i, self.net.PB[4][:, :].rearrange("p (j d) -> p j d", j=4), self.y_ps)
        self.chain.done()

    def scalar(self, e):
        self.ln_scalar(e)
        PB = self.net.PB
        e.activation(self.neg[:, 0:1], self.w["td"], ACT.Exp).then_inc(self.expw.sem, 1)
        seqs = lambda b: b[:, :].rearrange("p (b s) -> p b s", s=S)
        with e.Fori(0, self.iters) as i:
            e.wait_ge(self.xnT_ps.sem, self.xnT_ps.at(i))
            e.activation(self.xs[:, :, 1:33], seqs(PB[0]), ACT.Copy).then_inc(self.xnT_r.sem, 1)
            e.wait_ge(self.kvr_ps.sem, self.kvr_ps.at(i))
            e.activation(self.k[:, :, 1:33], seqs(PB[1]), ACT.Copy)
            e.activation(self.v[:], seqs(PB[2]), ACT.Copy)
            e.activation(self.sr[:], seqs(PB[3]), ACT.Sigmoid).then_inc(self.kvr_r.sem, 1)
            e.wait_ge(self.arg1.sem, self.arg1.at(i, 1))
            e.activation(self.e1[:, :, 1:33], self.p[:, 0], ACT.Exp)
            e.activation(self.e2[:, :, 1:33], self.p[:, 1], ACT.Exp).then_inc(self.exp1.sem, 1)
            e.wait_ge(self.arg1.sem, self.arg1.at(i, 2))
            e.activation(self.q[:], self.q[:], ACT.Exp).then_inc(self.exp1.sem, 1)

    def tensor(self, e):
        PB, w = self.net.PB, self.w
        with e.Fori(0, self.iters) as i:
            self.transpose_xn(e, i, PB[0])
            for j, m in enumerate(("wk", "wv", "wr")):
                e.wait_ge(self.mix_r.sem, self.mix_r.at(i, j + 1))
                ins = e.matmul(PB[1 + j][:, :], w[m], self.mix[:, j].rearrange("p b s -> p (b s)"), start=True, stop=True)
            ins.then_inc(self.kvr_ps.sem, 1)
            e.wait_ge(self.act_r.sem, self.act_r.at(i))
            self.project(e, PB[4], [self.q[:, 0].rearrange("p b s -> p (b s)")], [w["wo"]]).then_inc(self.y_ps.sem, 1)

    def gpsimd(self, e):
        pass

    def sync(self, e):
        pass


def router(c, i, e, block, lg, n, E, probs, floor, plus):
    r = block
    big = lambda t: t[:, :].rearrange("p (n o) -> p n o", o=1).to_broadcast([P, n, E])
    e.tensor_reduce(r.mx[:, :], lg, AX.X, ALU.max).then_inc(c.sem, 1)
    e.wait_ge(c.sem, c.next(i))
    e.tensor_tensor(r.ex[:], lg, big(r.mx), ALU.subtract).then_inc(r.lg_r.sem, 1)
    e.wait_ge(probs.sem, probs.at(i))
    e.tensor_reduce(r.mx[:, :], r.ex[:], AX.X, ALU.add).then_inc(c.sem, 1)
    e.wait_ge(c.sem, c.next(i))
    e.reciprocal(r.mx[:, :], r.mx[:, :]).then_inc(c.sem, 1)
    e.wait_ge(c.sem, c.next(i))
    e.tensor_tensor(r.ex[:], r.ex[:], big(r.mx), ALU.mult).then_inc(c.sem, 1)
    e.wait_ge(c.sem, c.next(i))
    e.memset(r.held[:, 0:1], 0.0)
    for j in range(n):
        ins = e.max(r.top[:, j, :], r.ex[:, j, :])
    ins.then_inc(c.sem, 1)
    e.wait_ge(c.sem, c.next(i))
    e.memset(r.held[:, 1:2], 0.0)
    for j in range(n):
        ins = e.max_index(r.idx[:, j, :], r.top[:, j, :], r.ex[:, j, :])
    ins.then_inc(c.sem, 1)
    e.wait_ge(c.sem, c.next(i))
    e.tensor_copy(r.idf[:], r.idx[:]).then_inc(c.sem, 1)
    e.wait_ge(c.sem, c.next(i))
    e.tensor_tensor(r.mx[:, :], r.top[:, :, 0], r.top[:, :, 1], ALU.add).then_inc(c.sem, 1)
    e.wait_ge(c.sem, c.next(i))
    e.tensor_scalar(r.mx[:, :], r.mx[:, :], plus, floor, ALU.add, ALU.max).then_inc(c.sem, 1)
    e.wait_ge(c.sem, c.next(i))
    e.reciprocal(r.mx[:, :], r.mx[:, :]).then_inc(c.sem, 1)
    e.wait_ge(c.sem, c.next(i))
    e.tensor_tensor(r.top[:, :, 0:2], r.top[:, :, 0:2],
                           r.mx[:, :].rearrange("p (n o) -> p n o", o=1).to_broadcast([P, n, 2]), ALU.mult).then_inc(c.sem, 1)
    e.wait_ge(c.sem, c.next(i))
    iota = r.net.const("iota14")[:, 0:E]
    for j in range(n):
        e.tensor_scalar(r.cw[:, j, :], iota, r.idf[:, j, 0:1], r.top[:, j, 0:1], ALU.is_equal, ALU.mult)
        ins = e.tensor_scalar(r.one[:, j, :], iota, r.idf[:, j, 1:2], r.top[:, j, 1:2], ALU.is_equal, ALU.mult)
    ins.then_inc(c.sem, 1)
    e.wait_ge(c.sem, c.next(i))
    return e.tensor_tensor(r.cw[:], r.cw[:], r.one[:], ALU.add)


def router_buffers(b, n, E):
    b.held = b.sb("held", [P, 2])
    b.mx = b.sb("rowmax", [P, n])
    b.ex = b.sb("probs", [P, n, E])
    b.top = b.sb("top", [P, n, 8])
    b.idx = b.sb("topindex", [P, n, 8], U32)
    b.idf = b.sb("topindexf", [P, n, 8])
    b.cw = b.sb("expertweights", [P, n, E])
    b.one = b.sb("second", [P, n, E])


class TokenMoE(Block):

    E, halves = 14, 2

    def plan(self):
        E = self.E
        router_buffers(self, 4, E)
        self.h = self.sb("hidden", [P, 4, 512])
        self.sg = self.sb("silu", [P, 2, 512])
        self.acc = self.sb("acc", [P, 4, D])
        self.cwT = self.sb("cwT", [P, 512])
        self.lg_ps = self.sig("logits_in_psum")
        self.lg_r = self.sig("logits_ready")
        self.ex_r = self.sig("probs_ready")
        self.cw_r = self.sig("expertweights_ready")
        if self.has_start:
            self.cwT_ps = self.sig("expertweights_in_psum")
            self.cwT_r = self.sig("expertweights_transposed")
            self.bias_ps = self.sig("expertbias_in_psum")
        self.hid_ps = self.sig("hidden_in_psum", 2 * E)
        if self.gated:
            self.silu_r = self.sig("silu_ready", 2 * E)
        self.hid_r = self.sig("hidden_ready", 2 * E)
        self.e_ps = self.sig("expert_in_psum", E)
        self.acc_r = self.sig("expert_added", E)

    def router_tensor(self, e, i):
        PB = self.net.PB
        for j in range(4):
            ins = e.matmul(PB[7][:, j * self.E:(j + 1) * self.E], self.xnT[:, j * P:(j + 1) * P], self.w["gate"], start=True, stop=True)
        ins.then_inc(self.lg_ps.sem, 1)

    def combine(self, e, i, x):
        for x in range(self.E):
            e.wait_ge(self.e_ps.sem, self.e_ps.at(i, x + 1))
            if x:
                e.wait_ge(self.acc_r.sem, self.acc_r.at(i, x))
            for j in range(4):
                y = self.net.PB[4 + x % 2][:, j * P:(j + 1) * P]
                if x == 0 and not self.has_start:
                    ins = e.tensor_scalar(self.acc[:, j, :], y, self.cw[:, j, x:x + 1], None, ALU.mult)
                else:
                    ins = e.scalar_tensor_tensor(out=self.acc[:, j, :], in0=y, scalar=self.cw[:, j, x:x + 1], in1=self.acc[:, j, :],
                                                 op0=ALU.mult, op1=ALU.add)
            ins.then_inc(self.acc_r.sem, 1)
            if self.gated and x + 1 < self.E:
                self.gate_vector(e, i, x + 1)
        e.wait_ge(self.acc_r.sem, self.acc_r.at(i))

    def down(self, e, i, x, w):
        e.wait_ge(self.hid_r.sem, self.hid_r.at(i, 2 * x + 2))
        if x >= 2:
            e.wait_ge(self.acc_r.sem, self.acc_r.at(i, x - 1))
        for j in range(4):
            for k in range(2):
                a = (2 * x + k) * P
                ins = e.matmul(self.net.PB[4 + x % 2][:, j * P:(j + 1) * P], self.h[:, (2 * x + k) % 4, j * P:(j + 1) * P],
                               w[:, a:a + P], start=(k == 0), stop=(k == 1))
        ins.then_inc(self.e_ps.sem, 1)

    def gpsimd(self, e):
        pass

    def sync(self, e):
        pass


class L2Ffn(TokenMoE):

    name, E, gated, has_start = "L2_ffn", 14, False, True
    vsteps = 15

    def vector(self, e):
        self.ln_vector(e)
        PB, c = self.net.PB, self.chain
        with e.Fori(0, self.iters) as i:
            c.start()
            self.norm(e, i)
            e.wait_ge(self.lg_ps.sem, self.lg_ps.at(i))
            router(c, i, e, self, PB[7][:, 0:4 * self.E].rearrange("p (n e) -> p n e", n=4), 4, self.E,
                   self.ex_r, 1e-10, 0.0).then_inc(self.cw_r.sem, 1)
            e.wait_ge(self.bias_ps.sem, self.bias_ps.at(i))
            e.tensor_tensor(self.acc[:], PB[6][:, :].rearrange("p (j d) -> p j d", j=4), self.xn[:], ALU.add).then_inc(c.sem, 1)
            e.wait_ge(c.sem, c.next(i))
            self.combine(e, i, 0)
            e.tensor_scalar(self.acc[:], self.acc[:], -100.0, 100.0, ALU.max, ALU.min).then_inc(c.sem, 1)
            e.wait_ge(c.sem, c.next(i))
            self.add_residual(e, i, self.acc[:], self.acc_r)
        c.done()

    def scalar(self, e):
        self.ln_scalar(e)
        PB = self.net.PB
        with e.Fori(0, self.iters) as i:
            self.copy_xnT(e, i, PB[6])
            e.wait_ge(self.lg_r.sem, self.lg_r.at(i))
            e.activation(self.ex[:], self.ex[:], ACT.Exp).then_inc(self.ex_r.sem, 1)
            e.wait_ge(self.cwT_ps.sem, self.cwT_ps.at(i))
            e.copy(self.cwT[0:self.E, :], PB[7][0:self.E, :]).then_inc(self.cwT_r.sem, 1)
            for n in range(2 * self.E):
                e.wait_ge(self.hid_ps.sem, self.hid_ps.at(i, n + 1))
                if n >= 4:
                    e.wait_ge(self.e_ps.sem, self.e_ps.at(i, n // 2 - 1))
                e.activation(self.h[:, n % 4, :], PB[n % 4][:, :], ACT.Gelu, bias=self.w["b1"][:, n:n + 1]).then_inc(self.hid_r.sem, 1)

    def tensor(self, e):
        PB, w, E = self.net.PB, self.w, self.E

        def up(x):
            for n in (2 * x, 2 * x + 1):
                if n >= 4:
                    e.wait_ge(self.hid_r.sem, self.hid_r.at(i, n - 3))
                e.matmul(PB[n % 4][:, :], w["w1"][:, n * P:(n + 1) * P], self.xnT[:, :], start=True, stop=True)\
                    .then_inc(self.hid_ps.sem, 1)

        with e.Fori(0, self.iters) as i:
            self.transpose_xn(e, i, PB[6])
            e.wait_ge(self.xnT_r.sem, self.xnT_r.at(i))
            self.router_tensor(e, i)
            up(0)
            e.wait_ge(self.cw_r.sem, self.cw_r.at(i))
            for j in range(4):
                ins = e.matmul(PB[7][0:E, j * P:(j + 1) * P], self.cw[:, j, :], self.net.const("ident"), start=True, stop=True)
            ins.then_inc(self.cwT_ps.sem, 1)
            up(1)
            e.wait_ge(self.cwT_r.sem, self.cwT_r.at(i))
            for j in range(4):
                ins = e.matmul(PB[6][:, j * P:(j + 1) * P], self.cwT[0:E, j * P:(j + 1) * P], w["b2"][0:E, :], start=True, stop=True)
            ins.then_inc(self.bias_ps.sem, 1)
            for x in range(E):
                if 1 < x + 1 < E:
                    up(x + 1)
                self.down(e, i, x, w["w2"])


class L3Ffn(TokenMoE):

    name, E, gated, has_start = "L3_ffn", 8, True, False
    vsteps = 13

    def gate_vector(self, e, i, x):
        for n in (2 * x, 2 * x + 1):
            e.wait_ge(self.silu_r.sem, self.silu_r.at(i, n + 1))
            if n >= 4:
                e.wait_ge(self.e_ps.sem, self.e_ps.at(i, n // 2 - 1))
            e.tensor_tensor(self.h[:, n % 4, :], self.net.PB[2 * (n % 2) + 1][:, :], self.sg[:, n % 2, :], ALU.mult)\
                .then_inc(self.hid_r.sem, 1)

    def vector(self, e):
        self.ln_vector(e)
        PB, c = self.net.PB, self.chain
        with e.Fori(0, self.iters) as i:
            c.start()
            self.norm(e, i)
            e.wait_ge(self.lg_ps.sem, self.lg_ps.at(i))
            router(c, i, e, self, PB[7][:, 0:4 * self.E].rearrange("p (n e) -> p n e", n=4), 4, self.E,
                   self.ex_r, 1e-30, 0.0).then_inc(self.cw_r.sem, 1)
            e.wait_ge(self.cw_r.sem, self.cw_r.at(i))
            self.gate_vector(e, i, 0)
            self.combine(e, i, 0)
            self.add_residual(e, i, self.acc[:], self.acc_r)
        c.done()

    def scalar(self, e):
        self.ln_scalar(e)
        PB = self.net.PB
        with e.Fori(0, self.iters) as i:
            self.copy_xnT(e, i, PB[6])
            e.wait_ge(self.lg_r.sem, self.lg_r.at(i))
            e.activation(self.ex[:], self.ex[:], ACT.Exp).then_inc(self.ex_r.sem, 1)
            for n in range(2 * self.E):
                e.wait_ge(self.hid_ps.sem, self.hid_ps.at(i, n + 1))
                if n >= 2:
                    e.wait_ge(self.hid_r.sem, self.hid_r.at(i, n - 1))
                e.activation(self.sg[:, n % 2, :], PB[2 * (n % 2)][:, :], ACT.Silu).then_inc(self.silu_r.sem, 1)

    def tensor(self, e):
        PB, w, E = self.net.PB, self.w, self.E

        def up(x):
            for n in (2 * x, 2 * x + 1):
                if n >= 2:
                    e.wait_ge(self.hid_r.sem, self.hid_r.at(i, n - 1))
                e.matmul(PB[2 * (n % 2)][:, :], w["wg"][:, n * P:(n + 1) * P], self.xnT[:, :], start=True, stop=True)
                e.matmul(PB[2 * (n % 2) + 1][:, :], w["wu"][:, n * P:(n + 1) * P], self.xnT[:, :], start=True, stop=True)\
                    .then_inc(self.hid_ps.sem, 1)

        with e.Fori(0, self.iters) as i:
            self.transpose_xn(e, i, PB[6])
            e.wait_ge(self.xnT_r.sem, self.xnT_r.at(i))
            self.router_tensor(e, i)
            up(0)
            for x in range(E):
                if x + 1 < E:
                    up(x + 1)
                self.down(e, i, x, w["wd"])


class L1Ffn(Block):

    name = "L1_ffn"
    E, C = 8, 64
    vsteps = 1
    setup_steps = 12

    def plan(self):
        router_buffers(self, 1, self.E)
        self.pooledT = self.sb("pooledT", [P, P])
        self.cwT = self.sb("cwT", [P, P])
        self.cwx = self.sb("cwx", [P, 4, P])
        self.cwe = self.sb("cwe", [P, 16, S])
        self.h = self.sb("h", [P, 4, 512])
        self.h2 = self.sb("h2", [P, 4, 512])
        self.pxn_r = self.sig("pool_xn_ready")
        self.pool_ps = self.sig("pooled_in_psum")
        self.pool_r = self.sig("pooled_ready")
        self.lg_ps = self.sig("logits_in_psum", 1, 1)
        self.lg_r = self.sig("logits_ready", 1, 1)
        self.ex_r = self.sig("probs_ready", 1, 1)
        self.cw_r = self.sig("expertweights_ready", 1, 1)
        self.cwT_ps = self.sig("expertweights_in_psum", 1, 1)
        self.cwT_r = self.sig("expertweights_transposed", 1, 1)
        self.cwx_ps = self.sig("expertbias_in_psum", 1, 1)
        self.cwx_r = self.sig("expert_added", 1, 1)
        self.cwe_r = self.sig("activated_ready")
        self.hid_ps = self.sig("hidden_in_psum")
        self.hid_r = self.sig("hidden_ready")
        self.h2_r = self.sig("mlp_hidden_ready")
        self.y_ps = self.sig("y_in_psum")

    def vector(self, e):
        self.ln_vector(e)
        n, PB = self.net, self.net.PB
        with e.Fori(0, self.iters) as i:
            for j in range(4):
                t = i * 4 + j
                ins = e.tensor_scalar(self.xn[:, j, :], n.X[:, bass.ds(t, 1), :], n.mean[:, bass.ds(t, 1)], n.rstd[:, bass.ds(t, 1)],
                                      ALU.subtract, ALU.mult)
            ins.then_inc(self.pxn_r.sem, 1)
            e.wait_ge(self.pool_ps.sem, self.pool_ps.at(i))
            e.tensor_copy(self.pooledT[:, bass.ds(i * 16, 16)], PB[6][:, 0:16]).then_inc(self.pool_r.sem, 1)
        e.wait_ge(self.lg_ps.sem, self.lg_ps.at(0))
        router(self.setup_chain, 0, e, self, PB[7][:, 0:8].rearrange("p (n e) -> p n e", n=1), 1, self.E,
               self.ex_r, 0.0, 1e-8).then_inc(self.cw_r.sem, 1)
        e.wait_ge(self.cwx_ps.sem, self.cwx_ps.at(0))
        e.tensor_copy(self.cwx[:], PB[6][:, :].rearrange("p (j b) -> p j b", j=4)).then_inc(self.cwx_r.sem, 1)
        e.wait_ge(self.cwx_r.sem, self.cwx_r.at(0))
        self.setup_chain.done()
        with e.Fori(0, self.iters) as i:
            self.chain.start()
            self.norm(e, i)
            e.tensor_copy(self.cwe[0:8], self.cwT[0:8, bass.ds(i * 16, 16)].rearrange("p (b o) -> p b o", o=1).to_broadcast([8, 16, S]))\
                .then_inc(self.cwe_r.sem, 1)
            e.wait_ge(self.hid_r.sem, self.hid_r.at(i))
            for j in range(4):
                ins = e.tensor_tensor(self.h2[:, j, :].rearrange("p (b s) -> p b s", s=S), self.h[:, j, :].rearrange("p (b s) -> p b s", s=S),
                                      self.cwx[:, j, bass.ds(i * 16, 16)].rearrange("p (b o) -> p b o", o=1).to_broadcast([P, 16, S]), ALU.mult)
            ins.then_inc(self.h2_r.sem, 1)
            self.add_residual(e, i, PB[5][:, :].rearrange("p (j d) -> p j d", j=4), self.y_ps)
        self.chain.done()

    def scalar(self, e):
        self.ln_scalar(e)
        PB = self.net.PB
        e.wait_ge(self.lg_r.sem, self.lg_r.at(0))
        e.activation(self.ex[:], self.ex[:], ACT.Exp).then_inc(self.ex_r.sem, 1)
        e.wait_ge(self.cwT_ps.sem, self.cwT_ps.at(0))
        e.copy(self.cwT[0:8, :], PB[7][0:8, 0:P]).then_inc(self.cwT_r.sem, 1)
        with e.Fori(0, self.iters) as i:
            self.copy_xnT(e, i, PB[0])
            e.wait_ge(self.hid_ps.sem, self.hid_ps.at(i))
            for j in range(4):
                ins = e.activation(self.h[:, j, :], PB[1 + j][:, :], ACT.Gelu, bias=self.w["bd"][:, j:j + 1])
            ins.then_inc(self.hid_r.sem, 1)

    def tensor(self, e):
        PB, w, n = self.net.PB, self.w, self.net
        with e.Fori(0, self.iters) as i:
            e.wait_ge(self.pxn_r.sem, self.pxn_r.at(i))
            for j in range(4):
                ins = e.matmul(PB[6][:, 4 * j:4 * j + 4], self.xn[:, j, :], n.const("seqmean"), start=True, stop=True)
            ins.then_inc(self.pool_ps.sem, 1)
        e.wait_ge(self.pool_r.sem, self.pool_r.at(self.iters - 1))
        e.matmul(PB[7][:, 0:8], self.pooledT[:, :], w["gate"], start=True, stop=True).then_inc(self.lg_ps.sem, 1)
        e.wait_ge(self.cw_r.sem, self.cw_r.at(0))
        e.matmul(PB[7][0:8, 0:P], self.cw[:, 0, :], n.const("ident"), start=True, stop=True).then_inc(self.cwT_ps.sem, 1)
        e.wait_ge(self.cwT_r.sem, self.cwT_r.at(0))
        for j in range(4):
            ins = e.matmul(PB[6][:, j * P:(j + 1) * P], n.const("exp2rows")[0:8, j * P:(j + 1) * P], self.cwT[0:8, :], start=True, stop=True)
        ins.then_inc(self.cwx_ps.sem, 1)
        with e.Fori(0, self.iters) as i:
            self.transpose_xn(e, i, PB[0])
            e.wait_ge(self.xnT_r.sem, self.xnT_r.at(i))
            for j in range(4):
                ins = e.matmul(PB[1 + j][:, :], w["down"][:, j * P:(j + 1) * P], self.xnT[:, :], start=True, stop=True)
            ins.then_inc(self.hid_ps.sem, 1)
            e.wait_ge(self.h2_r.sem, self.h2_r.at(i))
            e.wait_ge(self.cwe_r.sem, self.cwe_r.at(i))
            for j in range(4):
                o = PB[5][:, j * P:(j + 1) * P]
                e.matmul(o, self.cwe[0:8, 4 * j:4 * j + 4, :].rearrange("p b s -> p (b s)"), w["bu"][0:8, :], start=True, stop=False)
                for k in range(4):
                    ins = e.matmul(o, self.h2[:, k, j * P:(j + 1) * P], w["up"][:, k * P:(k + 1) * P], start=False, stop=(k == 3))
            ins.then_inc(self.y_ps.sem, 1)

    def gpsimd(self, e):
        pass

    def sync(self, e):
        pass

QSCALE = 1.0 / float(np.sqrt(8.0))


class SmallAttn(Block):

    vsteps = 5
    cross = False

    def plan(self):
        if self.cross:
            self.ct = self.sb("ctx", [P, 4, D])
            self.ctT = self.sb("ctxT", [P, 512])
            self.ctx_l = self.sig("context_loaded", 64)
            self.ctT_ps = self.sig("ctxT_in_psum")
            self.ctT_r = self.sig("ctxT_ready")
            self.bqs = self.sb("bqs", [P, 1])
            self.bqs_r = self.sig("scaled_bias_ready", 1, 1)
        self.qT = self.sb("qT", [P, 16, S])
        self.kx = self.sb("kx", [P, 16, C, S])
        self.vx = self.sb("vx", [P, 4, C, SEQS, 32])
        self.bks = self.sb("bks", [P, C])
        self.qx = self.sb("qx", [P, 16, 4, S])
        self.e = self.sb("e", [P, 64, S])
        self.pt = self.sb("pt", [P, C, 4, P])
        self.rm = self.sb("rm", [P, 4, 4, C, 32])
        self.o = self.sb("o", [P, 4, 4, C * 32])
        self.oT = self.sb("oT", [P, 512])
        self.mx = self.sb("mx", [P, 64])
        self.rs = self.sb("rs", [P, 64])
        self.qkv_ps = self.sig("hidden_in_psum")
        self.q_r = self.sig("hidden_ready")
        self.qx_r = self.sig("spread_ready")
        self.kx_r = self.sig("keys_spread_ready")
        self.vx_r = self.sig("values_spread_ready")
        self.s_ps = self.sig("scores_in_psum")
        self.d_r = self.sig("exponents_ready")
        self.e_r = self.sig("exps_ready")
        self.pt_ps = self.sig("probsT_in_psum")
        self.pta_r = self.sig("probsT_low_ready")
        self.ptv_r = self.sig("probsT_high_ready")
        self.o_ps = self.sig("heads_in_psum")
        self.o_r = self.sig("heads_ready")
        self.oT_ps = self.sig("headsT_in_psum")
        self.oT_r = self.sig("headsT_ready")
        self.y_ps = self.sig("y_in_psum")

    def vector(self, e):
        self.ln_vector(e)
        n, c = self.net, self.chain
        PS = n.PS
        with e.Fori(0, self.iters) as i:
            c.start()
            self.norm(e, i)
            e.wait_ge(self.q_r.sem, self.q_r.at(i))
            e.tensor_tensor(self.qx[:], self.qT[:].rearrange("p b (o s) -> p b o s", o=1).to_broadcast([P, 16, 4, S]),
                            n.const("head4").rearrange("p (a h b) -> p a h b", a=1, b=1).to_broadcast([P, 16, 4, S]), ALU.mult)\
                .then_inc(self.qx_r.sem, 1)
            e.wait_ge(self.s_ps.sem, self.s_ps.at(i))
            sc = PS[:, 0:4, :].rearrange("p t x -> p (t x)").rearrange("p (b c k) -> p c b k", c=C, k=S)
            ex = self.e[:].rearrange("p (c b) k -> p c b k", c=C)
            if self.cross:
                e.tensor_tensor(ex, sc, n.const("causal").rearrange("p (a o k) -> p a o k", a=1, o=1).to_broadcast([P, C, 16, S]), ALU.add)\
                    .then_inc(c.sem, 1)
                e.wait_ge(c.sem, c.next(i))
                sc = ex
            e.tensor_reduce(self.mx[:, :].rearrange("p (c b) -> p c b", c=C), sc, AX.X, ALU.max).then_inc(c.sem, 1)
            e.wait_ge(c.sem, c.next(i))
            e.tensor_tensor(ex, sc, self.mx[:, :].rearrange("p (c b o) -> p c b o", c=C, o=1).to_broadcast([P, C, 16, S]), ALU.subtract)\
                .then_inc(self.d_r.sem, 1)
            e.wait_ge(self.e_r.sem, self.e_r.at(i))
            e.tensor_reduce(self.rs[:, :], self.e[:], AX.X, ALU.add).then_inc(c.sem, 1)
            e.wait_ge(c.sem, c.next(i))
            e.reciprocal(self.rs[:, :], self.rs[:, :]).then_inc(c.sem, 1)
            e.wait_ge(c.sem, c.next(i))
            r4 = self.rs[:, :].rearrange("p (c t r) -> p r t c", c=C, r=4)
            for r in range(4):
                ins = e.tensor_tensor(self.rm[:, r], r4[:, r].rearrange("p t (c o) -> p t c o", o=1).to_broadcast([P, 4, C, 32]),
                                      n.const("odiag").rearrange("p (a b j) -> p a b j", a=1, b=1).to_broadcast([P, 4, C, 32]), ALU.mult)
            ins.then_inc(c.sem, 1)
            e.wait_ge(c.sem, c.next(i))
            e.wait_ge(self.pt_ps.sem, self.pt_ps.at(i))
            for q in (2, 3):
                ins = e.tensor_copy(self.pt[:, q].rearrange("p t h -> p (t h)"), PS[:, 4 + q, :])
            ins.then_inc(self.ptv_r.sem, 1)
            e.wait_ge(self.o_ps.sem, self.o_ps.at(i))
            for r in range(SEQS):
                ins = e.tensor_tensor(self.o[:, r].rearrange("p t (c j) -> p t c j", c=C),
                                      PS[:, 0:4, :].rearrange("p t (c r j) -> p r t c j", c=C, r=SEQS)[:, r], self.rm[:, r], ALU.mult)
            ins.then_inc(self.o_r.sem, 1)
            self.add_residual(e, i, PS[:, 5, :].rearrange("p (j d) -> p j d", j=4), self.y_ps)
        c.done()

    def scalar(self, e):
        self.ln_scalar(e)
        n, PB, w = self.net, self.net.PB, self.w
        seqs = lambda t: t.rearrange("p (b k) -> p b k", k=S)
        if self.cross:
            for c in range(C):
                e.mul(self.bks[:, c:c + 1], w["bk"], n.const("quarter")[:, c:c + 1])
            e.mul(self.bqs[:, :], w["bq"], QSCALE).then_inc(self.bqs_r.sem, 1)
            e.wait_ge(self.bqs_r.sem, self.bqs_r.at(0))
        with e.Fori(0, self.iters) as i:
            self.copy_xnT(e, i, PB[0])
            if self.cross:
                e.wait_ge(self.ctT_ps.sem, self.ctT_ps.at(i))
                e.copy(self.ctT[:, :], PB[1]).then_inc(self.ctT_r.sem, 1)
            e.wait_ge(self.qkv_ps.sem, self.qkv_ps.at(i))
            if self.cross:
                e.activation(self.qT[:].rearrange("p b s -> p (b s)"), PB[4], ACT.Identity, bias=self.bqs[:, :], scale=QSCALE)\
                    .then_inc(self.q_r.sem, 1)
            else:
                e.activation(self.qT[:].rearrange("p b s -> p (b s)"), PB[4], ACT.Copy, scale=QSCALE).then_inc(self.q_r.sem, 1)
            for c in range(C):
                k = n.const("quarter")[:, c:c + 1]
                ins = e.activation(self.kx[:, :, c, :], seqs(PB[5]), ACT.Identity, bias=self.bks[:, c:c + 1] if self.cross else 0.0, scale=k)
            ins.then_inc(self.kx_r.sem, 1)
            for r in range(SEQS):
                ins = e.activation(self.vx[:, :, :, r, :], PB[6].rearrange("p (t c j) -> p t c j", t=4, c=C), ACT.Identity,
                                   scale=n.const("quarter")[:, r:r + 1])
            ins.then_inc(self.vx_r.sem, 1)
            e.wait_ge(self.d_r.sem, self.d_r.at(i))
            e.activation(self.e[:], self.e[:], ACT.Exp).then_inc(self.e_r.sem, 1)
            e.wait_ge(self.pt_ps.sem, self.pt_ps.at(i))
            for q in (0, 1):
                ins = e.copy(self.pt[:, q].rearrange("p t h -> p (t h)"), PB[4 + q])
            ins.then_inc(self.pta_r.sem, 1)
            e.wait_ge(self.oT_ps.sem, self.oT_ps.at(i))
            if self.cross:
                e.activation(self.oT[:, :], PB[4], ACT.Identity, bias=w["bv"]).then_inc(self.oT_r.sem, 1)
            else:
                e.copy(self.oT[:, :], PB[4]).then_inc(self.oT_r.sem, 1)

    def tensor(self, e):
        PB, w, n = self.net.PB, self.w, self.net
        with e.Fori(0, self.iters) as i:
            self.transpose_xn(e, i, PB[0])
            if self.cross:
                e.wait_ge(self.ctx_l.sem, self.ctx_l.at(i))
                for j in range(4):
                    ins = e.transpose(PB[1][:, j * P:(j + 1) * P], self.ct[:, j, :], n.const("ident"))
                ins.then_inc(self.ctT_ps.sem, 1)
            e.wait_ge(self.xnT_r.sem, self.xnT_r.at(i))
            e.matmul(PB[4], w["wq"], self.xnT[:, :], start=True, stop=True)
            kv = self.xnT
            if self.cross:
                e.wait_ge(self.ctT_r.sem, self.ctT_r.at(i))
                kv = self.ctT
            e.matmul(PB[5], w["wk"], kv[:, :], start=True, stop=True)
            for j in range(4):
                ins = e.matmul(PB[6][:, j * P:(j + 1) * P], kv[:, j * P:(j + 1) * P], w["wv"], start=True, stop=True)
            ins.then_inc(self.qkv_ps.sem, 1)
            e.wait_ge(self.qx_r.sem, self.qx_r.at(i))
            e.wait_ge(self.kx_r.sem, self.kx_r.at(i))
            for b in range(16):
                ins = e.matmul(PB[b // 4][:, b % 4 * P:(b % 4 + 1) * P], self.qx[:, b].rearrange("p h s -> p (h s)"),
                               self.kx[:, b].rearrange("p c k -> p (c k)"), start=True, stop=True)
            ins.then_inc(self.s_ps.sem, 1)
            e.wait_ge(self.e_r.sem, self.e_r.at(i))
            for c in range(C):
                for t in range(4):
                    k = c * 16 + t * 4
                    ins = e.transpose(PB[4 + c][:, t * P:(t + 1) * P], self.e[:, k:k + 4, :].rearrange("p b k -> p (b k)"), n.const("ident"))
            ins.then_inc(self.pt_ps.sem, 1)
            e.wait_ge(self.pta_r.sem, self.pta_r.at(i))
            e.wait_ge(self.ptv_r.sem, self.ptv_r.at(i))
            e.wait_ge(self.vx_r.sem, self.vx_r.at(i))
            for t in range(4):
                for c in range(C):
                    ins = e.matmul(PB[t][:, c * P:(c + 1) * P], self.pt[:, c, t, :], self.vx[:, t, c].rearrange("p r j -> p (r j)"),
                                   start=True, stop=True)
            ins.then_inc(self.o_ps.sem, 1)
            e.wait_ge(self.o_r.sem, self.o_r.at(i))
            for t in range(4):
                for r in range(4):
                    b = 4 * t + r
                    ins = e.matmul(PB[4][:, b * S:(b + 1) * S], self.o[:, r, t, :], n.const("samequery"), start=True, stop=True)
            ins.then_inc(self.oT_ps.sem, 1)
            e.wait_ge(self.oT_r.sem, self.oT_r.at(i))
            self.project(e, PB[5], [self.oT[:, :]], [w["wo"]], w["bo"] if self.cross else None).then_inc(self.y_ps.sem, 1)

    def gpsimd(self, e):
        pass

    def sync(self, e):
        if self.cross:
            with e.Fori(0, self.iters) as i:
                e.wait_ge(self.res.sem, self.res.at(i, 0))
                for r in range(4):
                    src = self.net.ctx_dram[bass.ds(i * 16, 16), 0:S, :].rearrange("(t r) k d -> r k t d", r=4)[r]
                    e.dma_start(self.ct[32 * r:32 * r + 32], src).then_inc(self.ctx_l.sem, 16)


class L1Attn(SmallAttn):

    name = "L1_attn"


class L1Xattn(SmallAttn):

    name, cross, vsteps = "L1_xattn", True, 6


class L3Attn(Block):

    name = "L3_attn"
    vsteps = 7

    def plan(self):
        self.t = self.sb("t", [P, 4, 512])
        self.kr = self.sb("kr", [P, 512])
        self.qr = self.sb("qr", [P, 512])
        self.qm = self.sb("qm", [P, 2, 512])
        self.v = self.sb("v", [P, 4, 256])
        self.sg = self.sb("sg", [P, 2, 512])
        self.st = self.sb("st", [P, 4, 8, P])
        self.sq = self.sb("sq", [P, 2, 512])
        self.rt = self.sb("rt", [P, 2, 512])
        self.o = self.sb("o", [P, 2, 512])
        self.qk_ps = self.sig("hidden_in_psum")
        self.vg_ps = self.sig("value_gate_in_psum")
        self.v_r = self.sig("hidden_ready")
        self.sg_r = self.sig("silu_ready")
        self.q_r = self.sig("spread_ready")
        self.s_ps = self.sig("scores_in_psum", 4)
        self.st_r = self.sig("decayed_ready", 4)
        self.o_ps = self.sig("heads_in_psum")
        self.sq_r = self.sig("squares_summed")
        self.ms_ps = self.sig("meansquare_in_psum")
        self.rt_r = self.sig("root_ready")
        self.o_r = self.sig("heads_ready")
        self.y_ps = self.sig("y_in_psum")

    def vector(self, e):
        self.ln_vector(e)
        n, c, PS = self.net, self.chain, self.net.PS
        seqs = lambda b: b.rearrange("p (b s) -> p b s", s=S)
        table = lambda k: n.const(k).rearrange("p (o s) -> p o s", o=1).to_broadcast([P, 16, S])
        with e.Fori(0, self.iters) as i:
            c.start()
            self.norm(e, i)
            e.wait_ge(self.qk_ps.sem, self.qk_ps.at(i))
            for j, k in enumerate(("ropecos", "ropesin", "ropecos", "ropesin")):
                ins = e.tensor_tensor(seqs(self.t[:, j, :]), seqs(PS[:, 1 + j, :]), table(k), ALU.mult)
            ins.then_inc(c.sem, 1)
            e.wait_ge(c.sem, c.next(i))
            e.tensor_tensor(self.qr[:, :], self.t[:, 0, :], self.t[:, 1, :], ALU.add).then_inc(c.sem, 1)
            e.wait_ge(c.sem, c.next(i))
            e.tensor_tensor(self.kr[:, :], self.t[:, 2, :], self.t[:, 3, :], ALU.add).then_inc(c.sem, 1)
            e.wait_ge(c.sem, c.next(i))
            for h in range(2):
                ins = e.tensor_scalar(self.qm[:, h, :], self.qr[:, :], n.const("head2")[:, h:h + 1], None, ALU.mult)
            ins.then_inc(self.q_r.sem, 1)
            for j in range(4):
                e.wait_ge(self.s_ps.sem, self.s_ps.at(i, j + 1))
                b = 4 * (j % 2)
                e.tensor_tensor(self.st[:, j].rearrange("p (c h) q -> p c (h q)", h=2), PS[:, b:b + 4, 0:256],
                                n.const("decay").rearrange("p (c x) -> p c x", c=4), ALU.mult).then_inc(self.st_r.sem, 1)
            e.wait_ge(self.rt_r.sem, self.rt_r.at(i))
            e.reciprocal(self.rt[:], self.rt[:]).then_inc(c.sem, 1)
            e.wait_ge(c.sem, c.next(i))
            for j in range(2):
                ins = e.scalar_tensor_tensor(out=self.o[:, j, :], in0=PS[:, 4 + j, :], scalar=self.w["gn"], in1=self.rt[:, j, :],
                                             op0=ALU.mult, op1=ALU.mult)
                ins.then_inc(c.sem, 1)
                e.wait_ge(c.sem, c.next(i))
            e.wait_ge(self.sg_r.sem, self.sg_r.at(i))
            e.tensor_tensor(self.o[:], self.o[:], self.sg[:], ALU.mult).then_inc(self.o_r.sem, 1)
            self.add_residual(e, i, PS[:, 0, :].rearrange("p (j d) -> p j d", j=4), self.y_ps)
        c.done()

    def scalar(self, e):
        self.ln_scalar(e)
        PB, PS = self.net.PB, self.net.PS
        with e.Fori(0, self.iters) as i:
            self.copy_xnT(e, i, PB[0])
            e.wait_ge(self.vg_ps.sem, self.vg_ps.at(i))
            for j in range(2):
                ins = e.copy(self.v[:, 2 * j:2 * j + 2].rearrange("p a b -> p (a b)"), PB[5 + j])
            ins.then_inc(self.v_r.sem, 1)
            e.activation(self.sg[:, 0, :], PB[7], ACT.Silu)
            e.activation(self.sg[:, 1, :], PB[0], ACT.Silu).then_inc(self.sg_r.sem, 1)
            e.wait_ge(self.o_ps.sem, self.o_ps.at(i))
            e.activation(self.sq[:], PS[:, 4:6, :], ACT.Square).then_inc(self.sq_r.sem, 1)
            e.wait_ge(self.ms_ps.sem, self.ms_ps.at(i))
            e.activation(self.rt[:], PS[:, 6:8, :], ACT.Sqrt, bias=self.net.const("eps5")).then_inc(self.rt_r.sem, 1)

    def tensor(self, e):
        PB, w, n = self.net.PB, self.w, self.net
        with e.Fori(0, self.iters) as i:
            self.transpose_xn(e, i, PB[0])
            e.wait_ge(self.xnT_r.sem, self.xnT_r.at(i))
            for j, k in enumerate(("wq", "wqs", "wk", "wks")):
                ins = e.matmul(PB[1 + j], w[k], self.xnT[:, :], start=True, stop=True)
            ins.then_inc(self.qk_ps.sem, 1)
            for j in range(4):
                e.matmul(PB[5 + j // 2][:, (j % 2) * 256:(j % 2) * 256 + 256], self.xnT[:, j * P:(j + 1) * P], w["wv"], start=True, stop=True)
            e.matmul(PB[7], w["wg"][:, 0:P], self.xnT[:, :], start=True, stop=True)
            e.matmul(PB[0], w["wg"][:, P:2 * P], self.xnT[:, :], start=True, stop=True).then_inc(self.vg_ps.sem, 1)
            e.wait_ge(self.q_r.sem, self.q_r.at(i))
            e.wait_ge(self.sg_r.sem, self.sg_r.at(i))
            for j in range(4):
                if j >= 2:
                    e.wait_ge(self.st_r.sem, self.st_r.at(i, j - 1))
                t = slice(j * P, (j + 1) * P)
                for c in range(4):
                    r = slice(32 * c, 32 * c + 32)
                    for h in range(2):
                        ins = e.matmul(PB[4 * (j % 2) + c][:, h * P:(h + 1) * P], self.kr[r, t], self.qm[r, h, t], start=True, stop=True)
                ins.then_inc(self.s_ps.sem, 1)
            e.wait_ge(self.st_r.sem, self.st_r.at(i))
            for j in range(4):
                for h in range(8):
                    q = 32 * (h % 4)
                    ins = e.matmul(PB[4 + h // 4][q:q + 32, j * P:(j + 1) * P], self.v[:, j, 32 * h:32 * h + 32], self.st[:, j, h, :],
                                   start=True, stop=True)
            ins.then_inc(self.o_ps.sem, 1)
            e.wait_ge(self.sq_r.sem, self.sq_r.at(i))
            for j in range(2):
                ins = e.matmul(PB[6 + j], n.const("mean32"), self.sq[:, j, :], start=True, stop=True)
            ins.then_inc(self.ms_ps.sem, 1)
            e.wait_ge(self.o_r.sem, self.o_r.at(i))
            self.project(e, PB[0], [self.o[:, k, :] for k in range(2)], [w["wo"][:, k * P:(k + 1) * P] for k in range(2)])\
                .then_inc(self.y_ps.sem, 1)

    def gpsimd(self, e):
        pass

    def sync(self, e):
        pass


class Memory:

    ROWS = 4
    GROUPS = (T - 1) // ROWS
    W = 2 * D + 2 * H

    def __init__(self, net):
        n = self.ROWS
        self.net = net
        at, cols = net.where["L3_memory"]
        self.wbuf = net.sb("memory_weights", [P, cols])
        self.w = {k: self.wbuf[:, a:a + m] for k, (a, m) in at.items()}
        self.wkv = net.sb("memory_wkv", [P, self.W])
        self.bba = net.sb("memory_bba", [P, 2, H])
        self.rows = net.sb("memory_rows", [P, n, D])
        self.raw = net.sb("memory_raw", [P, n, self.W])
        self.kc = net.sb("memory_kc", [P, n, D])
        self.sq = net.sb("memory_sq", [P, n, D])
        self.ba = net.sb("memory_ba", [P, n, 2 * H])
        self.ss = net.sb("memory_ss", [P, 3, n * H])
        self.kb = net.sb("memory_kb", [P, n, D])
        self.vb = net.sb("memory_vb", [P, n, D])
        self.ab = net.sb("memory_ab", [P, n, H])
        self.M = net.sb("memory", [P, DH, H, DH])
        self.t1 = net.sb("memory_t1", [P, DH, H, DH])
        self.t2 = net.sb("memory_t2", [P, DH, H, 4])
        self.mk = net.sb("memory_mk", [P, DH, H])
        g = self.GROUPS + 1
        self.w_l = net.sig("memory_weights_loaded", 16, 1)
        self.w_ps = net.sig("memory_weights_in_psum", 1, 1)
        self.w_r = net.sig("memory_weights_ready", 1, 1)
        self.first_ps = net.sig("memory_first_row_in_psum", 2, 1)
        self.first_r = net.sig("memory_first_row_ready", 2, 1)
        self.rows_l = net.sig("memory_rows_loaded", 16, g)
        self.bx_r = net.sig("memory_gate_logits_ready", 1, g)
        self.ba_r = net.sig("memory_gate_exps_ready", 1, g)
        self.sq_r = net.sig("memory_squares_ready", 2, g)
        self.ms_r = net.sig("memory_meansquares_ready", 2, g)
        self.rt_r = net.sig("memory_roots_ready", 2, g)
        self.kn_r = net.sig("memory_keys_normed", 1, g)
        self.in_r = net.sig("memory_inputs_ready", 1, g)
        self.scan_r = net.sig("memory_scanned", 1, g)
        self.steps = Steps(net.sig("memory_steps", 9, g))
        self.m0_r = net.sig("memory_cleared", 1, 1)
        self.scan0 = Steps(net.sig("memory_scan_steps", 8 - 1, 1))
        self.scan = Steps(net.sig("memory_scan_steps", 8 * n - 1, self.GROUPS))

    def first_tensor(self, e):
        PB, w, n = self.net.PB, self.w, self.net
        e.wait_ge(self.w_l.sem, self.w_l.at(0))
        e.matmul(PB[7][:, 0:P], w["wk"], n.const("center8"), start=True, stop=True).then_inc(self.w_ps.sem, 1)
        e.wait_ge(self.rows_l.sem, self.rows_l.at(0))
        e.transpose(PB[0][:, 0:P], self.rows[:, 0, :], n.const("ident")).then_inc(self.first_ps.sem, 1)
        e.wait_ge(self.first_r.sem, self.first_r.at(0, 1))
        e.wait_ge(self.w_r.sem, self.w_r.at(0))
        e.matmul(PB[1][:, 0:self.W], self.kc[:, 0, :], self.wkv[:, :], start=True, stop=True).then_inc(self.first_ps.sem, 1)

    def first_scalar(self, e):
        w, n = self.w, self.net
        e.wait_ge(self.w_l.sem, self.w_l.at(0))
        e.wait_ge(self.w_ps.sem, self.w_ps.at(0))
        e.copy(self.wkv[:, 0:D], n.PB[7][:, 0:P])
        e.copy(self.wkv[:, D:2 * D], w["wv"])
        e.copy(self.wkv[:, 2 * D:2 * D + H], w["wb"])
        e.copy(self.bba[:, 0, :], w["bb"])
        e.copy(self.bba[:, 1, :], w["ba"])
        e.copy(self.wkv[:, 2 * D + H:self.W], w["wa"]).then_inc(self.w_r.sem, 1)
        e.wait_ge(self.first_ps.sem, self.first_ps.at(0, 1))
        e.copy(self.kc[:, 0, :], n.PB[0][:, 0:P]).then_inc(self.first_r.sem, 1)
        e.wait_ge(self.first_ps.sem, self.first_ps.at(0, 2))
        e.copy(self.raw[:, 0, :], n.PB[1][:, 0:self.W]).then_inc(self.first_r.sem, 1)
        self.gates_scalar(e, 0, 1)
        self.squares_scalar(e, 0, 1)
        self.units_scalar(e, 0, 1)

    def first_vector(self, e):
        self.steps.start()
        e.wait_ge(self.w_r.sem, self.w_r.at(0))
        e.wait_ge(self.first_r.sem, self.first_r.at(0, 2))
        self.gates_vector(e, 0, 1)
        self.stats_vector(e, 0, 1)
        self.normed_vector(e, 0, 1)
        self.units_vector(e, 0, 1)
        self.inputs_vector(e, 0, 1)

    def row_product(self, e, out, rowT):
        return e.matmul(out, rowT, self.wkv[:, :], start=True, stop=True)

    def gates_vector(self, e, g, n):
        e.tensor_tensor(self.ba[:, 0:n, :], self.raw[:, 0:n, 2 * D:self.W],
                        self.bba[:].rearrange("p (o two) h -> p o (two h)", o=1).to_broadcast([P, n, 2 * H]), ALU.add).then_inc(self.bx_r.sem, 1)

    def gates_scalar(self, e, g, n):
        e.wait_ge(self.bx_r.sem, self.bx_r.at(g))
        e.activation(self.ba[:, 0:n, :], self.ba[:, 0:n, :], ACT.Exp, scale=-1.0).then_inc(self.ba_r.sem, 1)

    def squares_scalar(self, e, g, n):
        e.activation(self.sq[:, 0:n, :], self.raw[:, 0:n, 0:D], ACT.Square).then_inc(self.sq_r.sem, 1)
        e.wait_ge(self.ms_r.sem, self.ms_r.at(g, 1))
        e.activation(self.ss[:, 1, 0:n * H], self.ss[:, 0, 0:n * H], ACT.Sqrt).then_inc(self.rt_r.sem, 1)

    def stats_vector(self, e, g, n):
        s, ss = self.steps, self.ss[:, :, 0:n * H]
        e.wait_ge(self.sq_r.sem, self.sq_r.at(g, 1))
        e.tensor_reduce(ss[:, 0, :], self.heads(self.sq, n), AX.X, ALU.add).then_inc(s.sem, 1)
        e.wait_ge(s.sem, s.next(g))
        e.tensor_scalar(ss[:, 0, :], ss[:, 0, :], 1.0 / DH, LN_EPS, ALU.mult, ALU.add).then_inc(self.ms_r.sem, 1)
        e.tensor_tensor(self.kc[:, 0:n, :], self.raw[:, 0:n, 0:D], self.every_row("gk", n), ALU.mult).then_inc(s.sem, 1)
        e.wait_ge(s.sem, s.next(g))

    def heads(self, t, n):
        return t[:, 0:n, :].rearrange("p t (h j) -> p (t h) j", j=DH)

    def every_head(self, t, n):
        return t.rearrange("p (n o) -> p n o", o=1).to_broadcast([P, n * H, DH])

    def every_row(self, name, n):
        return self.w[name].rearrange("p (o d) -> p o d", o=1).to_broadcast([P, n, D])

    def normed_vector(self, e, g, n):
        s, ss, ba = self.steps, self.ss[:, :, 0:n * H], self.ba[:, 0:n, :]
        e.wait_ge(self.rt_r.sem, self.rt_r.at(g, 1))
        e.reciprocal(ss[:, 2, :], ss[:, 1, :]).then_inc(s.sem, 1)
        e.wait_ge(s.sem, s.next(g))
        e.tensor_tensor(self.heads(self.kc, n), self.heads(self.kc, n), self.every_head(ss[:, 2, :], n), ALU.mult).then_inc(s.sem, 1)
        e.wait_ge(s.sem, s.next(g))
        e.tensor_tensor(self.kc[:, 0:n, :], self.kc[:, 0:n, :], self.every_row("bk", n), ALU.add).then_inc(self.kn_r.sem, 1)
        e.wait_ge(self.ba_r.sem, self.ba_r.at(g))
        e.tensor_scalar(ba, ba, 1.0, None, ALU.add).then_inc(s.sem, 1)
        e.wait_ge(s.sem, s.next(g))
        e.reciprocal(ba, ba).then_inc(s.sem, 1)
        e.wait_ge(s.sem, s.next(g))

    def units_scalar(self, e, g, n):
        e.wait_ge(self.kn_r.sem, self.kn_r.at(g))
        e.activation(self.sq[:, 0:n, :], self.kc[:, 0:n, :], ACT.Square).then_inc(self.sq_r.sem, 1)
        e.wait_ge(self.ms_r.sem, self.ms_r.at(g, 2))
        e.activation(self.ss[:, 1, 0:n * H], self.ss[:, 0, 0:n * H], ACT.Sqrt).then_inc(self.rt_r.sem, 1)

    def units_vector(self, e, g, n):
        s, ss = self.steps, self.ss[:, :, 0:n * H]
        e.wait_ge(self.sq_r.sem, self.sq_r.at(g, 2))
        e.tensor_reduce(ss[:, 0, :], self.heads(self.sq, n), AX.X, ALU.add).then_inc(self.ms_r.sem, 1)

    def inputs_vector(self, e, g, n):
        s, ss = self.steps, self.ss[:, :, 0:n * H]
        e.wait_ge(self.rt_r.sem, self.rt_r.at(g, 2))
        e.tensor_scalar(ss[:, 1, :], ss[:, 1, :], 1e-12, None, ALU.max).then_inc(s.sem, 1)
        e.wait_ge(s.sem, s.next(g))
        e.reciprocal(ss[:, 2, :], ss[:, 1, :]).then_inc(s.sem, 1)
        e.wait_ge(s.sem, s.next(g))
        if n > 1:
            e.wait_ge(self.scan_r.sem, self.scan_r.at(g, 0))
        e.tensor_tensor(self.heads(self.kb, n), self.heads(self.kc, n), self.every_head(ss[:, 2, :], n), ALU.mult).then_inc(s.sem, 1)
        e.wait_ge(s.sem, s.next(g))
        e.tensor_copy(self.ab[:, 0:n, :], self.ba[:, 0:n, H:2 * H])
        for t in range(n):
            ins = e.tensor_tensor(self.vb[:, t, :].rearrange("p (h j) -> p h j", j=DH), self.raw[:, t, D:2 * D].rearrange("p (h j) -> p h j", j=DH),
                                  self.ba[:, t, 0:H].rearrange("p (h o) -> p h o", o=1).to_broadcast([P, H, DH]), ALU.mult)
        ins.then_inc(self.in_r.sem, 1)

    def scan_pool(self, e, g, n, c, i):
        full = [P, DH, H, DH]
        c.start()
        e.wait_ge(self.in_r.sem, self.in_r.at(g))
        if n > 1:
            e.wait_ge(self.scan_r.sem, self.scan_r.at(g, 0))
        for t in range(n):
            k = self.kb[:, t, :].rearrange("p (o h j) -> p o h j", h=H, o=1).to_broadcast(full)
            a = self.ab[:, t, :].rearrange("p (o h) -> p o h", o=1).to_broadcast([P, DH, H])
            v = self.vb[:, t, :].rearrange("p (h i) -> p i h", h=H)
            e.tensor_tensor(self.t1[:], self.M[:], k, ALU.mult).then_inc(c.sem, 1)
            e.wait_ge(c.sem, c.next(i))
            e.tensor_tensor(self.t2[:], self.t1[:, :, :, 0:4], self.t1[:, :, :, 4:8], ALU.add).then_inc(c.sem, 1)
            e.wait_ge(c.sem, c.next(i))
            e.tensor_tensor(self.t1[:, :, :, 0:2], self.t2[:, :, :, 0:2], self.t2[:, :, :, 2:4], ALU.add).then_inc(c.sem, 1)
            e.wait_ge(c.sem, c.next(i))
            e.tensor_tensor(self.mk[:], self.t1[:, :, :, 0], self.t1[:, :, :, 1], ALU.add).then_inc(c.sem, 1)
            e.wait_ge(c.sem, c.next(i))
            e.tensor_tensor(self.mk[:], self.mk[:], a, ALU.mult).then_inc(c.sem, 1)
            e.wait_ge(c.sem, c.next(i))
            e.tensor_tensor(self.mk[:], v, self.mk[:], ALU.subtract).then_inc(c.sem, 1)
            e.wait_ge(c.sem, c.next(i))
            e.tensor_tensor(self.t1[:], self.mk[:].rearrange("p i (h o) -> p i h o", o=1).to_broadcast(full), k, ALU.mult).then_inc(c.sem, 1)
            e.wait_ge(c.sem, c.next(i))
            ins = e.tensor_tensor(self.M[:], self.M[:], self.t1[:], ALU.add)
            if t == n - 1:
                ins.then_inc(self.scan_r.sem, 1)
            else:
                ins.then_inc(c.sem, 1)
                e.wait_ge(c.sem, c.next(i))
        c.done()

    def first_pool(self, e):
        e.memset(self.M[:], 0.0).then_inc(self.m0_r.sem, 1)
        e.wait_ge(self.m0_r.sem, self.m0_r.at(0))
        self.scan_pool(e, 0, 1, self.scan0, 0)


class CrossAttn(Block):

    iters, group = TILES, 1
    KT = T // P

    def plan_common(self):
        self.qx = self.sb("qx", [P, SEQS, 16, S])
        self.cx = [self.sb(f"cx{b}", [P, self.KT, D]) for b in range(SEQS)]
        self.cT = [self.sb(f"cT{b}", [P, T + 1 + P]) for b in range(2)]
        self.mw = self.sb("maskwords", [P, T], U32)
        self.mb = self.sb("maskbias", [P, SEQS * T], BF16)
        self.onesb = self.sb("onesb", [P, P], BF16)
        self.e = [self.sb(f"e{k}", [P, 2, T]) for k in range(2)]
        self.pt = [self.sb(f"pt{k}", [P, self.KT, 2, P]) for k in range(2)]
        self.pl = [self.sb(f"pl{k}", [2, P]) for k in range(2)]
        self.nm = self.sb("negmax", [P, 8, 2])
        self.rs = self.sb("rowsum", [P, 8, 2])
        self.mask_l = self.sig("mask_loaded", 16)
        self.ones_r = self.sig("scaled_bias_ready", 1, 1)
        self.cx_l = [self.sig(f"context{b}_loaded", 16 * self.cx_dmas) for b in range(SEQS)]
        self.mb_r = self.sig("maskbias_ready")
        self.cT_ps = self.sig("ctxT_in_psum", 4)
        self.cT_r = self.sig("ctxT_ready", 4)
        self.s_ps = self.sig("scores_in_psum", 8)
        self.nm_r = self.sig("exponents_ready", 8)
        self.e_r = self.sig("exps_ready", 8)
        self.pt_ps = self.sig("probsT_in_psum", 8)
        self.pt_r = self.sig("probsT_low_ready", 8)
        self.o_ps = self.sig("heads_in_psum", 8)
        self.o_r = self.sig("heads_ready", 8)
        self.qx_r = self.sig("spread_ready")
        self.y_ps = self.sig("y_in_psum")
        self.mem = self.net.memory

    def maskbias(self, e, i):
        e.wait_ge(self.mask_l.sem, self.mask_l.at(i))
        m = self.mw[:, :].bitcast(U8)
        (s1, s2) = self.mask_ops
        e.tensor_scalar(self.mb[:, :], m, s1, s2, ALU.add, ALU.mult).then_inc(self.mb_r.sem, 1)

    def context_T(self, e, i, b):
        if b:
            self.bank6_free(e, i, b)
        e.wait_ge(self.cx_l[b].sem, self.cx_l[b].at(i))
        for k in range(self.KT):
            e.transpose(self.net.PB[6][:, k * P:(k + 1) * P], self.cx[b][:, k, :], self.net.const("ident"))
        if b == 0:
            e.wait_ge(self.mem.rows_l.sem, self.mem.rows_l.at(i + self.group0))
        e.transpose(self.net.PB[6][:, T + 1:T + 1 + P], self.mem.rows[:, b, :], self.net.const("ident"))
        e.matmul(self.net.PB[6][:, T - 1:T + 1], self.last_row(b), self.net.const("ones")[0:1, 0:2], start=True, stop=True)\
            .then_inc(self.cT_ps.sem, 1)

    def copy_context_T(self, e, i, b):
        e.wait_ge(self.cT_ps.sem, self.cT_ps.at(i, b + 1))
        if b >= 2:
            self.cT_free(e, i, b)
        e.copy(self.cT[b % 2][:, :], self.net.PB[6][:, 0:T + 1 + P]).then_inc(self.cT_r.sem, 1)

    def scores(self, e, i, u):
        b, half = u // 2, u % 2
        if u >= 2:
            e.wait_ge(self.pt_r.sem, self.pt_r.at(i, u - 1))
        for cc in range(2):
            c = 2 * half + cc
            bank = self.net.PB[2 * (u % 2) + cc][:, 0:T]
            r = self.mask_row(c)
            e.matmul(bank, self.onesb[r:r + 1, :], self.mb[r:r + 1, b * T:(b + 1) * T], start=True, stop=False)
            ins = self.score_product(e, bank, b, c)
        ins.then_inc(self.s_ps.sem, 1)

    def negmax(self, e, i, u):
        e.wait_ge(self.s_ps.sem, self.s_ps.at(i, u + 1))
        e.tensor_reduce(self.nm[:, u, :], self.net.PS[:, 2 * (u % 2):2 * (u % 2) + 2, 0:T], AX.X, ALU.max, negate=True)\
            .then_inc(self.nm_r.sem, 1)

    def exps(self, e, i, u):
        e.wait_ge(self.nm_r.sem, self.nm_r.at(i, u + 1))
        if u >= 2:
            e.wait_ge(self.pt_ps.sem, self.pt_ps.at(i, u - 1))
        for cc in range(2):
            ins = e.activation(self.e[u % 2][:, cc, :], self.net.PB[2 * (u % 2) + cc][:, 0:T], ACT.Exp, bias=self.nm[:, u, cc:cc + 1],
                               accum_out=self.rs[:, u, cc:cc + 1])
        ins.then_inc(self.e_r.sem, 1)

    def transposes(self, e, i, u):
        if u >= 2:
            e.wait_ge(self.pt_r.sem, self.pt_r.at(i, u - 1))
        for k in range(self.KT):
            for cc in range(2):
                a = (2 * k + cc) * P
                e.transpose(self.net.PB[4 + u % 2][:, a:a + P], self.e[u % 2][:, cc, k * P:(k + 1) * P], self.net.const("ident"))
        e.matmul(self.net.PB[2 * (u % 2)][0:2, 384:512], self.e[u % 2][:, :, T - 1:T].rearrange("p c o -> p (c o)"),
                 self.net.const("ident"), start=True, stop=True).then_inc(self.pt_ps.sem, 1)

    def copy_probs(self, e, i, u):
        e.wait_ge(self.pt_ps.sem, self.pt_ps.at(i, u + 1))
        if u >= 2:
            e.wait_ge(self.o_ps.sem, self.o_ps.at(i, u - 1))
        e.copy(self.pl[u % 2][:, :], self.net.PB[2 * (u % 2)][0:2, 384:512])
        e.copy(self.pt[u % 2][:].rearrange("p k c h -> p (k c h)"), self.net.PB[4 + u % 2]).then_inc(self.pt_r.sem, 1)

    def load_masks(self, e, i):
        e.dma_start(self.mw[:, :], self.mask[bass.ds(i, 1), :].to_broadcast([P, T])).then_inc(self.mask_l.sem, 16)

    def sync(self, e):
        e.wait_ge(self.res.sem, self.res.at(0, 0))
        e.wait_ge(self.ones_r.sem, self.ones_r.at(0))
        self.load_rows(e, 0)
        self.load_masks(e, 0)
        for b in range(SEQS):
            self.load(e, 0, b)
        with e.Fori(1, self.iters) as i:
            e.wait_ge(self.mb_r.sem, self.mb_r.at(i - 1))
            self.load_masks(e, i)
            for b in range(SEQS):
                self.slot_free(e, i - 1, b)
                self.load(e, i, b)
            self.load_rows(e, i)

    def load_rows(self, e, i):
        g = i + self.group0
        if self.group0 == 1 and isinstance(i, int) and i == 0:
            e.wait_ge(self.mem.first_ps.sem, self.mem.first_ps.at(0, 1))
        e.dma_start(self.mem.rows[:], self.net.ctx_dram[:, bass.ds(g * Memory.ROWS - (Memory.ROWS - 1), Memory.ROWS), :])\
            .then_inc(self.mem.rows_l.sem, 16)

    def gpsimd(self, e):
        with e.Fori(0, self.iters) as i:
            self.mem.scan_pool(e, i + self.group0, Memory.ROWS, self.mem.scan, i + (self.group0 - 1))


class L0Xattn(CrossAttn):

    name = "L0_xattn"
    vsteps = 9
    cx_dmas = 2
    group0 = 1
    mask_ops = (0.0, MASKED)

    def plan(self):
        self.mask = self.net.masks[0]
        self.plan_common()
        self.cl = self.sb("cl", [1, SEQS, D])
        self.bqs = self.sb("bqs", [P, 1])
        self.qT = self.sb("qT", [P, SEQS, S])
        self.kT = [self.sb(f"kT{b}", [P, T]) for b in range(2)]
        self.v = [self.sb(f"v{b}", [P, self.KT, D]) for b in range(2)]
        self.vl = [self.sb(f"vl{b}", [2, D]) for b in range(2)]
        self.rm = self.sb("rm", [P, 2, 2, 32])
        self.o = self.sb("o", [P, SEQS, C, 32])
        self.oT = self.sb("oT", [P, P])
        self.q_ps = self.sig("hidden_in_psum")
        self.q_r = self.sig("hidden_ready")
        self.kT_ps = self.sig("keysT_in_psum", 4)
        self.kT_r = self.sig("keysT_ready", 4)
        self.v_ps = self.sig("values_in_psum", 4)
        self.v_r = self.sig("values_ready", 4)
        self.rm_r = self.sig("reciprocals_ready", 8)
        self.oT_ps = self.sig("headsT_in_psum")
        self.oT_r = self.sig("headsT_ready")

    def mask_row(self, c):
        return 32 * c

    def bank6_free(self, e, i, b):
        e.wait_ge(self.v_r.sem, self.v_r.at(i, b))

    def cT_free(self, e, i, b):
        e.wait_ge(self.o_ps.sem, self.o_ps.at(i, 2 * b - 3))

    def last_row(self, b):
        return self.cl[0:1, b, :]

    def slot_free(self, e, i, b):
        e.wait_ge(self.cT_ps.sem, self.cT_ps.at(i, b + 1))

    def load(self, e, i, b):
        src = self.net.ctx_dram[bass.ds(i * SEQS + b, 1)]
        e.dma_start(self.cx[b][:], src[:, 0:self.KT * P, :].rearrange("o (k p) d -> p (o k) d", p=P)).then_inc(self.cx_l[b].sem, 16)
        e.dma_start(self.cl[0:1, b, :], src[:, T - 1, :]).then_inc(self.cx_l[b].sem, 16)

    def score_product(self, e, bank, b, c):
        r = slice(32 * c, 32 * c + 32)
        return e.matmul(bank, self.qx[r, b, 0:4, :].rearrange("p h s -> p (h s)"), self.kT[b % 2][r, :], start=False, stop=True)

    def keysT(self, e, i, b):
        e.wait_ge(self.cT_r.sem, self.cT_r.at(i, b + 1))
        e.matmul(self.net.PB[6][:, 0:T], self.w["wk"], self.cT[b % 2][:, 0:T], start=True, stop=True).then_inc(self.kT_ps.sem, 1)

    def values(self, e, i, b):
        e.wait_ge(self.kT_r.sem, self.kT_r.at(i, b + 1))
        for k in range(self.KT):
            e.matmul(self.net.PB[6][:, k * P:(k + 1) * P], self.cT[b % 2][:, k * P:(k + 1) * P], self.w["wv"], start=True, stop=True)
        e.matmul(self.net.PB[6][0:2, 2 * P:3 * P], self.cT[b % 2][:, T - 1:T + 1], self.w["wv"], start=True, stop=True)\
            .then_inc(self.v_ps.sem, 1)

    def heads(self, e, i, u):
        b, half = u // 2, u % 2
        e.wait_ge(self.pt_r.sem, self.pt_r.at(i, u + 1))
        if half == 0:
            e.wait_ge(self.v_r.sem, self.v_r.at(i, b + 1))
        if u:
            e.wait_ge(self.o_r.sem, self.o_r.at(i, u))
        for cc in range(2):
            f = slice(32 * (2 * half + cc), 32 * (2 * half + cc) + 32)
            o = self.net.PB[7][:, 32 * cc:32 * cc + 32]
            for k in range(self.KT):
                e.matmul(o, self.pt[u % 2][:, k, cc, :], self.v[b % 2][:, k, f], start=(k == 0), stop=False)
            ins = e.matmul(o, self.pl[u % 2][0:2, :], self.vl[b % 2][0:2, f], start=False, stop=True)
        if half == 0:
            ins = self.mem.row_product(e, self.net.PB[7][:, 64:64 + Memory.W], self.cT[b % 2][:, T + 1:T + 1 + P])
        ins.then_inc(self.o_ps.sem, 1)

    def tensor(self, e):
        PB, w, n = self.net.PB, self.w, self.net
        self.mem.first_tensor(e)
        with e.Fori(0, self.iters) as i:
            self.transpose_xn(e, i, PB[7])
            self.context_T(e, i, 0)
            self.keysT(e, i, 0)
            e.wait_ge(self.xnT_r.sem, self.xnT_r.at(i))
            e.matmul(PB[7][:, 0:P], w["wq"], self.xnT[:, :], start=True, stop=True).then_inc(self.q_ps.sem, 1)
            self.values(e, i, 0)
            e.wait_ge(self.qx_r.sem, self.qx_r.at(i))
            e.wait_ge(self.mb_r.sem, self.mb_r.at(i))
            self.scores(e, i, 0)
            for u in range(8):
                b, half = u // 2, u % 2
                if half == 0 and b < 3:
                    self.context_T(e, i, b + 1)
                if half == 1 and b < 3:
                    self.values(e, i, b + 1)
                if u + 1 < 8:
                    self.scores(e, i, u + 1)
                e.wait_ge(self.e_r.sem, self.e_r.at(i, u + 1))
                self.transposes(e, i, u)
                if half == 0 and b < 3:
                    self.keysT(e, i, b + 1)
                if u:
                    self.heads(e, i, u - 1)
            self.heads(e, i, 7)
            e.wait_ge(self.o_r.sem, self.o_r.at(i))
            for b in range(SEQS):
                ins = e.matmul(PB[7][:, b * S:(b + 1) * S], self.o[:, b].rearrange("p c j -> p (c j)"), n.const("samequery"), start=True, stop=True)
            ins.then_inc(self.oT_ps.sem, 1)
            e.wait_ge(self.oT_r.sem, self.oT_r.at(i))
            self.project(e, PB[7], [self.oT[:, :]], [w["wo"]], w["bo"], tiles=1).then_inc(self.y_ps.sem, 1)

    def scalar(self, e):
        self.ln_scalar(e)
        PB, w = self.net.PB, self.w
        e.mul(self.bqs[:, :], w["bq"], QSCALE)
        e.copy(self.onesb[:, :], self.net.const("ones")).then_inc(self.ones_r.sem, 1)
        e.wait_ge(self.ones_r.sem, self.ones_r.at(0))

        def keys(i, b):
            e.wait_ge(self.kT_ps.sem, self.kT_ps.at(i, b + 1))
            if b >= 2:
                e.wait_ge(self.s_ps.sem, self.s_ps.at(i, 2 * b - 2))
            e.activation(self.kT[b % 2][:, :], PB[6][:, 0:T], ACT.Identity, bias=w["bk"]).then_inc(self.kT_r.sem, 1)

        m = self.mem
        m.first_scalar(e)
        with e.Fori(0, self.iters) as i:
            g = i + self.group0
            self.copy_xnT(e, i, PB[7])
            self.copy_context_T(e, i, 0)
            keys(i, 0)
            e.wait_ge(self.q_ps.sem, self.q_ps.at(i))
            e.activation(self.qT[:].rearrange("p b s -> p (b s)"), PB[7][:, 0:P], ACT.Identity, bias=self.bqs[:, :], scale=QSCALE)\
                .then_inc(self.q_r.sem, 1)
            for u in range(8):
                b, half = u // 2, u % 2
                self.exps(e, i, u)
                if u == 7:
                    m.gates_scalar(e, g, m.ROWS)
                if half == 0 and b < 3:
                    self.copy_context_T(e, i, b + 1)
                self.copy_probs(e, i, u)
                if half == 0 and b < 3:
                    keys(i, b + 1)
                if u == 7:
                    m.squares_scalar(e, g, m.ROWS)
            e.wait_ge(self.oT_ps.sem, self.oT_ps.at(i))
            e.activation(self.oT[:, :], PB[7][:, 0:P], ACT.Identity, bias=w["bv"]).then_inc(self.oT_r.sem, 1)
            m.units_scalar(e, g, m.ROWS)

    def vector(self, e):
        self.ln_vector(e)
        n, c, PB = self.net, self.chain, self.net.PB

        def values(i, b):
            e.wait_ge(self.v_ps.sem, self.v_ps.at(i, b + 1))
            if b >= 2:
                e.wait_ge(self.o_ps.sem, self.o_ps.at(i, 2 * b - 2))
            e.tensor_copy(self.v[b % 2][:].rearrange("p k d -> p (k d)"), PB[6][:, 0:2 * P])
            e.tensor_tensor(self.vl[b % 2][:, :], PB[6][0:2, 2 * P:3 * P], n.const("rowquarter")[0:2, :], ALU.mult).then_inc(self.v_r.sem, 1)

        def normalise(i, u):
            b, half = u // 2, u % 2
            e.wait_ge(self.rm_r.sem, self.rm_r.at(i, u + 1))
            e.wait_ge(self.o_ps.sem, self.o_ps.at(i, u + 1))
            if half == 0:
                e.tensor_copy(self.mem.raw[:, b, :], PB[7][:, 64:64 + Memory.W])
            e.tensor_tensor(self.o[:, b, 2 * half:2 * half + 2], PB[7][:, 0:64].rearrange("p (c j) -> p c j", c=2), self.rm[:, u % 2], ALU.mult)\
                .then_inc(self.o_r.sem, 1)

        m = self.mem
        m.first_vector(e)
        with e.Fori(0, self.iters) as i:
            g = i + self.group0
            c.start()
            m.steps.start()
            self.norm(e, i)
            self.maskbias(e, i)
            values(i, 0)
            e.wait_ge(self.q_r.sem, self.q_r.at(i))
            e.tensor_tensor(self.qx[:, :, 0:4, :], self.qT[:].rearrange("p b (o s) -> p b o s", o=1).to_broadcast([P, SEQS, 4, S]),
                            n.const("head4").rearrange("p (a h b) -> p a h b", a=1, b=1).to_broadcast([P, SEQS, 4, S]), ALU.mult)\
                .then_inc(self.qx_r.sem, 1)
            self.negmax(e, i, 0)
            for u in range(8):
                if u % 2 == 1 and u < 7:
                    values(i, u // 2 + 1)
                if u + 1 < 8:
                    self.negmax(e, i, u + 1)
                if u:
                    normalise(i, u - 1)
                if u == 7:
                    e.wait_ge(self.o_r.sem, self.o_r.at(i, 7))
                    m.gates_vector(e, g, m.ROWS)
                e.wait_ge(self.e_r.sem, self.e_r.at(i, u + 1))
                e.reciprocal(self.rs[:, u, :], self.rs[:, u, :]).then_inc(c.sem, 1)
                e.wait_ge(c.sem, c.next(i))
                e.tensor_tensor(self.rm[:, u % 2], self.rs[:, u, :].rearrange("p (c o) -> p c o", o=1).to_broadcast([P, 2, 32]),
                                n.const("odiag").rearrange("p (a j) -> p a j", a=1).to_broadcast([P, 2, 32]), ALU.mult).then_inc(self.rm_r.sem, 1)
            m.stats_vector(e, g, m.ROWS)
            normalise(i, 7)
            m.normed_vector(e, g, m.ROWS)
            self.add_residual(e, i, PB[7][:, 0:P].rearrange("p (j d) -> p j d", j=1), self.y_ps)
            m.units_vector(e, g, m.ROWS)
            m.inputs_vector(e, g, m.ROWS)
            m.steps.done()
        c.done()

    def gpsimd(self, e):
        self.mem.first_pool(e)
        super().gpsimd(e)


class L2Xattn(CrossAttn):

    name = "L2_xattn"
    vsteps = 9
    cx_dmas = 3
    group0 = 1 + TILES
    mask_ops = (-1.0, -MASKED)

    def plan(self):
        self.mask = self.net.masks[1]
        self.plan_common()
        self.A = self.sb("wqk", [P, 16 * P])
        self.WVO = self.sb("wvo", [P, 16 * P])
        self.cl = [self.sb(f"cl{b}", [2, 2, D]) for b in range(SEQS)]
        self.oT = self.sb("oT", [P, 16, P])
        self.w_ps = self.sig("weights_product_in_psum", 1, 1)
        self.w_r = self.sig("weights_product_ready", 1, 1)
        self.cl_r = self.sig("last_rows_cleared", 1, 1)
        self.q_ps = self.sig("hidden_in_psum")
        self.qa_r = self.sig("hidden_ready")
        self.p_r = self.sig("activated_ready", 8)
        self.row_ps = self.sig("memory_row_in_psum", 4)
        self.row_r = self.sig("memory_row_ready", 4)

    def mask_row(self, c):
        return 0

    def bank6_free(self, e, i, b):
        e.wait_ge(self.cT_r.sem, self.cT_r.at(i, b))
        if b >= 2:
            e.wait_ge(self.row_r.sem, self.row_r.at(i, b - 1))

    def cT_free(self, e, i, b):
        e.wait_ge(self.s_ps.sem, self.s_ps.at(i, 2 * b - 2))
        e.wait_ge(self.row_ps.sem, self.row_ps.at(i, b - 1))

    def last_row(self, b):
        return self.cl[b][0:1, 0, :]

    def slot_free(self, e, i, b):
        e.wait_ge(self.o_ps.sem, self.o_ps.at(i, 2 * b + 2))

    def load(self, e, i, b):
        src = self.net.ctx_dram[bass.ds(i * SEQS + b, 1)]
        e.dma_start(self.cx[b][:], src[:, 0:self.KT * P, :].rearrange("o (k p) d -> p (o k) d", p=P)).then_inc(self.cx_l[b].sem, 16)
        for c in range(2):
            e.dma_start(self.cl[b][c:c + 1, c, :], src[:, T - 1, :]).then_inc(self.cx_l[b].sem, 16)

    def score_product(self, e, bank, b, c):
        return e.matmul(bank, self.qx[:, b, 4 * c:4 * c + 4, :].rearrange("p h s -> p (h s)"), self.cT[b % 2][:, 0:T], start=False, stop=True)

    def heads(self, e, i, u):
        b = u // 2
        e.wait_ge(self.pt_r.sem, self.pt_r.at(i, u + 1))
        if u:
            e.wait_ge(self.o_r.sem, self.o_r.at(i, u))
        o = self.net.PB[7]
        block = lambda k, **f: e.matmul(o[:, 0:2 * P], self.cx[b][:, k, :], self.pt[u % 2][:, k].rearrange("p c h -> p (c h)"), **f)
        block(0, start=True, stop=False)
        for cc in range(2):
            e.matmul(o[:, cc * P:(cc + 1) * P], self.cl[b][0:2, cc, :], self.pl[u % 2][0:2, :], start=False, stop=False, skip_group_check=True)
        ins = block(1, start=False, stop=True)
        ins.then_inc(self.o_ps.sem, 1)

    def tensor(self, e):
        PB, w, n = self.net.PB, self.w, self.net
        for h in range(16):
            a = slice(h * P, (h + 1) * P)
            o = slice(h % 4 * P, (h % 4 + 1) * P)
            e.matmul(PB[h // 4][:, o], w["wq"][0:64, a], w["wk"][0:64, a], start=True, stop=True)
            ins = e.matmul(PB[4 + h // 4][:, o], w["wv"][0:64, a], w["wo"][0:64, a], start=True, stop=True)
        ins.then_inc(self.w_ps.sem, 1)
        e.wait_ge(self.w_r.sem, self.w_r.at(0))
        with e.Fori(0, self.iters) as i:
            self.transpose_xn(e, i, PB[7])
            self.context_T(e, i, 0)
            e.wait_ge(self.xnT_r.sem, self.xnT_r.at(i))
            for h in range(16):
                ins = e.matmul(PB[h // 4][:, h % 4 * P:(h % 4 + 1) * P], self.A[:, h * P:(h + 1) * P], self.xnT[:, :], start=True, stop=True)
            ins.then_inc(self.q_ps.sem, 1)
            e.wait_ge(self.qx_r.sem, self.qx_r.at(i))
            e.wait_ge(self.qa_r.sem, self.qa_r.at(i))
            e.wait_ge(self.mb_r.sem, self.mb_r.at(i))
            e.wait_ge(self.cT_r.sem, self.cT_r.at(i, 1))
            self.scores(e, i, 0)
            for u in range(8):
                b, half = u // 2, u % 2
                if half == 0 and b < 3:
                    self.context_T(e, i, b + 1)
                if half == 1 and b < 3:
                    e.wait_ge(self.cT_r.sem, self.cT_r.at(i, b + 2))
                if half == 1:
                    self.mem.row_product(e, PB[6][:, 0:Memory.W], self.cT[b % 2][:, T + 1:T + 1 + P]).then_inc(self.row_ps.sem, 1)
                if u + 1 < 8:
                    self.scores(e, i, u + 1)
                e.wait_ge(self.p_r.sem, self.p_r.at(i, u + 1))
                self.transposes(e, i, u)
                if u:
                    self.heads(e, i, u - 1)
            self.heads(e, i, 7)
            e.wait_ge(self.o_r.sem, self.o_r.at(i))
            o = PB[7][:, 0:P]
            e.matmul(o, n.const("ones")[0:1, :], w["bo"][0:1, :], start=True, stop=False)
            for h in range(16):
                ins = e.matmul(o, self.oT[:, h, :], self.WVO[:, h * P:(h + 1) * P], start=False, stop=(h == 15))
            ins.then_inc(self.y_ps.sem, 1)

    def spread_q(self, e, i, k):
        src = self.net.PB[k].rearrange("p (h b s) -> p b h s", h=4, b=SEQS)
        f = e.copy if k < 2 else e.tensor_copy
        return f(self.qx[:, :, 4 * k:4 * k + 4, :], src)

    def scalar(self, e):
        self.ln_scalar(e)
        PB = self.net.PB
        e.wait_ge(self.w_ps.sem, self.w_ps.at(0))
        for k in range(4):
            a = slice(k * 512, (k + 1) * 512)
            e.mul(self.A[:, a], PB[k], 0.125)
            ins = e.copy(self.WVO[:, a], PB[4 + k])
        ins.then_inc(self.w_r.sem, 1)
        e.copy(self.onesb[:, :], self.net.const("ones")).then_inc(self.ones_r.sem, 1)
        m = self.mem
        with e.Fori(0, self.iters) as i:
            g = i + self.group0
            self.copy_xnT(e, i, PB[7])
            self.copy_context_T(e, i, 0)
            e.wait_ge(self.q_ps.sem, self.q_ps.at(i))
            self.spread_q(e, i, 0)
            self.spread_q(e, i, 1).then_inc(self.qa_r.sem, 1)
            for u in range(8):
                b, half = u // 2, u % 2
                self.exps(e, i, u)
                if u == 7:
                    m.gates_scalar(e, g, m.ROWS)
                if half == 0 and b < 3:
                    self.copy_context_T(e, i, b + 1)
                self.copy_probs(e, i, u)
            m.squares_scalar(e, g, m.ROWS)
            m.units_scalar(e, g, m.ROWS)

    def vector(self, e):
        self.ln_vector(e)
        n, c, PB = self.net, self.chain, self.net.PB
        for b in range(SEQS):
            ins = e.memset(self.cl[b][:], 0.0)
        ins.then_inc(self.cl_r.sem, 1)

        def copy_heads(i, u):
            b, half = u // 2, u % 2
            e.wait_ge(self.o_ps.sem, self.o_ps.at(i, u + 1))
            e.tensor_copy(self.oT[:, 8 * half:8 * half + 8, b * S:(b + 1) * S], PB[7][:, 0:2 * P].rearrange("p (h s) -> p h s", s=S))\
                .then_inc(self.o_r.sem, 1)

        m = self.mem
        with e.Fori(0, self.iters) as i:
            g = i + self.group0
            c.start()
            m.steps.start()
            self.norm(e, i)
            self.maskbias(e, i)
            e.wait_ge(self.q_ps.sem, self.q_ps.at(i))
            self.spread_q(e, i, 2)
            self.spread_q(e, i, 3).then_inc(self.qx_r.sem, 1)
            self.negmax(e, i, 0)
            for u in range(8):
                if u + 1 < 8:
                    self.negmax(e, i, u + 1)
                if u % 2:
                    e.wait_ge(self.row_ps.sem, self.row_ps.at(i, u // 2 + 1))
                    e.tensor_copy(m.raw[:, u // 2, :], PB[6][:, 0:Memory.W]).then_inc(self.row_r.sem, 1)
                if u == 7:
                    e.wait_ge(self.row_r.sem, self.row_r.at(i, 4))
                    m.gates_vector(e, g, m.ROWS)
                e.wait_ge(self.e_r.sem, self.e_r.at(i, u + 1))
                e.reciprocal(self.rs[:, u, :], self.rs[:, u, :]).then_inc(c.sem, 1)
                e.wait_ge(c.sem, c.next(i))
                for cc in range(2):
                    ins = e.tensor_scalar(self.e[u % 2][:, cc, :], self.e[u % 2][:, cc, :], self.rs[:, u, cc:cc + 1], None, ALU.mult)
                ins.then_inc(self.p_r.sem, 1)
                if u:
                    copy_heads(i, u - 1)
            m.stats_vector(e, g, m.ROWS)
            copy_heads(i, 7)
            m.normed_vector(e, g, m.ROWS)
            self.add_residual(e, i, PB[7][:, 0:P].rearrange("p (j d) -> p j d", j=1), self.y_ps)
            m.units_vector(e, g, m.ROWS)
            m.inputs_vector(e, g, m.ROWS)
            m.steps.done()
        c.done()

    def sync(self, e):
        e.wait_ge(self.cl_r.sem, self.cl_r.at(0))
        super().sync(e)


class L3Xattn(Block):

    name = "L3_xattn"
    vsteps = 5

    def plan(self):
        self.wqc = self.sb("wqc", [P, P])
        self.ss = self.sb("ss", [P, 3, 4 * H])
        self.MT = self.sb("MT", [P, DH, P])
        self.Mbd = self.sb("Mbd", [P, 16, H, DH])
        self.qc = self.sb("qc", [P, 4, D])
        self.qn = self.sb("qn", [P, 4, D])
        self.qT = self.sb("qT", [P, 512])
        self.oT = self.sb("oT", [P, 512])
        self.w_ps = self.sig("weights_product_in_psum", 1, 1)
        self.w_r = self.sig("weights_product_ready", 1, 1)
        self.MT_ps = self.sig("heads_in_psum", 1, 1)
        self.MT_r = self.sig("heads_ready", 1, 1)
        self.q_ps = self.sig("hidden_in_psum")
        self.qsq_r = self.sig("silu_ready")
        self.qms_r = self.sig("logits_ready")
        self.qrt_r = self.sig("probs_ready")
        self.qn_r = self.sig("spread_ready")
        self.qT_ps = self.sig("probsT_in_psum")
        self.qT_r = self.sig("probsT_low_ready")
        self.mbd_r = self.sig("expert_added")
        self.o_ps = self.sig("headsT_in_psum")
        self.oT_r = self.sig("headsT_ready")
        self.y_ps = self.sig("y_in_psum")

    def gpsimd(self, e):
        pass

    def sync(self, e):
        pass

    def tensor(self, e):
        PB, w, n = self.net.PB, self.w, self.net
        e.matmul(PB[7][:, 0:P], w["wq"], n.const("center8"), start=True, stop=True).then_inc(self.w_ps.sem, 1)
        m = n.memory
        e.wait_ge(m.scan_r.sem, m.scan_r.at(m.GROUPS))
        for k in range(DH):
            ins = e.transpose(PB[1 + k // 4][:, k % 4 * P:(k % 4 + 1) * P], m.M[:, k].rearrange("p h j -> p (h j)"), n.const("ident"))
        ins.then_inc(self.MT_ps.sem, 1)
        e.wait_ge(self.w_r.sem, self.w_r.at(0))
        with e.Fori(0, self.iters) as i:
            self.transpose_xn(e, i, PB[0])
            e.wait_ge(self.xnT_r.sem, self.xnT_r.at(i))
            for j in range(4):
                ins = e.matmul(PB[3][:, j * P:(j + 1) * P], self.xnT[:, j * P:(j + 1) * P], self.wqc[:, :], start=True, stop=True)
            ins.then_inc(self.q_ps.sem, 1)
            e.wait_ge(self.qn_r.sem, self.qn_r.at(i))
            for j in range(4):
                ins = e.transpose(PB[4][:, j * P:(j + 1) * P], self.qn[:, j, :], n.const("ident"))
            ins.then_inc(self.qT_ps.sem, 1)
            e.wait_ge(self.qT_r.sem, self.qT_r.at(i))
            e.wait_ge(self.mbd_r.sem, self.mbd_r.at(i))
            for b in range(16):
                ins = e.matmul(PB[5][:, b * S:(b + 1) * S], self.Mbd[:, b].rearrange("p h i -> p (h i)"), self.qT[:, b * S:(b + 1) * S],
                               start=True, stop=True)
            ins.then_inc(self.o_ps.sem, 1)
            e.wait_ge(self.oT_r.sem, self.oT_r.at(i))
            self.project(e, PB[6], [self.oT[:, :]], [w["wo"]], w["bo"]).then_inc(self.y_ps.sem, 1)

    def scalar(self, e):
        self.ln_scalar(e)
        n, w, PS = self.net, self.w, self.net.PS
        e.wait_ge(self.w_ps.sem, self.w_ps.at(0))
        e.copy(self.wqc[:, :], PS[:, 7, 0:P]).then_inc(self.w_r.sem, 1)
        e.wait_ge(self.MT_ps.sem, self.MT_ps.at(0))
        for k in range(2):
            ins = e.copy(self.MT[:, 4 * k:4 * k + 4, :].rearrange("p i b -> p (i b)"), n.PB[1 + k])
        ins.then_inc(self.MT_r.sem, 1)
        with e.Fori(0, self.iters) as i:
            self.copy_xnT(e, i, n.PB[0])
            e.wait_ge(self.q_ps.sem, self.q_ps.at(i))
            e.activation(self.qn[:].rearrange("p j d -> p (j d)"), n.PB[3], ACT.Square).then_inc(self.qsq_r.sem, 1)
            e.wait_ge(self.qms_r.sem, self.qms_r.at(i))
            e.activation(self.ss[:, 1, :], self.ss[:, 0, :], ACT.Sqrt).then_inc(self.qrt_r.sem, 1)
            e.wait_ge(self.qT_ps.sem, self.qT_ps.at(i))
            e.copy(self.qT[:, :], n.PB[4]).then_inc(self.qT_r.sem, 1)
            e.wait_ge(self.o_ps.sem, self.o_ps.at(i))
            e.copy(self.oT[:, :], n.PB[5]).then_inc(self.oT_r.sem, 1)

    def vector(self, e):
        self.ln_vector(e)
        n, w, PS, c = self.net, self.w, self.net.PS, self.chain
        e.wait_ge(self.MT_r.sem, self.MT_r.at(0))
        heads = lambda a: a.rearrange("p t (h j) -> p (t h) j", j=DH)
        wide = lambda a: a.rearrange("p (n o) -> p n o", o=1).to_broadcast([P, 4 * H, DH])
        rows = lambda a: a.rearrange("p (o d) -> p o d", o=1).to_broadcast([P, 4, D])
        with e.Fori(0, self.iters) as i:
            c.start()
            self.norm(e, i)
            for h in range(2):
                ins = e.tensor_tensor(self.Mbd[:, 8 * h:8 * h + 8], self.MT[:, :, bass.ds(i * 16 + 8 * h, 8)].rearrange("p i (b o) -> p b o i", o=1).to_broadcast([P, 8, H, DH]),
                                      n.const("headcol").rearrange("p (a h b) -> p a h b", a=1, b=1).to_broadcast([P, 8, H, DH]), ALU.mult)
            ins.then_inc(self.mbd_r.sem, 1)
            e.wait_ge(self.qsq_r.sem, self.qsq_r.at(i))
            e.tensor_reduce(self.ss[:, 0, :], heads(self.qn[:]), AX.X, ALU.add).then_inc(c.sem, 1)
            e.wait_ge(c.sem, c.next(i))
            e.tensor_scalar(self.ss[:, 0, :], self.ss[:, 0, :], 1.0 / DH, LN_EPS, ALU.mult, ALU.add).then_inc(self.qms_r.sem, 1)
            e.tensor_tensor(self.qc[:], PS[:, 3, :].rearrange("p (j d) -> p j d", j=4), rows(w["gq"]), ALU.mult).then_inc(c.sem, 1)
            e.wait_ge(c.sem, c.next(i))
            e.wait_ge(self.qrt_r.sem, self.qrt_r.at(i))
            e.reciprocal(self.ss[:, 2, :], self.ss[:, 1, :]).then_inc(c.sem, 1)
            e.wait_ge(c.sem, c.next(i))
            e.tensor_tensor(heads(self.qc[:]), heads(self.qc[:]), wide(self.ss[:, 2, :]), ALU.mult).then_inc(c.sem, 1)
            e.wait_ge(c.sem, c.next(i))
            e.tensor_tensor(self.qn[:], self.qc[:], rows(w["bq"]), ALU.add).then_inc(self.qn_r.sem, 1)
            self.add_residual(e, i, PS[:, 6, :].rearrange("p (j d) -> p j d", j=4), self.y_ps)
        c.done()


BLOCKS = [L0Ffn, L0Attn, L2Attn, L1Ffn, L2Ffn, L3Ffn, L1Attn, L1Xattn, L3Attn, L0Xattn, L2Xattn, L3Xattn]


def build(nc, x, context, mask0, mask1, consts, consts_at, wdram, where, out, names):
    blocks = {c.name: c for c in BLOCKS}
    with ExitStack() as ctx:
        net = Net(nc, ctx, wdram, where, consts_at, context, (mask0, mask1))
        loaded = net.sig("x_loaded", 16, 2)
        first = net.sig("residual_added", 1)
        stored = net.sig("output_stored", 16)
        net.memory = Memory(net)
        layers = [blocks[n](net, i) for i, n in enumerate(names)]
        xd = x.rearrange("(t p) d -> p t d", p=P)
        od = out.rearrange("(t p) d -> p t d", p=P)
        block = ctx.enter_context(nc.Block())

        @block.sync
        def _(e):
            e.dma_start(net.X[:], xd).then_inc(loaded.sem, 16)
            e.dma_start(net.K[:], consts).then_inc(loaded.sem, 16)
            m = net.memory
            e.dma_start(m.wbuf[:], wdram["L3_memory"]).then_inc(m.w_l.sem, 16)
            e.dma_start(m.rows[:, 0:1, :], context[:, 0:1, :]).then_inc(m.rows_l.sem, 16)
            for i, l in enumerate(layers):
                if i >= 1:
                    e.wait_ge(layers[i - 1].res.sem, layers[i - 1].res.at(0, 0))
                n = where[l.name][1]
                e.dma_start(net.W[i % 2][:, 0:n], wdram[l.name]).then_inc(l.weights.sem, 16)
                l.sync(e)
            last = layers[-1].res
            e.wait_ge(last.sem, last.at(layers[-1].iters - 1))
            e.dma_start(od, net.X[:]).then_inc(stored.sem, 16)
            e.wait_ge(stored.sem, stored.at(0))

        @block.vector
        def _(e):
            e.wait_ge(loaded.sem, loaded.at(1))
            for t in range(TILES):
                ins = e.bn_stats(net.stats[:, t, :], net.X[:, t, :])
            ins.then_inc(first.sem, 1)
            for l in layers:
                l.vector(e)

        @block.scalar
        def _(e):
            e.wait_ge(loaded.sem, loaded.at(1))
            for l in layers:
                l.scalar(e)

        @block.tensor
        def _(e):
            e.wait_ge(loaded.sem, loaded.at(1))
            for l in layers:
                e.wait_ge(l.res.sem, l.res.at(0, 0))
                e.wait_ge(l.weights.sem, l.weights.at(0))
                l.tensor(e)

        @block.gpsimd
        def _(e):
            e.wait_ge(loaded.sem, loaded.at(1))
            for l in layers:
                l.gpsimd(e)


NAMES = ["L0_xattn", "L0_attn", "L0_ffn", "L1_xattn", "L1_attn", "L1_ffn",
         "L2_xattn", "L2_attn", "L2_ffn", "L3_xattn", "L3_attn", "L3_ffn"]


def kernel(**inputs):
    import concourse.bacc as bacc
    from concourse.bass_utils import run_bass_kernel_spmd

    names = NAMES
    nc = bacc.Bacc("TRN2", target_bir_lowering=False, num_devices=1)
    a = {k: np.asarray(v) for k, v in inputs.items()}
    consts, consts_at = constants()
    arrays = {"x": a["x"].reshape(B * S, D), "context": a["ctx_1024"], "consts": consts,
              "mask0": a["mask_BxS2_bk0"].reshape(TILES, -1).view(np.uint32), "mask1": a["mask_BxS2_bf1"].reshape(TILES, -1).view(np.uint32)}
    parts = layouts(a)
    where = {k: columns(v) for k, v in parts.items()}
    for k in names + ["L3_memory"]:
        arrays["w_" + k] = np.concatenate([np.asarray(w) for _, w in parts[k]], 1)
    arrays = {k: np.ascontiguousarray(v) for k, v in arrays.items()}
    d = {k: nc.dram_tensor("in_" + k, v.shape, mybir.dt.from_np(v.dtype), kind="ExternalInput").ap() for k, v in arrays.items()}
    out = nc.dram_tensor("out", (B * S, D), F32, kind="ExternalOutput").ap()
    build(nc, d["x"], d["context"], d["mask0"], d["mask1"], d["consts"], consts_at,
          {k: d["w_" + k] for k in names + ["L3_memory"]}, {k: where[k] for k in names + ["L3_memory"]}, out, names)
    r = run_bass_kernel_spmd(nc, [{"in_" + k: v for k, v in arrays.items()}], core_ids=[0])
    return r.results[0]["out"].reshape(B, S, D)
```

```python
from contextlib import ExitStack

import numpy as np

import concourse.bass as bass
from concourse import mybir

F32 = mybir.dt.float32
BF16 = mybir.dt.bfloat16
U8 = mybir.dt.uint8
U32 = mybir.dt.uint32
ALU = mybir.AluOpType
ACT = mybir.ActivationFunctionType
AX = mybir.AxisListType

B, S, D = 128, 32, 128
T = 257
P = 128
TILES = B * S // P
SEQS = P // S
G = TILES // 4
H = 16
DH = D // H
C = 4
LN_EPS = 1e-5
MASKED = -float(2 ** 100)


class Signal:

    def __init__(self, sem):
        self.sem, self.total = sem, 0

    def use(self, per, iters):
        u = Use(self.sem, self.total, per)
        self.total += per * iters
        return u


class Use:

    def __init__(self, sem, base, per):
        self.sem, self.base, self.per = sem, base, per

    def at(self, i, k=None):
        return i * self.per + (self.base + (self.per if k is None else k))


class Steps:

    def __init__(self, use):
        self.u, self.sem, self.n = use, use.sem, 0

    def start(self):
        self.n = 0

    def next(self, i=0):
        self.n += 1
        return self.u.at(i, self.n)

    def done(self):
        assert self.n == self.u.per, ("steps", self.n, self.u.per)


def constants():
    p = np.arange(P)
    c = {}
    c["ident"] = np.eye(P)
    c["head4"] = (p[:, None] % 32 // 8 == np.arange(4)[None, :])
    c["odiag"] = (np.arange(32)[None, :] // 8 == p[:, None] // 32)
    c["samequery"] = (p[:, None] % 32 == np.arange(32)[None, :])
    c["causal"] = np.where(np.arange(32)[None, :] > p[:, None] % 32, MASKED, 0.0)
    c["seqmean"] = (p[:, None] // 32 == np.arange(4)[None, :]) / 32.0
    c["ones"] = np.ones((P, P))
    freq = 1.0 / 10000.0 ** (np.arange(0, 16, 2, dtype=np.float32) / 16)
    ang = (np.arange(S, dtype=np.float32)[None, :] * freq[p % 16 // 2][:, None].astype(np.float32))
    c["ropecos"] = np.cos(ang)
    c["ropesin"] = np.where(p % 2 == 0, -1.0, 1.0)[:, None] * np.sin(ang)
    s = np.log2(1.0 - np.exp2(-5.0 - np.arange(8)))
    diff = (p[None, :] - p[:, None])
    keep = (diff >= 0) & (p[None, :] // 32 == p[:, None] // 32)
    c["decay"] = np.concatenate([np.where(keep, np.exp2(np.where(keep, diff, 0) * s[h]), 0.0) for h in range(8)], 1) * 0.25
    c["head2"] = (p[:, None] % 32 // 16 == np.arange(2)[None, :])
    c["mean32"] = (p[:, None] // 32 == p[None, :] // 32) / 32.0
    c["exp2rows"] = np.concatenate([(p[:, None] == 2 * j + p[None, :] // 64) for j in range(4)], 1)
    c["iota14"] = np.broadcast_to(np.arange(14), (P, 14))
    c["quarter"] = (p[:, None] // 32 == np.arange(4)[None, :])
    c["rowquarter"] = (p[:, None] == p[None, :] // 32 % 2)
    c["center8"] = np.eye(P) - (p[:, None] // 8 == p[None, :] // 8) / 8.0
    c["headcol"] = (p[:, None] // 8 == np.arange(16)[None, :])
    c["eps8"] = np.full((P, 1), 1e-8)
    c["eps5"] = np.full((P, 1), 1e-5)
    c["ones33"] = np.broadcast_to(np.where(np.arange(33) == 0, 0.0, 1.0), (P, 33))
    out, at, n = [], {}, 0
    for k, v in c.items():
        v = np.asarray(v, np.float32)
        at[k] = (n, v.shape[1])
        n += v.shape[1]
        out.append(v)
    return np.ascontiguousarray(np.concatenate(out, 1)), at


def rows(w, k):
    n = w.shape[1]
    return w.reshape(k, P, n).transpose(1, 0, 2).reshape(P, k * n)


def bc(v):
    return np.broadcast_to(np.asarray(v).reshape(1, -1), (P, v.size))


def cols(v):
    return np.asarray(v).reshape(-1, P).T


def pad(w):
    out = np.zeros((P, w.shape[1]), w.dtype)
    out[:w.shape[0]] = w
    return out


def layouts(a):
    L = {}
    L["L0_xattn"] = [("wq", a["L0_xattn_W_Q"]), ("wk", a["L0_xattn_W_K"]), ("wv", a["L0_xattn_W_V"]),
                     ("wo", a["L0_xattn_W_O"]), ("bq", cols(a["L0_xattn_b_Q"])), ("bk", cols(a["L0_xattn_b_K"])),
                     ("bv", cols(a["L0_xattn_b_V"])), ("bo", bc(a["L0_xattn_b_O"]))]
    L["L0_attn"] = [("ln1", cols(a["L0_attn_ln1_w"])), ("ln2", cols(a["L0_attn_ln2_w"])), ("ap", cols(a["L0_attn_a_param"])),
                    ("win", a["L0_attn_w_in"].T), ("wgate", a["L0_attn_w_gate"].T), ("wa", rows(a["L0_attn_w_a"].T, 2)),
                    ("wout", rows(a["L0_attn_w_out"].T, 2)), ("wmg", a["L0_attn_w_mlp_gate"].T),
                    ("wmu", a["L0_attn_w_mlp_up"].T), ("wmd", rows(a["L0_attn_w_mlp_down"].T, 4))]
    L["L0_ffn"] = [("w1", a["L0_ffn_W1"]), ("b1", cols(a["L0_ffn_b1"])), ("theta", cols(a["L0_ffn_quantum_phases"])),
                   ("wr", cols(a["L0_ffn_quantum_weights_real"])), ("wi", cols(a["L0_ffn_quantum_weights_imag"])),
                   ("w2", rows(a["L0_ffn_W2"], 4)), ("b2", bc(a["L0_ffn_b2"]))]
    L["L1_xattn"] = [("wq", a["L1_xattn_Wq"].T), ("wk", a["L1_xattn_Wk"].T), ("wv", a["L1_xattn_Wv"].T),
                     ("wo", a["L1_xattn_Wo"].T), ("bq", cols(a["L1_xattn_bq"])), ("bk", cols(a["L1_xattn_bk"])),
                     ("bv", cols(a["L1_xattn_bv"])), ("bo", bc(a["L1_xattn_bo"]))]
    L["L1_attn"] = [("wq", a["L1_attn_W_q"]), ("wk", np.tile(a["L1_attn_W_k"], (1, H))),
                    ("wv", np.tile(a["L1_attn_W_v"], (1, H))), ("wo", a["L1_attn_W_o"])]
    L["L1_ffn"] = [("gate", a["L1_ffn_gate_w"].T), ("down", a["L1_ffn_down_w"].reshape(512, D).T),
                   ("bd", cols(a["L1_ffn_down_b"].reshape(-1))),
                   ("up", rows(a["L1_ffn_up_w"].transpose(0, 2, 1).reshape(512, D), 4)), ("bu", pad(a["L1_ffn_up_b"]))]
    wq, wk = (a[f"L2_xattn_W{n}"].reshape(D, 16, 64).transpose(2, 1, 0).reshape(64, -1) for n in "qk")
    wv = a["L2_xattn_Wv"].reshape(D, 16, 64).transpose(2, 1, 0).reshape(64, -1)
    wo = a["L2_xattn_Wo"].reshape(16, 64, D).transpose(1, 0, 2).reshape(64, -1)
    L["L2_xattn"] = [("wq", pad(wq)), ("wk", pad(wk)), ("wv", pad(wv)), ("wo", pad(wo)), ("bo", bc(a["L2_xattn_bo"]))]
    L["L2_attn"] = [("td", cols(a["L2_attn_time_decay"])), ("tf", cols(a["L2_attn_time_first"])),
                    ("mk", cols(a["L2_attn_time_mix_k"])), ("mv", cols(a["L2_attn_time_mix_v"])),
                    ("mr", cols(a["L2_attn_time_mix_r"])), ("wk", a["L2_attn_Wk"].T), ("wv", a["L2_attn_Wv"].T),
                    ("wr", a["L2_attn_Wr"].T), ("wo", a["L2_attn_Wo"].T)]
    L["L2_ffn"] = [("gate", a["L2_ffn_gate_w"].T), ("w1", a["L2_ffn_w1"].transpose(1, 0, 2).reshape(D, -1)),
                   ("b1", cols(a["L2_ffn_b1"].reshape(-1))), ("w2", rows(a["L2_ffn_w2"].reshape(-1, D), 28)),
                   ("b2", pad(a["L2_ffn_b2"]))]
    L["L3_memory"] = [("wk", a["L3_xattn_Wk"]), ("wv", a["L3_xattn_Wv"].T), ("wb", a["L3_xattn_Wbeta"].T),
                      ("wa", a["L3_xattn_Walpha"].T), ("bb", bc(a["L3_xattn_bbeta"])), ("ba", bc(a["L3_xattn_balpha"])),
                      ("gk", bc(np.tile(a["L3_xattn_gk"], H))), ("bk", bc(np.tile(a["L3_xattn_bk"], H)))]
    L["L3_xattn"] = [("wq", a["L3_xattn_Wq"]), ("wo", a["L3_xattn_Wo"].T), ("bo", bc(a["L3_xattn_bo"])),
                     ("gq", bc(np.tile(a["L3_xattn_gq"], H))), ("bq", bc(np.tile(a["L3_xattn_bq"], H)))]
    swap = np.arange(D) ^ 1
    L["L3_attn"] = [("wq", a["L3_attn_Wq"]), ("wk", a["L3_attn_Wk"]), ("wqs", a["L3_attn_Wq"][:, swap]),
                    ("wks", a["L3_attn_Wk"][:, swap]), ("wv", a["L3_attn_Wv"]), ("wg", a["L3_attn_Wg"]),
                    ("wo", rows(a["L3_attn_Wo"], 2)), ("gn", cols(np.tile(a["L3_attn_g_norm_w"], 4)))]
    L["L3_ffn"] = [("gate", a["L3_ffn_router_w"].T), ("wg", a["L3_ffn_w_gate"].reshape(-1, D).T),
                   ("wu", a["L3_ffn_w_up"].reshape(-1, D).T),
                   ("wd", rows(a["L3_ffn_w_down"].transpose(0, 2, 1).reshape(-1, D), 16))]
    return L


def columns(parts):
    at, n = {}, 0
    for name, w in parts:
        at[name] = (n, w.shape[1])
        n += w.shape[1]
    return at, n


class Net:

    def __init__(self, nc, ctx, wdram, where, consts_at, ctx_dram, masks):
        self.nc, self.ctx, self.wdram, self.where = nc, ctx, wdram, where
        self.ctx_dram, self.masks = ctx_dram, masks
        self.signals = {}
        self.X = self.sb("x", [P, TILES, D])
        self.stats = self.sb("stats", [P, TILES, 6])
        self.mean = self.sb("mean", [P, TILES])
        self.rstd = self.sb("rstd", [P, TILES])
        self.lntmp = self.sb("lntmp", [P, 4, TILES])
        nconst = max(a + n for a, n in consts_at.values())
        self.K = self.sb("consts", [P, nconst])
        self.consts_at = consts_at
        self.W = [self.sb(f"w{i}", [P, max(n for _, n in where.values())]) for i in range(2)]
        self.PS = ctx.enter_context(nc.psum_tensor("banks", [P, 8, 512], F32))
        self.PB = [self.PS[:, i, :] for i in range(8)]
        self.index = {}

    def sb(self, name, shape, dt=F32, ctx=None):
        return (ctx or self.ctx).enter_context(self.nc.sbuf_tensor(name, shape, dt))

    def const(self, name):
        a, n = self.consts_at[name]
        return self.K[:, a:a + n]

    def sig(self, name, per=1, iters=1):
        if name not in self.signals:
            self.signals[name] = Signal(self.ctx.enter_context(self.nc.semaphore(name)))
        return self.signals[name].use(per, iters)


class Block:

    iters, group, name = G, 4, None
    vsteps = 0

    def __init__(self, net, index):
        self.net, self.index = net, index
        at, _ = net.where[self.name]
        wbuf = net.W[index % 2]
        self.w = {k: wbuf[:, a:a + n] for k, (a, n) in at.items()}
        self.scratch = ExitStack()
        self.weights = net.sig(f"weights_loaded_{("even", "odd")[index % 2]}", 16)
        self.lnchain = Steps(net.sig("layernorm_steps", 7))
        self.var = net.sig("variance_ready")
        self.std = net.sig("std_ready")
        self.setup_chain = Steps(net.sig("setup_steps", self.setup_steps))
        self.chain = Steps(net.sig("vector_steps", self.vsteps, self.iters))
        self.xn_r = net.sig("xn_ready", 1, self.iters)
        if self.whole_xnT:
            self.xnT_ps = net.sig("xnT_in_psum", 1, self.iters)
            self.xnT_r = net.sig("xnT_ready", 1, self.iters)
        self.res = net.sig("residual_added", 1, self.iters)
        self.xn = self.sb("xn", [P, self.group, D])
        self.xnT = self.sb("xnT", [P, self.group * P])
        self.plan()
        self.scratch.close()

    setup_steps = 0
    whole_xnT = True

    def sb(self, name, shape, dt=F32):
        return self.net.sb(f"{self.name}_{name}", shape, dt, self.scratch)

    def sig(self, name, per=1, iters=None):
        return self.net.sig(name, per, self.iters if iters is None else iters)

    def ln_vector(self, e):
        n = self.net
        e.wait_ge(self.weights.sem, self.weights.at(0))
        e.wait_ge(self.res.sem, self.res.at(0, 0))
        st, c = n.stats, self.lnchain
        me, ve, mo, vo = (st[:, :, j] for j in (1, 2, 4, 5))
        t = n.lntmp
        c.start()
        e.tensor_tensor(t[:, 0, :], me, mo, ALU.add).then_inc(c.sem, 1)
        e.wait_ge(c.sem, c.next())
        e.tensor_scalar(n.mean[:, :], t[:, 0, :], 0.5, None, ALU.mult).then_inc(c.sem, 1)
        e.wait_ge(c.sem, c.next())
        e.tensor_tensor(t[:, 1, :], me, mo, ALU.subtract).then_inc(c.sem, 1)
        e.wait_ge(c.sem, c.next())
        e.scalar_tensor_tensor(out=t[:, 2, :], in0=t[:, 1, :], scalar=32.0, in1=t[:, 1, :], op0=ALU.mult, op1=ALU.mult).then_inc(c.sem, 1)
        e.wait_ge(c.sem, c.next())
        e.tensor_tensor(t[:, 3, :], ve, vo, ALU.add).then_inc(c.sem, 1)
        e.wait_ge(c.sem, c.next())
        e.tensor_tensor(t[:, 0, :], t[:, 3, :], t[:, 2, :], ALU.add).then_inc(c.sem, 1)
        e.wait_ge(c.sem, c.next())
        e.tensor_scalar(t[:, 1, :], t[:, 0, :], 1.0 / D, LN_EPS, ALU.mult, ALU.add).then_inc(self.var.sem, 1)
        e.wait_ge(self.std.sem, self.std.at(0))
        e.reciprocal(n.rstd[:, :], t[:, 2, :]).then_inc(c.sem, 1)
        e.wait_ge(c.sem, c.next())
        c.done()

    def ln_scalar(self, e):
        e.wait_ge(self.weights.sem, self.weights.at(0))
        e.wait_ge(self.var.sem, self.var.at(0))
        e.activation(self.net.lntmp[:, 2, :], self.net.lntmp[:, 1, :], ACT.Sqrt).then_inc(self.std.sem, 1)

    def norm(self, e, i):
        n = self.net
        e.wait_ge(self.res.sem, self.res.at(0, 0))
        for j in range(self.group):
            t = i * self.group + j
            ins = e.tensor_scalar(self.xn[:, j, :], n.X[:, bass.ds(t, 1), :], n.mean[:, bass.ds(t, 1)], n.rstd[:, bass.ds(t, 1)],
                                  ALU.subtract, ALU.mult)
        ins.then_inc(self.xn_r.sem, 1)

    def transpose_xn(self, e, i, bank):
        e.wait_ge(self.xn_r.sem, self.xn_r.at(i))
        for j in range(self.group):
            ins = e.transpose(bank[:, j * P:(j + 1) * P], self.xn[:, j, :], self.net.const("ident"))
        ins.then_inc(self.xnT_ps.sem, 1)

    def copy_xnT(self, e, i, bank):
        e.wait_ge(self.xnT_ps.sem, self.xnT_ps.at(i))
        e.copy(self.xnT[:, :], bank[:, 0:self.group * P]).then_inc(self.xnT_r.sem, 1)

    def add_residual(self, e, i, y, ready):
        n = self.net
        g = self.group
        e.wait_ge(ready.sem, ready.at(i))
        xs = n.X[:, bass.ds(i * g, g), :]
        e.tensor_tensor(xs, y, xs, ALU.add).then_inc(self.chain.sem, 1)
        e.wait_ge(self.chain.sem, self.chain.next(i))
        for j in range(g):
            ins = e.bn_stats(n.stats[:, bass.ds(i * g + j, 1), :], n.X[:, bass.ds(i * g + j, 1), :])
        ins.then_inc(self.res.sem, 1)

    def project(self, e, bank, lhs, w, bias=None, tiles=4):
        for j in range(tiles):
            o = bank[:, j * P:(j + 1) * P]
            if bias is not None:
                e.matmul(o, self.net.const("ones")[0:1, :], bias[0:1, :], start=True, stop=False)
            for k in range(len(lhs)):
                ins = e.matmul(o, lhs[k][:, j * P:(j + 1) * P], w[k], start=(k == 0 and bias is None), stop=(k == len(lhs) - 1))
        return ins


TWO_PI = 6.283185307179586
PI_IN = 3.1415925
ROUND = 12582912.0
PI_HI = 6.28125
PI_LO = TWO_PI - PI_HI


class L0Ffn(Block):

    name = "L0_ffn"
    vsteps = 7
    setup_steps = 13

    def plan(self):
        self.hid = self.sb("hid", [P, 4, 512])
        self.arg = self.sb("arg", [P, 4, 512])
        self.tmp = self.sb("tmp", [P, 4, 512])
        self.f = self.sb("features", [P, 8, 4])
        self.angles = self.sig("angles_ready", 1, 1)
        self.sines = self.sig("sines_ready", 1, 1)
        self.hid_ps = self.sig("hidden_in_psum")
        self.hid_r = self.sig("hidden_ready")
        self.arg_r = self.sig("argument_ready")
        self.sin_r = self.sig("sine_ready")
        self.act_r = self.sig("activated_ready")
        self.y_ps = self.sig("y_in_psum")

    def vector(self, e):
        self.ln_vector(e)
        w, f, c = self.w, self.f, self.setup_chain
        k, th, co, cf = f[:, 0, :], f[:, 1, :], f[:, 2, :], f[:, 7, :]
        e.tensor_scalar(k, w["theta"], 1 / TWO_PI, ROUND, ALU.mult, ALU.add).then_inc(c.sem, 1)
        e.wait_ge(c.sem, c.next())
        e.tensor_scalar(k, k, ROUND, None, ALU.subtract).then_inc(c.sem, 1)
        e.wait_ge(c.sem, c.next())
        e.scalar_tensor_tensor(out=th, in0=k, scalar=-PI_HI, in1=w["theta"], op0=ALU.mult, op1=ALU.add).then_inc(c.sem, 1)
        e.wait_ge(c.sem, c.next())
        e.scalar_tensor_tensor(out=th, in0=k, scalar=-PI_LO, in1=th, op0=ALU.mult, op1=ALU.add).then_inc(c.sem, 1)
        e.wait_ge(c.sem, c.next())
        e.tensor_scalar(th, th, PI_IN, -PI_IN, ALU.min, ALU.max).then_inc(c.sem, 1)
        e.wait_ge(c.sem, c.next())
        e.tensor_scalar(co, th, TWO_PI / 4, None, ALU.add).then_inc(c.sem, 1)
        e.wait_ge(c.sem, c.next())
        e.tensor_scalar(k, co, TWO_PI / 2, -TWO_PI, ALU.is_gt, ALU.mult).then_inc(c.sem, 1)
        e.wait_ge(c.sem, c.next())
        e.tensor_tensor(co, co, k, ALU.add).then_inc(c.sem, 1)
        e.wait_ge(c.sem, c.next())
        e.tensor_scalar(co, co, PI_IN, -PI_IN, ALU.min, ALU.max).then_inc(c.sem, 1)
        e.wait_ge(c.sem, c.next())
        e.tensor_copy(k, th).then_inc(self.angles.sem, 1)
        e.wait_ge(self.sines.sem, self.sines.at(0))
        e.tensor_tensor(f[:, 5, :], f[:, 4, :], w["wr"], ALU.mult).then_inc(c.sem, 1)
        e.wait_ge(c.sem, c.next())
        e.tensor_tensor(f[:, 6, :], f[:, 3, :], w["wi"], ALU.mult).then_inc(c.sem, 1)
        e.wait_ge(c.sem, c.next())
        e.tensor_tensor(f[:, 5, :], f[:, 5, :], f[:, 6, :], ALU.add).then_inc(c.sem, 1)
        e.wait_ge(c.sem, c.next())
        e.scalar_tensor_tensor(out=cf, in0=f[:, 5, :], scalar=0.1, in1=w["wi"], op0=ALU.mult, op1=ALU.mult).then_inc(c.sem, 1)
        e.wait_ge(c.sem, c.next())
        c.done()
        def group(i, last):
            self.chain.start()
            if not last:
                e.wait_ge(self.xnT_ps.sem, self.xnT_ps.at(i))
                self.norm(e, i + 1)
            e.wait_ge(self.hid_r.sem, self.hid_r.at(i))
            for j in range(4):
                ins = e.tensor_scalar(self.arg[:, j, :], self.hid[:, j, :], 0.1, th[:, j:j + 1], ALU.mult, ALU.add)
            ins.then_inc(self.chain.sem, 1)
            e.wait_ge(self.chain.sem, self.chain.next(i))
            e.tensor_scalar(self.tmp[:], self.arg[:], 1 / TWO_PI, ROUND, ALU.mult, ALU.add).then_inc(self.chain.sem, 1)
            e.wait_ge(self.chain.sem, self.chain.next(i))
            e.tensor_scalar(self.tmp[:], self.tmp[:], ROUND, -TWO_PI, ALU.subtract, ALU.mult).then_inc(self.chain.sem, 1)
            e.wait_ge(self.chain.sem, self.chain.next(i))
            e.tensor_tensor(self.arg[:], self.arg[:], self.tmp[:], ALU.add).then_inc(self.chain.sem, 1)
            e.wait_ge(self.chain.sem, self.chain.next(i))
            e.tensor_scalar(self.arg[:], self.arg[:], PI_IN, -PI_IN, ALU.min, ALU.max).then_inc(self.arg_r.sem, 1)
            e.wait_ge(self.sin_r.sem, self.sin_r.at(i))
            for j in range(4):
                ins = e.scalar_tensor_tensor(out=self.hid[:, j, :], in0=self.tmp[:, j, :], scalar=cf[:, j:j + 1],
                                             in1=self.hid[:, j, :], op0=ALU.mult, op1=ALU.add)
                if j == 2:
                    ins.then_inc(self.chain.sem, 1)
                    e.wait_ge(self.chain.sem, self.chain.next(i))
            ins.then_inc(self.chain.sem, 1)
            e.wait_ge(self.chain.sem, self.chain.next(i))
            e.tensor_scalar(self.arg[:], self.hid[:], 0.0, None, ALU.max).then_inc(self.act_r.sem, 1)
            self.add_residual(e, i, self.net.PB[5][:, :].rearrange("p (j d) -> p j d", j=4), self.y_ps)
            self.chain.done()

        self.norm(e, 0)
        with e.Fori(0, self.iters - 1) as i:
            group(i, False)
        group(self.iters - 1, True)

    def scalar(self, e):
        self.ln_scalar(e)
        f = self.f
        e.wait_ge(self.angles.sem, self.angles.at(0))
        e.activation(f[:, 3, :], f[:, 1, :], ACT.Sin)
        e.activation(f[:, 4, :], f[:, 2, :], ACT.Sin).then_inc(self.sines.sem, 1)
        def group(i, last):
            e.wait_ge(self.hid_ps.sem, self.hid_ps.at(i))
            for j in range(4):
                ins = e.activation(self.hid[:, j, :], self.net.PB[1 + j][:, :], ACT.Identity, bias=self.w["b1"][:, j:j + 1])
            ins.then_inc(self.hid_r.sem, 1)
            e.wait_ge(self.arg_r.sem, self.arg_r.at(i))
            e.activation(self.tmp[:], self.arg[:], ACT.Sin).then_inc(self.sin_r.sem, 1)
            if not last:
                self.copy_xnT(e, i + 1, self.net.PB[0])

        self.copy_xnT(e, 0, self.net.PB[0])
        with e.Fori(0, self.iters - 1) as i:
            group(i, False)
        group(self.iters - 1, True)

    def tensor(self, e):
        w, n = self.w, self.net
        e.wait_ge(self.weights.sem, self.weights.at(0))
        def group(i, last):
            e.wait_ge(self.xnT_r.sem, self.xnT_r.at(i))
            for j in range(4):
                ins = e.matmul(n.PB[1 + j][:, :], w["w1"][:, j * P:(j + 1) * P], self.xnT[:, :], start=True, stop=True)
            ins.then_inc(self.hid_ps.sem, 1)
            if not last:
                self.transpose_xn(e, i + 1, n.PB[0])
            e.wait_ge(self.act_r.sem, self.act_r.at(i))
            self.project(e, n.PB[5], [self.arg[:, k, :] for k in range(4)], [w["w2"][:, k * P:(k + 1) * P] for k in range(4)],
                         w["b2"]).then_inc(self.y_ps.sem, 1)

        self.transpose_xn(e, 0, n.PB[0])
        with e.Fori(0, self.iters - 1) as i:
            group(i, False)
        group(self.iters - 1, True)

    def gpsimd(self, e):
        pass

    def sync(self, e):
        pass


class L0Attn(Block):

    name = "L0_attn"
    whole_xnT = False
    vsteps = 12

    def plan(self):
        self.ms = self.sb("meansquare", [P, 2, 3, 4])
        self.sq = self.sb("squares", [P, 4, D])
        self.hn = self.sb("hn", [P, 4, D])
        self.hT = self.sb("hT", [P, 512])
        self.xin = self.sb("xin", [P, 2, 512])
        self.gate = self.sb("gate", [P, 2, 512])
        self.a = self.sb("decay", [P, 2, 512])
        self.t = self.sb("t", [P, 2, 512])
        self.y = self.sb("y", [P, 2, 512])
        self.x2 = self.sb("x2", [P, 4, D])
        self.sg = self.sb("sg", [P, 4, 512])
        self.m = self.sb("m", [P, 4, 512])
        self.rms1 = Steps(self.sig("rms_steps"))
        self.sq_r = self.sig("squares_summed", 2)
        self.ms_r = self.sig("meansquare_ready", 2)
        self.rt_r = self.sig("root_ready", 2)
        self.hn_r = self.sig("rms_normed", 2)
        self.x2_r = self.sig("x2_ready")
        self.hT_ps = self.sig("rms_in_psum", 2)
        self.hT_r = self.sig("rms_transposed", 2)
        self.in_ps = self.sig("hidden_in_psum")
        self.xin_r = self.sig("xin_ready")
        self.gate_r = self.sig("gate_ready")
        self.a_ps = self.sig("decay_in_psum")
        self.a_r = self.sig("decay_ready")
        self.t_r = self.sig("one_minus_square_ready")
        self.rest_r = self.sig("complement_ready")
        self.y_r = self.sig("activated_ready")
        self.wo_ps = self.sig("recurrence_in_psum")
        self.mlp_ps = self.sig("mlp_in_psum")
        self.sg_r = self.sig("mlp_sigmoid_ready")
        self.m_r = self.sig("mlp_hidden_ready")
        self.y_ps = self.sig("y_in_psum")

    def rms_vector(self, e, i, k, src):
        m, c = self.ms[:, k - 1], self.rms1 if k == 1 else self.chain
        if k == 1:
            c.start()
        e.wait_ge(self.sq_r.sem, self.sq_r.at(i, k))
        e.tensor_scalar(m[:, 1, :], m[:, 0, :], 1.0 / D, 1e-6, ALU.mult, ALU.add).then_inc(self.ms_r.sem, 1)
        e.wait_ge(self.rt_r.sem, self.rt_r.at(i, k))
        e.reciprocal(m[:, 2, :], m[:, 2, :]).then_inc(c.sem, 1)
        e.wait_ge(c.sem, c.next(i))
        for j in range(4):
            ins = e.tensor_scalar(self.hn[:, j, :], src[:, j, :], m[:, 2, j:j + 1], None, ALU.mult)
        ins.then_inc(self.hn_r.sem, 1)

    def rms_scalar(self, e, i, k, src, ln, bank, ready):
        m = self.ms[:, k - 1]
        e.wait_ge(ready.sem, ready.at(i))
        for j in range(4):
            ins = e.activation(self.sq[:, j, :], src[:, j, :], ACT.Square, accum_out=m[:, 0, j:j + 1])
        ins.then_inc(self.sq_r.sem, 1)
        e.wait_ge(self.ms_r.sem, self.ms_r.at(i, k))
        e.activation(m[:, 2, :], m[:, 1, :], ACT.Sqrt).then_inc(self.rt_r.sem, 1)
        e.wait_ge(self.hT_ps.sem, self.hT_ps.at(i, k))
        e.activation(self.hT[:, :], bank[:, :], ACT.Copy, scale=ln).then_inc(self.hT_r.sem, 1)

    def rms_tensor(self, e, i, k, bank):
        e.wait_ge(self.hn_r.sem, self.hn_r.at(i, k))
        for j in range(4):
            ins = e.transpose(bank[:, j * P:(j + 1) * P], self.hn[:, j, :], self.net.const("ident"))
        ins.then_inc(self.hT_ps.sem, 1)
        e.wait_ge(self.hT_r.sem, self.hT_r.at(i, k))

    def vector(self, e):
        self.ln_vector(e)
        PB = self.net.PB
        c = self.chain

        def group(i, last):
            c.start()
            e.wait_ge(self.in_ps.sem, self.in_ps.at(i))
            for j in range(2):
                ins = e.tensor_copy(self.xin[:, j, :], PB[1 + j][:, :])
            ins.then_inc(self.xin_r.sem, 1)
            e.wait_ge(self.a_r.sem, self.a_r.at(i))
            e.tensor_tensor(self.t[:], self.a[:], self.a[:], ALU.mult).then_inc(c.sem, 1)
            e.wait_ge(c.sem, c.next(i))
            e.tensor_scalar(self.t[:], self.t[:], -1.0, 1.0, ALU.mult, ALU.add).then_inc(self.t_r.sem, 1)
            e.memset(self.a[:].rearrange("p j (b s) -> p (j b) s", s=S)[:, :, 0:1], 0.0).then_inc(c.sem, 1)
            e.wait_ge(c.sem, c.next(i))
            e.wait_ge(self.rest_r.sem, self.rest_r.at(i))
            e.tensor_tensor(self.t[:], self.t[:], self.xin[:], ALU.mult).then_inc(c.sem, 1)
            e.wait_ge(c.sem, c.next(i))
            for j in range(2):
                e.tensor_tensor_scan(self.y[:, j, :], self.a[:, j, :], self.t[:, j, :], 0.0, ALU.mult, ALU.add).then_inc(c.sem, 1)
                e.wait_ge(c.sem, c.next(i))
            e.wait_ge(self.gate_r.sem, self.gate_r.at(i))
            e.tensor_tensor(self.y[:], self.y[:], self.gate[:], ALU.mult).then_inc(self.y_r.sem, 1)
            e.wait_ge(self.wo_ps.sem, self.wo_ps.at(i))
            e.tensor_tensor(self.x2[:], PB[7][:, :].rearrange("p (j d) -> p j d", j=4), self.xn[:], ALU.add).then_inc(self.x2_r.sem, 1)
            if not last:
                e.wait_ge(self.x2_r.sem, self.x2_r.at(i))
                self.norm(e, i + 1)
            self.rms_vector(e, i, 2, self.x2)
            e.wait_ge(self.sg_r.sem, self.sg_r.at(i))
            for j in range(4):
                e.tensor_tensor(self.sg[:, j, :], PB[j][:, :], self.sg[:, j, :], ALU.mult).then_inc(c.sem, 1)
                e.wait_ge(c.sem, c.next(i))
            for j in range(4):
                ins = e.tensor_tensor(self.m[:, j, :], PB[4 + j][:, :], self.sg[:, j, :], ALU.mult)
            ins.then_inc(self.m_r.sem, 1)
            if not last:
                self.rms_vector(e, i + 1, 1, self.xn)
            xs = self.net.X[:, bass.ds(i * 4, 4), :]
            e.tensor_tensor(xs, self.x2[:], xs, ALU.add).then_inc(c.sem, 1)
            e.wait_ge(c.sem, c.next(i))
            self.add_residual(e, i, PB[0][:, :].rearrange("p (j d) -> p j d", j=4), self.y_ps)
            c.done()

        self.norm(e, 0)
        self.rms_vector(e, 0, 1, self.xn)
        with e.Fori(0, self.iters - 1) as i:
            group(i, False)
        group(self.iters - 1, True)

    def scalar(self, e):
        self.ln_scalar(e)
        PB, w = self.net.PB, self.w
        def group(i, last):
            e.wait_ge(self.in_ps.sem, self.in_ps.at(i))
            for j in range(2):
                ins = e.activation(self.gate[:, j, :], PB[3 + j][:, :], ACT.Sigmoid)
            ins.then_inc(self.gate_r.sem, 1)
            e.wait_ge(self.a_ps.sem, self.a_ps.at(i))
            for j in range(2):
                ins = e.activation(self.a[:, j, :], PB[5 + j][:, :], ACT.Sigmoid, bias=w["ap"][:, j:j + 1])
            ins.then_inc(self.a_r.sem, 1)
            e.wait_ge(self.t_r.sem, self.t_r.at(i))
            e.activation(self.t[:], self.t[:], ACT.Sqrt, bias=self.net.const("eps8")).then_inc(self.rest_r.sem, 1)
            self.rms_scalar(e, i, 2, self.x2, w["ln2"], PB[0], self.x2_r)
            e.wait_ge(self.mlp_ps.sem, self.mlp_ps.at(i))
            for j in range(4):
                ins = e.activation(self.sg[:, j, :], PB[j][:, :], ACT.Sigmoid)
            ins.then_inc(self.sg_r.sem, 1)
            if not last:
                self.rms_scalar(e, i + 1, 1, self.xn, w["ln1"], PB[1], self.xn_r)

        self.rms_scalar(e, 0, 1, self.xn, w["ln1"], PB[1], self.xn_r)
        with e.Fori(0, self.iters - 1) as i:
            group(i, False)
        group(self.iters - 1, True)

    def tensor(self, e):
        PB, w = self.net.PB, self.w
        def group(i, last):
            for j in range(2):
                e.matmul(PB[1 + j][:, :], w["win"][:, j * P:(j + 1) * P], self.hT[:, :], start=True, stop=True)
            for j in range(2):
                ins = e.matmul(PB[3 + j][:, :], w["wgate"][:, j * P:(j + 1) * P], self.hT[:, :], start=True, stop=True)
            ins.then_inc(self.in_ps.sem, 1)
            e.wait_ge(self.xin_r.sem, self.xin_r.at(i))
            for j in range(2):
                for k in range(2):
                    a = k * 256 + j * P
                    ins = e.matmul(PB[5 + j][:, :], w["wa"][:, a:a + P], self.xin[:, k, :], start=(k == 0), stop=(k == 1))
            ins.then_inc(self.a_ps.sem, 1)
            e.wait_ge(self.y_r.sem, self.y_r.at(i))
            self.project(e, PB[7], [self.y[:, k, :] for k in range(2)], [w["wout"][:, k * P:(k + 1) * P] for k in range(2)])\
                .then_inc(self.wo_ps.sem, 1)
            self.rms_tensor(e, i, 2, PB[0])
            for name, b in (("wmg", 0), ("wmu", 4)):
                for j in range(4):
                    ins = e.matmul(PB[b + j][:, :], w[name][:, j * P:(j + 1) * P], self.hT[:, :], start=True, stop=True)
            ins.then_inc(self.mlp_ps.sem, 1)
            e.wait_ge(self.m_r.sem, self.m_r.at(i))
            self.project(e, PB[0], [self.m[:, k, :] for k in range(4)], [w["wmd"][:, k * P:(k + 1) * P] for k in range(4)])\
                .then_inc(self.y_ps.sem, 1)
            if not last:
                self.rms_tensor(e, i + 1, 1, PB[1])

        self.rms_tensor(e, 0, 1, PB[1])
        with e.Fori(0, self.iters - 1) as i:
            group(i, False)
        group(self.iters - 1, True)

    def gpsimd(self, e):
        pass

    def sync(self, e):
        pass


class L2Attn(Block):

    name = "L2_attn"
    vsteps = 17
    setup_steps = 4

    def plan(self):
        s3 = [P, 16, 33]
        self.xs = self.sb("xs", s3)
        self.mix = self.sb("mixed", [P, 3, 16, S])
        self.dx = self.sb("dx", [P, 16, S])
        self.k = self.sb("k", s3)
        self.v = self.sb("v", [P, 16, S])
        self.sr = self.sb("sr", [P, 16, S])
        self.wdec = self.sb("wdecay", s3)
        self.pp = self.sb("pp", s3)
        self.e1 = self.sb("e1", s3)
        self.e2 = self.sb("e2", s3)
        self.ev = self.sb("ev", s3)
        self.aa = self.sb("aa", s3)
        self.bb = self.sb("bb", s3)
        self.p = self.sb("p", [P, 2, 16, S])
        self.q = self.sb("q", [P, 2, 16, S])
        self.num = self.sb("num", [P, 2, 16, S])
        self.neg = self.sb("negw", [P, 2])
        self.expw = self.sig("decay_exp_ready", 1, 1)
        self.mix_r = self.sig("mixed_ready", 3)
        self.kvr_ps = self.sig("hidden_in_psum")
        self.kvr_r = self.sig("kvr_ready")
        self.arg1 = self.sig("exponents_ready", 2)
        self.exp1 = self.sig("exps_ready", 2)
        self.act_r = self.sig("activated_ready")
        self.y_ps = self.sig("y_in_psum")

    def vector(self, e):
        self.ln_vector(e)
        w, c = self.w, self.setup_chain
        now, before = slice(1, 33), slice(0, 32)
        e.memset(self.xs[:, :, 0:1], 0.0)
        e.memset(self.k[:, :, 0:1], -1e38)
        e.memset(self.e1[:, :, 0:1], 0.0)
        e.memset(self.e2[:, :, 0:1], 0.0)
        e.memset(self.ev[:, :, 0:1], 0.0).then_inc(c.sem, 1)
        e.wait_ge(c.sem, c.next())
        e.wait_ge(self.expw.sem, self.expw.at(0))
        e.tensor_scalar(self.neg[:, 1:2], self.neg[:, 0:1], -1.0, None, ALU.mult).then_inc(c.sem, 1)
        e.wait_ge(c.sem, c.next())
        e.memset(self.wdec[:], 0.0).then_inc(c.sem, 1)
        e.wait_ge(c.sem, c.next())
        e.tensor_scalar(self.wdec[:, :, now], self.wdec[:, :, now], self.neg[:, 1:2], None, ALU.add)
        e.memset(self.wdec[:, :, 0:1], -1e38).then_inc(c.sem, 1)
        e.wait_ge(c.sem, c.next())
        c.done()
        flat = lambda t: t[:].rearrange("p b s -> p (b s)")
        def group(i, last):
            c = self.chain
            c.start()
            e.wait_ge(self.xnT_r.sem, self.xnT_r.at(i))
            e.tensor_tensor(self.dx[:], self.xs[:, :, now], self.xs[:, :, before], ALU.subtract).then_inc(c.sem, 1)
            e.wait_ge(c.sem, c.next(i))
            for j, m in enumerate(("mk", "mv", "mr")):
                e.scalar_tensor_tensor(out=self.mix[:, j], in0=self.dx[:], scalar=w[m], in1=self.xs[:, :, before],
                                       op0=ALU.mult, op1=ALU.add).then_inc(self.mix_r.sem, 1)
            if not last:
                self.norm(e, i + 1)
            e.wait_ge(self.kvr_r.sem, self.kvr_r.at(i))
            e.tensor_tensor_scan(flat(self.pp), flat(self.wdec), flat(self.k), -1e38, ALU.add, ALU.max).then_inc(c.sem, 1)
            e.wait_ge(c.sem, c.next(i))
            pb, pn, kn = self.pp[:, :, before], self.pp[:, :, now], self.k[:, :, now]
            e.scalar_tensor_tensor(out=self.p[:, 0], in0=pb, scalar=self.neg[:, 1:2], in1=pn, op0=ALU.add, op1=ALU.subtract).then_inc(c.sem, 1)
            e.wait_ge(c.sem, c.next(i))
            e.tensor_tensor(self.p[:, 1], kn, pn, ALU.subtract).then_inc(self.arg1.sem, 1)
            e.tensor_scalar(self.num[:, 0], kn, w["tf"], None, ALU.add).then_inc(c.sem, 1)
            e.wait_ge(c.sem, c.next(i))
            e.tensor_tensor(self.num[:, 1], self.num[:, 0], pb, ALU.max).then_inc(c.sem, 1)
            e.wait_ge(c.sem, c.next(i))
            e.tensor_tensor(self.q[:, 0], pb, self.num[:, 1], ALU.subtract).then_inc(c.sem, 1)
            e.wait_ge(c.sem, c.next(i))
            e.tensor_tensor(self.q[:, 1], self.num[:, 0], self.num[:, 1], ALU.subtract).then_inc(self.arg1.sem, 1)
            e.wait_ge(self.exp1.sem, self.exp1.at(i, 1))
            e.tensor_tensor(self.ev[:, :, now], self.e2[:, :, now], self.v[:], ALU.mult).then_inc(c.sem, 1)
            e.wait_ge(c.sem, c.next(i))
            e.tensor_tensor_scan(flat(self.aa), flat(self.e1), flat(self.ev), 0.0, ALU.mult, ALU.add).then_inc(c.sem, 1)
            e.wait_ge(c.sem, c.next(i))
            e.tensor_tensor_scan(flat(self.bb), flat(self.e1), flat(self.e2), 0.0, ALU.mult, ALU.add).then_inc(c.sem, 1)
            e.wait_ge(c.sem, c.next(i))
            e.wait_ge(self.exp1.sem, self.exp1.at(i, 2))
            e.tensor_tensor(self.num[:, 0], self.q[:, 0], self.aa[:, :, before], ALU.mult).then_inc(c.sem, 1)
            e.wait_ge(c.sem, c.next(i))
            e.tensor_tensor(self.num[:, 1], self.q[:, 0], self.bb[:, :, before], ALU.mult).then_inc(c.sem, 1)
            e.wait_ge(c.sem, c.next(i))
            e.tensor_tensor(self.p[:, 0], self.q[:, 1], self.v[:], ALU.mult).then_inc(c.sem, 1)
            e.wait_ge(c.sem, c.next(i))
            e.tensor_tensor(self.p[:, 0], self.p[:, 0], self.num[:, 0], ALU.add).then_inc(c.sem, 1)
            e.wait_ge(c.sem, c.next(i))
            e.tensor_tensor(self.p[:, 1], self.q[:, 1], self.num[:, 1], ALU.add).then_inc(c.sem, 1)
            e.wait_ge(c.sem, c.next(i))
            e.reciprocal(self.p[:, 1], self.p[:, 1]).then_inc(c.sem, 1)
            e.wait_ge(c.sem, c.next(i))
            e.tensor_tensor(self.p[:, 0], self.p[:, 0], self.p[:, 1], ALU.mult).then_inc(c.sem, 1)
            e.wait_ge(c.sem, c.next(i))
            e.tensor_tensor(self.q[:, 0], self.p[:, 0], self.sr[:], ALU.mult).then_inc(self.act_r.sem, 1)
            self.add_residual(e, i, self.net.PB[4][:, :].rearrange("p (j d) -> p j d", j=4), self.y_ps)
            self.chain.done()

        self.norm(e, 0)
        with e.Fori(0, self.iters - 1) as i:
            group(i, False)
        group(self.iters - 1, True)

    def scalar(self, e):
        self.ln_scalar(e)
        PB = self.net.PB
        e.activation(self.neg[:, 0:1], self.w["td"], ACT.Exp).then_inc(self.expw.sem, 1)
        seqs = lambda b: b[:, :].rearrange("p (b s) -> p b s", s=S)
        def head(i):
            e.wait_ge(self.xnT_ps.sem, self.xnT_ps.at(i))
            e.activation(self.xs[:, :, 1:33], seqs(PB[0]), ACT.Copy).then_inc(self.xnT_r.sem, 1)

        def group(i, last):
            e.wait_ge(self.kvr_ps.sem, self.kvr_ps.at(i))
            e.activation(self.k[:, :, 1:33], seqs(PB[1]), ACT.Copy)
            e.activation(self.v[:], seqs(PB[2]), ACT.Copy)
            e.activation(self.sr[:], seqs(PB[3]), ACT.Sigmoid).then_inc(self.kvr_r.sem, 1)
            e.wait_ge(self.arg1.sem, self.arg1.at(i, 1))
            e.activation(self.e1[:, :, 1:33], self.p[:, 0], ACT.Exp)
            e.activation(self.e2[:, :, 1:33], self.p[:, 1], ACT.Exp).then_inc(self.exp1.sem, 1)
            e.wait_ge(self.arg1.sem, self.arg1.at(i, 2))
            e.activation(self.q[:], self.q[:], ACT.Exp).then_inc(self.exp1.sem, 1)
            if not last:
                head(i + 1)

        head(0)
        with e.Fori(0, self.iters - 1) as i:
            group(i, False)
        group(self.iters - 1, True)

    def tensor(self, e):
        PB, w = self.net.PB, self.w
        def group(i, last):
            for j, m in enumerate(("wk", "wv", "wr")):
                e.wait_ge(self.mix_r.sem, self.mix_r.at(i, j + 1))
                ins = e.matmul(PB[1 + j][:, :], w[m], self.mix[:, j].rearrange("p b s -> p (b s)"), start=True, stop=True)
            ins.then_inc(self.kvr_ps.sem, 1)
            if not last:
                self.transpose_xn(e, i + 1, PB[0])
            e.wait_ge(self.act_r.sem, self.act_r.at(i))
            self.project(e, PB[4], [self.q[:, 0].rearrange("p b s -> p (b s)")], [w["wo"]]).then_inc(self.y_ps.sem, 1)

        self.transpose_xn(e, 0, PB[0])
        with e.Fori(0, self.iters - 1) as i:
            group(i, False)
        group(self.iters - 1, True)

    def gpsimd(self, e):
        pass

    def sync(self, e):
        pass


def router(c, i, e, block, lg, n, E, probs, floor, plus):
    r = block
    big = lambda t: t[:, :].rearrange("p (n o) -> p n o", o=1).to_broadcast([P, n, E])
    e.tensor_reduce(r.mx[:, :], lg, AX.X, ALU.max).then_inc(c.sem, 1)
    e.wait_ge(c.sem, c.next(i))
    e.tensor_tensor(r.ex[:], lg, big(r.mx), ALU.subtract).then_inc(r.lg_r.sem, 1)
    e.wait_ge(probs.sem, probs.at(i))
    e.tensor_reduce(r.mx[:, :], r.ex[:], AX.X, ALU.add).then_inc(c.sem, 1)
    e.wait_ge(c.sem, c.next(i))
    e.reciprocal(r.mx[:, :], r.mx[:, :]).then_inc(c.sem, 1)
    e.wait_ge(c.sem, c.next(i))
    e.tensor_tensor(r.ex[:], r.ex[:], big(r.mx), ALU.mult).then_inc(c.sem, 1)
    e.wait_ge(c.sem, c.next(i))
    e.memset(r.held[:, 0:1], 0.0)
    for j in range(n):
        ins = e.max(r.top[:, j, :], r.ex[:, j, :])
    ins.then_inc(c.sem, 1)
    e.wait_ge(c.sem, c.next(i))
    e.memset(r.held[:, 1:2], 0.0)
    for j in range(n):
        ins = e.max_index(r.idx[:, j, :], r.top[:, j, :], r.ex[:, j, :])
    ins.then_inc(c.sem, 1)
    e.wait_ge(c.sem, c.next(i))
    e.tensor_copy(r.idf[:], r.idx[:]).then_inc(c.sem, 1)
    e.wait_ge(c.sem, c.next(i))
    e.tensor_tensor(r.mx[:, :], r.top[:, :, 0], r.top[:, :, 1], ALU.add).then_inc(c.sem, 1)
    e.wait_ge(c.sem, c.next(i))
    e.tensor_scalar(r.mx[:, :], r.mx[:, :], plus, floor, ALU.add, ALU.max).then_inc(c.sem, 1)
    e.wait_ge(c.sem, c.next(i))
    e.reciprocal(r.mx[:, :], r.mx[:, :]).then_inc(c.sem, 1)
    e.wait_ge(c.sem, c.next(i))
    e.tensor_tensor(r.top[:, :, 0:2], r.top[:, :, 0:2],
                           r.mx[:, :].rearrange("p (n o) -> p n o", o=1).to_broadcast([P, n, 2]), ALU.mult).then_inc(c.sem, 1)
    e.wait_ge(c.sem, c.next(i))
    iota = r.net.const("iota14")[:, 0:E]
    for j in range(n):
        e.tensor_scalar(r.cw[:, j, :], iota, r.idf[:, j, 0:1], r.top[:, j, 0:1], ALU.is_equal, ALU.mult)
        ins = e.tensor_scalar(r.one[:, j, :], iota, r.idf[:, j, 1:2], r.top[:, j, 1:2], ALU.is_equal, ALU.mult)
    ins.then_inc(c.sem, 1)
    e.wait_ge(c.sem, c.next(i))
    return e.tensor_tensor(r.cw[:], r.cw[:], r.one[:], ALU.add)


def router_buffers(b, n, E):
    b.held = b.sb("held", [P, 2])
    b.mx = b.sb("rowmax", [P, n])
    b.ex = b.sb("probs", [P, n, E])
    b.top = b.sb("top", [P, n, 8])
    b.idx = b.sb("topindex", [P, n, 8], U32)
    b.idf = b.sb("topindexf", [P, n, 8])
    b.cw = b.sb("expertweights", [P, n, E])
    b.one = b.sb("second", [P, n, E])


class TokenMoE(Block):

    E, halves = 14, 2

    def plan(self):
        E = self.E
        router_buffers(self, 4, E)
        self.h = self.sb("hidden", [P, 4, 512])
        self.sg = self.sb("silu", [P, 2, 512])
        self.acc = self.sb("acc", [P, 4, D])
        self.cwT = self.sb("cwT", [P, 512])
        self.lg_ps = self.sig("logits_in_psum")
        self.lg_r = self.sig("logits_ready")
        self.ex_r = self.sig("probs_ready")
        self.cw_r = self.sig("expertweights_ready")
        if self.has_start:
            self.cwT_ps = self.sig("expertweights_in_psum")
            self.cwT_r = self.sig("expertweights_transposed")
            self.bias_ps = self.sig("expertbias_in_psum")
        self.hid_ps = self.sig("hidden_in_psum", 2 * E)
        if self.gated:
            self.silu_r = self.sig("silu_ready", 2 * E)
        self.hid_r = self.sig("hidden_ready", 2 * E)
        self.e_ps = self.sig("expert_in_psum", E)
        self.acc_r = self.sig("expert_added", E)

    def router_tensor(self, e, i):
        PB = self.net.PB
        for j in range(4):
            ins = e.matmul(PB[7][:, j * self.E:(j + 1) * self.E], self.xnT[:, j * P:(j + 1) * P], self.w["gate"], start=True, stop=True)
        ins.then_inc(self.lg_ps.sem, 1)

    def combine(self, e, i, x):
        for x in range(self.E):
            if self.gated and x + 1 < self.E:
                self.gate_vector(e, i, x + 1)
            e.wait_ge(self.e_ps.sem, self.e_ps.at(i, x + 1))
            if x:
                e.wait_ge(self.acc_r.sem, self.acc_r.at(i, x))
            for j in range(4):
                y = self.net.PB[4 + x % 2][:, j * P:(j + 1) * P]
                if x == 0 and not self.has_start:
                    ins = e.tensor_scalar(self.acc[:, j, :], y, self.cw[:, j, x:x + 1], None, ALU.mult)
                else:
                    ins = e.scalar_tensor_tensor(out=self.acc[:, j, :], in0=y, scalar=self.cw[:, j, x:x + 1], in1=self.acc[:, j, :],
                                                 op0=ALU.mult, op1=ALU.add)
            ins.then_inc(self.acc_r.sem, 1)
        e.wait_ge(self.acc_r.sem, self.acc_r.at(i))

    def down(self, e, i, x, w):
        e.wait_ge(self.hid_r.sem, self.hid_r.at(i, 2 * x + 2))
        if x >= 2:
            e.wait_ge(self.acc_r.sem, self.acc_r.at(i, x - 1))
        for j in range(4):
            for k in range(2):
                a = (2 * x + k) * P
                ins = e.matmul(self.net.PB[4 + x % 2][:, j * P:(j + 1) * P], self.h[:, (2 * x + k) % 4, j * P:(j + 1) * P],
                               w[:, a:a + P], start=(k == 0), stop=(k == 1))
        ins.then_inc(self.e_ps.sem, 1)

    def gpsimd(self, e):
        pass

    def sync(self, e):
        pass


class L2Ffn(TokenMoE):

    name, E, gated, has_start = "L2_ffn", 14, False, True
    vsteps = 15

    def vector(self, e):
        self.ln_vector(e)
        PB, c = self.net.PB, self.chain
        def group(i, last):
            c.start()
            e.wait_ge(self.lg_ps.sem, self.lg_ps.at(i))
            router(c, i, e, self, PB[7][:, 0:4 * self.E].rearrange("p (n e) -> p n e", n=4), 4, self.E,
                   self.ex_r, 1e-10, 0.0).then_inc(self.cw_r.sem, 1)
            e.wait_ge(self.bias_ps.sem, self.bias_ps.at(i))
            e.tensor_tensor(self.acc[:], PB[6][:, :].rearrange("p (j d) -> p j d", j=4), self.xn[:], ALU.add).then_inc(c.sem, 1)
            e.wait_ge(c.sem, c.next(i))
            if not last:
                self.norm(e, i + 1)
            self.combine(e, i, 0)
            e.tensor_scalar(self.acc[:], self.acc[:], -100.0, 100.0, ALU.max, ALU.min).then_inc(c.sem, 1)
            e.wait_ge(c.sem, c.next(i))
            self.add_residual(e, i, self.acc[:], self.acc_r)
            c.done()

        self.norm(e, 0)
        with e.Fori(0, self.iters - 1) as i:
            group(i, False)
        group(self.iters - 1, True)

    def scalar(self, e):
        self.ln_scalar(e)
        PB = self.net.PB
        def group(i, last):
            e.wait_ge(self.lg_r.sem, self.lg_r.at(i))
            e.activation(self.ex[:], self.ex[:], ACT.Exp).then_inc(self.ex_r.sem, 1)
            e.wait_ge(self.cwT_ps.sem, self.cwT_ps.at(i))
            e.copy(self.cwT[0:self.E, :], PB[7][0:self.E, :]).then_inc(self.cwT_r.sem, 1)
            for n in range(2 * self.E):
                e.wait_ge(self.hid_ps.sem, self.hid_ps.at(i, n + 1))
                if n >= 4:
                    e.wait_ge(self.e_ps.sem, self.e_ps.at(i, n // 2 - 1))
                e.activation(self.h[:, n % 4, :], PB[n % 4][:, :], ACT.Gelu, bias=self.w["b1"][:, n:n + 1]).then_inc(self.hid_r.sem, 1)
            if not last:
                self.copy_xnT(e, i + 1, PB[6])

        self.copy_xnT(e, 0, PB[6])
        with e.Fori(0, self.iters - 1) as i:
            group(i, False)
        group(self.iters - 1, True)

    def tensor(self, e):
        PB, w, E = self.net.PB, self.w, self.E

        def up(i, x):
            for n in (2 * x, 2 * x + 1):
                if n >= 4:
                    e.wait_ge(self.hid_r.sem, self.hid_r.at(i, n - 3))
                e.matmul(PB[n % 4][:, :], w["w1"][:, n * P:(n + 1) * P], self.xnT[:, :], start=True, stop=True)\
                    .then_inc(self.hid_ps.sem, 1)

        def group(i, last):
            e.wait_ge(self.xnT_r.sem, self.xnT_r.at(i))
            self.router_tensor(e, i)
            up(i, 0)
            e.wait_ge(self.cw_r.sem, self.cw_r.at(i))
            for j in range(4):
                ins = e.matmul(PB[7][0:E, j * P:(j + 1) * P], self.cw[:, j, :], self.net.const("ident"), start=True, stop=True)
            ins.then_inc(self.cwT_ps.sem, 1)
            up(i, 1)
            e.wait_ge(self.cwT_r.sem, self.cwT_r.at(i))
            for j in range(4):
                ins = e.matmul(PB[6][:, j * P:(j + 1) * P], self.cwT[0:E, j * P:(j + 1) * P], w["b2"][0:E, :], start=True, stop=True)
            ins.then_inc(self.bias_ps.sem, 1)
            for x in range(E):
                if 1 < x + 1 < E:
                    up(i, x + 1)
                if x + 1 == E and not last:
                    self.transpose_xn(e, i + 1, PB[6])
                self.down(e, i, x, w["w2"])

        self.transpose_xn(e, 0, PB[6])
        with e.Fori(0, self.iters - 1) as i:
            group(i, False)
        group(self.iters - 1, True)


class L3Ffn(TokenMoE):

    name, E, gated, has_start = "L3_ffn", 8, True, False
    vsteps = 13

    def gate_vector(self, e, i, x):
        for n in (2 * x, 2 * x + 1):
            e.wait_ge(self.silu_r.sem, self.silu_r.at(i, n + 1))
            if n >= 4:
                e.wait_ge(self.e_ps.sem, self.e_ps.at(i, n // 2 - 1))
            e.tensor_tensor(self.h[:, n % 4, :], self.net.PB[2 * (n % 2) + 1][:, :], self.sg[:, n % 2, :], ALU.mult)\
                .then_inc(self.hid_r.sem, 1)

    def vector(self, e):
        self.ln_vector(e)
        PB, c = self.net.PB, self.chain
        def group(i, last):
            c.start()
            e.wait_ge(self.lg_ps.sem, self.lg_ps.at(i))
            router(c, i, e, self, PB[7][:, 0:4 * self.E].rearrange("p (n e) -> p n e", n=4), 4, self.E,
                   self.ex_r, 1e-30, 0.0).then_inc(self.cw_r.sem, 1)
            e.wait_ge(self.cw_r.sem, self.cw_r.at(i))
            self.gate_vector(e, i, 0)
            if not last:
                self.norm(e, i + 1)
            self.combine(e, i, 0)
            self.add_residual(e, i, self.acc[:], self.acc_r)
            c.done()

        self.norm(e, 0)
        with e.Fori(0, self.iters - 1) as i:
            group(i, False)
        group(self.iters - 1, True)

    def scalar(self, e):
        self.ln_scalar(e)
        PB = self.net.PB
        def group(i, last):
            e.wait_ge(self.lg_r.sem, self.lg_r.at(i))
            e.activation(self.ex[:], self.ex[:], ACT.Exp).then_inc(self.ex_r.sem, 1)
            for n in range(2 * self.E):
                e.wait_ge(self.hid_ps.sem, self.hid_ps.at(i, n + 1))
                if n >= 2:
                    e.wait_ge(self.hid_r.sem, self.hid_r.at(i, n - 1))
                e.activation(self.sg[:, n % 2, :], PB[2 * (n % 2)][:, :], ACT.Silu).then_inc(self.silu_r.sem, 1)
            if not last:
                self.copy_xnT(e, i + 1, PB[6])

        self.copy_xnT(e, 0, PB[6])
        with e.Fori(0, self.iters - 1) as i:
            group(i, False)
        group(self.iters - 1, True)

    def tensor(self, e):
        PB, w, E = self.net.PB, self.w, self.E

        def up(i, x):
            for n in (2 * x, 2 * x + 1):
                if n >= 2:
                    e.wait_ge(self.hid_r.sem, self.hid_r.at(i, n - 1))
                e.matmul(PB[2 * (n % 2)][:, :], w["wg"][:, n * P:(n + 1) * P], self.xnT[:, :], start=True, stop=True)
                e.matmul(PB[2 * (n % 2) + 1][:, :], w["wu"][:, n * P:(n + 1) * P], self.xnT[:, :], start=True, stop=True)\
                    .then_inc(self.hid_ps.sem, 1)

        def group(i, last):
            e.wait_ge(self.xnT_r.sem, self.xnT_r.at(i))
            self.router_tensor(e, i)
            up(i, 0)
            for x in range(E):
                if x + 1 < E:
                    up(i, x + 1)
                if x + 1 == E and not last:
                    self.transpose_xn(e, i + 1, PB[6])
                self.down(e, i, x, w["wd"])

        self.transpose_xn(e, 0, PB[6])
        with e.Fori(0, self.iters - 1) as i:
            group(i, False)
        group(self.iters - 1, True)


class L1Ffn(Block):

    name = "L1_ffn"
    E, C = 8, 64
    vsteps = 1
    setup_steps = 12

    def plan(self):
        router_buffers(self, 1, self.E)
        self.pooledT = self.sb("pooledT", [P, P])
        self.cwT = self.sb("cwT", [P, P])
        self.cwx = self.sb("cwx", [P, 4, P])
        self.cwe = self.sb("cwe", [P, 16, S])
        self.h = self.sb("h", [P, 4, 512])
        self.h2 = self.sb("h2", [P, 4, 512])
        self.pxn_r = self.sig("pool_xn_ready")
        self.pool_ps = self.sig("pooled_in_psum")
        self.pool_r = self.sig("pooled_ready")
        self.lg_ps = self.sig("logits_in_psum", 1, 1)
        self.lg_r = self.sig("logits_ready", 1, 1)
        self.ex_r = self.sig("probs_ready", 1, 1)
        self.cw_r = self.sig("expertweights_ready", 1, 1)
        self.cwT_ps = self.sig("expertweights_in_psum", 1, 1)
        self.cwT_r = self.sig("expertweights_transposed", 1, 1)
        self.cwx_ps = self.sig("expertbias_in_psum", 1, 1)
        self.cwx_r = self.sig("expert_added", 1, 1)
        self.cwe_r = self.sig("activated_ready")
        self.hid_ps = self.sig("hidden_in_psum")
        self.hid_r = self.sig("hidden_ready")
        self.h2_r = self.sig("mlp_hidden_ready")
        self.y_ps = self.sig("y_in_psum")

    def vector(self, e):
        self.ln_vector(e)
        n, PB = self.net, self.net.PB
        with e.Fori(0, self.iters) as i:
            for j in range(4):
                t = i * 4 + j
                ins = e.tensor_scalar(self.xn[:, j, :], n.X[:, bass.ds(t, 1), :], n.mean[:, bass.ds(t, 1)], n.rstd[:, bass.ds(t, 1)],
                                      ALU.subtract, ALU.mult)
            ins.then_inc(self.pxn_r.sem, 1)
            e.wait_ge(self.pool_ps.sem, self.pool_ps.at(i))
            e.tensor_copy(self.pooledT[:, bass.ds(i * 16, 16)], PB[6][:, 0:16]).then_inc(self.pool_r.sem, 1)
        e.wait_ge(self.lg_ps.sem, self.lg_ps.at(0))
        router(self.setup_chain, 0, e, self, PB[7][:, 0:8].rearrange("p (n e) -> p n e", n=1), 1, self.E,
               self.ex_r, 0.0, 1e-8).then_inc(self.cw_r.sem, 1)
        e.wait_ge(self.cwx_ps.sem, self.cwx_ps.at(0))
        e.tensor_copy(self.cwx[:], PB[6][:, :].rearrange("p (j b) -> p j b", j=4)).then_inc(self.cwx_r.sem, 1)
        e.wait_ge(self.cwx_r.sem, self.cwx_r.at(0))
        self.setup_chain.done()
        def group(i, last):
            self.chain.start()
            if not last:
                e.wait_ge(self.xnT_ps.sem, self.xnT_ps.at(i))
                self.norm(e, i + 1)
            e.tensor_copy(self.cwe[0:8], self.cwT[0:8, bass.ds(i * 16, 16)].rearrange("p (b o) -> p b o", o=1).to_broadcast([8, 16, S]))\
                .then_inc(self.cwe_r.sem, 1)
            e.wait_ge(self.hid_r.sem, self.hid_r.at(i))
            for j in range(4):
                ins = e.tensor_tensor(self.h2[:, j, :].rearrange("p (b s) -> p b s", s=S), self.h[:, j, :].rearrange("p (b s) -> p b s", s=S),
                                      self.cwx[:, j, bass.ds(i * 16, 16)].rearrange("p (b o) -> p b o", o=1).to_broadcast([P, 16, S]), ALU.mult)
            ins.then_inc(self.h2_r.sem, 1)
            self.add_residual(e, i, PB[5][:, :].rearrange("p (j d) -> p j d", j=4), self.y_ps)
            self.chain.done()

        self.norm(e, 0)
        with e.Fori(0, self.iters - 1) as i:
            group(i, False)
        group(self.iters - 1, True)

    def scalar(self, e):
        self.ln_scalar(e)
        PB = self.net.PB
        e.wait_ge(self.lg_r.sem, self.lg_r.at(0))
        e.activation(self.ex[:], self.ex[:], ACT.Exp).then_inc(self.ex_r.sem, 1)
        e.wait_ge(self.cwT_ps.sem, self.cwT_ps.at(0))
        e.copy(self.cwT[0:8, :], PB[7][0:8, 0:P]).then_inc(self.cwT_r.sem, 1)
        def group(i, last):
            e.wait_ge(self.hid_ps.sem, self.hid_ps.at(i))
            for j in range(4):
                ins = e.activation(self.h[:, j, :], PB[1 + j][:, :], ACT.Gelu, bias=self.w["bd"][:, j:j + 1])
            ins.then_inc(self.hid_r.sem, 1)
            if not last:
                self.copy_xnT(e, i + 1, PB[0])

        self.copy_xnT(e, 0, PB[0])
        with e.Fori(0, self.iters - 1) as i:
            group(i, False)
        group(self.iters - 1, True)

    def tensor(self, e):
        PB, w, n = self.net.PB, self.w, self.net
        with e.Fori(0, self.iters) as i:
            e.wait_ge(self.pxn_r.sem, self.pxn_r.at(i))
            for j in range(4):
                ins = e.matmul(PB[6][:, 4 * j:4 * j + 4], self.xn[:, j, :], n.const("seqmean"), start=True, stop=True)
            ins.then_inc(self.pool_ps.sem, 1)
        e.wait_ge(self.pool_r.sem, self.pool_r.at(self.iters - 1))
        e.matmul(PB[7][:, 0:8], self.pooledT[:, :], w["gate"], start=True, stop=True).then_inc(self.lg_ps.sem, 1)
        e.wait_ge(self.cw_r.sem, self.cw_r.at(0))
        e.matmul(PB[7][0:8, 0:P], self.cw[:, 0, :], n.const("ident"), start=True, stop=True).then_inc(self.cwT_ps.sem, 1)
        e.wait_ge(self.cwT_r.sem, self.cwT_r.at(0))
        for j in range(4):
            ins = e.matmul(PB[6][:, j * P:(j + 1) * P], n.const("exp2rows")[0:8, j * P:(j + 1) * P], self.cwT[0:8, :], start=True, stop=True)
        ins.then_inc(self.cwx_ps.sem, 1)
        def group(i, last):
            e.wait_ge(self.xnT_r.sem, self.xnT_r.at(i))
            for j in range(4):
                ins = e.matmul(PB[1 + j][:, :], w["down"][:, j * P:(j + 1) * P], self.xnT[:, :], start=True, stop=True)
            ins.then_inc(self.hid_ps.sem, 1)
            if not last:
                self.transpose_xn(e, i + 1, PB[0])
            e.wait_ge(self.h2_r.sem, self.h2_r.at(i))
            e.wait_ge(self.cwe_r.sem, self.cwe_r.at(i))
            for j in range(4):
                o = PB[5][:, j * P:(j + 1) * P]
                e.matmul(o, self.cwe[0:8, 4 * j:4 * j + 4, :].rearrange("p b s -> p (b s)"), w["bu"][0:8, :], start=True, stop=False)
                for k in range(4):
                    ins = e.matmul(o, self.h2[:, k, j * P:(j + 1) * P], w["up"][:, k * P:(k + 1) * P], start=False, stop=(k == 3))
            ins.then_inc(self.y_ps.sem, 1)

        self.transpose_xn(e, 0, PB[0])
        with e.Fori(0, self.iters - 1) as i:
            group(i, False)
        group(self.iters - 1, True)

    def gpsimd(self, e):
        pass

    def sync(self, e):
        pass

QSCALE = 1.0 / float(np.sqrt(8.0))


class SmallAttn(Block):

    vsteps = 5
    cross = False

    def plan(self):
        if self.cross:
            self.ct = self.sb("ctx", [P, 4, D])
            self.ctT = self.sb("ctxT", [P, 512])
            self.ctx_l = self.sig("context_loaded", 64)
            self.ctT_ps = self.sig("ctxT_in_psum")
            self.ctT_r = self.sig("ctxT_ready")
            self.bqs = self.sb("bqs", [P, 1])
            self.bqs_r = self.sig("scaled_bias_ready", 1, 1)
        self.qT = self.sb("qT", [P, 16, S])
        self.kx = self.sb("kx", [P, 16, C, S])
        self.vx = self.sb("vx", [P, 4, C, SEQS, 32])
        self.bks = self.sb("bks", [P, C])
        self.qx = self.sb("qx", [P, 16, 4, S])
        self.e = self.sb("e", [P, 64, S])
        self.pt = self.sb("pt", [P, C, 4, P])
        self.rm = self.sb("rm", [P, 4, 4, C, 32])
        self.o = self.sb("o", [P, 4, 4, C * 32])
        self.oT = self.sb("oT", [P, 512])
        self.mx = self.sb("mx", [P, 64])
        self.rs = self.sb("rs", [P, 64])
        self.qkv_ps = self.sig("hidden_in_psum")
        self.q_r = self.sig("hidden_ready")
        self.qx_r = self.sig("spread_ready")
        self.kx_r = self.sig("keys_spread_ready")
        self.vx_r = self.sig("values_spread_ready")
        self.s_ps = self.sig("scores_in_psum")
        self.d_r = self.sig("exponents_ready")
        self.e_r = self.sig("exps_ready")
        self.pt_ps = self.sig("probsT_in_psum")
        self.pta_r = self.sig("probsT_low_ready")
        self.ptv_r = self.sig("probsT_high_ready")
        self.o_ps = self.sig("heads_in_psum")
        self.o_r = self.sig("heads_ready")
        self.oT_ps = self.sig("headsT_in_psum")
        self.oT_r = self.sig("headsT_ready")
        self.y_ps = self.sig("y_in_psum")

    def vector(self, e):
        self.ln_vector(e)
        n, c = self.net, self.chain
        PS = n.PS
        def group(i, last):
            c.start()
            e.wait_ge(self.q_r.sem, self.q_r.at(i))
            e.tensor_tensor(self.qx[:], self.qT[:].rearrange("p b (o s) -> p b o s", o=1).to_broadcast([P, 16, 4, S]),
                            n.const("head4").rearrange("p (a h b) -> p a h b", a=1, b=1).to_broadcast([P, 16, 4, S]), ALU.mult)\
                .then_inc(self.qx_r.sem, 1)
            e.wait_ge(self.s_ps.sem, self.s_ps.at(i))
            sc = PS[:, 0:4, :].rearrange("p t x -> p (t x)").rearrange("p (b c k) -> p c b k", c=C, k=S)
            ex = self.e[:].rearrange("p (c b) k -> p c b k", c=C)
            if self.cross:
                e.tensor_tensor(ex, sc, n.const("causal").rearrange("p (a o k) -> p a o k", a=1, o=1).to_broadcast([P, C, 16, S]), ALU.add)\
                    .then_inc(c.sem, 1)
                e.wait_ge(c.sem, c.next(i))
                sc = ex
            e.tensor_reduce(self.mx[:, :].rearrange("p (c b) -> p c b", c=C), sc, AX.X, ALU.max).then_inc(c.sem, 1)
            e.wait_ge(c.sem, c.next(i))
            e.tensor_tensor(ex, sc, self.mx[:, :].rearrange("p (c b o) -> p c b o", c=C, o=1).to_broadcast([P, C, 16, S]), ALU.subtract)\
                .then_inc(self.d_r.sem, 1)
            e.wait_ge(self.e_r.sem, self.e_r.at(i))
            e.tensor_reduce(self.rs[:, :], self.e[:], AX.X, ALU.add).then_inc(c.sem, 1)
            e.wait_ge(c.sem, c.next(i))
            e.reciprocal(self.rs[:, :], self.rs[:, :]).then_inc(c.sem, 1)
            e.wait_ge(c.sem, c.next(i))
            r4 = self.rs[:, :].rearrange("p (c t r) -> p r t c", c=C, r=4)
            for r in range(4):
                ins = e.tensor_tensor(self.rm[:, r], r4[:, r].rearrange("p t (c o) -> p t c o", o=1).to_broadcast([P, 4, C, 32]),
                                      n.const("odiag").rearrange("p (a b j) -> p a b j", a=1, b=1).to_broadcast([P, 4, C, 32]), ALU.mult)
            ins.then_inc(c.sem, 1)
            e.wait_ge(c.sem, c.next(i))
            e.wait_ge(self.pt_ps.sem, self.pt_ps.at(i))
            for q in (2, 3):
                ins = e.tensor_copy(self.pt[:, q].rearrange("p t h -> p (t h)"), PS[:, 4 + q, :])
            ins.then_inc(self.ptv_r.sem, 1)
            if not last:
                self.norm(e, i + 1)
            e.wait_ge(self.o_ps.sem, self.o_ps.at(i))
            for r in range(SEQS):
                ins = e.tensor_tensor(self.o[:, r].rearrange("p t (c j) -> p t c j", c=C),
                                      PS[:, 0:4, :].rearrange("p t (c r j) -> p r t c j", c=C, r=SEQS)[:, r], self.rm[:, r], ALU.mult)
            ins.then_inc(self.o_r.sem, 1)
            self.add_residual(e, i, PS[:, 7, :].rearrange("p (j d) -> p j d", j=4), self.y_ps)
            c.done()

        self.norm(e, 0)
        with e.Fori(0, self.iters - 1) as i:
            group(i, False)
        group(self.iters - 1, True)

    def scalar(self, e):
        self.ln_scalar(e)
        n, PB, w = self.net, self.net.PB, self.w
        seqs = lambda t: t.rearrange("p (b k) -> p b k", k=S)
        if self.cross:
            for c in range(C):
                e.mul(self.bks[:, c:c + 1], w["bk"], n.const("quarter")[:, c:c + 1])
            e.mul(self.bqs[:, :], w["bq"], QSCALE).then_inc(self.bqs_r.sem, 1)
            e.wait_ge(self.bqs_r.sem, self.bqs_r.at(0))
        def head(i):
            self.copy_xnT(e, i, PB[0])
            if self.cross:
                e.wait_ge(self.ctT_ps.sem, self.ctT_ps.at(i))
                e.copy(self.ctT[:, :], PB[1]).then_inc(self.ctT_r.sem, 1)

        def group(i, last):
            e.wait_ge(self.qkv_ps.sem, self.qkv_ps.at(i))
            if self.cross:
                e.activation(self.qT[:].rearrange("p b s -> p (b s)"), PB[4], ACT.Identity, bias=self.bqs[:, :], scale=QSCALE)\
                    .then_inc(self.q_r.sem, 1)
            else:
                e.activation(self.qT[:].rearrange("p b s -> p (b s)"), PB[4], ACT.Copy, scale=QSCALE).then_inc(self.q_r.sem, 1)
            for c in range(C):
                k = n.const("quarter")[:, c:c + 1]
                ins = e.activation(self.kx[:, :, c, :], seqs(PB[5]), ACT.Identity, bias=self.bks[:, c:c + 1] if self.cross else 0.0, scale=k)
            ins.then_inc(self.kx_r.sem, 1)
            for r in range(SEQS):
                ins = e.activation(self.vx[:, :, :, r, :], PB[6].rearrange("p (t c j) -> p t c j", t=4, c=C), ACT.Identity,
                                   scale=n.const("quarter")[:, r:r + 1])
            ins.then_inc(self.vx_r.sem, 1)
            e.wait_ge(self.d_r.sem, self.d_r.at(i))
            e.activation(self.e[:], self.e[:], ACT.Exp).then_inc(self.e_r.sem, 1)
            e.wait_ge(self.pt_ps.sem, self.pt_ps.at(i))
            for q in (0, 1):
                ins = e.copy(self.pt[:, q].rearrange("p t h -> p (t h)"), PB[4 + q])
            ins.then_inc(self.pta_r.sem, 1)
            e.wait_ge(self.oT_ps.sem, self.oT_ps.at(i))
            if self.cross:
                e.activation(self.oT[:, :], PB[4], ACT.Identity, bias=w["bv"]).then_inc(self.oT_r.sem, 1)
            else:
                e.copy(self.oT[:, :], PB[4]).then_inc(self.oT_r.sem, 1)
            if not last:
                head(i + 1)

        head(0)
        with e.Fori(0, self.iters - 1) as i:
            group(i, False)
        group(self.iters - 1, True)

    def tensor(self, e):
        PB, w, n = self.net.PB, self.w, self.net
        def head(i):
            self.transpose_xn(e, i, PB[0])
            if self.cross:
                e.wait_ge(self.ctx_l.sem, self.ctx_l.at(i))
                for j in range(4):
                    ins = e.transpose(PB[1][:, j * P:(j + 1) * P], self.ct[:, j, :], n.const("ident"))
                ins.then_inc(self.ctT_ps.sem, 1)

        def group(i, last):
            e.wait_ge(self.xnT_r.sem, self.xnT_r.at(i))
            e.matmul(PB[4], w["wq"], self.xnT[:, :], start=True, stop=True)
            kv = self.xnT
            if self.cross:
                e.wait_ge(self.ctT_r.sem, self.ctT_r.at(i))
                kv = self.ctT
            e.matmul(PB[5], w["wk"], kv[:, :], start=True, stop=True)
            for j in range(4):
                ins = e.matmul(PB[6][:, j * P:(j + 1) * P], kv[:, j * P:(j + 1) * P], w["wv"], start=True, stop=True)
            ins.then_inc(self.qkv_ps.sem, 1)
            e.wait_ge(self.qx_r.sem, self.qx_r.at(i))
            e.wait_ge(self.kx_r.sem, self.kx_r.at(i))
            for b in range(16):
                ins = e.matmul(PB[b // 4][:, b % 4 * P:(b % 4 + 1) * P], self.qx[:, b].rearrange("p h s -> p (h s)"),
                               self.kx[:, b].rearrange("p c k -> p (c k)"), start=True, stop=True)
            ins.then_inc(self.s_ps.sem, 1)
            e.wait_ge(self.e_r.sem, self.e_r.at(i))
            for c in range(C):
                for t in range(4):
                    k = c * 16 + t * 4
                    ins = e.transpose(PB[4 + c][:, t * P:(t + 1) * P], self.e[:, k:k + 4, :].rearrange("p b k -> p (b k)"), n.const("ident"))
            ins.then_inc(self.pt_ps.sem, 1)
            e.wait_ge(self.pta_r.sem, self.pta_r.at(i))
            e.wait_ge(self.ptv_r.sem, self.ptv_r.at(i))
            e.wait_ge(self.vx_r.sem, self.vx_r.at(i))
            for t in range(4):
                for c in range(C):
                    ins = e.matmul(PB[t][:, c * P:(c + 1) * P], self.pt[:, c, t, :], self.vx[:, t, c].rearrange("p r j -> p (r j)"),
                                   start=True, stop=True)
            ins.then_inc(self.o_ps.sem, 1)
            e.wait_ge(self.o_r.sem, self.o_r.at(i))
            for t in range(4):
                for r in range(4):
                    b = 4 * t + r
                    ins = e.matmul(PB[4][:, b * S:(b + 1) * S], self.o[:, r, t, :], n.const("samequery"), start=True, stop=True)
            ins.then_inc(self.oT_ps.sem, 1)
            if not last:
                head(i + 1)
            e.wait_ge(self.oT_r.sem, self.oT_r.at(i))
            self.project(e, PB[7], [self.oT[:, :]], [w["wo"]], w["bo"] if self.cross else None).then_inc(self.y_ps.sem, 1)

        head(0)
        with e.Fori(0, self.iters - 1) as i:
            group(i, False)
        group(self.iters - 1, True)

    def gpsimd(self, e):
        pass

    def sync(self, e):
        if self.cross:
            e.wait_ge(self.res.sem, self.res.at(0, 0))
            self.load(e, 0)
            with e.Fori(1, self.iters) as i:
                e.wait_ge(self.ctT_ps.sem, self.ctT_ps.at(i - 1))
                self.load(e, i)

    def load(self, e, i):
        for r in range(4):
            src = self.net.ctx_dram[bass.ds(i * 16, 16), 0:S, :].rearrange("(t r) k d -> r k t d", r=4)[r]
            e.dma_start(self.ct[32 * r:32 * r + 32], src).then_inc(self.ctx_l.sem, 16)


class L1Attn(SmallAttn):

    name = "L1_attn"


class L1Xattn(SmallAttn):

    name, cross, vsteps = "L1_xattn", True, 6


class L3Attn(Block):

    name = "L3_attn"
    vsteps = 7

    def plan(self):
        self.t = self.sb("t", [P, 4, 512])
        self.kr = self.sb("kr", [P, 512])
        self.qr = self.sb("qr", [P, 512])
        self.qm = self.sb("qm", [P, 2, 512])
        self.v = self.sb("v", [P, 4, 256])
        self.sg = self.sb("sg", [P, 2, 512])
        self.st = self.sb("st", [P, 4, 8, P])
        self.sq = self.sb("sq", [P, 2, 512])
        self.rt = self.sb("rt", [P, 2, 512])
        self.o = self.sb("o", [P, 2, 512])
        self.qk_ps = self.sig("hidden_in_psum")
        self.vg_ps = self.sig("value_gate_in_psum")
        self.v_r = self.sig("hidden_ready")
        self.sg_r = self.sig("silu_ready")
        self.q_r = self.sig("spread_ready")
        self.s_ps = self.sig("scores_in_psum", 4)
        self.st_r = self.sig("decayed_ready", 4)
        self.o_ps = self.sig("heads_in_psum")
        self.sq_r = self.sig("squares_summed")
        self.ms_ps = self.sig("meansquare_in_psum")
        self.rt_r = self.sig("root_ready")
        self.o_r = self.sig("heads_ready")
        self.y_ps = self.sig("y_in_psum")

    def vector(self, e):
        self.ln_vector(e)
        n, c, PS = self.net, self.chain, self.net.PS
        seqs = lambda b: b.rearrange("p (b s) -> p b s", s=S)
        table = lambda k: n.const(k).rearrange("p (o s) -> p o s", o=1).to_broadcast([P, 16, S])
        def group(i, last):
            c.start()
            e.wait_ge(self.qk_ps.sem, self.qk_ps.at(i))
            for j, k in enumerate(("ropecos", "ropesin", "ropecos", "ropesin")):
                ins = e.tensor_tensor(seqs(self.t[:, j, :]), seqs(PS[:, 1 + j, :]), table(k), ALU.mult)
            ins.then_inc(c.sem, 1)
            e.wait_ge(c.sem, c.next(i))
            e.tensor_tensor(self.qr[:, :], self.t[:, 0, :], self.t[:, 1, :], ALU.add).then_inc(c.sem, 1)
            e.wait_ge(c.sem, c.next(i))
            e.tensor_tensor(self.kr[:, :], self.t[:, 2, :], self.t[:, 3, :], ALU.add).then_inc(c.sem, 1)
            e.wait_ge(c.sem, c.next(i))
            for h in range(2):
                ins = e.tensor_scalar(self.qm[:, h, :], self.qr[:, :], n.const("head2")[:, h:h + 1], None, ALU.mult)
            ins.then_inc(self.q_r.sem, 1)
            for j in range(4):
                e.wait_ge(self.s_ps.sem, self.s_ps.at(i, j + 1))
                b = 4 * (j % 2)
                e.tensor_tensor(self.st[:, j].rearrange("p (c h) q -> p c (h q)", h=2), PS[:, b:b + 4, 0:256],
                                n.const("decay").rearrange("p (c x) -> p c x", c=4), ALU.mult).then_inc(self.st_r.sem, 1)
            if not last:
                self.norm(e, i + 1)
            e.wait_ge(self.rt_r.sem, self.rt_r.at(i))
            e.reciprocal(self.rt[:], self.rt[:]).then_inc(c.sem, 1)
            e.wait_ge(c.sem, c.next(i))
            for j in range(2):
                ins = e.scalar_tensor_tensor(out=self.o[:, j, :], in0=PS[:, 4 + j, :], scalar=self.w["gn"], in1=self.rt[:, j, :],
                                             op0=ALU.mult, op1=ALU.mult)
                ins.then_inc(c.sem, 1)
                e.wait_ge(c.sem, c.next(i))
            e.wait_ge(self.sg_r.sem, self.sg_r.at(i))
            e.tensor_tensor(self.o[:], self.o[:], self.sg[:], ALU.mult).then_inc(self.o_r.sem, 1)
            self.add_residual(e, i, PS[:, 0, :].rearrange("p (j d) -> p j d", j=4), self.y_ps)
            c.done()

        self.norm(e, 0)
        with e.Fori(0, self.iters - 1) as i:
            group(i, False)
        group(self.iters - 1, True)

    def scalar(self, e):
        self.ln_scalar(e)
        PB, PS = self.net.PB, self.net.PS
        def group(i, last):
            e.wait_ge(self.vg_ps.sem, self.vg_ps.at(i))
            for j in range(2):
                ins = e.copy(self.v[:, 2 * j:2 * j + 2].rearrange("p a b -> p (a b)"), PB[5 + j])
            ins.then_inc(self.v_r.sem, 1)
            e.activation(self.sg[:, 0, :], PB[7], ACT.Silu)
            e.activation(self.sg[:, 1, :], PB[0], ACT.Silu).then_inc(self.sg_r.sem, 1)
            e.wait_ge(self.o_ps.sem, self.o_ps.at(i))
            e.activation(self.sq[:], PS[:, 4:6, :], ACT.Square).then_inc(self.sq_r.sem, 1)
            e.wait_ge(self.ms_ps.sem, self.ms_ps.at(i))
            e.activation(self.rt[:], PS[:, 6:8, :], ACT.Sqrt, bias=self.net.const("eps5")).then_inc(self.rt_r.sem, 1)
            if not last:
                self.copy_xnT(e, i + 1, PB[1])

        self.copy_xnT(e, 0, PB[1])
        with e.Fori(0, self.iters - 1) as i:
            group(i, False)
        group(self.iters - 1, True)

    def tensor(self, e):
        PB, w, n = self.net.PB, self.w, self.net
        def group(i, last):
            e.wait_ge(self.xnT_r.sem, self.xnT_r.at(i))
            for j, k in enumerate(("wq", "wqs", "wk", "wks")):
                ins = e.matmul(PB[1 + j], w[k], self.xnT[:, :], start=True, stop=True)
            ins.then_inc(self.qk_ps.sem, 1)
            for j in range(4):
                e.matmul(PB[5 + j // 2][:, (j % 2) * 256:(j % 2) * 256 + 256], self.xnT[:, j * P:(j + 1) * P], w["wv"], start=True, stop=True)
            e.wait_ge(self.res.sem, self.res.at(i, 0))
            e.matmul(PB[7], w["wg"][:, 0:P], self.xnT[:, :], start=True, stop=True)
            e.matmul(PB[0], w["wg"][:, P:2 * P], self.xnT[:, :], start=True, stop=True).then_inc(self.vg_ps.sem, 1)
            e.wait_ge(self.q_r.sem, self.q_r.at(i))
            e.wait_ge(self.sg_r.sem, self.sg_r.at(i))
            for j in range(4):
                if j >= 2:
                    e.wait_ge(self.st_r.sem, self.st_r.at(i, j - 1))
                t = slice(j * P, (j + 1) * P)
                for c in range(4):
                    r = slice(32 * c, 32 * c + 32)
                    for h in range(2):
                        ins = e.matmul(PB[4 * (j % 2) + c][:, h * P:(h + 1) * P], self.kr[r, t], self.qm[r, h, t], start=True, stop=True)
                ins.then_inc(self.s_ps.sem, 1)
            e.wait_ge(self.st_r.sem, self.st_r.at(i))
            for j in range(4):
                for h in range(8):
                    q = 32 * (h % 4)
                    ins = e.matmul(PB[4 + h // 4][q:q + 32, j * P:(j + 1) * P], self.v[:, j, 32 * h:32 * h + 32], self.st[:, j, h, :],
                                   start=True, stop=True)
            ins.then_inc(self.o_ps.sem, 1)
            e.wait_ge(self.sq_r.sem, self.sq_r.at(i))
            for j in range(2):
                ins = e.matmul(PB[6 + j], n.const("mean32"), self.sq[:, j, :], start=True, stop=True)
            ins.then_inc(self.ms_ps.sem, 1)
            if not last:
                self.transpose_xn(e, i + 1, PB[1])
            e.wait_ge(self.o_r.sem, self.o_r.at(i))
            self.project(e, PB[0], [self.o[:, k, :] for k in range(2)], [w["wo"][:, k * P:(k + 1) * P] for k in range(2)])\
                .then_inc(self.y_ps.sem, 1)

        self.transpose_xn(e, 0, PB[1])
        with e.Fori(0, self.iters - 1) as i:
            group(i, False)
        group(self.iters - 1, True)

    def gpsimd(self, e):
        pass

    def sync(self, e):
        pass


class Memory:

    ROWS = 4
    GROUPS = (T - 1) // ROWS
    W = 2 * D + 2 * H

    def __init__(self, net):
        n = self.ROWS
        self.net = net
        at, cols = net.where["L3_memory"]
        self.wbuf = net.sb("memory_weights", [P, cols])
        self.w = {k: self.wbuf[:, a:a + m] for k, (a, m) in at.items()}
        self.wkv = net.sb("memory_wkv", [P, self.W])
        self.bba = net.sb("memory_bba", [P, 2, H])
        self.rows = net.sb("memory_rows", [P, n, D])
        self.raw = net.sb("memory_raw", [P, n, self.W])
        self.kc = net.sb("memory_kc", [P, n, D])
        self.sq = net.sb("memory_sq", [P, n, D])
        self.ba = net.sb("memory_ba", [P, n, 2 * H])
        self.ss = net.sb("memory_ss", [P, 3, n * H])
        self.vt = net.sb("memory_vt", [P, n, D])
        self.kb = net.sb("memory_kb", [P, n, D])
        self.vb = net.sb("memory_vb", [P, n, D])
        self.ab = net.sb("memory_ab", [P, n, H])
        self.M = net.sb("memory", [P, DH, H, DH])
        self.t1 = net.sb("memory_t1", [P, DH, H, DH])
        self.t2 = net.sb("memory_t2", [P, DH, H, 4])
        self.mk = net.sb("memory_mk", [P, DH, H])
        g = self.GROUPS + 1
        self.w_l = net.sig("memory_weights_loaded", 16, 1)
        self.w_ps = net.sig("memory_weights_in_psum", 1, 1)
        self.w_r = net.sig("memory_weights_ready", 1, 1)
        self.first_ps = net.sig("memory_first_row_in_psum", 2, 1)
        self.first_r = net.sig("memory_first_row_ready", 2, 1)
        self.rows_l = net.sig("memory_rows_loaded", 16, g)
        self.bx_r = net.sig("memory_gate_logits_ready", 1, g)
        self.ba_r = net.sig("memory_gate_exps_ready", 1, g)
        self.sq_r = net.sig("memory_squares_ready", 2, g)
        self.ms_r = net.sig("memory_meansquares_ready", 2, g)
        self.rt_r = net.sig("memory_roots_ready", 2, g)
        self.kn_r = net.sig("memory_keys_normed", 1, g)
        self.in_r = net.sig("memory_inputs_ready", 1, g)
        self.scan_r = net.sig("memory_scanned", 1, g)
        self.steps = Steps(net.sig("memory_steps", 9, g))
        self.m0_r = net.sig("memory_cleared", 1, 1)
        self.scan0 = Steps(net.sig("memory_scan_steps", 8 - 1, 1))
        self.scan = Steps(net.sig("memory_scan_steps", 8 * n - 1, self.GROUPS))

    def first_tensor(self, e):
        PB, w, n = self.net.PB, self.w, self.net
        e.wait_ge(self.w_l.sem, self.w_l.at(0))
        e.matmul(PB[7][:, 0:P], w["wk"], n.const("center8"), start=True, stop=True).then_inc(self.w_ps.sem, 1)
        e.wait_ge(self.rows_l.sem, self.rows_l.at(0))
        e.transpose(PB[0][:, 0:P], self.rows[:, 0, :], n.const("ident")).then_inc(self.first_ps.sem, 1)
        e.wait_ge(self.first_r.sem, self.first_r.at(0, 1))
        e.wait_ge(self.w_r.sem, self.w_r.at(0))
        e.matmul(PB[1][:, 0:self.W], self.kc[:, 0, :], self.wkv[:, :], start=True, stop=True).then_inc(self.first_ps.sem, 1)

    def first_scalar(self, e):
        w, n = self.w, self.net
        e.wait_ge(self.w_l.sem, self.w_l.at(0))
        e.wait_ge(self.w_ps.sem, self.w_ps.at(0))
        e.copy(self.wkv[:, 0:D], n.PB[7][:, 0:P])
        e.copy(self.wkv[:, D:2 * D], w["wv"])
        e.copy(self.wkv[:, 2 * D:2 * D + H], w["wb"])
        e.copy(self.bba[:, 0, :], w["bb"])
        e.copy(self.bba[:, 1, :], w["ba"])
        e.copy(self.wkv[:, 2 * D + H:self.W], w["wa"]).then_inc(self.w_r.sem, 1)
        e.wait_ge(self.first_ps.sem, self.first_ps.at(0, 1))
        e.copy(self.kc[:, 0, :], n.PB[0][:, 0:P]).then_inc(self.first_r.sem, 1)
        e.wait_ge(self.first_ps.sem, self.first_ps.at(0, 2))
        e.copy(self.raw[:, 0, :], n.PB[1][:, 0:self.W]).then_inc(self.first_r.sem, 1)
        self.gates_scalar(e, 0, 1)
        self.squares_scalar(e, 0, 1)
        self.units_scalar(e, 0, 1)

    def first_vector(self, e):
        e.wait_ge(self.w_r.sem, self.w_r.at(0))
        e.wait_ge(self.first_r.sem, self.first_r.at(0, 2))
        self.gates_vector(e, 0, 1)
        self.stats_vector(e, 0, 1)
        self.normed_vector(e, 0, 1)
        self.units_vector(e, 0, 1)
        self.inputs_vector(e, 0, 1)

    def row_product(self, e, out, rowT):
        return e.matmul(out, rowT, self.wkv[:, :], start=True, stop=True)

    def gates_vector(self, e, g, n):
        e.tensor_tensor(self.ba[:, 0:n, :], self.raw[:, 0:n, 2 * D:self.W],
                        self.bba[:].rearrange("p (o two) h -> p o (two h)", o=1).to_broadcast([P, n, 2 * H]), ALU.add).then_inc(self.bx_r.sem, 1)

    def gates_scalar(self, e, g, n):
        e.wait_ge(self.bx_r.sem, self.bx_r.at(g))
        e.activation(self.ba[:, 0:n, :], self.ba[:, 0:n, :], ACT.Exp, scale=-1.0).then_inc(self.ba_r.sem, 1)

    def squares_scalar(self, e, g, n):
        e.activation(self.sq[:, 0:n, :], self.raw[:, 0:n, 0:D], ACT.Square).then_inc(self.sq_r.sem, 1)
        e.wait_ge(self.ms_r.sem, self.ms_r.at(g, 1))
        e.activation(self.ss[:, 1, 0:n * H], self.ss[:, 0, 0:n * H], ACT.Sqrt).then_inc(self.rt_r.sem, 1)

    def stats_vector(self, e, g, n):
        s, ss, ba = self.steps, self.ss[:, :, 0:n * H], self.ba[:, 0:n, :]
        s.start()
        e.wait_ge(self.sq_r.sem, self.sq_r.at(g, 1))
        e.tensor_reduce(ss[:, 0, :], self.heads(self.sq, n), AX.X, ALU.add).then_inc(s.sem, 1)
        e.wait_ge(s.sem, s.next(g))
        e.tensor_scalar(ss[:, 0, :], ss[:, 0, :], 1.0 / DH, LN_EPS, ALU.mult, ALU.add).then_inc(self.ms_r.sem, 1)
        e.tensor_tensor(self.kc[:, 0:n, :], self.raw[:, 0:n, 0:D], self.every_row("gk", n), ALU.mult)
        e.wait_ge(self.ba_r.sem, self.ba_r.at(g))
        e.tensor_scalar(ba, ba, 1.0, None, ALU.add).then_inc(s.sem, 1)
        e.wait_ge(s.sem, s.next(g))
        e.reciprocal(ba, ba).then_inc(s.sem, 1)
        e.wait_ge(s.sem, s.next(g))
        for t in range(n):
            ins = e.tensor_tensor(self.vt[:, t, :].rearrange("p (h j) -> p h j", j=DH), self.raw[:, t, D:2 * D].rearrange("p (h j) -> p h j", j=DH),
                                  self.ba[:, t, 0:H].rearrange("p (h o) -> p h o", o=1).to_broadcast([P, H, DH]), ALU.mult)
        ins.then_inc(s.sem, 1)
        e.wait_ge(s.sem, s.next(g))

    def heads(self, t, n):
        return t[:, 0:n, :].rearrange("p t (h j) -> p (t h) j", j=DH)

    def every_head(self, t, n):
        return t.rearrange("p (n o) -> p n o", o=1).to_broadcast([P, n * H, DH])

    def every_row(self, name, n):
        return self.w[name].rearrange("p (o d) -> p o d", o=1).to_broadcast([P, n, D])

    def normed_vector(self, e, g, n):
        s, ss = self.steps, self.ss[:, :, 0:n * H]
        e.wait_ge(self.rt_r.sem, self.rt_r.at(g, 1))
        e.reciprocal(ss[:, 2, :], ss[:, 1, :]).then_inc(s.sem, 1)
        e.wait_ge(s.sem, s.next(g))
        e.tensor_tensor(self.heads(self.kc, n), self.heads(self.kc, n), self.every_head(ss[:, 2, :], n), ALU.mult).then_inc(s.sem, 1)
        e.wait_ge(s.sem, s.next(g))
        e.tensor_tensor(self.kc[:, 0:n, :], self.kc[:, 0:n, :], self.every_row("bk", n), ALU.add).then_inc(self.kn_r.sem, 1)

    def units_scalar(self, e, g, n):
        e.wait_ge(self.kn_r.sem, self.kn_r.at(g))
        e.activation(self.sq[:, 0:n, :], self.kc[:, 0:n, :], ACT.Square).then_inc(self.sq_r.sem, 1)
        e.wait_ge(self.ms_r.sem, self.ms_r.at(g, 2))
        e.activation(self.ss[:, 1, 0:n * H], self.ss[:, 0, 0:n * H], ACT.Sqrt).then_inc(self.rt_r.sem, 1)

    def units_vector(self, e, g, n):
        s, ss = self.steps, self.ss[:, :, 0:n * H]
        e.wait_ge(self.sq_r.sem, self.sq_r.at(g, 2))
        e.tensor_reduce(ss[:, 0, :], self.heads(self.sq, n), AX.X, ALU.add).then_inc(self.ms_r.sem, 1)

    def inputs_vector(self, e, g, n):
        s, ss = self.steps, self.ss[:, :, 0:n * H]
        e.wait_ge(self.rt_r.sem, self.rt_r.at(g, 2))
        e.tensor_scalar(ss[:, 1, :], ss[:, 1, :], 1e-12, None, ALU.max).then_inc(s.sem, 1)
        e.wait_ge(s.sem, s.next(g))
        e.reciprocal(ss[:, 2, :], ss[:, 1, :]).then_inc(s.sem, 1)
        e.wait_ge(s.sem, s.next(g))
        if n > 1:
            e.wait_ge(self.scan_r.sem, self.scan_r.at(g, 0))
        e.tensor_tensor(self.heads(self.kb, n), self.heads(self.kc, n), self.every_head(ss[:, 2, :], n), ALU.mult).then_inc(s.sem, 1)
        e.wait_ge(s.sem, s.next(g))
        e.tensor_copy(self.ab[:, 0:n, :], self.ba[:, 0:n, H:2 * H])
        e.tensor_copy(self.vb[:, 0:n, :], self.vt[:, 0:n, :]).then_inc(self.in_r.sem, 1)
        s.done()

    def scan_pool(self, e, g, n, c, i):
        full = [P, DH, H, DH]
        c.start()
        e.wait_ge(self.in_r.sem, self.in_r.at(g))
        if n > 1:
            e.wait_ge(self.scan_r.sem, self.scan_r.at(g, 0))
        for t in range(n):
            k = self.kb[:, t, :].rearrange("p (o h j) -> p o h j", h=H, o=1).to_broadcast(full)
            a = self.ab[:, t, :].rearrange("p (o h) -> p o h", o=1).to_broadcast([P, DH, H])
            v = self.vb[:, t, :].rearrange("p (h i) -> p i h", h=H)
            e.tensor_tensor(self.t1[:], self.M[:], k, ALU.mult).then_inc(c.sem, 1)
            e.wait_ge(c.sem, c.next(i))
            e.tensor_tensor(self.t2[:], self.t1[:, :, :, 0:4], self.t1[:, :, :, 4:8], ALU.add).then_inc(c.sem, 1)
            e.wait_ge(c.sem, c.next(i))
            e.tensor_tensor(self.t1[:, :, :, 0:2], self.t2[:, :, :, 0:2], self.t2[:, :, :, 2:4], ALU.add).then_inc(c.sem, 1)
            e.wait_ge(c.sem, c.next(i))
            e.tensor_tensor(self.mk[:], self.t1[:, :, :, 0], self.t1[:, :, :, 1], ALU.add).then_inc(c.sem, 1)
            e.wait_ge(c.sem, c.next(i))
            e.tensor_tensor(self.mk[:], self.mk[:], a, ALU.mult).then_inc(c.sem, 1)
            e.wait_ge(c.sem, c.next(i))
            e.tensor_tensor(self.mk[:], v, self.mk[:], ALU.subtract).then_inc(c.sem, 1)
            e.wait_ge(c.sem, c.next(i))
            e.tensor_tensor(self.t1[:], self.mk[:].rearrange("p i (h o) -> p i h o", o=1).to_broadcast(full), k, ALU.mult).then_inc(c.sem, 1)
            e.wait_ge(c.sem, c.next(i))
            ins = e.tensor_tensor(self.M[:], self.M[:], self.t1[:], ALU.add)
            if t == n - 1:
                ins.then_inc(self.scan_r.sem, 1)
            else:
                ins.then_inc(c.sem, 1)
                e.wait_ge(c.sem, c.next(i))
        c.done()

    def first_pool(self, e):
        e.memset(self.M[:], 0.0).then_inc(self.m0_r.sem, 1)
        e.wait_ge(self.m0_r.sem, self.m0_r.at(0))
        self.scan_pool(e, 0, 1, self.scan0, 0)


def late(i, k, per, n):
    return not isinstance(i, int) or i * per + k >= n


class CrossAttn(Block):

    iters, group = TILES, 1
    KT = T // P

    def plan_common(self):
        self.qx = self.sb("qx", [P, SEQS, 16, S])
        self.cx = [self.sb(f"cx{b}", [P, self.KT, D]) for b in range(SEQS)]
        self.cT = [self.sb(f"cT{b}", [P, T + 1 + P]) for b in range(2)]
        self.mw = self.sb("maskwords", [P, T], U32)
        self.mb = self.sb("maskbias", [P, SEQS * T], BF16)
        self.onesb = self.sb("onesb", [P, P], BF16)
        self.e = [self.sb(f"e{k}", [P, 2, T]) for k in range(2)]
        self.pt = [self.sb(f"pt{k}", [P, self.KT, 2, P]) for k in range(2)]
        self.pl = [self.sb(f"pl{k}", [2, P]) for k in range(2)]
        self.nm = self.sb("negmax", [P, 8, 2])
        self.rs = self.sb("rowsum", [P, 8, 2])
        self.mask_l = self.sig("mask_loaded", 16)
        self.ones_r = self.sig("scaled_bias_ready", 1, 1)
        self.cx_l = [self.sig(f"context{b}_loaded", 16 * self.cx_dmas) for b in range(SEQS)]
        self.mb_r = self.sig("maskbias_ready")
        self.cT_ps = self.sig("ctxT_in_psum", 4)
        self.cT_r = self.sig("ctxT_ready", 4)
        self.s_ps = self.sig("scores_in_psum", 8)
        self.nm_r = self.sig("exponents_ready", 8)
        self.e_r = self.sig("exps_ready", 8)
        self.pt_ps = self.sig("probsT_in_psum", 8)
        self.pt_r = self.sig("probsT_low_ready", 8)
        self.o_ps = self.sig("heads_in_psum", 8)
        self.o_r = self.sig("heads_ready", 8)
        self.qx_r = self.sig("spread_ready")
        self.y_ps = self.sig("y_in_psum")
        self.added = Steps(self.sig("add_steps"))
        self.mem = self.net.memory

    def maskbias(self, e, i):
        e.wait_ge(self.mask_l.sem, self.mask_l.at(i))
        m = self.mw[:, :].bitcast(U8)
        (s1, s2) = self.mask_ops
        e.tensor_scalar(self.mb[:, :], m, s1, s2, ALU.add, ALU.mult).then_inc(self.mb_r.sem, 1)

    def context_T(self, e, i, b):
        if late(i, b, 4, 1):
            self.bank6_free(e, i, b)
        e.wait_ge(self.cx_l[b].sem, self.cx_l[b].at(i))
        for k in range(self.KT):
            e.transpose(self.net.PB[6][:, k * P:(k + 1) * P], self.cx[b][:, k, :], self.net.const("ident"))
        if b == 0:
            e.wait_ge(self.mem.rows_l.sem, self.mem.rows_l.at(i + self.group0))
        e.transpose(self.net.PB[6][:, T + 1:T + 1 + P], self.mem.rows[:, b, :], self.net.const("ident"))
        e.matmul(self.net.PB[6][:, T - 1:T + 1], self.last_row(b), self.net.const("ones")[0:1, 0:2], start=True, stop=True)\
            .then_inc(self.cT_ps.sem, 1)

    def copy_context_T(self, e, i, b):
        e.wait_ge(self.cT_ps.sem, self.cT_ps.at(i, b + 1))
        if late(i, b, 4, 2):
            self.cT_free(e, i, b)
        e.copy(self.cT[b % 2][:, :], self.net.PB[6][:, 0:T + 1 + P]).then_inc(self.cT_r.sem, 1)

    def scores(self, e, i, u):
        b, half = u // 2, u % 2
        if late(i, u, 8, 2):
            e.wait_ge(self.pt_r.sem, self.pt_r.at(i, u - 1))
        for cc in range(2):
            c = 2 * half + cc
            bank = self.net.PB[2 * (u % 2) + cc][:, 0:T]
            r = self.mask_row(c)
            e.matmul(bank, self.onesb[r:r + 1, :], self.mb[r:r + 1, b * T:(b + 1) * T], start=True, stop=False)
            ins = self.score_product(e, bank, b, c)
        ins.then_inc(self.s_ps.sem, 1)

    def negmax(self, e, i, u):
        e.wait_ge(self.s_ps.sem, self.s_ps.at(i, u + 1))
        e.tensor_reduce(self.nm[:, u, :], self.net.PS[:, 2 * (u % 2):2 * (u % 2) + 2, 0:T], AX.X, ALU.max, negate=True)\
            .then_inc(self.nm_r.sem, 1)

    def exps(self, e, i, u):
        e.wait_ge(self.nm_r.sem, self.nm_r.at(i, u + 1))
        if late(i, u, 8, 2):
            e.wait_ge(self.pt_ps.sem, self.pt_ps.at(i, u - 1))
        for cc in range(2):
            ins = e.activation(self.e[u % 2][:, cc, :], self.net.PB[2 * (u % 2) + cc][:, 0:T], ACT.Exp, bias=self.nm[:, u, cc:cc + 1],
                               accum_out=self.rs[:, u, cc:cc + 1])
        ins.then_inc(self.e_r.sem, 1)

    def transposes(self, e, i, u):
        if late(i, u, 8, 2):
            e.wait_ge(self.pt_r.sem, self.pt_r.at(i, u - 1))
        for k in range(self.KT):
            for cc in range(2):
                a = (2 * k + cc) * P
                e.transpose(self.net.PB[4 + u % 2][:, a:a + P], self.e[u % 2][:, cc, k * P:(k + 1) * P], self.net.const("ident"))
        e.matmul(self.net.PB[2 * (u % 2)][0:2, 384:512], self.e[u % 2][:, :, T - 1:T].rearrange("p c o -> p (c o)"),
                 self.net.const("ident"), start=True, stop=True).then_inc(self.pt_ps.sem, 1)

    def copy_probs(self, e, i, u):
        e.wait_ge(self.pt_ps.sem, self.pt_ps.at(i, u + 1))
        if late(i, u, 8, 2):
            e.wait_ge(self.o_ps.sem, self.o_ps.at(i, u - 1))
        e.copy(self.pl[u % 2][:, :], self.net.PB[2 * (u % 2)][0:2, 384:512])
        e.copy(self.pt[u % 2][:].rearrange("p k c h -> p (k c h)"), self.net.PB[4 + u % 2]).then_inc(self.pt_r.sem, 1)

    def load_masks(self, e, i):
        e.dma_start(self.mw[:, :], self.mask[bass.ds(i, 1), :].to_broadcast([P, T])).then_inc(self.mask_l.sem, 16)

    def sync(self, e):
        e.wait_ge(self.res.sem, self.res.at(0, 0))
        e.wait_ge(self.ones_r.sem, self.ones_r.at(0))
        self.load_rows(e, 0)
        self.load_masks(e, 0)
        for b in range(SEQS):
            self.load(e, 0, b)
        with e.Fori(1, self.iters) as i:
            e.wait_ge(self.mb_r.sem, self.mb_r.at(i - 1))
            self.load_masks(e, i)
            for b in range(SEQS):
                self.slot_free(e, i - 1, b)
                self.load(e, i, b)
                if b == 1:
                    e.wait_ge(self.cT_ps.sem, self.cT_ps.at(i - 1, 4))
                    self.load_rows(e, i)

    def next_seq(self, i, b, last):
        return (i, b + 1) if b < 3 else None if last else (i + 1, 0)

    def norm_tile(self, e, i):
        n = self.net
        t = bass.ds(i, 1)
        e.wait_ge(self.res.sem, self.res.at(0, 0))
        e.tensor_scalar(self.xn[:, 0, :], n.X[:, t, :], n.mean[:, t], n.rstd[:, t], ALU.subtract, ALU.mult).then_inc(self.xn_r.sem, 1)

    def add_tile(self, e, i, bank):
        n, c = self.net, self.added
        e.wait_ge(self.y_ps.sem, self.y_ps.at(i))
        xs = n.X[:, bass.ds(i, 1), :]
        c.start()
        e.tensor_tensor(xs, bank[:, 384:512].rearrange("p (j d) -> p j d", j=1), xs, ALU.add).then_inc(c.sem, 1)
        e.wait_ge(c.sem, c.next(i))
        e.bn_stats(n.stats[:, bass.ds(i, 1), :], n.X[:, bass.ds(i, 1), :]).then_inc(self.res.sem, 1)

    def load_rows(self, e, i):
        g = i + self.group0
        if self.group0 == 1 and isinstance(i, int) and i == 0:
            e.wait_ge(self.mem.first_ps.sem, self.mem.first_ps.at(0, 1))
        e.dma_start(self.mem.rows[:], self.net.ctx_dram[:, bass.ds(g * Memory.ROWS - (Memory.ROWS - 1), Memory.ROWS), :])\
            .then_inc(self.mem.rows_l.sem, 16)

    def gpsimd(self, e):
        with e.Fori(0, self.iters) as i:
            self.mem.scan_pool(e, i + self.group0, Memory.ROWS, self.mem.scan, i + (self.group0 - 1))


class L0Xattn(CrossAttn):

    name = "L0_xattn"
    vsteps = 11
    cx_dmas = 2
    group0 = 1
    mask_ops = (0.0, MASKED)

    def plan(self):
        self.mask = self.net.masks[0]
        self.plan_common()
        self.cl = self.sb("cl", [1, SEQS, D])
        self.bqs = self.sb("bqs", [P, 1])
        self.qT = self.sb("qT", [P, SEQS, S])
        self.kT = [self.sb(f"kT{b}", [P, T]) for b in range(2)]
        self.v = [self.sb(f"v{b}", [P, self.KT, D]) for b in range(2)]
        self.vl = [self.sb(f"vl{b}", [2, D]) for b in range(2)]
        self.own = self.sb("own", [P, 4, S])
        self.o = self.sb("o", [P, SEQS, S])
        self.oT = self.sb("oT", [P, P])
        self.q_ps = self.sig("hidden_in_psum")
        self.q_r = self.sig("hidden_ready")
        self.kT_ps = self.sig("keysT_in_psum", 4)
        self.kT_r = self.sig("keysT_ready", 4)
        self.v_ps = self.sig("values_in_psum", 4)
        self.v_r = self.sig("values_ready", 4)
        self.p_r = self.sig("activated_ready", 8)
        self.joined = Steps(self.sig("join_steps"))
        self.oT_r = self.sig("headsT_ready")

    def mask_row(self, c):
        return 32 * c

    def bank6_free(self, e, i, b):
        e.wait_ge(self.v_r.sem, self.v_r.at(i, b))

    def cT_free(self, e, i, b):
        e.wait_ge(self.o_ps.sem, self.o_ps.at(i, 2 * b - 3))

    def last_row(self, b):
        return self.cl[0:1, b, :]

    def slot_free(self, e, i, b):
        e.wait_ge(self.cT_ps.sem, self.cT_ps.at(i, b + 1))

    def load(self, e, i, b):
        src = self.net.ctx_dram[bass.ds(i * SEQS + b, 1)]
        e.dma_start(self.cx[b][:], src[:, 0:self.KT * P, :].rearrange("o (k p) d -> p (o k) d", p=P)).then_inc(self.cx_l[b].sem, 16)
        e.dma_start(self.cl[0:1, b, :], src[:, T - 1, :]).then_inc(self.cx_l[b].sem, 16)

    def score_product(self, e, bank, b, c):
        r = slice(32 * c, 32 * c + 32)
        return e.matmul(bank, self.qx[r, b, 0:4, :].rearrange("p h s -> p (h s)"), self.kT[b % 2][r, :], start=False, stop=True)

    def keysT(self, e, i, b):
        e.wait_ge(self.cT_r.sem, self.cT_r.at(i, b + 1))
        e.matmul(self.net.PB[6][:, 0:T], self.w["wk"], self.cT[b % 2][:, 0:T], start=True, stop=True).then_inc(self.kT_ps.sem, 1)

    def values(self, e, i, b):
        e.wait_ge(self.kT_r.sem, self.kT_r.at(i, b + 1))
        for k in range(self.KT):
            e.matmul(self.net.PB[6][:, k * P:(k + 1) * P], self.cT[b % 2][:, k * P:(k + 1) * P], self.w["wv"], start=True, stop=True)
        e.matmul(self.net.PB[6][0:2, 2 * P:3 * P], self.cT[b % 2][:, T - 1:T + 1], self.w["wv"], start=True, stop=True)\
            .then_inc(self.v_ps.sem, 1)

    def heads(self, e, i, u):
        b, half = u // 2, u % 2
        e.wait_ge(self.pt_r.sem, self.pt_r.at(i, u + 1))
        if half == 0:
            e.wait_ge(self.v_r.sem, self.v_r.at(i, b + 1))
        if late(i, u, 8, 1):
            e.wait_ge(self.o_r.sem, self.o_r.at(i, u))
        for cc in range(2):
            c = 2 * half + cc
            f = slice(32 * c, 32 * c + 32)
            o = self.net.PB[7][f, 0:P]
            for k in range(self.KT):
                e.matmul(o, self.v[b % 2][:, k, f], self.pt[u % 2][:, k, cc, :], start=(k == 0), stop=False)
            ins = e.matmul(o, self.vl[b % 2][0:2, f], self.pl[u % 2][0:2, :], start=False, stop=True)
        if half == 0:
            ins = self.mem.row_product(e, self.net.PB[7][:, P:P + Memory.W], self.cT[b % 2][:, T + 1:T + 1 + P])
        ins.then_inc(self.o_ps.sem, 1)

    def query(self, e, i):
        e.wait_ge(self.xnT_r.sem, self.xnT_r.at(i))
        e.matmul(self.net.PB[1][:, 384:512], self.w["wq"], self.xnT[:, :], start=True, stop=True).then_inc(self.q_ps.sem, 1)

    def output(self, e, i):
        e.wait_ge(self.oT_r.sem, self.oT_r.at(i))
        self.project(e, self.net.PB[3][:, 384:512], [self.oT[:, :]], [self.w["wo"]], self.w["bo"], tiles=1).then_inc(self.y_ps.sem, 1)

    def tensor(self, e):
        PB = self.net.PB
        self.mem.first_tensor(e)

        def first_scores(i):
            e.wait_ge(self.qx_r.sem, self.qx_r.at(i))
            e.wait_ge(self.mb_r.sem, self.mb_r.at(i))
            self.scores(e, i, 0)

        def tile(i, first, last):
            for u in range(8):
                b, half = u // 2, u % 2
                seq = self.next_seq(i, b, last)
                if half == 0 and seq:
                    self.context_T(e, *seq)
                if half == 1 and seq:
                    self.values(e, *seq)
                if u == 3 and not last:
                    e.wait_ge(self.xnT_r.sem, self.xnT_r.at(i + 1))
                if u == 4 and not first:
                    e.wait_ge(self.res.sem, self.res.at(i - 1))
                if u == 5 and not last:
                    e.wait_ge(self.q_r.sem, self.q_r.at(i + 1))
                if u + 1 < 8:
                    self.scores(e, i, u + 1)
                elif not last:
                    first_scores(i + 1)
                e.wait_ge(self.p_r.sem, self.p_r.at(i, u + 1))
                self.transposes(e, i, u)
                if u == 2 and not last:
                    self.transpose_xn(e, i + 1, PB[1][:, 384:512])
                if u == 4 and not last:
                    self.query(e, i + 1)
                if half == 0 and seq:
                    self.keysT(e, *seq)
                if u == 3 and not first:
                    self.output(e, i - 1)
                if u:
                    self.heads(e, i, u - 1)
                elif not first:
                    self.heads(e, i - 1, 7)

        self.transpose_xn(e, 0, PB[1][:, 384:512])
        self.context_T(e, 0, 0)
        self.keysT(e, 0, 0)
        self.query(e, 0)
        self.values(e, 0, 0)
        first_scores(0)
        tile(0, True, False)
        with e.Fori(1, TILES - 1) as i:
            tile(i, False, False)
        tile(TILES - 1, False, True)
        self.heads(e, TILES - 1, 7)
        self.output(e, TILES - 1)

    def scalar(self, e):
        self.ln_scalar(e)
        PB, w, m = self.net.PB, self.w, self.mem
        e.mul(self.bqs[:, :], w["bq"], QSCALE)
        e.copy(self.onesb[:, :], self.net.const("ones")).then_inc(self.ones_r.sem, 1)
        e.wait_ge(self.ones_r.sem, self.ones_r.at(0))
        m.first_scalar(e)

        def keys(i, b):
            e.wait_ge(self.kT_ps.sem, self.kT_ps.at(i, b + 1))
            if late(i, b, 4, 2):
                e.wait_ge(self.s_ps.sem, self.s_ps.at(i, 2 * b - 2))
            e.activation(self.kT[b % 2][:, :], PB[6][:, 0:T], ACT.Identity, bias=w["bk"]).then_inc(self.kT_r.sem, 1)

        def query(i):
            e.wait_ge(self.q_ps.sem, self.q_ps.at(i))
            e.activation(self.qT[:].rearrange("p b s -> p (b s)"), PB[1][:, 384:512], ACT.Identity, bias=self.bqs[:, :], scale=QSCALE)\
                .then_inc(self.q_r.sem, 1)

        def bias_heads(i):
            e.wait_ge(self.o_r.sem, self.o_r.at(i))
            e.activation(self.oT[:, :], self.o[:].rearrange("p b s -> p (b s)"), ACT.Identity, bias=w["bv"]).then_inc(self.oT_r.sem, 1)

        def tile(i, first, last):
            g = i + self.group0
            for u in range(8):
                b, half = u // 2, u % 2
                seq = self.next_seq(i, b, last)
                self.exps(e, i, u)
                if half == 0 and seq:
                    self.copy_context_T(e, *seq)
                self.copy_probs(e, i, u)
                if half == 0 and seq:
                    keys(*seq)
                if u == 0 and not first:
                    m.squares_scalar(e, g - 1, m.ROWS)
                if u == 1 and not first:
                    bias_heads(i - 1)
                if u == 2 and not last:
                    self.copy_xnT(e, i + 1, PB[1][:, 384:512])
                if u == 2 and not first:
                    m.units_scalar(e, g - 1, m.ROWS)
                if u == 4 and not last:
                    query(i + 1)
                if u == 7:
                    m.gates_scalar(e, g, m.ROWS)

        self.copy_xnT(e, 0, PB[1][:, 384:512])
        self.copy_context_T(e, 0, 0)
        keys(0, 0)
        query(0)
        tile(0, True, False)
        with e.Fori(1, TILES - 1) as i:
            tile(i, False, False)
        tile(TILES - 1, False, True)
        g = TILES - 1 + self.group0
        m.squares_scalar(e, g, m.ROWS)
        bias_heads(TILES - 1)
        m.units_scalar(e, g, m.ROWS)

    def vector(self, e):
        self.ln_vector(e)
        n, c, PB, m = self.net, self.chain, self.net.PB, self.mem
        m.first_vector(e)

        def values(i, b):
            e.wait_ge(self.v_ps.sem, self.v_ps.at(i, b + 1))
            if late(i, b, 4, 2):
                e.wait_ge(self.o_ps.sem, self.o_ps.at(i, 2 * b - 2))
            e.tensor_copy(self.v[b % 2][:].rearrange("p k d -> p (k d)"), PB[6][:, 0:2 * P])
            e.tensor_tensor(self.vl[b % 2][:, :], PB[6][0:2, 2 * P:3 * P], n.const("rowquarter")[0:2, :], ALU.mult).then_inc(self.v_r.sem, 1)

        def keep_own(i, u, c, j):
            b, half = u // 2, u % 2
            e.wait_ge(self.o_ps.sem, self.o_ps.at(i, u + 1))
            if half == 0:
                e.tensor_copy(self.mem.raw[:, b, :], PB[7][:, P:P + Memory.W]).then_inc(self.o_r.sem, 1)
                return
            e.tensor_tensor(self.own[:], PB[7][:, 0:P].rearrange("p (h s) -> p h s", h=4),
                            n.const("head4").rearrange("p (h o) -> p h o", o=1).to_broadcast([P, 4, S]), ALU.mult).then_inc(c.sem, 1)
            e.wait_ge(c.sem, c.next(j))
            if b == 0 and late(i, 0, 1, 1):
                e.wait_ge(self.oT_r.sem, self.oT_r.at(i - 1))
            e.tensor_reduce(self.o[:, b, :], self.own[:].rearrange("p h s -> p s h"), AX.X, ALU.add).then_inc(self.o_r.sem, 1)

        def spread(i):
            e.wait_ge(self.q_r.sem, self.q_r.at(i))
            e.tensor_tensor(self.qx[:, :, 0:4, :], self.qT[:].rearrange("p b (o s) -> p b o s", o=1).to_broadcast([P, SEQS, 4, S]),
                            n.const("head4").rearrange("p (a h b) -> p a h b", a=1, b=1).to_broadcast([P, SEQS, 4, S]), ALU.mult)\
                .then_inc(self.qx_r.sem, 1)

        def tile(i, first, last):
            g = i + self.group0
            c.start()
            self.joined.start()
            for u in range(8):
                seq = self.next_seq(i, u // 2, last)
                e.wait_ge(self.e_r.sem, self.e_r.at(i, u + 1))
                e.reciprocal(self.rs[:, u, :], self.rs[:, u, :]).then_inc(c.sem, 1)
                e.wait_ge(c.sem, c.next(i))
                for cc in range(2):
                    ins = e.tensor_scalar(self.e[u % 2][:, cc, :], self.e[u % 2][:, cc, :], self.rs[:, u, cc:cc + 1], None, ALU.mult)
                ins.then_inc(self.p_r.sem, 1)
                if u % 2 == 1 and seq:
                    values(*seq)
                if u + 1 < 8:
                    self.negmax(e, i, u + 1)
                elif not last:
                    self.negmax(e, i + 1, 0)
                if u == 6 and not last:
                    spread(i + 1)
                    self.maskbias(e, i + 1)
                if u:
                    keep_own(i, u - 1, c, i)
                elif not first:
                    keep_own(i - 1, 7, self.joined, i - 1)
                if u == 7:
                    e.wait_ge(self.o_r.sem, self.o_r.at(i, 7))
                    m.gates_vector(e, g, m.ROWS)
                if u == 1 and not last:
                    self.norm_tile(e, i + 1)
                if u == 3 and not first:
                    self.add_tile(e, i - 1, PB[3])
                if not first and u < 4:
                    (m.stats_vector, m.normed_vector, m.units_vector, m.inputs_vector)[u](e, g - 1, m.ROWS)
            c.done()

        self.norm_tile(e, 0)
        self.maskbias(e, 0)
        values(0, 0)
        spread(0)
        self.negmax(e, 0, 0)
        tile(0, True, False)
        with e.Fori(1, TILES - 1) as i:
            tile(i, False, False)
        tile(TILES - 1, False, True)
        g = TILES - 1 + self.group0
        self.joined.start()
        keep_own(TILES - 1, 7, self.joined, TILES - 1)
        m.stats_vector(e, g, m.ROWS)
        m.normed_vector(e, g, m.ROWS)
        self.add_tile(e, TILES - 1, PB[3])
        m.units_vector(e, g, m.ROWS)
        m.inputs_vector(e, g, m.ROWS)

    def gpsimd(self, e):
        self.mem.first_pool(e)
        super().gpsimd(e)


class L2Xattn(CrossAttn):

    name = "L2_xattn"
    vsteps = 8
    cx_dmas = 3
    group0 = 1 + TILES
    mask_ops = (-1.0, -MASKED)

    def plan(self):
        self.mask = self.net.masks[1]
        self.plan_common()
        self.A = self.sb("wqk", [P, 16 * P])
        self.WVO = self.sb("wvo", [P, 16 * P])
        self.cl = [self.sb(f"cl{b}", [2, 2, D]) for b in range(SEQS)]
        self.oT = self.sb("oT", [P, 16, P])
        self.w_ps = self.sig("weights_product_in_psum", 1, 1)
        self.w_r = self.sig("weights_product_ready", 1, 1)
        self.cl_r = self.sig("last_rows_cleared", 1, 1)
        self.qs = self.sb("qs", [P, 4, 512])
        self.q_ps = self.sig("hidden_in_psum", 4)
        self.q_r = self.sig("hidden_ready", 4)
        self.qa_r = self.sig("keys_spread_ready")
        self.p_r = self.sig("activated_ready", 8)
        self.row_ps = self.sig("memory_row_in_psum", 4)
        self.row_r = self.sig("memory_row_ready", 4)

    def mask_row(self, c):
        return 0

    def bank6_free(self, e, i, b):
        e.wait_ge(self.cT_r.sem, self.cT_r.at(i, b))
        if late(i, b, 4, 2):
            e.wait_ge(self.row_r.sem, self.row_r.at(i, b - 1))

    def cT_free(self, e, i, b):
        e.wait_ge(self.s_ps.sem, self.s_ps.at(i, 2 * b - 2))
        e.wait_ge(self.row_ps.sem, self.row_ps.at(i, b - 1))

    def last_row(self, b):
        return self.cl[b][0:1, 0, :]

    def slot_free(self, e, i, b):
        e.wait_ge(self.o_ps.sem, self.o_ps.at(i, 2 * b + 2))

    def load(self, e, i, b):
        src = self.net.ctx_dram[bass.ds(i * SEQS + b, 1)]
        e.dma_start(self.cx[b][:], src[:, 0:self.KT * P, :].rearrange("o (k p) d -> p (o k) d", p=P)).then_inc(self.cx_l[b].sem, 16)
        for c in range(2):
            e.dma_start(self.cl[b][c:c + 1, c, :], src[:, T - 1, :]).then_inc(self.cx_l[b].sem, 16)

    def score_product(self, e, bank, b, c):
        return e.matmul(bank, self.qx[:, b, 4 * c:4 * c + 4, :].rearrange("p h s -> p (h s)"), self.cT[b % 2][:, 0:T], start=False, stop=True)

    def heads(self, e, i, u):
        b = u // 2
        e.wait_ge(self.pt_r.sem, self.pt_r.at(i, u + 1))
        if late(i, u, 8, 1):
            e.wait_ge(self.o_r.sem, self.o_r.at(i, u))
        o = self.net.PB[7]
        block = lambda k, **f: e.matmul(o[:, 0:2 * P], self.cx[b][:, k, :], self.pt[u % 2][:, k].rearrange("p c h -> p (c h)"), **f)
        block(0, start=True, stop=False)
        for cc in range(2):
            e.matmul(o[:, cc * P:(cc + 1) * P], self.cl[b][0:2, cc, :], self.pl[u % 2][0:2, :], start=False, stop=False, skip_group_check=True)
        ins = block(1, start=False, stop=True)
        ins.then_inc(self.o_ps.sem, 1)

    def tensor(self, e):
        PB, w, n = self.net.PB, self.w, self.net
        for h in range(16):
            a = slice(h * P, (h + 1) * P)
            o = slice(h % 4 * P, (h % 4 + 1) * P)
            e.matmul(PB[h // 4][:, o], w["wq"][0:64, a], w["wk"][0:64, a], start=True, stop=True)
            ins = e.matmul(PB[4 + h // 4][:, o], w["wv"][0:64, a], w["wo"][0:64, a], start=True, stop=True)
        ins.then_inc(self.w_ps.sem, 1)
        e.wait_ge(self.w_r.sem, self.w_r.at(0))

        def queries(i, k):
            if k == 0:
                e.wait_ge(self.xnT_r.sem, self.xnT_r.at(i))
            for j in range(4):
                a = (4 * k + j) * P
                ins = e.matmul(PB[6][:, j * P:(j + 1) * P], self.A[:, a:a + P], self.xnT[:, :], start=True, stop=True)
            ins.then_inc(self.q_ps.sem, 1)

        def first_scores(i):
            e.wait_ge(self.qx_r.sem, self.qx_r.at(i))
            e.wait_ge(self.qa_r.sem, self.qa_r.at(i))
            e.wait_ge(self.mb_r.sem, self.mb_r.at(i))
            e.wait_ge(self.cT_r.sem, self.cT_r.at(i, 1))
            self.scores(e, i, 0)

        def output(i):
            e.wait_ge(self.o_r.sem, self.o_r.at(i))
            o = PB[3][:, 384:512]
            e.matmul(o, n.const("ones")[0:1, :], w["bo"][0:1, :], start=True, stop=False)
            for h in range(16):
                ins = e.matmul(o, self.oT[:, h, :], self.WVO[:, h * P:(h + 1) * P], start=False, stop=(h == 15))
            ins.then_inc(self.y_ps.sem, 1)

        def tile(i, first, last):
            for u in range(8):
                b, half = u // 2, u % 2
                seq = self.next_seq(i, b, last)
                if u in (3, 4, 5, 6) and not last:
                    e.wait_ge(self.q_r.sem, self.q_r.at(i + 1, u - 2))
                if half == 0 and seq:
                    self.context_T(e, *seq)
                if half == 1:
                    if seq:
                        e.wait_ge(self.cT_r.sem, self.cT_r.at(seq[0], seq[1] + 1))
                    self.mem.row_product(e, PB[6][:, 0:Memory.W], self.cT[b % 2][:, T + 1:T + 1 + P]).then_inc(self.row_ps.sem, 1)
                if u == 1 and not last:
                    e.wait_ge(self.xnT_r.sem, self.xnT_r.at(i + 1))
                if u == 2 and not first:
                    e.wait_ge(self.res.sem, self.res.at(i - 1))
                if u + 1 < 8:
                    self.scores(e, i, u + 1)
                elif not last:
                    first_scores(i + 1)
                e.wait_ge(self.p_r.sem, self.p_r.at(i, u + 1))
                self.transposes(e, i, u)
                if u == 0 and not last:
                    self.transpose_xn(e, i + 1, PB[1][:, 384:512])
                if u in (2, 4) and not last:
                    e.wait_ge(self.cT_r.sem, self.cT_r.at(i, b + 2))
                    queries(i + 1, u - 2)
                if u in (3, 5) and not last:
                    e.wait_ge(self.row_r.sem, self.row_r.at(i, b + 1))
                    queries(i + 1, u - 2)
                if u == 1 and not first:
                    output(i - 1)
                if u:
                    self.heads(e, i, u - 1)
                elif not first:
                    self.heads(e, i - 1, 7)

        self.transpose_xn(e, 0, PB[1][:, 384:512])
        self.context_T(e, 0, 0)
        e.wait_ge(self.cT_r.sem, self.cT_r.at(0, 1))
        for k in range(4):
            if k:
                e.wait_ge(self.q_r.sem, self.q_r.at(0, k))
            queries(0, k)
        first_scores(0)
        tile(0, True, False)
        with e.Fori(1, TILES - 1) as i:
            tile(i, False, False)
        tile(TILES - 1, False, True)
        self.heads(e, TILES - 1, 7)
        output(TILES - 1)

    def spread_q(self, f, k):
        return f(self.qx[:, :, 4 * k:4 * k + 4, :], self.qs[:, k, :].rearrange("p (h b s) -> p b h s", h=4, b=SEQS))

    def scalar(self, e):
        self.ln_scalar(e)
        PB = self.net.PB
        e.wait_ge(self.w_ps.sem, self.w_ps.at(0))
        for k in range(4):
            a = slice(k * 512, (k + 1) * 512)
            e.mul(self.A[:, a], PB[k], 0.125)
            ins = e.copy(self.WVO[:, a], PB[4 + k])
        ins.then_inc(self.w_r.sem, 1)
        e.copy(self.onesb[:, :], self.net.const("ones")).then_inc(self.ones_r.sem, 1)
        m = self.mem

        def queries(i, k):
            e.wait_ge(self.q_ps.sem, self.q_ps.at(i, k + 1))
            e.copy(self.qs[:, k, :], PB[6]).then_inc(self.q_r.sem, 1)

        def spread(i):
            self.spread_q(e.copy, 0)
            self.spread_q(e.copy, 1).then_inc(self.qa_r.sem, 1)

        def tile(i, first, last):
            g = i + self.group0
            for u in range(8):
                b, half = u // 2, u % 2
                seq = self.next_seq(i, b, last)
                self.exps(e, i, u)
                if half == 0 and seq:
                    self.copy_context_T(e, *seq)
                self.copy_probs(e, i, u)
                if u == 0 and not last:
                    self.copy_xnT(e, i + 1, PB[1][:, 384:512])
                if u in (2, 3, 4, 5) and not last:
                    queries(i + 1, u - 2)
                if u == 0 and not first:
                    m.squares_scalar(e, g - 1, m.ROWS)
                if u == 2 and not first:
                    m.units_scalar(e, g - 1, m.ROWS)
                if u == 6 and not last:
                    e.wait_ge(self.s_ps.sem, self.s_ps.at(i))
                    spread(i + 1)
                if u == 7:
                    m.gates_scalar(e, g, m.ROWS)

        self.copy_xnT(e, 0, PB[1][:, 384:512])
        self.copy_context_T(e, 0, 0)
        for k in range(4):
            queries(0, k)
        e.wait_ge(self.q_r.sem, self.q_r.at(0))
        spread(0)
        tile(0, True, False)
        with e.Fori(1, TILES - 1) as i:
            tile(i, False, False)
        tile(TILES - 1, False, True)
        g = TILES - 1 + self.group0
        m.squares_scalar(e, g, m.ROWS)
        m.units_scalar(e, g, m.ROWS)

    def vector(self, e):
        self.ln_vector(e)
        n, c, PB = self.net, self.chain, self.net.PB
        for b in range(SEQS):
            ins = e.memset(self.cl[b][:], 0.0)
        ins.then_inc(self.cl_r.sem, 1)

        def copy_heads(i, u):
            b, half = u // 2, u % 2
            e.wait_ge(self.o_ps.sem, self.o_ps.at(i, u + 1))
            e.tensor_copy(self.oT[:, 8 * half:8 * half + 8, b * S:(b + 1) * S], PB[7][:, 0:2 * P].rearrange("p (h s) -> p h s", s=S))\
                .then_inc(self.o_r.sem, 1)

        m = self.mem

        def spread(i):
            e.wait_ge(self.q_r.sem, self.q_r.at(i))
            self.spread_q(e.tensor_copy, 2)
            self.spread_q(e.tensor_copy, 3).then_inc(self.qx_r.sem, 1)

        def tile(i, first, last):
            g = i + self.group0
            c.start()
            for u in range(8):
                e.wait_ge(self.e_r.sem, self.e_r.at(i, u + 1))
                e.reciprocal(self.rs[:, u, :], self.rs[:, u, :]).then_inc(c.sem, 1)
                e.wait_ge(c.sem, c.next(i))
                for cc in range(2):
                    ins = e.tensor_scalar(self.e[u % 2][:, cc, :], self.e[u % 2][:, cc, :], self.rs[:, u, cc:cc + 1], None, ALU.mult)
                ins.then_inc(self.p_r.sem, 1)
                if u % 2:
                    e.wait_ge(self.row_ps.sem, self.row_ps.at(i, u // 2 + 1))
                    e.tensor_copy(m.raw[:, u // 2, :], PB[6][:, 0:Memory.W]).then_inc(self.row_r.sem, 1)
                if u == 7:
                    e.wait_ge(self.row_r.sem, self.row_r.at(i, 4))
                    m.gates_vector(e, g, m.ROWS)
                if u + 1 < 8:
                    self.negmax(e, i, u + 1)
                elif not last:
                    self.negmax(e, i + 1, 0)
                if u == 0 and not last:
                    self.norm_tile(e, i + 1)
                if u == 6 and not last:
                    spread(i + 1)
                    self.maskbias(e, i + 1)
                if u == 1 and not first:
                    self.add_tile(e, i - 1, PB[3])
                if u:
                    copy_heads(i, u - 1)
                elif not first:
                    copy_heads(i - 1, 7)
                if not first and u < 4:
                    (m.stats_vector, m.normed_vector, m.units_vector, m.inputs_vector)[u](e, g - 1, m.ROWS)
            c.done()

        self.norm_tile(e, 0)
        self.maskbias(e, 0)
        spread(0)
        self.negmax(e, 0, 0)
        tile(0, True, False)
        with e.Fori(1, TILES - 1) as i:
            tile(i, False, False)
        tile(TILES - 1, False, True)
        g = TILES - 1 + self.group0
        copy_heads(TILES - 1, 7)
        m.stats_vector(e, g, m.ROWS)
        m.normed_vector(e, g, m.ROWS)
        self.add_tile(e, TILES - 1, PB[3])
        m.units_vector(e, g, m.ROWS)
        m.inputs_vector(e, g, m.ROWS)

    def sync(self, e):
        e.wait_ge(self.cl_r.sem, self.cl_r.at(0))
        super().sync(e)


class L3Xattn(Block):

    name = "L3_xattn"
    vsteps = 5

    def plan(self):
        self.wqc = self.sb("wqc", [P, P])
        self.ss = self.sb("ss", [P, 3, 4 * H])
        self.MT = self.sb("MT", [P, DH, P])
        self.Mbd = self.sb("Mbd", [P, 16, H, DH])
        self.qc = self.sb("qc", [P, 4, D])
        self.qn = self.sb("qn", [P, 4, D])
        self.qT = self.sb("qT", [P, 512])
        self.oT = self.sb("oT", [P, 512])
        self.w_ps = self.sig("weights_product_in_psum", 1, 1)
        self.w_r = self.sig("weights_product_ready", 1, 1)
        self.MT_ps = self.sig("heads_in_psum", 1, 1)
        self.MT_r = self.sig("heads_ready", 1, 1)
        self.q_ps = self.sig("hidden_in_psum")
        self.qsq_r = self.sig("silu_ready")
        self.qms_r = self.sig("logits_ready")
        self.qrt_r = self.sig("probs_ready")
        self.qn_r = self.sig("spread_ready")
        self.qT_ps = self.sig("probsT_in_psum")
        self.qT_r = self.sig("probsT_low_ready")
        self.mbd_r = self.sig("expert_added")
        self.o_ps = self.sig("headsT_in_psum")
        self.oT_r = self.sig("headsT_ready")
        self.y_ps = self.sig("y_in_psum")

    def gpsimd(self, e):
        pass

    def sync(self, e):
        pass

    def tensor(self, e):
        PB, w, n = self.net.PB, self.w, self.net
        e.matmul(PB[7][:, 0:P], w["wq"], n.const("center8"), start=True, stop=True).then_inc(self.w_ps.sem, 1)
        m = n.memory
        e.wait_ge(m.scan_r.sem, m.scan_r.at(m.GROUPS))
        for k in range(DH):
            ins = e.transpose(PB[1 + k // 4][:, k % 4 * P:(k % 4 + 1) * P], m.M[:, k].rearrange("p h j -> p (h j)"), n.const("ident"))
        ins.then_inc(self.MT_ps.sem, 1)
        e.wait_ge(self.w_r.sem, self.w_r.at(0))
        def group(i, last):
            e.wait_ge(self.xnT_r.sem, self.xnT_r.at(i))
            for j in range(4):
                ins = e.matmul(PB[3][:, j * P:(j + 1) * P], self.xnT[:, j * P:(j + 1) * P], self.wqc[:, :], start=True, stop=True)
            ins.then_inc(self.q_ps.sem, 1)
            e.wait_ge(self.qn_r.sem, self.qn_r.at(i))
            for j in range(4):
                ins = e.transpose(PB[4][:, j * P:(j + 1) * P], self.qn[:, j, :], n.const("ident"))
            ins.then_inc(self.qT_ps.sem, 1)
            e.wait_ge(self.qT_r.sem, self.qT_r.at(i))
            e.wait_ge(self.mbd_r.sem, self.mbd_r.at(i))
            for b in range(16):
                ins = e.matmul(PB[5][:, b * S:(b + 1) * S], self.Mbd[:, b].rearrange("p h i -> p (h i)"), self.qT[:, b * S:(b + 1) * S],
                               start=True, stop=True)
            ins.then_inc(self.o_ps.sem, 1)
            if not last:
                self.transpose_xn(e, i + 1, PB[0])
            e.wait_ge(self.oT_r.sem, self.oT_r.at(i))
            self.project(e, PB[6], [self.oT[:, :]], [w["wo"]], w["bo"]).then_inc(self.y_ps.sem, 1)

        self.transpose_xn(e, 0, PB[0])
        with e.Fori(0, self.iters - 1) as i:
            group(i, False)
        group(self.iters - 1, True)

    def scalar(self, e):
        self.ln_scalar(e)
        n, w, PS = self.net, self.w, self.net.PS
        e.wait_ge(self.w_ps.sem, self.w_ps.at(0))
        e.copy(self.wqc[:, :], PS[:, 7, 0:P]).then_inc(self.w_r.sem, 1)
        e.wait_ge(self.MT_ps.sem, self.MT_ps.at(0))
        for k in range(2):
            ins = e.copy(self.MT[:, 4 * k:4 * k + 4, :].rearrange("p i b -> p (i b)"), n.PB[1 + k])
        ins.then_inc(self.MT_r.sem, 1)
        def group(i, last):
            e.wait_ge(self.q_ps.sem, self.q_ps.at(i))
            e.activation(self.qn[:].rearrange("p j d -> p (j d)"), n.PB[3], ACT.Square).then_inc(self.qsq_r.sem, 1)
            e.wait_ge(self.qms_r.sem, self.qms_r.at(i))
            e.activation(self.ss[:, 1, :], self.ss[:, 0, :], ACT.Sqrt).then_inc(self.qrt_r.sem, 1)
            e.wait_ge(self.qT_ps.sem, self.qT_ps.at(i))
            e.copy(self.qT[:, :], n.PB[4]).then_inc(self.qT_r.sem, 1)
            e.wait_ge(self.o_ps.sem, self.o_ps.at(i))
            e.copy(self.oT[:, :], n.PB[5]).then_inc(self.oT_r.sem, 1)
            if not last:
                self.copy_xnT(e, i + 1, n.PB[0])

        self.copy_xnT(e, 0, n.PB[0])
        with e.Fori(0, self.iters - 1) as i:
            group(i, False)
        group(self.iters - 1, True)

    def vector(self, e):
        self.ln_vector(e)
        n, w, PS, c = self.net, self.w, self.net.PS, self.chain
        e.wait_ge(self.MT_r.sem, self.MT_r.at(0))
        heads = lambda a: a.rearrange("p t (h j) -> p (t h) j", j=DH)
        wide = lambda a: a.rearrange("p (n o) -> p n o", o=1).to_broadcast([P, 4 * H, DH])
        rows = lambda a: a.rearrange("p (o d) -> p o d", o=1).to_broadcast([P, 4, D])
        def group(i, last):
            c.start()
            for h in range(2):
                ins = e.tensor_tensor(self.Mbd[:, 8 * h:8 * h + 8], self.MT[:, :, bass.ds(i * 16 + 8 * h, 8)].rearrange("p i (b o) -> p b o i", o=1).to_broadcast([P, 8, H, DH]),
                                      n.const("headcol").rearrange("p (a h b) -> p a h b", a=1, b=1).to_broadcast([P, 8, H, DH]), ALU.mult)
            ins.then_inc(self.mbd_r.sem, 1)
            e.wait_ge(self.qsq_r.sem, self.qsq_r.at(i))
            e.tensor_reduce(self.ss[:, 0, :], heads(self.qn[:]), AX.X, ALU.add).then_inc(c.sem, 1)
            e.wait_ge(c.sem, c.next(i))
            e.tensor_scalar(self.ss[:, 0, :], self.ss[:, 0, :], 1.0 / DH, LN_EPS, ALU.mult, ALU.add).then_inc(self.qms_r.sem, 1)
            e.tensor_tensor(self.qc[:], PS[:, 3, :].rearrange("p (j d) -> p j d", j=4), rows(w["gq"]), ALU.mult).then_inc(c.sem, 1)
            e.wait_ge(c.sem, c.next(i))
            e.wait_ge(self.qrt_r.sem, self.qrt_r.at(i))
            e.reciprocal(self.ss[:, 2, :], self.ss[:, 1, :]).then_inc(c.sem, 1)
            e.wait_ge(c.sem, c.next(i))
            e.tensor_tensor(heads(self.qc[:]), heads(self.qc[:]), wide(self.ss[:, 2, :]), ALU.mult).then_inc(c.sem, 1)
            e.wait_ge(c.sem, c.next(i))
            e.tensor_tensor(self.qn[:], self.qc[:], rows(w["bq"]), ALU.add).then_inc(self.qn_r.sem, 1)
            if not last:
                self.norm(e, i + 1)
            self.add_residual(e, i, PS[:, 6, :].rearrange("p (j d) -> p j d", j=4), self.y_ps)
            c.done()

        self.norm(e, 0)
        with e.Fori(0, self.iters - 1) as i:
            group(i, False)
        group(self.iters - 1, True)



BLOCKS = [L0Ffn, L0Attn, L2Attn, L1Ffn, L2Ffn, L3Ffn, L1Attn, L1Xattn, L3Attn, L0Xattn, L2Xattn, L3Xattn]


def build(nc, x, context, mask0, mask1, consts, consts_at, wdram, where, out, names):
    blocks = {c.name: c for c in BLOCKS}
    with ExitStack() as ctx:
        net = Net(nc, ctx, wdram, where, consts_at, context, (mask0, mask1))
        loaded = net.sig("x_loaded", 16, 2)
        first = net.sig("residual_added", 1)
        stored = net.sig("output_stored", 16)
        net.memory = Memory(net)
        layers = [blocks[n](net, i) for i, n in enumerate(names)]
        xd = x.rearrange("(t p) d -> p t d", p=P)
        od = out.rearrange("(t p) d -> p t d", p=P)
        block = ctx.enter_context(nc.Block())

        @block.sync
        def _(e):
            e.dma_start(net.X[:], xd).then_inc(loaded.sem, 16)
            e.dma_start(net.K[:], consts).then_inc(loaded.sem, 16)
            m = net.memory
            e.dma_start(m.wbuf[:], wdram["L3_memory"]).then_inc(m.w_l.sem, 16)
            e.dma_start(m.rows[:, 0:1, :], context[:, 0:1, :]).then_inc(m.rows_l.sem, 16)
            for i, l in enumerate(layers):
                if i >= 1:
                    e.wait_ge(layers[i - 1].res.sem, layers[i - 1].res.at(0, 0))
                n = where[l.name][1]
                e.dma_start(net.W[i % 2][:, 0:n], wdram[l.name]).then_inc(l.weights.sem, 16)
                l.sync(e)
            last = layers[-1].res
            e.wait_ge(last.sem, last.at(layers[-1].iters - 1))
            e.dma_start(od, net.X[:]).then_inc(stored.sem, 16)
            e.wait_ge(stored.sem, stored.at(0))

        @block.vector
        def _(e):
            e.wait_ge(loaded.sem, loaded.at(1))
            for t in range(TILES):
                ins = e.bn_stats(net.stats[:, t, :], net.X[:, t, :])
            ins.then_inc(first.sem, 1)
            for l in layers:
                l.vector(e)

        @block.scalar
        def _(e):
            e.wait_ge(loaded.sem, loaded.at(1))
            for l in layers:
                l.scalar(e)

        @block.tensor
        def _(e):
            e.wait_ge(loaded.sem, loaded.at(1))
            for l in layers:
                e.wait_ge(l.res.sem, l.res.at(0, 0))
                e.wait_ge(l.weights.sem, l.weights.at(0))
                l.tensor(e)

        @block.gpsimd
        def _(e):
            e.wait_ge(loaded.sem, loaded.at(1))
            for l in layers:
                l.gpsimd(e)


NAMES = ["L0_xattn", "L0_attn", "L0_ffn", "L1_xattn", "L1_attn", "L1_ffn",
         "L2_xattn", "L2_attn", "L2_ffn", "L3_xattn", "L3_attn", "L3_ffn"]


def kernel(**inputs):
    import concourse.bacc as bacc
    from concourse.bass_utils import run_bass_kernel_spmd

    names = NAMES
    nc = bacc.Bacc("TRN2", target_bir_lowering=False, num_devices=1)
    a = {k: np.asarray(v) for k, v in inputs.items()}
    consts, consts_at = constants()
    arrays = {"x": a["x"].reshape(B * S, D), "context": a["ctx_1024"], "consts": consts,
              "mask0": a["mask_BxS2_bk0"].reshape(TILES, -1).view(np.uint32), "mask1": a["mask_BxS2_bf1"].reshape(TILES, -1).view(np.uint32)}
    parts = layouts(a)
    where = {k: columns(v) for k, v in parts.items()}
    for k in names + ["L3_memory"]:
        arrays["w_" + k] = np.concatenate([np.asarray(w) for _, w in parts[k]], 1)
    arrays = {k: np.ascontiguousarray(v) for k, v in arrays.items()}
    d = {k: nc.dram_tensor("in_" + k, v.shape, mybir.dt.from_np(v.dtype), kind="ExternalInput").ap() for k, v in arrays.items()}
    out = nc.dram_tensor("out", (B * S, D), F32, kind="ExternalOutput").ap()
    build(nc, d["x"], d["context"], d["mask0"], d["mask1"], d["consts"], consts_at,
          {k: d["w_" + k] for k in names + ["L3_memory"]}, {k: where[k] for k in names + ["L3_memory"]}, out, names)
    r = run_bass_kernel_spmd(nc, [{"in_" + k: v for k, v in arrays.items()}], core_ids=[0])
    return r.results[0]["out"].reshape(B, S, D)
```
